# Optimizing a Trainium2 kernel written in Bass

```python
import numpy as np
import jax
import jax.numpy as jnp

def _softmax(x, axis=-1):
    return jax.nn.softmax(x, axis=axis)

def _gelu(x):
    return jax.nn.gelu(x, approximate=True)

def _silu(x):
    return jax.nn.silu(x)

def _sigmoid(x):
    return jax.nn.sigmoid(x)

def _layernorm(x, axis=-1, eps=1e-05):
    m = jnp.mean(x, axis=axis, keepdims=True)
    v = jnp.var(x, axis=axis, keepdims=True)
    return (x - m) / jnp.sqrt(v + eps)

def _scatter_add(tgt, idx, src, axis=0):
    return tgt.at[idx].add(src)

def _segment_sum(src, seg, n):
    return jax.ops.segment_sum(src, seg, n)
kernel_name = 'mk_seq_preln_d4_jaxref_r8_61da82'

def setup_inputs(seed: int=0):
    np.random.seed(seed)
    _w = jnp.asarray

    def _L0_attn_setup():
        import jax, jax.numpy as jnp
        import numpy as np
        D_MODEL = 128
        H = 4
        DK = 128
        DV = 256
        HQK = DK // H
        HV = DV // H
        LOW_RANK = 32
        CHUNK = 16
        GATE_NORM = 32.0
        GATE_MULT = 1.0
        EPS = 1e-05

        def gla_fused_chunk(q, k, v, g, chunk=CHUNK):
            B, Hh, N, Dk = q.shape
            Dv = v.shape[-1]
            q = q * Dk ** (-0.5)
            nc = N // chunk

            def to_chunks(t, d):
                return t.reshape(B, Hh, nc, chunk, d).transpose(2, 0, 1, 3, 4)
            qc, kc, vc, gc = (to_chunks(q, Dk), to_chunks(k, Dk), to_chunks(v, Dv), to_chunks(g, Dk))
            bc = jnp.cumsum(gc, axis=-2)
            causal = jnp.tril(jnp.ones((chunk, chunk), bool))

            def step(S, inp):
                qi, ki, vi, bi = inp
                o_inter = jnp.einsum('bhtd,bhde->bhte', qi * jnp.exp(bi), S)
                diff = bi[:, :, :, None, :] - bi[:, :, None, :, :]
                diff = jnp.where(causal[None, None, :, :, None], diff, -jnp.inf)
                A = jnp.einsum('bhtd,bhjd,bhtjd->bhtj', qi, ki, jnp.exp(diff))
                o_intra = jnp.einsum('bhtj,bhje->bhte', A, vi)
                blast = bi[:, :, -1:, :]
                kdec = ki * jnp.exp(blast - bi)
                S_new = jnp.exp(blast)[:, :, 0, :, None] * S + jnp.einsum('bhtd,bhte->bhde', kdec, vi)
                return (S_new, o_inter + o_intra)
            S0 = jnp.zeros((B, Hh, Dk, Dv), q.dtype)
            _, o = jax.lax.scan(step, S0, (qc, kc, vc, bc))
            return o.transpose(1, 2, 0, 3, 4).reshape(B, Hh, N, Dv)
        key = jax.random.key(seed)
        ks = jax.random.split(key, 10)
        B, N = (2, 512)
        s = 0.02
        return {'x': jax.random.normal(ks[0], (B, N, D_MODEL), jnp.float32), 'Wq': jax.random.normal(ks[1], (DK, D_MODEL), jnp.float32) * s, 'Wk': jax.random.normal(ks[2], (DK, D_MODEL), jnp.float32) * s, 'Wv': jax.random.normal(ks[3], (DV, D_MODEL), jnp.float32) * s, 'Wg': jax.random.normal(ks[4], (DV, D_MODEL), jnp.float32) * s, 'Wgk1': jax.random.normal(ks[5], (LOW_RANK, D_MODEL), jnp.float32) * s, 'Wgk2': jax.random.normal(ks[6], (DK, LOW_RANK), jnp.float32) * s, 'bgk2': jax.random.normal(ks[7], (DK,), jnp.float32) * 0.1, 'Wout': jax.random.normal(ks[8], (D_MODEL, DV), jnp.float32) * s, 'rms_w': jnp.ones((HV,), jnp.float32)}
    _L0_attn_in = _L0_attn_setup()

    def _L0_ffn_setup():
        import jax, jax.numpy as jnp
        import numpy as np
        B, S, H = (2, 128, 128)
        E, F = (16, 64)
        G, TOPK_G, TOPK = (4, 2, 4)
        N_SHARED = 2
        ROUTE_SCALE = 1.0
        FS = N_SHARED * F

        def _gate(x, w_gate):
            T = x.shape[0]
            scores = jax.nn.sigmoid(x @ w_gate.T)
            sv = scores.reshape(T, G, E // G)
            group_scores = jax.lax.top_k(sv, 2)[0].sum(-1)
            top_groups = jax.lax.top_k(group_scores, TOPK_G)[1]
            allowed = jnp.zeros((T, G), dtype=bool).at[jnp.arange(T)[:, None], top_groups].set(True)
            masked = jnp.where(allowed[:, :, None], sv, -jnp.inf).reshape(T, E)
            _, idx = jax.lax.top_k(masked, TOPK)
            w = jnp.take_along_axis(scores, idx, axis=1)
            w = w / (w.sum(-1, keepdims=True) + 1e-06) * ROUTE_SCALE
            return (w, idx)

        def _swiglu(x, w1, w3, w2):
            return jax.nn.silu(x @ w1.T) * (x @ w3.T) @ w2.T
        key = jax.random.key(seed)
        ks = jax.random.split(key, 8)
        scale = 0.02
        return {'hidden_states': jax.random.normal(ks[0], (B, S, H), dtype=jnp.float32), 'w_gate': jax.random.normal(ks[1], (E, H), dtype=jnp.float32) * scale, 'w1_e': jax.random.normal(ks[2], (E, F, H), dtype=jnp.float32) * scale, 'w3_e': jax.random.normal(ks[3], (E, F, H), dtype=jnp.float32) * scale, 'w2_e': jax.random.normal(ks[4], (E, H, F), dtype=jnp.float32) * scale, 'w1_s': jax.random.normal(ks[5], (FS, H), dtype=jnp.float32) * scale, 'w3_s': jax.random.normal(ks[6], (FS, H), dtype=jnp.float32) * scale, 'w2_s': jax.random.normal(ks[7], (H, FS), dtype=jnp.float32) * scale}
    _L0_ffn_in = _L0_ffn_setup()

    def _L1_attn_setup():
        import jax, jax.numpy as jnp
        import numpy as np
        B, T, D, H, R = (1, 512, 128, 16, 64)
        HD = D // H
        STD = 0.02

        def _low_rank_proj(x, a, b):
            mid = jnp.einsum('btd,hdr->bhtr', x, a)
            return jnp.einsum('bhtr,hrd->bhtd', mid, b)
        key = jax.random.key(seed)
        ks = jax.random.split(key, 8)
        return {'hidden_states': jax.random.normal(ks[0], (B, T, D), jnp.float32), 'q_a': STD * jax.random.normal(ks[1], (H, D, R), jnp.float32), 'q_b': STD * jax.random.normal(ks[2], (H, R, HD), jnp.float32), 'k_a': STD * jax.random.normal(ks[3], (H, D, R), jnp.float32), 'k_b': STD * jax.random.normal(ks[4], (H, R, HD), jnp.float32), 'v_w': STD * jax.random.normal(ks[5], (D, D), jnp.float32), 'v_b': jnp.zeros((D,), jnp.float32), 'o_w': STD * jax.random.normal(ks[6], (D, D), jnp.float32), 'o_b': jnp.zeros((D,), jnp.float32)}
    _L1_attn_in = _L1_attn_setup()

    def _L1_ffn_setup():
        import jax, jax.numpy as jnp
        import numpy as np
        B, T, C, H, E = (1, 32, 128, 256, 8)
        STD = 0.02
        key = jax.random.key(seed)
        ks = jax.random.split(key, 8)
        f32 = jnp.float32
        return {'x': jax.random.normal(ks[0], (B, T, C), f32), 'up': jax.random.normal(ks[1], (E, H, C), f32) * STD, 'gate': jax.random.normal(ks[2], (E, H, C), f32) * STD, 'down': jax.random.normal(ks[3], (E, C, H), f32) * STD, 'router': jax.random.normal(ks[4], (E, C), f32) * STD, 'w_up_s': jax.random.normal(ks[5], (H, C), f32) * STD, 'w_gate_s': jax.random.normal(ks[6], (H, C), f32) * STD, 'w_down_s': jax.random.normal(ks[7], (C, H), f32) * STD}
    _L1_ffn_in = _L1_ffn_setup()

    def _L2_attn_setup():
        import jax, jax.numpy as jnp
        import numpy as np
        B, S, D, H, I, A = (2, 256, 128, 16, 512, 2)
        HD = D // H

        def _gen_param(sub, Wl, W, Bp):
            p = jnp.einsum('a...,a->...', sub, Wl[0])
            return jnp.tanh(p) * W + Bp

        def _student_linear(x, sub_w, Wl_w, W_w, B_w, sub_b, Wl_b, W_b, B_b):
            w = _gen_param(sub_w, Wl_w, W_w, B_w)
            b = _gen_param(sub_b, Wl_b, W_b, B_b)
            return x @ w.T + b

        def _layernorm(x, g, b, eps=1e-05):
            m = jnp.mean(x, axis=-1, keepdims=True)
            v = jnp.mean((x - m) ** 2, axis=-1, keepdims=True)
            return (x - m) * jax.lax.rsqrt(v + eps) * g + b

        def _gelu_new(x):
            c = 0.7978845608028654
            return 0.5 * x * (1.0 + jnp.tanh(c * (x + 0.044715 * x ** 3)))

        def _block(hs, ln1_g, ln1_b, ln2_g, ln2_b, *p):
            ca, cp, cf, cm = (p[0:8], p[8:16], p[16:24], p[24:32])
            b_, s_, d_ = hs.shape
            h = _layernorm(hs, ln1_g, ln1_b)
            qkv = _student_linear(h, *ca)
            q, k, v = jnp.split(qkv, 3, axis=-1)
            split = lambda t: t.reshape(b_, s_, H, HD).transpose(0, 2, 1, 3)
            q, k, v = (split(q), split(k), split(v))
            scores = jnp.einsum('bhqd,bhkd->bhqk', q, k) / float(HD) ** 0.5
            causal = jnp.tril(jnp.ones((s_, s_), dtype=bool))
            scores = jnp.where(causal, scores, jnp.asarray(-10000.0, scores.dtype))
            attn = jax.nn.softmax(scores, axis=-1)
            o = jnp.einsum('bhqk,bhkd->bhqd', attn, v)
            o = o.transpose(0, 2, 1, 3).reshape(b_, s_, d_)
            o = _student_linear(o, *cp)
            hs = hs + o
            h2 = _layernorm(hs, ln2_g, ln2_b)
            m = _student_linear(h2, *cf)
            m = _gelu_new(m)
            m = _student_linear(m, *cm)
            return hs + m
        key = jax.random.key(seed)
        ks = iter(jax.random.split(key, 32))

        def lin(out_f, in_f):
            return {'sub_w': jax.random.normal(next(ks), (A, out_f, in_f), jnp.float32) * 0.02, 'Wl_w': jax.random.normal(next(ks), (1, A), jnp.float32) * 0.5, 'W_w': jnp.ones((out_f, in_f), jnp.float32), 'B_w': jnp.zeros((out_f, in_f), jnp.float32), 'sub_b': jax.random.normal(next(ks), (A, out_f), jnp.float32) * 0.02, 'Wl_b': jax.random.normal(next(ks), (1, A), jnp.float32) * 0.5, 'W_b': jnp.ones((out_f,), jnp.float32), 'B_b': jnp.zeros((out_f,), jnp.float32)}
        inp = {'hs': jax.random.normal(next(ks), (B, S, D), jnp.float32)}
        for name, (o, i) in (('ca', (3 * D, D)), ('cp', (D, D)), ('cf', (I, D)), ('cm', (D, I))):
            for k2, v in lin(o, i).items():
                inp[name + '_' + k2] = v
        inp['ln1_g'] = jnp.ones((D,), jnp.float32)
        inp['ln1_b'] = jnp.zeros((D,), jnp.float32)
        inp['ln2_g'] = jnp.ones((D,), jnp.float32)
        inp['ln2_b'] = jnp.zeros((D,), jnp.float32)
        return inp
    _L2_attn_in = _L2_attn_setup()

    def _L2_ffn_setup():
        import jax, jax.numpy as jnp
        import numpy as np
        D_IN, D_HID = (128, 512)

        def _ternary(key, shape):
            return jax.random.randint(key, shape, -1, 2).astype(jnp.float32)

        def _tlin(x, w, s):
            return jnp.einsum('bsi,oi->bso', x, w) * s
        key = jax.random.key(seed)
        ks = jax.random.split(key, 12)
        inv = lambda fan: 1.0 / np.sqrt(fan).astype(np.float32)
        return {'x': jax.random.normal(ks[0], (4, 256, D_IN), dtype=jnp.float32), 'w1_w': _ternary(ks[1], (D_HID, D_IN)), 'w1_s': jax.random.uniform(ks[2], (D_HID,), dtype=jnp.float32) * inv(D_IN), 'w2_w': _ternary(ks[3], (D_HID, D_IN)), 'w2_s': jax.random.uniform(ks[4], (D_HID,), dtype=jnp.float32) * inv(D_IN), 'h1_w': _ternary(ks[5], (D_HID, D_HID)), 'h1_s': jax.random.uniform(ks[6], (D_HID,), dtype=jnp.float32) * inv(D_HID), 'h2_w': _ternary(ks[7], (D_HID, D_HID)), 'h2_s': jax.random.uniform(ks[8], (D_HID,), dtype=jnp.float32) * inv(D_HID), 'w3_w': _ternary(ks[9], (D_IN, D_HID)), 'w3_s': jax.random.uniform(ks[10], (D_IN,), dtype=jnp.float32) * inv(D_HID)}
    _L2_ffn_in = _L2_ffn_setup()

    def _L3_attn_setup():
        import jax, jax.numpy as jnp
        import numpy as np
        EMB = 128
        H = 16
        DH = 64
        key = jax.random.key(seed)
        ks = jax.random.split(key, 9)
        s = 1.0 / np.sqrt(EMB)
        so = 1.0 / np.sqrt(H * DH)
        return {'x': jax.random.normal(ks[0], (4, 256, EMB), dtype=jnp.float32), 'Wq': jax.random.uniform(ks[1], (H * DH, EMB), jnp.float32, -s, s), 'bq': jax.random.uniform(ks[2], (H * DH,), jnp.float32, -s, s), 'Wk': jax.random.uniform(ks[3], (H * DH, EMB), jnp.float32, -s, s), 'bk': jax.random.uniform(ks[4], (H * DH,), jnp.float32, -s, s), 'Wv': jax.random.uniform(ks[5], (H * DH, EMB), jnp.float32, -s, s), 'bv': jax.random.uniform(ks[6], (H * DH,), jnp.float32, -s, s), 'Wo': jax.random.uniform(ks[7], (EMB, H * DH), jnp.float32, -so, so), 'bo': jax.random.uniform(ks[8], (EMB,), jnp.float32, -so, so)}
    _L3_attn_in = _L3_attn_setup()

    def _L3_ffn_setup():
        import jax, jax.numpy as jnp
        import numpy as np
        B, S, D = (2, 256, 128)
        E, K, H = (8, 2, 512)
        CAP_FACTOR = 1.0

        def _moe_forward(x, wg, w1, b1, w2, b2):
            Bb, Ss, Dd = x.shape
            T = Bb * Ss
            cap = int(K * CAP_FACTOR * ((T + E - 1) // E))
            xt = x.reshape(T, Dd)
            logits = xt @ wg
            scores = jax.nn.softmax(logits, axis=-1)
            gates_k, idx_k = jax.lax.top_k(scores, K)
            gates_k = gates_k / jnp.sum(gates_k, axis=-1, keepdims=True)
            masks = jax.nn.one_hot(idx_k, E, dtype=jnp.int32)
            m = jnp.transpose(masks, (1, 0, 2)).reshape(K * T, E)
            locs_full = jnp.cumsum(m, axis=0) - 1
            loc = jnp.sum(locs_full * m, axis=-1)
            loc = loc.reshape(K, T).T
            valid = (loc < cap).astype(xt.dtype)
            loc_c = jnp.clip(loc, 0, cap - 1)
            contrib = (xt[:, None, :] * valid[:, :, None]).reshape(T * K, Dd)
            disp = jnp.zeros((E, cap, Dd), xt.dtype)
            disp = disp.at[idx_k.reshape(-1), loc_c.reshape(-1)].add(contrib)
            h = jax.nn.relu(jnp.einsum('ecd,edh->ech', disp, w1) + b1[:, None, :])
            out = jnp.einsum('ech,ehd->ecd', h, w2) + b2[:, None, :]
            gathered = out[idx_k, loc_c]
            y = jnp.einsum('tk,tkd->td', gates_k * valid, gathered)
            return y.reshape(Bb, Ss, Dd)
        key = jax.random.key(seed)
        ks = jax.random.split(key, 6)
        scale_in = 1.0 / np.sqrt(D)
        scale_h = 1.0 / np.sqrt(H)
        return {'x': jax.random.normal(ks[0], (B, S, D), jnp.float32), 'wg': jax.random.normal(ks[1], (D, E), jnp.float32) * scale_in, 'w1': jax.random.normal(ks[2], (E, D, H), jnp.float32) * scale_in, 'b1': jnp.zeros((E, H), jnp.float32), 'w2': jax.random.normal(ks[3], (E, H, D), jnp.float32) * scale_h, 'b2': jnp.zeros((E, D), jnp.float32)}
    _L3_ffn_in = _L3_ffn_setup()
    _d = {'L0_attn_x': _L0_attn_in['x'], 'L0_attn_Wq': _L0_attn_in['Wq'], 'L0_attn_Wk': _L0_attn_in['Wk'], 'L0_attn_Wv': _L0_attn_in['Wv'], 'L0_attn_Wg': _L0_attn_in['Wg'], 'L0_attn_Wgk1': _L0_attn_in['Wgk1'], 'L0_attn_Wgk2': _L0_attn_in['Wgk2'], 'L0_attn_bgk2': _L0_attn_in['bgk2'], 'L0_attn_Wout': _L0_attn_in['Wout'], 'L0_attn_rms_w': _L0_attn_in['rms_w'], 'L0_ffn_w_gate': _L0_ffn_in['w_gate'], 'L0_ffn_w1_e': _L0_ffn_in['w1_e'], 'L0_ffn_w3_e': _L0_ffn_in['w3_e'], 'L0_ffn_w2_e': _L0_ffn_in['w2_e'], 'L0_ffn_w1_s': _L0_ffn_in['w1_s'], 'L0_ffn_w3_s': _L0_ffn_in['w3_s'], 'L0_ffn_w2_s': _L0_ffn_in['w2_s'], 'L1_attn_q_a': _L1_attn_in['q_a'], 'L1_attn_q_b': _L1_attn_in['q_b'], 'L1_attn_k_a': _L1_attn_in['k_a'], 'L1_attn_k_b': _L1_attn_in['k_b'], 'L1_attn_v_w': _L1_attn_in['v_w'], 'L1_attn_v_b': _L1_attn_in['v_b'], 'L1_attn_o_w': _L1_attn_in['o_w'], 'L1_attn_o_b': _L1_attn_in['o_b'], 'L1_ffn_up': _L1_ffn_in['up'], 'L1_ffn_gate': _L1_ffn_in['gate'], 'L1_ffn_down': _L1_ffn_in['down'], 'L1_ffn_router': _L1_ffn_in['router'], 'L1_ffn_w_up_s': _L1_ffn_in['w_up_s'], 'L1_ffn_w_gate_s': _L1_ffn_in['w_gate_s'], 'L1_ffn_w_down_s': _L1_ffn_in['w_down_s'], 'L2_attn_ln1_g': _L2_attn_in['ln1_g'], 'L2_attn_ln1_b': _L2_attn_in['ln1_b'], 'L2_attn_ln2_g': _L2_attn_in['ln2_g'], 'L2_attn_ln2_b': _L2_attn_in['ln2_b'], 'L2_attn_ca_sub_w': _L2_attn_in['ca_sub_w'], 'L2_attn_ca_Wl_w': _L2_attn_in['ca_Wl_w'], 'L2_attn_ca_W_w': _L2_attn_in['ca_W_w'], 'L2_attn_ca_B_w': _L2_attn_in['ca_B_w'], 'L2_attn_ca_sub_b': _L2_attn_in['ca_sub_b'], 'L2_attn_ca_Wl_b': _L2_attn_in['ca_Wl_b'], 'L2_attn_ca_W_b': _L2_attn_in['ca_W_b'], 'L2_attn_ca_B_b': _L2_attn_in['ca_B_b'], 'L2_attn_cp_sub_w': _L2_attn_in['cp_sub_w'], 'L2_attn_cp_Wl_w': _L2_attn_in['cp_Wl_w'], 'L2_attn_cp_W_w': _L2_attn_in['cp_W_w'], 'L2_attn_cp_B_w': _L2_attn_in['cp_B_w'], 'L2_attn_cp_sub_b': _L2_attn_in['cp_sub_b'], 'L2_attn_cp_Wl_b': _L2_attn_in['cp_Wl_b'], 'L2_attn_cp_W_b': _L2_attn_in['cp_W_b'], 'L2_attn_cp_B_b': _L2_attn_in['cp_B_b'], 'L2_attn_cf_sub_w': _L2_attn_in['cf_sub_w'], 'L2_attn_cf_Wl_w': _L2_attn_in['cf_Wl_w'], 'L2_attn_cf_W_w': _L2_attn_in['cf_W_w'], 'L2_attn_cf_B_w': _L2_attn_in['cf_B_w'], 'L2_attn_cf_sub_b': _L2_attn_in['cf_sub_b'], 'L2_attn_cf_Wl_b': _L2_attn_in['cf_Wl_b'], 'L2_attn_cf_W_b': _L2_attn_in['cf_W_b'], 'L2_attn_cf_B_b': _L2_attn_in['cf_B_b'], 'L2_attn_cm_sub_w': _L2_attn_in['cm_sub_w'], 'L2_attn_cm_Wl_w': _L2_attn_in['cm_Wl_w'], 'L2_attn_cm_W_w': _L2_attn_in['cm_W_w'], 'L2_attn_cm_B_w': _L2_attn_in['cm_B_w'], 'L2_attn_cm_sub_b': _L2_attn_in['cm_sub_b'], 'L2_attn_cm_Wl_b': _L2_attn_in['cm_Wl_b'], 'L2_attn_cm_W_b': _L2_attn_in['cm_W_b'], 'L2_attn_cm_B_b': _L2_attn_in['cm_B_b'], 'L2_ffn_w1_w': _L2_ffn_in['w1_w'], 'L2_ffn_w1_s': _L2_ffn_in['w1_s'], 'L2_ffn_w2_w': _L2_ffn_in['w2_w'], 'L2_ffn_w2_s': _L2_ffn_in['w2_s'], 'L2_ffn_h1_w': _L2_ffn_in['h1_w'], 'L2_ffn_h1_s': _L2_ffn_in['h1_s'], 'L2_ffn_h2_w': _L2_ffn_in['h2_w'], 'L2_ffn_h2_s': _L2_ffn_in['h2_s'], 'L2_ffn_w3_w': _L2_ffn_in['w3_w'], 'L2_ffn_w3_s': _L2_ffn_in['w3_s'], 'L3_attn_Wq': _L3_attn_in['Wq'], 'L3_attn_bq': _L3_attn_in['bq'], 'L3_attn_Wk': _L3_attn_in['Wk'], 'L3_attn_bk': _L3_attn_in['bk'], 'L3_attn_Wv': _L3_attn_in['Wv'], 'L3_attn_bv': _L3_attn_in['bv'], 'L3_attn_Wo': _L3_attn_in['Wo'], 'L3_attn_bo': _L3_attn_in['bo'], 'L3_ffn_wg': _L3_ffn_in['wg'], 'L3_ffn_w1': _L3_ffn_in['w1'], 'L3_ffn_b1': _L3_ffn_in['b1'], 'L3_ffn_w2': _L3_ffn_in['w2'], 'L3_ffn_b2': _L3_ffn_in['b2']}
    _x0 = _d['L0_attn_x']
    _d['L0_attn_x'] = jax.random.normal(jax.random.fold_in(jax.random.key(seed), 1), (4, 512, 128), dtype=_x0.dtype)
    del _x0
    return _d

def reference(L0_attn_x, L0_attn_Wq, L0_attn_Wk, L0_attn_Wv, L0_attn_Wg, L0_attn_Wgk1, L0_attn_Wgk2, L0_attn_bgk2, L0_attn_Wout, L0_attn_rms_w, L0_ffn_w_gate, L0_ffn_w1_e, L0_ffn_w3_e, L0_ffn_w2_e, L0_ffn_w1_s, L0_ffn_w3_s, L0_ffn_w2_s, L1_attn_q_a, L1_attn_q_b, L1_attn_k_a, L1_attn_k_b, L1_attn_v_w, L1_attn_v_b, L1_attn_o_w, L1_attn_o_b, L1_ffn_up, L1_ffn_gate, L1_ffn_down, L1_ffn_router, L1_ffn_w_up_s, L1_ffn_w_gate_s, L1_ffn_w_down_s, L2_attn_ln1_g, L2_attn_ln1_b, L2_attn_ln2_g, L2_attn_ln2_b, L2_attn_ca_sub_w, L2_attn_ca_Wl_w, L2_attn_ca_W_w, L2_attn_ca_B_w, L2_attn_ca_sub_b, L2_attn_ca_Wl_b, L2_attn_ca_W_b, L2_attn_ca_B_b, L2_attn_cp_sub_w, L2_attn_cp_Wl_w, L2_attn_cp_W_w, L2_attn_cp_B_w, L2_attn_cp_sub_b, L2_attn_cp_Wl_b, L2_attn_cp_W_b, L2_attn_cp_B_b, L2_attn_cf_sub_w, L2_attn_cf_Wl_w, L2_attn_cf_W_w, L2_attn_cf_B_w, L2_attn_cf_sub_b, L2_attn_cf_Wl_b, L2_attn_cf_W_b, L2_attn_cf_B_b, L2_attn_cm_sub_w, L2_attn_cm_Wl_w, L2_attn_cm_W_w, L2_attn_cm_B_w, L2_attn_cm_sub_b, L2_attn_cm_Wl_b, L2_attn_cm_W_b, L2_attn_cm_B_b, L2_ffn_w1_w, L2_ffn_w1_s, L2_ffn_w2_w, L2_ffn_w2_s, L2_ffn_h1_w, L2_ffn_h1_s, L2_ffn_h2_w, L2_ffn_h2_s, L2_ffn_w3_w, L2_ffn_w3_s, L3_attn_Wq, L3_attn_bq, L3_attn_Wk, L3_attn_bk, L3_attn_Wv, L3_attn_bv, L3_attn_Wo, L3_attn_bo, L3_ffn_wg, L3_ffn_w1, L3_ffn_b1, L3_ffn_w2, L3_ffn_b2):

    def _L0_attn_ref(x, Wq, Wk, Wv, Wg, Wgk1, Wgk2, bgk2, Wout, rms_w):
        import jax, jax.numpy as jnp
        import numpy as np
        D_MODEL = 128
        H = 4
        DK = 128
        DV = 256
        HQK = DK // H
        HV = DV // H
        LOW_RANK = 32
        CHUNK = 16
        GATE_NORM = 32.0
        GATE_MULT = 1.0
        EPS = 1e-05

        def gla_fused_chunk(q, k, v, g, chunk=CHUNK):
            B, Hh, N, Dk = q.shape
            Dv = v.shape[-1]
            q = q * Dk ** (-0.5)
            nc = N // chunk

            def to_chunks(t, d):
                return t.reshape(B, Hh, nc, chunk, d).transpose(2, 0, 1, 3, 4)
            qc, kc, vc, gc = (to_chunks(q, Dk), to_chunks(k, Dk), to_chunks(v, Dv), to_chunks(g, Dk))
            bc = jnp.cumsum(gc, axis=-2)
            causal = jnp.tril(jnp.ones((chunk, chunk), bool))

            def step(S, inp):
                qi, ki, vi, bi = inp
                o_inter = jnp.einsum('bhtd,bhde->bhte', qi * jnp.exp(bi), S)
                diff = bi[:, :, :, None, :] - bi[:, :, None, :, :]
                diff = jnp.where(causal[None, None, :, :, None], diff, -jnp.inf)
                A = jnp.einsum('bhtd,bhjd,bhtjd->bhtj', qi, ki, jnp.exp(diff))
                o_intra = jnp.einsum('bhtj,bhje->bhte', A, vi)
                blast = bi[:, :, -1:, :]
                kdec = ki * jnp.exp(blast - bi)
                S_new = jnp.exp(blast)[:, :, 0, :, None] * S + jnp.einsum('bhtd,bhte->bhde', kdec, vi)
                return (S_new, o_inter + o_intra)
            S0 = jnp.zeros((B, Hh, Dk, Dv), q.dtype)
            _, o = jax.lax.scan(step, S0, (qc, kc, vc, bc))
            return o.transpose(1, 2, 0, 3, 4).reshape(B, Hh, N, Dv)
        B, N, _ = x.shape
        split = lambda t, hd: t.reshape(B, N, H, hd).transpose(0, 2, 1, 3)
        q = split(x @ Wq.T, HQK)
        k = split(x @ Wk.T, HQK)
        v = split(x @ Wv.T, HV)
        g_logits = x @ Wgk1.T @ Wgk2.T + bgk2
        g = jax.nn.log_sigmoid(g_logits * GATE_MULT) / GATE_NORM
        g = split(g, HQK)
        o = gla_fused_chunk(q, k, v, g)
        o = o.transpose(0, 2, 1, 3)
        o = o * jax.lax.rsqrt(jnp.mean(o * o, axis=-1, keepdims=True) + EPS) * rms_w
        gate = jax.nn.silu(x @ Wg.T)
        return o.reshape(B, N, DV) * gate @ Wout.T

    def _L0_ffn_ref(hidden_states, w_gate, w1_e, w3_e, w2_e, w1_s, w3_s, w2_s):
        import jax, jax.numpy as jnp
        import numpy as np
        B, S, H = (2, 128, 128)
        E, F = (16, 64)
        G, TOPK_G, TOPK = (4, 2, 4)
        N_SHARED = 2
        ROUTE_SCALE = 1.0
        FS = N_SHARED * F

        def _gate(x, w_gate):
            T = x.shape[0]
            scores = jax.nn.sigmoid(x @ w_gate.T)
            sv = scores.reshape(T, G, E // G)
            group_scores = jax.lax.top_k(sv, 2)[0].sum(-1)
            top_groups = jax.lax.top_k(group_scores, TOPK_G)[1]
            allowed = jnp.zeros((T, G), dtype=bool).at[jnp.arange(T)[:, None], top_groups].set(True)
            masked = jnp.where(allowed[:, :, None], sv, -jnp.inf).reshape(T, E)
            _, idx = jax.lax.top_k(masked, TOPK)
            w = jnp.take_along_axis(scores, idx, axis=1)
            w = w / (w.sum(-1, keepdims=True) + 1e-06) * ROUTE_SCALE
            return (w, idx)

        def _swiglu(x, w1, w3, w2):
            return jax.nn.silu(x @ w1.T) * (x @ w3.T) @ w2.T
        shape = hidden_states.shape
        x = hidden_states.reshape(-1, H)
        weights, idx = _gate(x, w_gate)
        combine = (jax.nn.one_hot(idx, E, dtype=x.dtype) * weights[..., None]).sum(1)
        g = jax.nn.silu(jnp.einsum('th,efh->tef', x, w1_e))
        u = jnp.einsum('th,efh->tef', x, w3_e)
        routed = jnp.einsum('tef,ehf,te->th', g * u, w2_e, combine)
        shared = _swiglu(x, w1_s, w3_s, w2_s)
        return (routed + shared).reshape(shape)

    def _L1_attn_ref(hidden_states, q_a, q_b, k_a, k_b, v_w, v_b, o_w, o_b):
        import jax, jax.numpy as jnp
        import numpy as np
        B, T, D, H, R = (1, 512, 128, 16, 64)
        HD = D // H
        STD = 0.02

        def _low_rank_proj(x, a, b):
            mid = jnp.einsum('btd,hdr->bhtr', x, a)
            return jnp.einsum('bhtr,hrd->bhtd', mid, b)
        Bc, Tc, Dc = hidden_states.shape
        q = _low_rank_proj(hidden_states, q_a, q_b)
        k = _low_rank_proj(hidden_states, k_a, k_b)
        v = hidden_states @ v_w.T + v_b
        v = v.reshape(Bc, Tc, H, HD).transpose(0, 2, 1, 3)
        scale = 1.0 / np.sqrt(HD).astype(np.float32)
        att = jnp.einsum('bhtd,bhsd->bhts', q, k) * scale
        causal = jnp.tril(jnp.ones((Tc, Tc), dtype=bool))
        att = jnp.where(causal[None, None], att, jnp.finfo(att.dtype).min)
        att = jax.nn.softmax(att, axis=-1)
        y = jnp.einsum('bhts,bhsd->bhtd', att, v)
        y = y.transpose(0, 2, 1, 3).reshape(Bc, Tc, Dc)
        return y @ o_w.T + o_b

    def _L1_ffn_ref(x, up, gate, down, router, w_up_s, w_gate_s, w_down_s):
        import jax, jax.numpy as jnp
        import numpy as np
        B, T, C, H, E = (1, 32, 128, 256, 8)
        STD = 0.02
        b, t, c = x.shape
        x_ = x.reshape(b * t, c)
        logits = x_ @ router.T
        idx = jnp.argmax(logits, axis=-1)
        onehot = jax.nn.one_hot(idx, router.shape[0], dtype=x.dtype)
        u = jnp.einsum('bc,ehc->ebh', x_, up)
        g = jnp.einsum('bc,ehc->ebh', x_, gate)
        h = jax.nn.silu(g) * u
        ye = jnp.einsum('ebh,ech->ebc', h, down)
        y = jnp.einsum('ebc,be->bc', ye, onehot)
        ys = jax.nn.silu(x_ @ w_gate_s.T) * (x_ @ w_up_s.T) @ w_down_s.T
        return (y + ys).reshape(b, t, c)

    def _L2_attn_ref(hs, ln1_g, ln1_b, ln2_g, ln2_b, ca_sub_w, ca_Wl_w, ca_W_w, ca_B_w, ca_sub_b, ca_Wl_b, ca_W_b, ca_B_b, cp_sub_w, cp_Wl_w, cp_W_w, cp_B_w, cp_sub_b, cp_Wl_b, cp_W_b, cp_B_b, cf_sub_w, cf_Wl_w, cf_W_w, cf_B_w, cf_sub_b, cf_Wl_b, cf_W_b, cf_B_b, cm_sub_w, cm_Wl_w, cm_W_w, cm_B_w, cm_sub_b, cm_Wl_b, cm_W_b, cm_B_b):
        import jax, jax.numpy as jnp
        import numpy as np
        B, S, D, H, I, A = (2, 256, 128, 16, 512, 2)
        HD = D // H

        def _gen_param(sub, Wl, W, Bp):
            p = jnp.einsum('a...,a->...', sub, Wl[0])
            return jnp.tanh(p) * W + Bp

        def _student_linear(x, sub_w, Wl_w, W_w, B_w, sub_b, Wl_b, W_b, B_b):
            w = _gen_param(sub_w, Wl_w, W_w, B_w)
            b = _gen_param(sub_b, Wl_b, W_b, B_b)
            return x @ w.T + b

        def _layernorm(x, g, b, eps=1e-05):
            m = jnp.mean(x, axis=-1, keepdims=True)
            v = jnp.mean((x - m) ** 2, axis=-1, keepdims=True)
            return (x - m) * jax.lax.rsqrt(v + eps) * g + b

        def _gelu_new(x):
            c = 0.7978845608028654
            return 0.5 * x * (1.0 + jnp.tanh(c * (x + 0.044715 * x ** 3)))

        def _block(hs, ln1_g, ln1_b, ln2_g, ln2_b, *p):
            ca, cp, cf, cm = (p[0:8], p[8:16], p[16:24], p[24:32])
            b_, s_, d_ = hs.shape
            h = _layernorm(hs, ln1_g, ln1_b)
            qkv = _student_linear(h, *ca)
            q, k, v = jnp.split(qkv, 3, axis=-1)
            split = lambda t: t.reshape(b_, s_, H, HD).transpose(0, 2, 1, 3)
            q, k, v = (split(q), split(k), split(v))
            scores = jnp.einsum('bhqd,bhkd->bhqk', q, k) / float(HD) ** 0.5
            causal = jnp.tril(jnp.ones((s_, s_), dtype=bool))
            scores = jnp.where(causal, scores, jnp.asarray(-10000.0, scores.dtype))
            attn = jax.nn.softmax(scores, axis=-1)
            o = jnp.einsum('bhqk,bhkd->bhqd', attn, v)
            o = o.transpose(0, 2, 1, 3).reshape(b_, s_, d_)
            o = _student_linear(o, *cp)
            hs = hs + o
            h2 = _layernorm(hs, ln2_g, ln2_b)
            m = _student_linear(h2, *cf)
            m = _gelu_new(m)
            m = _student_linear(m, *cm)
            return hs + m
        return _block(hs, ln1_g, ln1_b, ln2_g, ln2_b, ca_sub_w, ca_Wl_w, ca_W_w, ca_B_w, ca_sub_b, ca_Wl_b, ca_W_b, ca_B_b, cp_sub_w, cp_Wl_w, cp_W_w, cp_B_w, cp_sub_b, cp_Wl_b, cp_W_b, cp_B_b, cf_sub_w, cf_Wl_w, cf_W_w, cf_B_w, cf_sub_b, cf_Wl_b, cf_W_b, cf_B_b, cm_sub_w, cm_Wl_w, cm_W_w, cm_B_w, cm_sub_b, cm_Wl_b, cm_W_b, cm_B_b)

    def _L2_ffn_ref(x, w1_w, w1_s, w2_w, w2_s, h1_w, h1_s, h2_w, h2_s, w3_w, w3_s):
        import jax, jax.numpy as jnp
        import numpy as np
        D_IN, D_HID = (128, 512)

        def _ternary(key, shape):
            return jax.random.randint(key, shape, -1, 2).astype(jnp.float32)

        def _tlin(x, w, s):
            return jnp.einsum('bsi,oi->bso', x, w) * s
        h = jax.nn.silu(_tlin(x, w1_w, w1_s)) * _tlin(x, w2_w, w2_s)
        h = jax.nn.gelu(_tlin(h, h1_w, h1_s), approximate=False)
        h = jax.nn.gelu(_tlin(h, h2_w, h2_s), approximate=False)
        return _tlin(h, w3_w, w3_s)

    def _L3_attn_ref(x, Wq, bq, Wk, bk, Wv, bv, Wo, bo):
        import jax, jax.numpy as jnp
        import numpy as np
        EMB = 128
        H = 16
        DH = 64
        B, S, E = x.shape

        def proj(W, b):
            return (jnp.einsum('bse,de->bsd', x, W) + b).reshape(B, S, H, DH).transpose(0, 2, 1, 3)
        q = proj(Wq, bq)
        k = proj(Wk, bk)
        v = proj(Wv, bv)
        scores = jnp.einsum('bhsd,bhtd->bhst', q / jnp.sqrt(jnp.float32(DH)), k)
        attn = jax.nn.softmax(scores, axis=-1)
        out = jnp.einsum('bhst,bhtd->bhsd', attn, v)
        out = out.transpose(0, 2, 1, 3).reshape(B, S, H * DH)
        return jnp.einsum('bsd,ed->bse', out, Wo) + bo

    def _L3_ffn_ref(x, wg, w1, b1, w2, b2):
        import jax, jax.numpy as jnp
        import numpy as np
        B, S, D = (2, 256, 128)
        E, K, H = (8, 2, 512)
        CAP_FACTOR = 1.0

        def _moe_forward(x, wg, w1, b1, w2, b2):
            Bb, Ss, Dd = x.shape
            T = Bb * Ss
            cap = int(K * CAP_FACTOR * ((T + E - 1) // E))
            xt = x.reshape(T, Dd)
            logits = xt @ wg
            scores = jax.nn.softmax(logits, axis=-1)
            gates_k, idx_k = jax.lax.top_k(scores, K)
            gates_k = gates_k / jnp.sum(gates_k, axis=-1, keepdims=True)
            masks = jax.nn.one_hot(idx_k, E, dtype=jnp.int32)
            m = jnp.transpose(masks, (1, 0, 2)).reshape(K * T, E)
            locs_full = jnp.cumsum(m, axis=0) - 1
            loc = jnp.sum(locs_full * m, axis=-1)
            loc = loc.reshape(K, T).T
            valid = (loc < cap).astype(xt.dtype)
            loc_c = jnp.clip(loc, 0, cap - 1)
            contrib = (xt[:, None, :] * valid[:, :, None]).reshape(T * K, Dd)
            disp = jnp.zeros((E, cap, Dd), xt.dtype)
            disp = disp.at[idx_k.reshape(-1), loc_c.reshape(-1)].add(contrib)
            h = jax.nn.relu(jnp.einsum('ecd,edh->ech', disp, w1) + b1[:, None, :])
            out = jnp.einsum('ech,ehd->ecd', h, w2) + b2[:, None, :]
            gathered = out[idx_k, loc_c]
            y = jnp.einsum('tk,tkd->td', gates_k * valid, gathered)
            return y.reshape(Bb, Ss, Dd)
        return _moe_forward(x, wg, w1, b1, w2, b2)
    x = L0_attn_x
    x = x + _L0_attn_ref(_layernorm(x, axis=-1), L0_attn_Wq, L0_attn_Wk, L0_attn_Wv, L0_attn_Wg, L0_attn_Wgk1, L0_attn_Wgk2, L0_attn_bgk2, L0_attn_Wout, L0_attn_rms_w)
    x = x + _L0_ffn_ref(_layernorm(x, axis=-1), L0_ffn_w_gate, L0_ffn_w1_e, L0_ffn_w3_e, L0_ffn_w2_e, L0_ffn_w1_s, L0_ffn_w3_s, L0_ffn_w2_s)
    x = x + _L1_attn_ref(_layernorm(x, axis=-1), L1_attn_q_a, L1_attn_q_b, L1_attn_k_a, L1_attn_k_b, L1_attn_v_w, L1_attn_v_b, L1_attn_o_w, L1_attn_o_b)
    x = x + _L1_ffn_ref(_layernorm(x, axis=-1), L1_ffn_up, L1_ffn_gate, L1_ffn_down, L1_ffn_router, L1_ffn_w_up_s, L1_ffn_w_gate_s, L1_ffn_w_down_s)
    x = x + _L2_attn_ref(_layernorm(x, axis=-1), L2_attn_ln1_g, L2_attn_ln1_b, L2_attn_ln2_g, L2_attn_ln2_b, L2_attn_ca_sub_w, L2_attn_ca_Wl_w, L2_attn_ca_W_w, L2_attn_ca_B_w, L2_attn_ca_sub_b, L2_attn_ca_Wl_b, L2_attn_ca_W_b, L2_attn_ca_B_b, L2_attn_cp_sub_w, L2_attn_cp_Wl_w, L2_attn_cp_W_w, L2_attn_cp_B_w, L2_attn_cp_sub_b, L2_attn_cp_Wl_b, L2_attn_cp_W_b, L2_attn_cp_B_b, L2_attn_cf_sub_w, L2_attn_cf_Wl_w, L2_attn_cf_W_w, L2_attn_cf_B_w, L2_attn_cf_sub_b, L2_attn_cf_Wl_b, L2_attn_cf_W_b, L2_attn_cf_B_b, L2_attn_cm_sub_w, L2_attn_cm_Wl_w, L2_attn_cm_W_w, L2_attn_cm_B_w, L2_attn_cm_sub_b, L2_attn_cm_Wl_b, L2_attn_cm_W_b, L2_attn_cm_B_b)
    x = x + _L2_ffn_ref(_layernorm(x, axis=-1), L2_ffn_w1_w, L2_ffn_w1_s, L2_ffn_w2_w, L2_ffn_w2_s, L2_ffn_h1_w, L2_ffn_h1_s, L2_ffn_h2_w, L2_ffn_h2_s, L2_ffn_w3_w, L2_ffn_w3_s)
    x = x + _L3_attn_ref(_layernorm(x, axis=-1), L3_attn_Wq, L3_attn_bq, L3_attn_Wk, L3_attn_bk, L3_attn_Wv, L3_attn_bv, L3_attn_Wo, L3_attn_bo)
    x = x + _L3_ffn_ref(_layernorm(x, axis=-1), L3_ffn_wg, L3_ffn_w1, L3_ffn_b1, L3_ffn_w2, L3_ffn_b2)
    return x

_drawn_inputs = setup_inputs


def setup_inputs(seed=0):
    import zlib

    import numpy as np

    out = dict(_drawn_inputs(seed))
    spreads = {'L0_attn_rms_w': (1.0, 0.2),
     'L1_attn_v_b': (0.0, 0.1),
     'L1_attn_o_b': (0.0, 0.1),
     'L2_attn_ln1_g': (1.0, 0.2),
     'L2_attn_ln1_b': (0.0, 0.1),
     'L2_attn_ln2_g': (1.0, 0.2),
     'L2_attn_ln2_b': (0.0, 0.1),
     'L2_attn_ca_W_w': (1.0, 0.2),
     'L2_attn_ca_B_w': (0.0, 0.1),
     'L2_attn_ca_W_b': (1.0, 0.2),
     'L2_attn_ca_B_b': (0.0, 0.1),
     'L2_attn_cp_W_w': (1.0, 0.2),
     'L2_attn_cp_B_w': (0.0, 0.1),
     'L2_attn_cp_W_b': (1.0, 0.2),
     'L2_attn_cp_B_b': (0.0, 0.1),
     'L2_attn_cf_W_w': (1.0, 0.2),
     'L2_attn_cf_B_w': (0.0, 0.1),
     'L2_attn_cf_W_b': (1.0, 0.2),
     'L2_attn_cf_B_b': (0.0, 0.1),
     'L2_attn_cm_W_w': (1.0, 0.2),
     'L2_attn_cm_B_w': (0.0, 0.1),
     'L2_attn_cm_W_b': (1.0, 0.2),
     'L2_attn_cm_B_b': (0.0, 0.1),
     'L3_ffn_b1': (0.0, 0.1),
     'L3_ffn_b2': (0.0, 0.1)}
    factors = {}
    for name, (base, spread) in spreads.items():
        noise = np.random.default_rng([zlib.crc32(name.encode()), seed]).standard_normal(out[name].shape)
        drawn = base * np.exp(spread * noise) if base else spread * noise
        out[name] = jnp.asarray(drawn.astype(out[name].dtype))
    for name, factor in factors.items():
        out[name] = (out[name] * factor).astype(out[name].dtype)
    return out
```

```python
from contextlib import ExitStack

import concourse.bass as bass
from concourse import mybir

STAGES = (0, 1, 2, 3, 4, 5, 6, 7)

ALU = mybir.AluOpType
ACT = mybir.ActivationFunctionType
AX = mybir.AxisListType
F32 = mybir.dt.float32
BF16 = mybir.dt.bfloat16
U32 = mybir.dt.uint32

P = 128
B, S, D = 4, 512, 128
TPC = S // P
NT = B * TPC
T = B * S
H8, HD8 = 16, 8
LN_EPS = 1e-5
NEG = -1.0e30


def tiles(c, n=TPC):
    return bass.ds(c * n, n)


def cols(c, n=S):
    return bass.ds(c * n, n)


class Steps:

    def __init__(self, eng, sem, base, total):
        self.eng, self.sem, self.base, self.total, self.n = eng, sem, base, total, 0

    def did(self, ins):
        self.n += 1
        ins.then_inc(self.sem, 1)
        return self.n

    def wait(self, n=None):
        self.eng.wait_ge(self.sem, self.base + (self.n if n is None else n))

    def then(self, ins):
        self.did(ins)
        self.wait()

    def end(self):
        assert self.n == self.total, (self.sem, self.n, self.total)


class Shared:

    def __init__(self, nc, ctx, weights, extra):
        self.nc, self.weights, self.extra = nc, weights, extra
        self.x = ctx.enter_context(nc.sbuf_tensor("x_resid", [P, NT, D], F32))
        self.xnT = ctx.enter_context(nc.sbuf_tensor("xnT", [P, T], F32))
        self.ident = ctx.enter_context(nc.sbuf_tensor("ident", [P, P], F32))
        self.identb = ctx.enter_context(nc.sbuf_tensor("identb", [P, P], BF16))
        self.scratch_qk = nc.dram_tensor("scratch_qk", [B, 2, H8, 3, HD8, S], BF16, kind="Internal").ap()
        self.scratch_max = nc.dram_tensor("scratch_max", [B, 3 * H8, S], BF16, kind="Internal").ap()
        self.mhalf = ctx.enter_context(nc.sbuf_tensor("mhalf", [P, NT], F32))
        self.sems, self.old_sems, self.fresh, self.stale = ExitStack(), ExitStack(), [], []
        order = list(weights.values())
        width = [max([w.shape[1] for w, _ in order[i::2]] or [1]) for i in range(2)]
        self.wbuf = [ctx.enter_context(nc.sbuf_tensor(f"wbuf{i}", [P, width[i]], F32)) for i in range(2)]
        self.wsem = {s: ctx.enter_context(nc.semaphore(f"weights_loaded_{s}")) for s in weights}

    def sem(self, name):
        s = self.sems.enter_context(self.nc.semaphore(name))
        self.fresh.append(s)
        return s

    def stage_over(self):
        self.old_sems.close()
        self.old_sems, self.sems = self.sems, ExitStack()
        self.stale, self.fresh = self.fresh, []

    def w(self, stage):
        buf = self.wbuf[list(self.weights).index(stage) % 2]
        out, at = {}, 0
        for name, rows, n in self.weights[stage][1]:
            out[name] = buf[0:rows, at:at + n]
            at += n
        return out

    def spare(self, ctx, name, stage, n):
        order = list(self.weights)
        at = order.index(stage) + 1
        used = self.weights[order[at]][0].shape[1] if at < len(order) else 0
        buf = self.wbuf[at % 2]
        if buf.shape[1] - used >= n:
            return buf[:, buf.shape[1] - n:]
        return ctx.enter_context(self.nc.sbuf_tensor(name, [P, n], F32))[:, :]

    def gen(self, w):
        out, at = {}, 0
        for name, n in L2_SEGMENTS:
            out[name] = w["sub0"][:, at:at + n]
            at += n
        return out

    def load_weights(self, eng, stage):
        buf = self.wbuf[list(self.weights).index(stage) % 2]
        src = self.weights[stage][0]
        eng.dma_start(buf[:, 0:src.shape[1]], src).then_inc(self.wsem[stage], 16)

    def load_next(self, eng, stage):
        for s in self.stale:
            eng.sem_clear(s)
        order = list(self.weights)
        at = order.index(stage) + 1
        if at < len(order):
            self.load_weights(eng, order[at])


class LayerNorm:

    def __init__(self, sh, ctx, tag, ps=None, src=None, keep=None, affine=None):
        nc = sh.nc
        self.sh, self.ps, self.keep, self.affine = sh, ps, keep, affine
        self.src = sh.x if src is None else src
        sb = lambda n, shape: ctx.enter_context(nc.sbuf_tensor(f"{tag}_{n}", shape, F32))
        sem = lambda n: sh.sem(f"{tag}_{n}")
        self.stats = sb("ln_stats", [P, NT, 6])
        self.mv = sb("ln_mv", [P, NT, 2])
        self.rstd = sb("ln_rstd", [P, NT])
        self.xn = keep if keep is not None else sb("ln_xn", [P, 2, TPC, D])
        self.s_stats, self.s_mv = sem("ln_stats_done"), sem("ln_moments_done")
        self.s_eps, self.s_rstd = sem("ln_eps_added"), sem("ln_rstd_done")
        self.s_xn, self.s_T, self.ready = sem("ln_scaled"), sem("ln_transposed"), sem("xnT_ready")

    def xn_tile(self, c, i):
        return self.xn[:, c * TPC + i, :] if self.keep is not None else self.xn[:, c % 2, i, :]

    def vector(self, dve):
        nc = self.sh.nc
        for t in range(NT):
            nc.vector.bn_stats(self.stats[:, t, :], self.src[:, t, :]).then_inc(self.s_stats, 1)
            if t >= 1:
                dve.wait_ge(self.s_stats, t)
                nc.vector.bn_aggr(self.mv[:, t - 1, :], self.stats[:, t - 1, :]).then_inc(self.s_mv, 1)
        dve.wait_ge(self.s_stats, NT)
        nc.vector.bn_aggr(self.mv[:, NT - 1, :], self.stats[:, NT - 1, :]).then_inc(self.s_mv, 1)
        for t in range(NT):
            c, i = divmod(t, TPC)
            if i == 0:
                dve.wait_ge(self.s_rstd, c + 1)
                if c >= 2 and self.keep is None:
                    dve.wait_ge(self.s_T, c - 1)
            nc.vector.tensor_scalar(self.xn_tile(c, i), self.src[:, t, :], self.mv[:, t, 0:1],
                                    self.rstd[:, t:t + 1], ALU.subtract, ALU.mult).then_inc(self.s_xn, 1)

    def gpsimd(self, pool):
        nc = self.sh.nc
        for c in range(B):
            ts = slice(c * TPC, (c + 1) * TPC)
            pool.wait_ge(self.s_mv, (c + 1) * TPC)
            nc.gpsimd.tensor_scalar(self.rstd[:, ts], self.mv[:, ts, 1], LN_EPS, 1.0,
                                    ALU.add, ALU.mult).then_inc(self.s_eps, 1)
            pool.wait_ge(self.s_eps, c + 1)
            nc.gpsimd.tensor_tensor(self.rstd[:, ts], self.rstd[:, ts], self.sh.mhalf[:, ts],
                                    ALU.pow).then_inc(self.s_rstd, 1)

    def tensor(self, pe):
        nc = self.sh.nc
        for c in range(B):
            if c >= 2:
                pe.wait_ge(self.ready, c - 1)
            for i in range(TPC):
                pe.wait_ge(self.s_xn, c * TPC + i + 1)
                last = nc.tensor.transpose(self.ps[c % 2][:, i * P:(i + 1) * P], self.xn_tile(c, i),
                                           self.sh.ident[:, :])
            last.then_inc(self.s_T, 1)

    def scalar(self, act):
        nc = self.sh.nc
        for c in range(B):
            act.wait_ge(self.s_T, c + 1)
            dst, ps = self.sh.xnT[:, c * S:(c + 1) * S], self.ps[c % 2][:, :]
            if self.affine:
                last = nc.scalar.activation(dst, ps, ACT.Identity, bias=self.affine[1], scale=self.affine[0])
            else:
                last = nc.scalar.copy(dst, ps)
            last.then_inc(self.ready, 1)


def ranks(nc, st, rank, s, before, gt, eq):
    n, e = s.shape[1], s.shape[2]
    mine = s.unsqueeze(3).broadcast_to([P, n, e, e])
    other = s.unsqueeze(2).broadcast_to([P, n, e, e])
    st.did(nc.vector.tensor_tensor(gt, other, mine, ALU.is_gt))
    st.then(nc.vector.tensor_tensor(eq, other, mine, ALU.is_equal))
    st.then(nc.vector.tensor_tensor(eq, eq, before.unsqueeze(1).broadcast_to([P, n, e, e]), ALU.mult))
    st.then(nc.vector.tensor_tensor(gt, gt, eq, ALU.add))
    st.then(nc.vector.tensor_reduce(rank, gt, AX.X, ALU.add))


def make_before(nc, pool, before, e, sem):
    nc.gpsimd.memset(before[:, :, :], 1.0).then_inc(sem, 1)
    pool.wait_ge(sem, 1)
    nc.gpsimd.affine_select(out=before[:, :, :], in_=before[:, :, :], compare_op=ALU.is_gt, fill=0.0,
                            base=0, pattern=[[1, e], [-1, e]], channel_multiplier=0).then_inc(sem, 1)


def split3(nc, st, parts, src, rest):
    st.then(nc.vector.tensor_copy(parts[0], src))
    st.then(nc.vector.tensor_tensor(rest[0], src, parts[0], ALU.subtract))
    st.then(nc.vector.tensor_copy(parts[1], rest[0]))
    st.then(nc.vector.tensor_tensor(rest[1], rest[0], parts[1], ALU.subtract))
    st.then(nc.vector.tensor_copy(parts[2], rest[1]))


GLA_LEVELS = (64, 32, 16, 8, 4, 2, 1)
GLA_STEPS = 28


def gated_linear_attention(sh, stage, heads=4, dk=32, dv=64, rank=32, gate_norm=32.0, rms_eps=1e-5):
    nc, w, tag = sh.nc, sh.w(stage), f"s{stage}"
    E, W = heads * dv, P // TPC
    NL = len(GLA_LEVELS)
    F_LAST, F_ALL = NL, NL + 1
    MUL, ADD, SUB = ALU.mult, ALU.add, ALU.subtract
    with ExitStack() as ctx:
        sb = lambda m, shape, dt=F32: ctx.enter_context(nc.sbuf_tensor(f"{tag}_{m}", shape, dt))
        sem = lambda m: sh.sem(f"{tag}_{m}")
        bank = lambda m, n=1: ctx.enter_context(nc.psum_tensor(f"{tag}_{m}", [P, n, S], F32))
        odd = [bank(f"odd_jobs{i}")[:, 0, :] for i in range(2)]
        ps_a, ps_o = bank("pair_products", heads), bank("o", 2)
        ln = LayerNorm(sh, ctx, tag, odd)
        xc = sb("xnT_of_sequence", [P, S])
        qT, kT, gk = sb("qT", [P, S]), sb("kT", [P, S]), sb("gk", [rank, S])
        z, soft, g = sb("z", [P, S]), sb("softplus", [P, S]), sb("log_decay", [P, S])
        v, gate = sb("v", [P, TPC, E]), sb("gate", [P, TPC, E])
        b = sb("decay_sums", [P, S])
        expo, fac = sb("exponents", [P, NL + 2, S]), sb("factors", [P, NL + 2, S])
        zkq = sb("scaled_kq", [P, NL + 2, S])
        near = sb("near_pairs", [P, heads, TPC, W])
        pairs = sb("pairs", [P, heads, TPC, P])
        kdec = sb("k_to_end", [P, TPC, P])
        state = sb("state", [P, E])
        sq, ss, rrms = sb("o_squared", [P, TPC, E]), sb("o_square_sums", [P, TPC * heads]), sb("rrms", [P, TPC * heads])
        og, ogT = sb("o_gated", [P, TPC, E]), sb("o_gatedT", [P, 2, S])
        tri = sb("tri", [P, P])
        it, ij = sb("iota_t", [P, W], mybir.dt.int32), sb("iota_j", [P, W], mybir.dt.int32)
        ix = sb("iota_xor", [P, W], mybir.dt.int32)
        ft, fj, fx = sb("query_no", [P, W]), sb("key_no", [P, W]), sb("xor", [P, W])
        later, below = sb("later", [P, W]), sb("below", [P, W])
        low = [m for m in GLA_LEVELS if m < W]
        turn = sb("wait_carrier", [P, 1])
        masks = sb("masks", [P, len(low) + 1, W])
        s_const, s_mask = sem("constants_made"), sem("mask_steps")
        s_xc, s_proj, s_gk, s_qk = sem("xc_copied"), sem("projected"), sem("gk_ready"), sem("qk_ready")
        s_z, s_vg, s_vgs = sem("z_ready"), sem("v_gate_projected"), sem("v_done")
        s_gates = sem("gate_done")
        s_st, s_e, s_l = sem("vector_steps"), sem("exp_done"), sem("log_done")
        s_b, s_bs, s_expo, s_fac = sem("sums_ready"), sem("sums_in_sbuf"), sem("exponents_done"), sem("factors_ready")
        s_zkq, s_round, s_taken, s_rect = sem("scaled_ready"), sem("pairs_round"), sem("round_taken"), sem("rects_copied")
        s_near, s_win = sem("near_done"), sem("windows_copied")
        s_kdT, s_kd = sem("k_to_end_turned"), sem("k_to_end_ready")
        s_inc, s_state, s_o = sem("state_added"), sem("state_ready"), sem("o_ready")
        s_sq, s_ss, s_rms = sem("squares_done"), sem("square_sums_done"), sem("rrms_done")
        s_gw = sem("gate_weighted")
        s_og, s_ogT, s_ogTs, s_y, s_x = sem("o_gated_ready"), sem("og_turned"), sem("ogT_ready"), sem("y_ready"), sem("x_updated")
        s_free = [sem(f"odd_bank_free{i}") for i in range(2)]
        jobs = ["gk", "q", "k", "z"] + [("vg", i) for i in range(TPC)] + ["b", "kd"] + \
            [("S", i) for i in range(TPC - 1)] + ["y"]
        job = {name: n for n, name in enumerate(jobs)}
        JOBS = len(jobs) // 2
        assert len(jobs) % 2 == 0
        rounds = [(0,), (64, 32, 16), (8, 4, 2, 1)]
        place = {0: 0, 64: 0, 32: 256, 16: 384, 8: 0, 4: 128, 2: 256, 1: 384}
        blocks = lambda a, m: a.rearrange("p (n u) -> p n u", u=2 * m)
        by_chunk = lambda a: a.rearrange("p (i t) -> p i t", i=TPC)
        block = ctx.enter_context(nc.Block())

        @block.sync
        def _(sp):
            sh.load_next(sp, stage)

        def freed(eng, name):
            eng.sem_inc(s_free[job[name] % 2], 1)

        @block.gpsimd
        def _(pool):
            nc.gpsimd.iota(it[:, :], pattern=[[1, W]], base=0, channel_multiplier=0).then_inc(s_const, 1)
            nc.gpsimd.iota(ij[:, :], pattern=[[0, W]], base=0, channel_multiplier=1).then_inc(s_const, 1)
            nc.gpsimd.memset(tri[:, :], 1.0 / gate_norm).then_inc(s_const, 1)
            nc.gpsimd.memset(pairs[:, :, :, :], 0.0).then_inc(s_const, 1)
            nc.gpsimd.memset(state[:, :], 0.0).then_inc(s_const, 1)
            pool.wait_ge(s_const, 5)
            nc.gpsimd.affine_select(out=tri[:, :], in_=tri[:, :], compare_op=ALU.is_ge, fill=0.0, base=0,
                                    pattern=[[1, P]], channel_multiplier=-1).then_inc(s_const, 1)
            ln.gpsimd(pool)
            pool.wait_ge(sh.wsem[stage], 16)
            with pool.Fori(0, B) as c:
                pool.wait_ge(s_x, 1 + c)
                pool.wait_ge(s_bs, c + 1)
                for n, m in enumerate(GLA_LEVELS):
                    src, dst = blocks(b[:, :], m), blocks(expo[:, n, :], m)
                    mid = src[:, :, m - 1:m].broadcast_to([P, S // (2 * m), m])
                    nc.gpsimd.tensor_tensor(dst[:, :, 0:m], mid, src[:, :, 0:m], SUB).then_inc(s_expo, 1)
                    nc.gpsimd.tensor_tensor(dst[:, :, m:], src[:, :, m:], mid, SUB).then_inc(s_expo, 1)
                nc.gpsimd.tensor_tensor(by_chunk(expo[:, F_LAST, :]),
                                        by_chunk(b[:, :])[:, :, P - 1:P].broadcast_to([P, TPC, P]),
                                        by_chunk(b[:, :]), SUB).then_inc(s_expo, 1)
                pool.wait_ge(s_gates, (c + 1) * TPC)
                nc.gpsimd.tensor_tensor(gate[:, :, :].rearrange("p i (h e) -> p (i h) e", h=heads),
                                        gate[:, :, :].rearrange("p i (h e) -> p (i h) e", h=heads),
                                        w["rms_w"].unsqueeze(1).broadcast_to([P, TPC * heads, dv]), MUL).then_inc(s_gw, 1)
                pool.wait_ge(s_ss, c + 1)
                nc.gpsimd.tensor_tensor(rrms[:, :], ss[:, :], sh.mhalf[:, 0:TPC * heads], ALU.pow).then_inc(s_rms, 1)

        @block.tensor
        def _(pe):
            pe.sem_inc(s_free[0], 1)
            pe.sem_inc(s_free[1], 1)
            pe.wait_ge(sh.wsem[stage], 16)
            ln.tensor(pe)
            pe.wait_ge(ln.ready, B)
            pe.wait_ge(s_const, 6)
            with pe.Fori(0, B) as c:
                pe.wait_ge(s_x, 1 + c)

                def take(name):
                    k = job[name]
                    pe.wait_ge(s_free[k % 2], c * JOBS + k // 2 + 1)
                    return odd[k % 2]

                ps = take("gk")
                nc.tensor.matmul(ps[0:rank, :], w["wgk1"], sh.xnT[:, cols(c)], start=True, stop=True).then_inc(s_proj, 1)
                for name in "qk":
                    ps = take(name)
                    nc.tensor.matmul(ps, w["w" + name], sh.xnT[:, cols(c)], start=True, stop=True).then_inc(s_proj, 1)
                ps = take("z")
                pe.wait_ge(s_gk, c + 1)
                for i in range(TPC):
                    last = nc.tensor.matmul(ps[:, i * P:(i + 1) * P], gk[:, i * P:(i + 1) * P], w["wgk2"],
                                            start=True, stop=True)
                last.then_inc(s_z, 1)
                pe.wait_ge(s_xc, c + 1)
                for i in range(TPC):
                    ps = take(("vg", i))
                    nc.tensor.matmul(ps, xc[:, i * P:(i + 1) * P], w["wvg"], start=True, stop=True).then_inc(s_vg, 1)
                ps = take("b")
                pe.wait_ge(s_st, c * GLA_STEPS + 3)
                pe.wait_ge(s_qk, (c + 1) * 2)
                for i in range(TPC):
                    last = nc.tensor.matmul(ps[:, i * P:(i + 1) * P], g[:, i * P:(i + 1) * P], tri[:, :],
                                            start=True, stop=True)
                last.then_inc(s_b, 1)
                for r, levels in enumerate(rounds):
                    if r:
                        pe.wait_ge(s_zkq, c * (NL + 2) + GLA_LEVELS.index(levels[-1]) + 1)
                        pe.wait_ge(s_taken, c * 3 + r)
                    if r == 2:
                        ps = take("kd")
                        pe.wait_ge(s_zkq, c * (NL + 2) + NL + 1)
                        for i in range(TPC):
                            last = nc.tensor.transpose(ps[:, i * P:(i + 1) * P], zkq[:, F_LAST, i * P:(i + 1) * P],
                                                       sh.ident[:, :])
                        last.then_inc(s_kdT, 1)
                    for m in levels:
                        n = GLA_LEVELS.index(m) if m else 0
                        keys, queries = (zkq[:, n, :],) * 2 if m else (kT, qT)
                        for i in range(TPC):
                            at = i * P
                            for h in range(heads):
                                rows = slice(h * dk, (h + 1) * dk)
                                if m == 64:
                                    to = place[m] + i * m
                                    last = nc.tensor.matmul(ps_a[0:m, h, to:to + m], keys[rows, at:at + m],
                                                            queries[rows, at + m:at + 2 * m], start=True, stop=True)
                                elif m == 32:
                                    to = place[m] + i * m
                                    for k in (0, 64):
                                        last = nc.tensor.matmul(ps_a[k:k + m, h, to:to + m], keys[rows, at + k:at + k + m],
                                                                queries[rows, at + k + m:at + k + 2 * m],
                                                                start=True, stop=True)
                                else:
                                    to = place[m] + i * W
                                    for k in range(0, P, W):
                                        last = nc.tensor.matmul(ps_a[k:k + W, h, to:to + W], keys[rows, at + k:at + k + W],
                                                                queries[rows, at + k:at + k + W], start=True, stop=True)
                    last.then_inc(s_round, 1)
                pe.wait_ge(s_zkq, (c + 1) * (NL + 2))
                pe.wait_ge(s_win, (c + 1) * TPC)
                pe.wait_ge(s_vgs, (c + 1) * TPC)
                for i in range(TPC):
                    half = ps_o[:, i // 2, (i % 2) * E:(i % 2 + 1) * E]
                    for h in range(heads):
                        last = nc.tensor.matmul(half[:, h * dv:(h + 1) * dv], pairs[:, h, i, :], v[:, i, h * dv:(h + 1) * dv],
                                                start=(i % 2 == 0 and h == 0), stop=False, skip_group_check=True)
                    if i < TPC - 1:
                        ps = take(("S", i))
                        pe.wait_ge(s_kd, c + 1)
                        nc.tensor.matmul(ps[:, 0:E], kdec[:, i, :], v[:, i, :], start=True, stop=True).then_inc(s_inc, 1)
                    if i:
                        pe.wait_ge(s_state, c * (TPC - 1) + i)
                        last = nc.tensor.matmul(half, zkq[:, F_ALL, i * P:(i + 1) * P], state[:, :],
                                                start=False, stop=True, skip_group_check=True)
                    last.then_inc(s_o, 1)
                pe.wait_ge(s_og, c + 1)
                for i in range(TPC):
                    for k in range(2):
                        last = nc.tensor.transpose(ps_a[:, k, i * P:(i + 1) * P], og[:, i, k * P:(k + 1) * P], sh.ident[:, :])
                last.then_inc(s_ogT, 1)
                ps = take("y")
                pe.wait_ge(s_ogTs, (c + 1) * 2)
                for i in range(TPC):
                    for k in range(2):
                        last = nc.tensor.matmul(ps[:, i * P:(i + 1) * P], ogT[:, k, i * P:(i + 1) * P],
                                                w["wout"][:, k * D:(k + 1) * D], start=(i == 0 and k == 0), stop=(k == 1),
                                                skip_group_check=True)
                last.then_inc(s_y, 1)

        @block.scalar
        def _(act):
            ln.scalar(act)
            act.wait_ge(ln.ready, B)
            with act.Fori(0, B) as c:
                act.wait_ge(s_x, 1 + c)
                nc.scalar.copy(xc[:, :], sh.xnT[:, cols(c)]).then_inc(s_xc, 1)
                act.wait_ge(s_proj, c * 3 + 1)
                nc.scalar.copy(gk[:, :], odd[job["gk"] % 2][0:rank, :]).then_inc(s_gk, 1)
                act.wait_ge(s_gk, c + 1)
                freed(act, "gk")
                for n, (name, dst) in enumerate((("q", qT), ("k", kT))):
                    act.wait_ge(s_proj, c * 3 + n + 2)
                    nc.scalar.activation(dst[:, :], odd[job[name] % 2], ACT.Copy,
                                         scale=dk ** -0.5 if name == "q" else 1.0).then_inc(s_qk, 1)
                    act.wait_ge(s_qk, c * 2 + n + 1)
                    freed(act, name)
                act.wait_ge(s_st, c * GLA_STEPS + 2)
                nc.scalar.activation(soft[:, :], soft[:, :], ACT.Exp, scale=-1.0).then_inc(s_e, 1)
                act.wait_ge(s_e, c + 1)
                nc.scalar.activation(soft[:, :], soft[:, :], ACT.Ln, bias=1.0).then_inc(s_l, 1)
                for i in range(TPC):
                    act.wait_ge(s_vg, c * TPC + i + 1)
                    nc.scalar.activation(gate[:, i, :], odd[job["vg", i] % 2][:, E:2 * E], ACT.Silu).then_inc(s_gates, 1)
                act.wait_ge(s_b, c + 1)
                nc.scalar.copy(b[:, :], odd[job["b"] % 2]).then_inc(s_bs, 1)
                act.wait_ge(s_bs, c + 1)
                freed(act, "b")
                nc.scalar.activation(fac[:, F_ALL, :], b[:, :], ACT.Exp).then_inc(s_fac, 1)
                for n in range(NL + 1):
                    act.wait_ge(s_expo, c * (2 * NL + 1) + min(2 * n + 2, 2 * NL + 1))
                    nc.scalar.activation(fac[:, n, :], expo[:, n, :], ACT.Exp).then_inc(s_fac, 1)
                act.wait_ge(s_round, c * 3 + 2)
                cut = lambda k, m, at: ps_a[k:k + m, :, at:at + TPC * m].rearrange("p h (i t) -> p h i t", i=TPC)
                nc.scalar.copy(pairs[0:64, :, :, 64:P], cut(0, 64, place[64])).then_inc(s_rect, 1)
                for k in (0, 64):
                    nc.scalar.copy(pairs[k:k + 32, :, :, k + 32:k + 64], cut(k, 32, place[32])).then_inc(s_rect, 1)
                act.wait_ge(s_kdT, c + 1)
                nc.scalar.copy(kdec[:, :, :].rearrange("p i d -> p (i d)"), odd[job["kd"] % 2]).then_inc(s_kd, 1)
                act.wait_ge(s_kd, c + 1)
                freed(act, "kd")
                act.wait_ge(s_near, c + 1)
                for k in range(TPC):
                    r = slice(k * W, (k + 1) * W)
                    nc.scalar.copy(pairs[r, :, :, r], near[r, :, :, :]).then_inc(s_win, 1)
                for k in range(2):
                    act.wait_ge(s_o, c * TPC + 2 * k + 2)
                    nc.scalar.activation(sq[:, 2 * k:2 * k + 2, :].rearrange("p i e -> p (i e)"), ps_o[:, k, :],
                                         ACT.Square).then_inc(s_sq, 1)
                act.wait_ge(s_ogT, c + 1)
                for k in range(2):
                    nc.scalar.copy(ogT[:, k, :], ps_a[:, k, :]).then_inc(s_ogTs, 1)

        @block.vector
        def _(dve):
            dve.sem_inc(s_x, 1)
            mk = Steps(dve, s_mask, 0, 7 + 3 * len(low))
            dve.wait_ge(s_const, 2)
            mk.then(nc.vector.tensor_scalar(ij[:, :], ij[:, :], W - 1, None, ALU.bitwise_and))
            mk.then(nc.vector.tensor_tensor(ix[:, :], it[:, :], ij[:, :], ALU.bitwise_xor))
            mk.did(nc.vector.tensor_copy(ft[:, :], it[:, :]))
            mk.did(nc.vector.tensor_copy(fj[:, :], ij[:, :]))
            mk.then(nc.vector.tensor_copy(fx[:, :], ix[:, :]))
            mk.did(nc.vector.tensor_tensor(later[:, :], ft[:, :], fj[:, :], ALU.is_gt))
            mk.then(nc.vector.tensor_tensor(masks[:, len(low), :], ft[:, :], fj[:, :], ALU.is_equal))
            for n, m in enumerate(low):
                mk.did(nc.vector.tensor_scalar(below[:, :], fx[:, :], 2 * m - 0.5, None, ALU.is_lt))
                mk.then(nc.vector.scalar_tensor_tensor(out=masks[:, n, :], in0=fx[:, :], scalar=m - 0.5, in1=later[:, :],
                                                       op0=ALU.is_gt, op1=MUL))
                mk.then(nc.vector.tensor_tensor(masks[:, n, :], masks[:, n, :], below[:, :], MUL))
            mk.end()
            dve.wait_ge(sh.wsem[stage], 16)
            ln.vector(dve)
            dve.wait_ge(s_const, 5)
            with dve.Fori(0, B) as c:
                st = Steps(dve, s_st, c * GLA_STEPS, GLA_STEPS)
                dve.wait_ge(s_z, c + 1)
                st.then(nc.vector.tensor_tensor(by_chunk(z[:, :]), by_chunk(odd[job["z"] % 2]),
                                                w["bgk2"].unsqueeze(1).broadcast_to([P, TPC, P]), ADD))
                freed(dve, "z")
                st.did(nc.vector.scalar_tensor_tensor(out=soft[:, :], in0=z[:, :], scalar=-1.0, in1=z[:, :],
                                                      op0=MUL, op1=ALU.max))
                dve.wait_ge(s_l, c + 1)
                st.did(nc.vector.scalar_tensor_tensor(out=g[:, :], in0=z[:, :], scalar=0.0, in1=soft[:, :],
                                                      op0=ALU.min, op1=SUB))
                for i in range(TPC):
                    dve.wait_ge(s_gates, c * TPC + i + 1)
                    nc.vector.tensor_copy(v[:, i, :], odd[job["vg", i] % 2][:, 0:E]).then_inc(s_vgs, 1)
                    dve.wait_ge(s_vgs, c * TPC + i + 1)
                    freed(dve, ("vg", i))
                dve.wait_ge(s_round, c * 3 + 1)
                low_round = lambda m: ps_a[:, :, place[m]:place[m] + TPC * W].rearrange("p h (i t) -> p h i t", i=TPC)
                wide = lambda n: masks[:, n, :].unsqueeze(1).unsqueeze(1).broadcast_to([P, heads, TPC, W])
                st.then(nc.vector.tensor_tensor(near[:, :, :, :], low_round(0), wide(len(low)), MUL))
                dve.sem_inc(s_taken, 1)
                for n, m in enumerate(GLA_LEVELS):
                    if n == 0:
                        dve.wait_ge(s_qk, (c + 1) * 2)
                    dve.wait_ge(s_fac, c * (NL + 2) + n + 2)
                    for src, half in ((kT, slice(0, m)), (qT, slice(m, 2 * m))):
                        last = nc.vector.tensor_tensor(blocks(zkq[:, n, :], m)[:, :, half], blocks(fac[:, n, :], m)[:, :, half],
                                                       blocks(src[:, :], m)[:, :, half], MUL)
                    last.then_inc(s_zkq, 1)
                dve.wait_ge(s_fac, (c + 1) * (NL + 2))
                nc.vector.tensor_tensor(zkq[:, F_LAST, :], fac[:, F_LAST, :], kT[:, :], MUL).then_inc(s_zkq, 1)
                nc.vector.tensor_tensor(zkq[:, F_ALL, :], fac[:, F_ALL, :], qT[:, :], MUL).then_inc(s_zkq, 1)
                for r, levels in enumerate(rounds):
                    if r:
                        dve.wait_ge(s_round, c * 3 + r + 1)
                        if r == 1:
                            dve.wait_ge(s_rect, c * 3 + 3)
                        for m in levels:
                            if m < W:
                                st.did(nc.vector.memset(turn[:, :], 0.0))
                                st.then(nc.vector.copy_predicated(near[:, :, :, :], wide(low.index(m)).bitcast(U32),
                                                                  low_round(m)))
                        dve.sem_inc(s_taken, 1)
                dve.sem_inc(s_near, 1)
                for i in range(TPC - 1):
                    dve.wait_ge(s_inc, c * (TPC - 1) + i + 1)
                    if i:
                        dve.wait_ge(s_o, c * TPC + i + 1)
                    for h in range(heads):
                        r, e = slice(h * dk, (h + 1) * dk), slice(h * dv, (h + 1) * dv)
                        if i == 0:
                            st.did(nc.vector.tensor_copy(state[r, e], odd[job["S", i] % 2][r, e]))
                        else:
                            at = (i + 1) * P - 1
                            st.did(nc.vector.scalar_tensor_tensor(out=state[r, e], in0=state[r, e],
                                                                  scalar=fac[r, F_ALL, at:at + 1],
                                                                  in1=odd[job["S", i] % 2][r, e], op0=MUL, op1=ADD))
                    st.wait()
                    freed(dve, ("S", i))
                    dve.sem_inc(s_state, 1)
                by_head = lambda a: a.rearrange("p i (h e) -> p (i h) e", h=heads)
                dve.wait_ge(s_sq, (c + 1) * 2)
                st.then(nc.vector.tensor_reduce(ss[:, :], by_head(sq[:, :, :]), AX.X, ADD))
                nc.vector.tensor_scalar(ss[:, :], ss[:, :], 1.0 / dv, rms_eps, MUL, ADD).then_inc(s_ss, 1)
                dve.wait_ge(s_rms, c + 1)
                st.then(nc.vector.tensor_tensor(by_head(og[:, :, :]),
                                                ps_o[:, :, :].rearrange("p k (i h e) -> p (k i h) e", h=heads, e=dv),
                                                rrms[:, :].unsqueeze(2).broadcast_to([P, TPC * heads, dv]), MUL))
                dve.wait_ge(s_gw, c + 1)
                nc.vector.tensor_tensor(og[:, :, :], og[:, :, :], gate[:, :, :], MUL).then_inc(s_og, 1)
                dve.wait_ge(s_y, c + 1)
                st.end()
                nc.vector.tensor_tensor(sh.x[:, tiles(c), :], sh.x[:, tiles(c), :],
                                        odd[job["y"] % 2].rearrange("p (t d) -> p t d", t=TPC), ADD).then_inc(s_x, 1)
                dve.wait_ge(s_x, c + 2)
                freed(dve, "y")


def route_top1(nc, st, s, comb, before, gt, eq, small):
    rank = small[:, 0, :].rearrange("p (t e) -> p t e", t=TPC)
    ranks(nc, st, rank, s, before[:, :, :], gt[:, :, :, :], eq[:, :, :, :])
    st.then(nc.vector.tensor_scalar(comb, rank, 0.5, None, ALU.is_lt))


def route_groups(nc, st, s, comb, before, gt, eq, small, groups=4, top_groups=2, top=4):
    e = s.shape[2]
    g = e // groups
    n = TPC * groups
    assert g == 4
    by_group = lambda a: a.rearrange("p t (h k) -> p (t h) k", h=groups)
    region = lambda k, m: small[:, k, 0:TPC * m].rearrange("p (t m) -> p t m", t=TPC)
    s4 = by_group(s).rearrange("p n (a b) -> p n a b", a=2)
    pmax, psum = (small[:, k, 0:2 * n].rearrange("p (n a) -> p n a", a=2) for k in (0, 1))
    best, pair, grank, allowed = (small[:, k, 0:n] for k in (2, 3, 4, 5))
    masked, rank, total = region(0, e), region(1, e), region(2, 1)
    per_tile = lambda a: a.rearrange("p (t h) -> p t h", t=TPC)
    st.did(nc.vector.tensor_tensor(pmax, s4[:, :, :, 0], s4[:, :, :, 1], ALU.max))
    st.then(nc.vector.tensor_tensor(psum, s4[:, :, :, 0], s4[:, :, :, 1], ALU.add))
    st.did(nc.vector.tensor_tensor(best, pmax[:, :, 0], pmax[:, :, 1], ALU.add))
    st.then(nc.vector.tensor_tensor(pair, psum[:, :, 0], psum[:, :, 1], ALU.max))
    st.then(nc.vector.tensor_tensor(best, best, pair, ALU.max))
    ranks(nc, st, per_tile(grank), per_tile(best), before[:, 0:groups, 0:groups],
          gt[:, :, 0:groups, 0:groups], eq[:, :, 0:groups, 0:groups])
    st.then(nc.vector.tensor_scalar(allowed, grank, top_groups - 0.5, None, ALU.is_lt))
    wide = allowed.unsqueeze(2).broadcast_to([P, n, g])
    st.then(nc.vector.tensor_tensor(by_group(masked), by_group(s), wide, ALU.mult))
    st.then(nc.vector.scalar_tensor_tensor(out=by_group(masked), in0=wide, scalar=-1.0, in1=by_group(masked),
                                           op0=ALU.add, op1=ALU.add))
    ranks(nc, st, rank, masked, before[:, :, :], gt[:, :, :, :], eq[:, :, :, :])
    st.then(nc.vector.scalar_tensor_tensor(out=masked, in0=rank, scalar=top - 0.5, in1=s,
                                           op0=ALU.is_lt, op1=ALU.mult))
    st.then(nc.vector.tensor_reduce(total, masked, AX.X, ALU.add))
    st.then(nc.vector.tensor_scalar(total, total, 1e-6, None, ALU.add))
    st.then(nc.vector.reciprocal(total, total))
    st.then(nc.vector.tensor_tensor(comb, masked, total.broadcast_to([P, TPC, e]), ALU.mult))


ROUTE_TOP1_STEPS = 11
ROUTE_GROUPS_STEPS = 28


def routed_ffn(sh, stage, n_exp, f_exp, f_shared, score_func, route, route_steps):
    nc, w, tag = sh.nc, sh.w(stage), f"s{stage}"
    n_shared = f_shared // P
    units = n_exp * f_exp // P + n_shared
    K = 3 * n_exp
    with ExitStack() as ctx:
        sb = lambda n, shape, dt=F32: ctx.enter_context(nc.sbuf_tensor(f"{tag}_{n}", shape, dt))
        sem = lambda n: sh.sem(f"{tag}_{n}")
        bank = lambda n, shape=(P, S), dt=F32: ctx.enter_context(nc.psum_tensor(f"{tag}_{n}", list(shape), dt))
        ps_gate = [bank(f"gate{i}") for i in range(2)]
        ps_up = [bank(f"up{i}") for i in range(2)]
        ps_comb = [bank(f"comb{i}") for i in range(2)]
        ps_y = bank("y", (P, TPC, D))
        ps_route = bank("route")
        ps_logits = ps_route[:, 0:NT * n_exp].rearrange("p (t e) -> p t e", t=NT)
        ps_combT = ps_route[:, 256:512].bitcast(BF16)
        ln = LayerNorm(sh, ctx, tag, [ps_route, ps_y[:, :, :].rearrange("p t d -> p (t d)")])
        silu = sb("silu", [P, 2, S])
        gated = sb("gated", [P, 2, S])
        hidden = sb("hidden", [P, 2, S])
        comb = sb("comb", [P, TPC, n_exp])
        parts_wide = sb("comb_parts", [P, TPC, P], BF16)
        parts = parts_wide[:, :, 0:K].rearrange("p t (a e) -> p t a e", a=3)
        rest = sb("comb_rest", [P, 2, TPC, n_exp])
        combT = sb("combT", [K, S], BF16)
        scores = sb("scores", [P, NT, n_exp])
        small = sb("small", [P, 6, TPC * n_exp])
        sel = sb("sel", [K, units - n_shared, P], BF16)
        before = sb("before", [P, n_exp, n_exp])
        gt = sb("gt", [P, TPC, n_exp, n_exp])
        eq = sb("eq", [P, TPC, n_exp, n_exp])
        s_sel, s_before, s_zero = sem("sel_made"), sem("before_made"), sem("parts_cleared")
        s_logits, s_scores = sem("logits_ready"), sem("scores_ready")
        s_route = sem("route_steps")
        s_partsT, s_combT = sem("parts_transposed"), sem("combT_ready")
        s_up, s_silu = sem("gate_up_ready"), sem("silu_ready")
        s_gated, s_hidden = sem("gated_done"), sem("hidden_ready")
        s_down, s_x = sem("down_done"), sem("x_updated")
        block = ctx.enter_context(nc.Block())

        @block.sync
        def _(sp):
            sh.load_next(sp, stage)

        @block.gpsimd
        def _(pool):
            make_before(nc, pool, before, n_exp, s_before)
            nc.gpsimd.memset(sel[:, :, :], 0.0).then_inc(s_sel, 1)
            pool.wait_ge(s_sel, 1)
            n = 1
            for part in range(3):
                if f_exp >= P:
                    k = f_exp // P
                    view = sel[:, :, :].rearrange("r (e k) f -> r e (k f)", k=k)
                    pattern = [[-1, n_exp], [0, k * P]]
                else:
                    view = sel[:, :, :].rearrange("r u (e f) -> r (u e) f", f=f_exp)
                    pattern = [[-1, n_exp], [0, f_exp]]
                nc.gpsimd.affine_select(out=view, in_=view, compare_op=ALU.not_equal, fill=1.0,
                                        base=-part * n_exp, pattern=pattern,
                                        channel_multiplier=1).then_inc(s_sel, 1)
                n += 1
                pool.wait_ge(s_sel, n)
            ln.gpsimd(pool)

        @block.tensor
        def _(pe):
            pe.sem_inc(s_down, 1)
            pe.wait_ge(sh.wsem[stage], 16)
            ln.tensor(pe)
            pe.wait_ge(s_sel, 4)
            pe.wait_ge(ln.ready, B)
            for t in range(NT):
                last = nc.tensor.matmul(ps_logits[:, t, :], sh.xnT[:, t * P:(t + 1) * P], w["router"],
                                        start=True, stop=True)
            last.then_inc(s_logits, 1)
            pe.wait_ge(s_scores, 1)
            with pe.Fori(0, B) as c:
                def gate_up(u):
                    pe.wait_ge(s_hidden, 1 + c * units + (u - 1 if u else 0))
                    nc.tensor.matmul(ps_gate[u % 2][:, :], w["gate"][:, u * P:(u + 1) * P],
                                     sh.xnT[:, cols(c)], start=True, stop=True)
                    last = nc.tensor.matmul(ps_up[u % 2][:, :], w["up"][:, u * P:(u + 1) * P],
                                            sh.xnT[:, cols(c)], start=True, stop=True)
                    if u >= n_shared:
                        pe.wait_ge(s_combT, c + 1)
                        last = nc.tensor.matmul(ps_comb[u % 2][:, :], sel[:, u - n_shared, :], combT[:, :],
                                                start=True, stop=True)
                    last.then_inc(s_up, 1)

                def down(u):
                    pe.wait_ge(s_hidden, 1 + c * units + u + 1)
                    if u == 0:
                        pe.wait_ge(s_x, 1 + c)
                    for i in range(TPC):
                        last = nc.tensor.matmul(ps_y[:, i, :], hidden[:, u % 2, i * P:(i + 1) * P],
                                                w["down"][:, u * P:(u + 1) * P],
                                                start=(u == 0 and i == 0), stop=(u == units - 1),
                                                skip_group_check=True)
                    last.then_inc(s_down, 1)

                for u in range(units):
                    gate_up(u)
                    if u == n_shared - 1:
                        pe.wait_ge(s_route, (c + 1) * route_steps)
                        for i in range(TPC):
                            last = nc.tensor.transpose(ps_combT[:, i * P:(i + 1) * P], parts_wide[:, i, :],
                                                       sh.identb[:, :])
                        last.then_inc(s_partsT, 1)
                    if u:
                        down(u - 1)
                down(units - 1)

        @block.scalar
        def _(act):
            ln.scalar(act)
            act.wait_ge(s_logits, 1)
            nc.scalar.activation(scores[:, :, :], ps_logits, score_func).then_inc(s_scores, 1)
            with act.Fori(0, B) as c:
                for u in range(units):
                    act.wait_ge(s_up, c * units + u + 1)
                    nc.scalar.activation(silu[:, u % 2, :], ps_gate[u % 2][:, :], ACT.Silu).then_inc(s_silu, 1)

        @block.vector
        def _(dve):
            dve.sem_inc(s_hidden, 1)
            dve.sem_inc(s_x, 1)
            nc.vector.memset(parts_wide[:, :, :], 0.0).then_inc(s_zero, 1)
            ln.vector(dve)
            dve.wait_ge(s_zero, 1)
            dve.wait_ge(s_before, 2)
            dve.wait_ge(s_scores, 1)
            with dve.Fori(0, B) as c:
                st = Steps(dve, s_route, c * route_steps, route_steps)
                route(nc, st, scores[:, tiles(c), :], comb[:, :, :], before, gt, eq, small)
                split3(nc, st, [parts[:, :, k, :] for k in range(3)], comb[:, :, :],
                       [rest[:, k, :, :] for k in range(2)])
                st.end()
                for u in range(units):
                    if u == n_shared:
                        dve.wait_ge(s_partsT, c + 1)
                        nc.vector.tensor_copy(combT[:, :], ps_combT[0:K, :]).then_inc(s_combT, 1)
                    dve.wait_ge(s_silu, c * units + u + 1)
                    dve.wait_ge(s_down, 1 + c * units + (u - 1 if u else 0))
                    if u < n_shared:
                        nc.vector.tensor_tensor(hidden[:, u % 2, :], silu[:, u % 2, :], ps_up[u % 2][:, :],
                                                ALU.mult).then_inc(s_hidden, 1)
                    else:
                        nc.vector.tensor_tensor(gated[:, u % 2, :], silu[:, u % 2, :], ps_up[u % 2][:, :],
                                                ALU.mult).then_inc(s_gated, 1)
                        dve.wait_ge(s_gated, c * (units - n_shared) + u - n_shared + 1)
                        nc.vector.tensor_tensor(hidden[:, u % 2, :], gated[:, u % 2, :], ps_comb[u % 2][:, :],
                                                ALU.mult).then_inc(s_hidden, 1)
                dve.wait_ge(s_down, 1 + (c + 1) * units)
                nc.vector.tensor_tensor(sh.x[:, tiles(c), :], sh.x[:, tiles(c), :], ps_y[:, :, :],
                                        ALU.add).then_inc(s_x, 1)


def ternary_ffn(sh, stage, hid=512):
    nc, w, tag = sh.nc, sh.w(stage), f"s{stage}"
    n = hid // P
    with ExitStack() as ctx:
        sb = lambda m, shape, dt=F32: ctx.enter_context(nc.sbuf_tensor(f"{tag}_{m}", shape, dt))
        sem = lambda m: sh.sem(f"{tag}_{m}")
        bank = lambda m, shape=(P, S): ctx.enter_context(nc.psum_tensor(f"{tag}_{m}", list(shape), F32))
        ps_a = [bank(f"a{i}") for i in range(2)]
        ps_b = [bank(f"b{i}") for i in range(2)]
        ps_y = [bank(f"y{i}", (P, TPC, D)) for i in range(2)]
        ps_t = [bank(f"t{i}") for i in range(2)]
        ln = LayerNorm(sh, ctx, tag, ps_t)
        silu = sb("silu", [P, 2, S])
        h0 = sb("h0", [P, n, S])
        h1 = sb("h1", [P, n, S])
        h2 = sb("h2", [P, n, S])
        w3s = sb("w3_scaled", [P, n, D])
        s_w3 = sem("w3_scaled_done")
        s_up, s_silu, s_h0 = sem("gate_up_ready"), sem("silu_ready"), sem("h0_ready")
        s_p1, s_h1, s_p2, s_h2 = sem("h1_summed"), sem("h1_ready"), sem("h2_summed"), sem("h2_ready")
        s_y, s_x = sem("y_summed"), sem("x_updated")
        block = ctx.enter_context(nc.Block())

        @block.sync
        def _(sp):
            sh.load_next(sp, stage)

        @block.gpsimd
        def _(pool):
            ln.gpsimd(pool)

        @block.tensor
        def _(pe):
            pe.sem_inc(s_p1, 1)
            pe.sem_inc(s_y, 1)
            pe.wait_ge(sh.wsem[stage], 16)
            ln.tensor(pe)
            pe.wait_ge(ln.ready, B)
            pe.wait_ge(s_w3, n)
            with pe.Fori(0, B) as c:
                for f in range(n):
                    pe.wait_ge(s_h0, 1 + c * n + (f - 1 if f else 0))
                    nc.tensor.matmul(ps_a[f % 2][:, :], w["w1"][:, f * P:(f + 1) * P], sh.xnT[:, cols(c)],
                                     start=True, stop=True)
                    nc.tensor.matmul(ps_b[f % 2][:, :], w["w2"][:, f * P:(f + 1) * P], sh.xnT[:, cols(c)],
                                     start=True, stop=True).then_inc(s_up, 1)
                for name, src, s_src, first, ps, s_free, s_done in (("h1", h0, s_h0, 1, ps_a, s_h1, s_p1),
                                                                    ("h2", h1, s_h1, 0, ps_b, s_h2, s_p2)):
                    wt = w[name].rearrange("p (k o) -> p k o", k=n)
                    for f in range(n):
                        if f < 2:
                            pe.wait_ge(s_h0, 1 + (c + 1) * n)
                        else:
                            pe.wait_ge(s_free, c * n + f - 1)
                        for k in range(n):
                            if f == 0:
                                pe.wait_ge(s_src, first + c * n + k + 1)
                            last = nc.tensor.matmul(ps[f % 2][:, :], wt[:, k, f * P:(f + 1) * P], src[:, k, :],
                                                    start=(k == 0), stop=(k == n - 1))
                        last.then_inc(s_done, 1)
                pe.wait_ge(s_x, 1 + c)
                for k in range(n):
                    pe.wait_ge(s_h2, c * n + k + 1)
                    for i in range(TPC):
                        last = nc.tensor.matmul(ps_y[0][:, i, :], h2[:, k, i * P:(i + 1) * P], w3s[:, k, :],
                                                start=(k == 0 and i == 0), stop=(k == n - 1),
                                                skip_group_check=True)
                last.then_inc(s_y, 1)

        @block.scalar
        def _(act):
            ln.scalar(act)
            act.wait_ge(sh.wsem[stage], 16)
            with act.Fori(0, B) as c:
                for f in range(n):
                    act.wait_ge(s_up, c * n + f + 1)
                    nc.scalar.activation(silu[:, f % 2, :], ps_a[f % 2][:, :], ACT.Silu,
                                         scale=w["w1_s"][:, f:f + 1]).then_inc(s_silu, 1)
                for s_sum, first, ps, out, scale, s_out in ((s_p1, 1, ps_a, h1, w["h1_s"], s_h1),
                                                            (s_p2, 0, ps_b, h2, w["h2_s"], s_h2)):
                    for f in range(n):
                        act.wait_ge(s_sum, first + c * n + f + 1)
                        if s_out is s_h2 and f == 0:
                            act.wait_ge(s_y, 1 + c)
                        nc.scalar.activation(out[:, f, :], ps[f % 2][:, :], ACT.Gelu,
                                             scale=scale[:, f:f + 1]).then_inc(s_out, 1)

        @block.vector
        def _(dve):
            dve.sem_inc(s_h0, 1)
            dve.sem_inc(s_x, 1)
            dve.wait_ge(sh.wsem[stage], 16)
            for k in range(n):
                nc.vector.tensor_tensor(w3s[:, k, :], w["w3"][:, k * D:(k + 1) * D], w["w3_s"],
                                        ALU.mult).then_inc(s_w3, 1)
            ln.vector(dve)
            with dve.Fori(0, B) as c:
                for f in range(n):
                    dve.wait_ge(s_silu, c * n + f + 1)
                    if f == 0:
                        dve.wait_ge(s_p1, 1 + c * n)
                    nc.vector.scalar_tensor_tensor(out=h0[:, f, :], in0=ps_b[f % 2][:, :],
                                                   scalar=w["w2_s"][:, f:f + 1], in1=silu[:, f % 2, :],
                                                   op0=ALU.mult, op1=ALU.mult).then_inc(s_h0, 1)
                dve.wait_ge(s_y, 1 + c + 1)
                nc.vector.tensor_tensor(sh.x[:, tiles(c), :], sh.x[:, tiles(c), :], ps_y[0][:, :, :],
                                        ALU.add).then_inc(s_x, 1)


def causal_plan(c):
    per_bank = {0: 4, 1: 2, 2: 1, 3: 1}
    first = [("max", k, i, h, per_bank[i]) for k, (i, h) in
             enumerate((i, h) for i in range(TPC) for h in range(0, H8, per_bank[i]))]
    if c < 0:
        return [("q",), ("k",), ("split",)] + first + [("maxT",)]
    nxt = c + 1 < B
    plan = []
    for u in range(5 * H8 // 4):
        if u == 0:
            plan.append(("v",))
        if nxt and 1 <= u < 4:
            plan.append((("q",), ("k",), ("split",))[u - 1])
        plan.append(("exp", u))
        if u % 5 == 1 and u > 5:
            plan.append(("pv", u // 5 - 1))
        if u % 5 == 3 and u > 5:
            plan.append(("turn", u // 5 - 1))
        if nxt and u >= 8:
            plan += first[4 * (u - 8):4 * (u - 7)]
    return plan + [("pv", 3)] + [("maxT",)] * nxt + [("turn", 3), ("out",)]


def causal_attention(sh, stage, ctx, ln, pa, p1, p2, po, pm, wq, wk, wv, wo, qk_bias, v_bias, o_bias, scale,
                     before_scalar, before_vector, before_tensor, before_gpsimd, hs=None, extra=None):
    nc, tag = sh.nc, f"s{stage}"
    W = 3 * HD8
    R = 9 * HD8
    sb = lambda m, shape, dt=F32: ctx.enter_context(nc.sbuf_tensor(f"{tag}_{m}", shape, dt))
    sem = lambda m: sh.sem(f"{tag}_{m}")
    qkf = sb("qk_f32", [P, 2, S])
    parts = sb("qk_parts", [P, 3, 2, S], BF16)
    rest = sb("qk_rest", [P, 2, S])
    qs = sb("q_stack", [R + 3, 2, H8, S], BF16)
    ks = sb("k_stack", [P, 2, H8, S], BF16)
    v32 = sb("v_and_one", [P, TPC, H8, 32])
    mask_qk = sb("mask_qk", [P, P], BF16)
    mask_kq = sb("mask_kq", [P, P], BF16)
    negmax = sb("negmax", [P, TPC, H8])
    mparts = sb("max_parts", [P, TPC, 3, H8], BF16)
    mrest = sb("max_rest", [P, 2, TPC, H8])
    mT = sb("maxT", [3 * H8, S], BF16)
    pb = sb("probs_b", [P, 2, 4, 256])
    oq = sb("o_quad", [P, S])
    recip = sb("recip", [P, TPC, 4])
    o = sb("o", [P, TPC, D])
    oT = ln.xn[:, 0, :, :].rearrange("p i d -> p (i d)")
    s_mask, s_ones = sem("masks_made"), sem("ones_made")
    s_q, s_qf = sem("qk_projected"), sem("qk_in_sbuf")
    s_v, s_v32 = sem("v_projected"), sem("v_in_sbuf")
    s_split, s_wrote, s_stack = sem("qk_split_steps"), sem("qk_parts_stored"), sem("stack_loaded")
    s_max, s_neg, s_msplit = sem("scores_for_max"), sem("max_done"), sem("max_split_steps")
    s_maxT, s_mT, s_mwrote, s_mrow = (sem("max_transposed"), sem("maxT_in_sbuf"), sem("maxT_stored"),
                                      sem("max_rows_loaded"))
    s_sc, s_exp, s_pv = sem("scores_less_max"), sem("probs_ready"), sem("pv_done")
    s_oq, s_turn = sem("o_quad_in_sbuf"), sem("o_quad_transposed")
    s_rec, s_norm = sem("recip_done"), sem("o_normalised")
    s_oT, s_oTs, s_y, s_x = sem("o_transposed"), sem("oT_in_sbuf"), sem("y_ready"), sem("x_updated")
    s_bias = sem("o_bias_added")
    s_used = sem("misc_bank_free")
    UNITS = 44
    EXPS = 5 * H8 // 4
    plans = [(c, causal_plan(c)) for c in range(-1, B)]
    fills = {}
    for c, plan in plans:
        for item in plan:
            if item[0] in ("q", "k", "maxT"):
                fills[item[0], c + 1] = len(fills)
            elif item[0] == "v":
                fills["v", c] = len(fills)
            elif item[0] == "turn":
                fills["turn", 4 * c + item[1]] = len(fills)
            elif item[0] == "out":
                fills["oT", c] = len(fills)
                fills["y", c] = len(fills)
    block = ctx.enter_context(nc.Block())

    @block.sync
    def _(sp):
        if extra:
            sp.dma_start(extra[0], extra[1]).then_inc(extra[2], 16)
        sh.load_next(sp, stage)

        def stack(c):
            b = c % 2
            sp.wait_ge(s_split, 5 * (c + 1))
            for qk in range(2):
                for k in range(3):
                    sp.dma_start(sh.scratch_qk[c, qk, :, k], parts[:, k, qk, :]).then_inc(s_wrote, 16)
            sp.wait_ge(s_wrote, 16 * 6 * (c + 1))
            if c >= 2:
                sp.wait_ge(s_sc, EXPS * (c - 1))
            rows = lambda qk, k0, k1: sh.scratch_qk[c, qk, :, k0:k1].rearrange("h k d n -> (k d) h n")
            for a in range(3):
                sp.dma_start(ks[a * W:(a + 1) * W, b, :, :], rows(1, 0, 3)).then_inc(s_stack, 16)
                n = 3 - a
                sp.dma_start(qs[a * W:a * W + n * HD8, b, :, :], rows(0, a, 3)).then_inc(s_stack, 16)
                if a:
                    sp.dma_start(qs[a * W + n * HD8:(a + 1) * W, b, :, :], rows(0, 0, a)).then_inc(s_stack, 16)

        def max_rows(c):
            sp.wait_ge(s_mT, c + 1)
            sp.dma_start(sh.scratch_max[c], mT[:, :]).then_inc(s_mwrote, 16)
            sp.wait_ge(s_mwrote, 16 * (c + 1))
            sp.dma_start(qs[R:R + 3, c % 2, :, :],
                         sh.scratch_max[c].rearrange("(k h) n -> k h n", k=3)).then_inc(s_mrow, 16)

        sp.wait_ge(s_ones, 1)
        for c in range(B):
            stack(c)
            max_rows(c)

    @block.gpsimd
    def _(pool):
        nc.gpsimd.memset(ks[64:96, :, :, :], 1.0).then_inc(s_ones, 1)
        pool.wait_ge(s_ones, 1)
        nc.gpsimd.memset(v32[:, :, :, HD8:32], 0.0).then_inc(s_ones, 1)
        pool.wait_ge(s_ones, 2)
        nc.gpsimd.memset(v32[:, :, :, HD8:HD8 + 1], 1.0).then_inc(s_ones, 1)
        nc.gpsimd.memset(mask_qk[:, :], 0.0).then_inc(s_mask, 1)
        nc.gpsimd.memset(mask_kq[:, :], 0.0).then_inc(s_mask, 1)
        pool.wait_ge(s_mask, 2)
        nc.gpsimd.affine_select(out=mask_qk[:, :], in_=mask_qk[:, :], compare_op=ALU.is_ge, fill=NEG,
                                base=0, pattern=[[-1, P]], channel_multiplier=1).then_inc(s_mask, 1)
        nc.gpsimd.affine_select(out=mask_kq[:, :], in_=mask_kq[:, :], compare_op=ALU.is_ge, fill=NEG,
                                base=0, pattern=[[1, P]], channel_multiplier=-1).then_inc(s_mask, 1)
        before_gpsimd(pool)

        resid = sh.x if hs is None else hs
        pool.wait_ge(ln.s_xn, NT)
        for c in range(B):
            ts = slice(c * TPC, (c + 1) * TPC)
            nc.gpsimd.tensor_tensor(resid[:, ts, :], resid[:, ts, :],
                                    o_bias.unsqueeze(1).broadcast_to([P, TPC, D]), ALU.add).then_inc(s_bias, 1)
        if hs is not None:
            for c in range(B):
                ts = slice(c * TPC, (c + 1) * TPC)
                pool.wait_ge(s_x, c + 1)
                nc.gpsimd.tensor_tensor(sh.x[:, ts, :], sh.x[:, ts, :], hs[:, ts, :], ALU.add)

    @block.tensor
    def _(pe):
        pe.wait_ge(sh.wsem[stage], 16)
        before_tensor(pe)
        ln.tensor(pe)
        pe.wait_ge(ln.ready, B)
        pe.wait_ge(s_mask, 4)
        pe.wait_ge(s_ones, 3)

        def project(c, name):
            pe.wait_ge(s_used, fills[name, c]) if fills[name, c] else None
            x = sh.xnT[:, c * S:(c + 1) * S]
            if name == "v":
                for i in range(TPC):
                    last = nc.tensor.matmul(pm[:, i * P:(i + 1) * P], x[:, i * P:(i + 1) * P], wv,
                                            start=True, stop=True)
                last.then_inc(s_v, 1)
            else:
                nc.tensor.matmul(pm[:, :], wq if name == "q" else wk, x, start=True, stop=True).then_inc(s_q, 1)

        def scores_for_max(c, k, i, h0, n):
            k += UNITS * c
            if k >= 2:
                pe.wait_ge(s_neg, k - 1)
            m = (i + 1) * P
            for x in range(n):
                out = p1[k % 2][:, x * m:(x + 1) * m]
                nc.tensor.matmul(out, qs[0:R, c % 2, h0 + x, i * P:(i + 1) * P], ks[0:R, c % 2, h0 + x, 0:m],
                                 start=True, stop=False)
                last = nc.tensor.matmul(out[:, i * P:m], sh.identb[:, :], mask_qk[:, :], start=False, stop=True)
            last.then_inc(s_max, 1)

        def scores_less_max(c, u):
            n = EXPS * c + u
            if n >= 2:
                pe.wait_ge(s_exp, n - 1)
            ps = p2[n % 2]
            g, r = divmod(u, 5)
            blocks = [(0, 0, 4 * g + r), (1, 512, 4 * g + r), (3, 896, 4 * g + r)] if r < 4 else \
                     [(2, 256 * x, 4 * g + x) for x in range(4)]
            for j, at, h in blocks:
                n = S - j * P
                nc.tensor.matmul(ps[:, at:at + n], ks[0:R + 3, c % 2, h, j * P:(j + 1) * P],
                                 qs[0:R + 3, c % 2, h, j * P:S], start=True, stop=False)
                last = nc.tensor.matmul(ps[:, at:at + P], sh.identb[:, :], mask_kq[:, :], start=False, stop=True)
            last.then_inc(s_sc, 1)

        def values(c, g):
            q = 4 * c + g
            pe.wait_ge(s_exp, EXPS * c + 5 * (g + 1))
            if g == 0:
                pe.wait_ge(s_v32, c + 1)
            if q:
                pe.wait_ge(s_oq, q)
            for j in range(TPC):
                at, n = {0: 0, 1: 512, 3: 896}.get(j), S - j * P
                for x in range(4):
                    prob = pb[:, q % 2, x, :] if j == 2 else pa[:, q % 2, x, at:at + n]
                    last = nc.tensor.matmul(po[32 * x:32 * x + 32, j * P:S], v32[:, j, 4 * g + x, :], prob,
                                            start=(j == 0), stop=(j == TPC - 1), skip_group_check=True)
            last.then_inc(s_pv, 1)

        def turn(c, g):
            q = 4 * c + g
            pe.wait_ge(s_oq, q + 1)
            pe.wait_ge(s_used, fills["turn", q])
            for i in range(TPC):
                last = nc.tensor.transpose(pm[:, i * P:(i + 1) * P], oq[:, i * P:(i + 1) * P], sh.ident[:, :])
            last.then_inc(s_turn, 1)

        def max_transposes(c):
            pe.wait_ge(s_msplit, 5 * (c + 1))
            pe.wait_ge(s_used, fills["maxT", c])
            out = pm[:, 0:S // 2].bitcast(BF16)
            for i in range(TPC):
                last = nc.tensor.transpose(out[0:3 * H8, i * P:(i + 1) * P],
                                           mparts[:, i, :, :].rearrange("p k h -> p (k h)"), sh.identb[:, :])
            last.then_inc(s_maxT, 1)

        def project_out(c):
            pe.wait_ge(s_norm, 4 * (c + 1))
            pe.wait_ge(s_used, fills["oT", c])
            for i in range(TPC):
                last = nc.tensor.transpose(pm[:, i * P:(i + 1) * P], o[:, i, :], sh.ident[:, :])
            last.then_inc(s_oT, 1)
            pe.wait_ge(s_used, fills["y", c])
            for i in range(TPC):
                last = nc.tensor.matmul(pm[:, i * P:(i + 1) * P], oT[:, i * P:(i + 1) * P], wo, start=True, stop=True)
            last.then_inc(s_y, 1)

        for c, plan in plans:
            for item in plan:
                if item[0] in ("q", "k"):
                    project(c + 1, item[0])
                elif item[0] == "v":
                    project(c, "v")
                elif item[0] == "max":
                    if item[1] == 0:
                        pe.wait_ge(s_stack, 16 * 8 * (c + 2))
                    scores_for_max(c + 1, *item[1:])
                elif item[0] == "maxT":
                    max_transposes(c + 1)
                elif item[0] == "exp":
                    if item[1] == 0:
                        pe.wait_ge(s_mrow, 16 * (c + 1))
                    scores_less_max(c, item[1])
                elif item[0] == "pv":
                    values(c, item[1])
                elif item[0] == "turn":
                    turn(c, item[1])
                elif item[0] == "out":
                    project_out(c)

    @block.scalar
    def _(act):
        before_scalar(act)
        ln.scalar(act)
        for c, plan in plans:
            for item in plan:
                if item[0] in ("q", "k"):
                    d, k = c + 1, "qk".index(item[0])
                    if d >= 1:
                        act.wait_ge(s_split, 5 * d)
                    act.wait_ge(s_q, 2 * d + k + 1)
                    nc.scalar.activation(qkf[:, k, :], pm[:, :], ACT.Identity,
                                         bias=qk_bias[k] if qk_bias else 0.0).then_inc(s_qf, 1)
                    act.wait_ge(s_qf, 2 * d + k + 1)
                    act.sem_inc(s_used, 1)
                elif item[0] == "maxT":
                    act.wait_ge(s_maxT, c + 2)
                    if c >= 0:
                        act.wait_ge(s_mwrote, 16 * (c + 1))
                    nc.scalar.copy(mT[:, :], pm[0:3 * H8, 0:S // 2].bitcast(BF16)).then_inc(s_mT, 1)
                    act.wait_ge(s_mT, c + 2)
                    act.sem_inc(s_used, 1)
                elif item[0] == "exp":
                    n = EXPS * c + item[1]
                    g, r = divmod(item[1], 5)
                    q = 4 * c + g
                    act.wait_ge(s_sc, n + 1)
                    if r == 0 and q >= 2:
                        act.wait_ge(s_pv, q - 1)
                    out = pa[:, q % 2, r, :] if r < 4 else pb[:, q % 2, :, :].rearrange("p x n -> p (x n)")
                    nc.scalar.activation(out, p2[n % 2][:, :], ACT.Exp, scale=scale).then_inc(s_exp, 1)
                elif item[0] == "pv":
                    q = 4 * c + item[1]
                    act.wait_ge(s_pv, q + 1)
                    if q:
                        act.wait_ge(s_turn, q)
                    nc.scalar.copy(oq[:, :], po[:, :]).then_inc(s_oq, 1)
                elif item[0] == "out":
                    act.wait_ge(s_oT, c + 1)
                    nc.scalar.copy(oT, pm[:, :]).then_inc(s_oTs, 1)
                    act.wait_ge(s_oTs, c + 1)
                    act.sem_inc(s_used, 1)

    @block.vector
    def _(dve):
        before_vector(dve)
        ln.vector(dve)
        resid = sh.x if hs is None else hs
        for c, plan in plans:
            for item in plan:
                if item[0] == "v":
                    dve.wait_ge(s_v, c + 1)
                    if c == 0:
                        dve.wait_ge(s_ones, 3)
                    else:
                        dve.wait_ge(s_pv, 4 * c)
                    for i in range(TPC):
                        last = nc.vector.tensor_tensor(v32[:, i, :, 0:HD8],
                                                       pm[:, i * P:(i + 1) * P].rearrange("p (h d) -> p h d", h=H8),
                                                       v_bias.rearrange("p (h d) -> p h d", h=H8), ALU.add)
                    last.then_inc(s_v32, 1)
                    dve.wait_ge(s_v32, c + 1)
                    dve.sem_inc(s_used, 1)
                elif item[0] == "split":
                    d = c + 1
                    if d >= 1:
                        dve.wait_ge(s_wrote, 16 * 6 * d)
                    dve.wait_ge(s_qf, 2 * (d + 1))
                    st = Steps(dve, s_split, 5 * d, 5)
                    split3(nc, st, [parts[:, k] for k in range(3)], qkf[:, :, :],
                           [rest[:, :, :], qkf[:, :, :]])
                    st.end()
                elif item[0] == "max":
                    _, k, i, h0, n = item
                    k += UNITS * (c + 1)
                    m = (i + 1) * P
                    dve.wait_ge(s_max, k + 1)
                    nc.vector.tensor_reduce(negmax[:, i, h0:h0 + n],
                                            p1[k % 2][:, 0:n * m].rearrange("p (n m) -> p n m", n=n),
                                            AX.X, ALU.max, negate=True).then_inc(s_neg, 1)
                elif item[0] == "maxT":
                    d = c + 1
                    dve.wait_ge(s_neg, UNITS * (d + 1))
                    if d >= 1:
                        dve.wait_ge(s_maxT, d)
                    st = Steps(dve, s_msplit, 5 * d, 5)
                    split3(nc, st, [mparts[:, :, k, :] for k in range(3)], negmax[:, :, :],
                           [mrest[:, k, :, :] for k in range(2)])
                    st.end()
                elif item[0] == "turn":
                    g = item[1]
                    q = 4 * c + g
                    quad = pm[:, :].rearrange("p (t x d) -> p t x d", t=TPC, x=4)
                    dve.wait_ge(s_turn, q + 1)
                    nc.vector.reciprocal(recip[:, :, :], quad[:, :, :, HD8]).then_inc(s_rec, 1)
                    dve.wait_ge(s_rec, q + 1)
                    if g == 0 and c >= 1:
                        dve.wait_ge(s_oT, c)
                    nc.vector.tensor_tensor(
                        o[:, :, 32 * g:32 * g + 32].rearrange("p t (x d) -> p t x d", x=4), quad[:, :, :, 0:HD8],
                        recip[:, :, :].unsqueeze(3).broadcast_to([P, TPC, 4, HD8]), ALU.mult).then_inc(s_norm, 1)
                    dve.wait_ge(s_norm, q + 1)
                    dve.sem_inc(s_used, 1)
                elif item[0] == "out":
                    dve.wait_ge(s_y, c + 1)
                    dve.wait_ge(s_bias, c + 1)
                    ts = slice(c * TPC, (c + 1) * TPC)
                    nc.vector.tensor_tensor(resid[:, ts, :], resid[:, ts, :],
                                            pm[:, :].rearrange("p (t d) -> p t d", t=TPC), ALU.add).then_inc(s_x, 1)
                    dve.wait_ge(s_x, c + 1)
                    dve.sem_inc(s_used, 1)


def low_rank_attention(sh, stage):
    nc, w, tag = sh.nc, sh.w(stage), f"s{stage}"
    R = 64
    with ExitStack() as ctx:
        bank = lambda m, shape=(P, S): ctx.enter_context(nc.psum_tensor(f"{tag}_{m}", list(shape), F32))
        p1 = [bank(f"for_max{i}") for i in range(2)]
        p2 = [bank(f"scores{i}", (P, 1024)) for i in range(2)]
        po, pm = bank("pv"), bank("odd_jobs")
        weff = ctx.enter_context(nc.sbuf_tensor(f"{tag}_weff", [P, 2, D], F32))
        s_prod, s_weff = (sh.sem(f"{tag}_{m}") for m in ("factors_multiplied", "weff_ready"))
        ln = LayerNorm(sh, ctx, tag, p1)
        pa = ctx.enter_context(nc.sbuf_tensor(f"{tag}_probs_a", [P, 2, 4, 1024], F32))

        def factors_tensor(pe):
            for k in range(2):
                rows = slice(k * R, (k + 1) * R)
                for h in range(H8):
                    last = nc.tensor.matmul(p2[k][:, h * HD8:(h + 1) * HD8],
                                            w["a"][rows, h * D:(h + 1) * D], w["b"][rows, h * HD8:(h + 1) * HD8],
                                            start=True, stop=True)
                last.then_inc(s_prod, 1)
            pe.wait_ge(s_weff, 2)

        def factors_scalar(act):
            for k in range(2):
                act.wait_ge(s_prod, k + 1)
                nc.scalar.copy(weff[:, k, :], p2[k][:, 0:D]).then_inc(s_weff, 1)

        def weights_vector(dve):
            dve.wait_ge(sh.wsem[stage], 16)

        def weights_gpsimd(pool):
            ln.gpsimd(pool)
            pool.wait_ge(sh.wsem[stage], 16)

        causal_attention(sh, stage, ctx, ln, pa, p1, p2, po, pm, weff[:, 0, :], weff[:, 1, :], w["v"], w["o"], None,
                         w["v_b"], w["o_b"], HD8 ** -0.5, factors_scalar, weights_vector, factors_tensor,
                         weights_gpsimd)


L2_SEGMENTS = [("ca_w", 3 * D), ("cp_w", D), ("cf_w", 512), ("cm_w", 512), ("ca_b", 2 + D), ("cp_b", D),
               ("cf_b", 4), ("cm_b", D)]


def generated_attention(sh, stage):
    nc, w, tag = sh.nc, sh.w(stage), f"s{stage}"
    width = sum(n for _, n in L2_SEGMENTS)
    with ExitStack() as ctx:
        bank = lambda m, shape=(P, S): ctx.enter_context(nc.psum_tensor(f"{tag}_{m}", list(shape), F32))
        sem = lambda m: sh.sem(f"{tag}_{m}")
        p1 = [bank(f"for_max{i}") for i in range(2)]
        p2 = [bank(f"scores{i}", (P, 1024)) for i in range(2)]
        po, pm = bank("pv"), bank("odd_jobs")
        s_mix, s_tanh, s_gen = sem("subs_mixed"), sem("tanh_done"), sem("params_steps")
        n = len(L2_SEGMENTS)
        outer = LayerNorm(sh, ctx, tag + "a", keep=sh.hs)
        ln = LayerNorm(sh, ctx, tag, p1, src=sh.hs, affine=(w["ln1_g"], w["ln1_b"]))
        gen = sh.gen(w)
        pa = ctx.enter_context(nc.sbuf_tensor(f"{tag}_probs_a", [P, 2, 4, 1024], F32))
        s_extra = sem("generators_loaded")
        flat = pa[:, :, :, :].rearrange("p a x n -> p (a x n)")
        sub1, W, bias = (flat[:, k * width:(k + 1) * width] for k in range(3))

        def params_vector(dve):
            dve.wait_ge(sh.wsem[stage], 16)
            outer.vector(dve)
            dve.wait_ge(outer.s_xn, NT)
            dve.wait_ge(s_extra, 16)
            at = 0
            for k, (name, m) in enumerate(L2_SEGMENTS):
                c = slice(at, at + m)
                nc.vector.tensor_scalar(w["sub0"][:, c], w["sub0"][:, c], w["a"][:, 2 * k:2 * k + 1], None,
                                        ALU.mult).then_inc(s_mix, 1)
                dve.wait_ge(s_mix, 2 * k + 1)
                nc.vector.scalar_tensor_tensor(out=w["sub0"][:, c], in0=sub1[:, c],
                                               scalar=w["a"][:, 2 * k + 1:2 * k + 2], in1=w["sub0"][:, c],
                                               op0=ALU.mult, op1=ALU.add).then_inc(s_mix, 1)
                at += m
            dve.wait_ge(s_tanh, 1)
            nc.vector.tensor_tensor(w["sub0"], w["sub0"], W, ALU.mult).then_inc(s_gen, 1)
            dve.wait_ge(s_gen, 1)
            nc.vector.tensor_tensor(w["sub0"], w["sub0"], bias, ALU.add).then_inc(s_gen, 1)

        def tanh_scalar(act):
            act.wait_ge(s_mix, 2 * n)
            nc.scalar.activation(w["sub0"], w["sub0"], ACT.Tanh).then_inc(s_tanh, 1)
            act.wait_ge(s_gen, 2)

        def wait_tensor(pe):
            pe.wait_ge(s_gen, 2)

        def norms_gpsimd(pool):
            pool.wait_ge(sh.wsem[stage], 16)
            outer.gpsimd(pool)
            ln.gpsimd(pool)
            pool.wait_ge(s_gen, 2)

        ca, cab = gen["ca_w"], gen["ca_b"]
        causal_attention(sh, stage, ctx, ln, pa, p1, p2, po, pm, ca[:, 0:D], ca[:, D:2 * D], ca[:, 2 * D:3 * D],
                         gen["cp_w"], (cab[:, 0:1], cab[:, 1:2]), cab[:, 2:2 + D], gen["cp_b"], HD8 ** -0.5,
                         tanh_scalar, params_vector, wait_tensor, norms_gpsimd, hs=sh.hs,
                         extra=(flat[:, 0:3 * width], sh.extra[stage], s_extra))


def generated_mlp(sh, stage, hid=512):
    nc, w, tag = sh.nc, sh.w(stage), f"s{stage}b"
    n = hid // P
    gen = sh.gen(w)
    with ExitStack() as ctx:
        sb = lambda m, shape, dt=F32: ctx.enter_context(nc.sbuf_tensor(f"{tag}_{m}", shape, dt))
        sem = lambda m: sh.sem(f"{tag}_{m}")
        bank = lambda m, shape=(P, S): ctx.enter_context(nc.psum_tensor(f"{tag}_{m}", list(shape), F32))
        ps_h = [bank(f"h{i}") for i in range(4)]
        ps_y = [bank(f"y{i}", (P, TPC, D)) for i in range(2)]
        ps_t = [bank(f"t{i}") for i in range(2)]
        ln = LayerNorm(sh, ctx, tag, ps_t, src=sh.hs, affine=(w["ln2_g"], w["ln2_b"]))
        h = sb("h", [P, 4, S])
        s_h, s_gelu, s_y, s_x, s_bias = (sem("h_summed"), sem("h_ready"), sem("y_summed"), sem("x_updated"),
                                         sem("bias_added"))
        block = ctx.enter_context(nc.Block())

        @block.gpsimd
        def _(pool):
            ln.gpsimd(pool)
            for c in range(B):
                ts = slice(c * TPC, (c + 1) * TPC)
                nc.gpsimd.tensor_tensor(sh.x[:, ts, :], sh.x[:, ts, :],
                                        gen["cm_b"].unsqueeze(1).broadcast_to([P, TPC, D]), ALU.add).then_inc(s_bias, 1)

        @block.tensor
        def _(pe):
            pe.sem_inc(s_y, 1)
            ln.tensor(pe)
            pe.wait_ge(ln.ready, B)
            with pe.Fori(0, B) as c:
                for f in range(n):
                    pe.wait_ge(s_gelu, 1 + c * n + f)
                    nc.tensor.matmul(ps_h[f][:, :], gen["cf_w"][:, f * P:(f + 1) * P], sh.xnT[:, cols(c)],
                                     start=True, stop=True).then_inc(s_h, 1)
                pe.wait_ge(s_x, 1 + c)
                for k in range(n):
                    pe.wait_ge(s_gelu, 4 + c * n + k + 1)
                    for i in range(TPC):
                        last = nc.tensor.matmul(ps_y[0][:, i, :], h[:, k, i * P:(i + 1) * P],
                                                gen["cm_w"][:, k * D:(k + 1) * D], start=(k == 0 and i == 0),
                                                stop=(k == n - 1), skip_group_check=True)
                last.then_inc(s_y, 1)

        @block.scalar
        def _(act):
            act.sem_inc(s_gelu, 4)
            ln.scalar(act)
            with act.Fori(0, B) as c:
                for f in range(n):
                    act.wait_ge(s_h, c * n + f + 1)
                    if f == 0:
                        act.wait_ge(s_y, 1 + c)
                    nc.scalar.activation(h[:, f, :], ps_h[f][:, :], ACT.Gelu_apprx_tanh,
                                         bias=gen["cf_b"][:, f:f + 1]).then_inc(s_gelu, 1)

        @block.vector
        def _(dve):
            dve.sem_inc(s_x, 1)
            ln.vector(dve)
            dve.wait_ge(s_bias, B)
            with dve.Fori(0, B) as c:
                dve.wait_ge(s_y, 1 + c + 1)
                nc.vector.tensor_tensor(sh.x[:, tiles(c), :], sh.x[:, tiles(c), :], ps_y[0][:, :, :],
                                        ALU.add).then_inc(s_x, 1)


def generated_block(sh, stage):
    nc = sh.nc
    with ExitStack() as ctx:
        sh.hs = ctx.enter_context(nc.sbuf_tensor("hs", [P, NT, D], F32))
        generated_attention(sh, stage)
        generated_mlp(sh, stage)


def full_plan(g, groups):
    nxt, cur = g + 1 < groups, g >= 0
    plan = []
    if not cur:
        plan += [("v", u) for u in range(2 * TPC)]
    for x in range(4):
        late = [("exp", x, j) for j in range(4)] if cur else []
        todo = []
        if nxt:
            todo = [[("q", 0), ("k", 0)], [("q", 1), ("k", 1)] + [("max", 0, i) for i in range(4)],
                    [("q", 2), ("k", 2)] + [("max", 1, i) for i in range(4)] + [("q", 3), ("k", 3)],
                    [("max", y, i) for y in (2, 3) for i in range(4)] + [("maxT",)]][x]
        if x == 1 and g >= 1:
            todo = [("sum", 2 * g - 1)] + todo
        if x == 2 and cur:
            todo = todo + [("pv", 2 * g)]
        n = max(len(late), len(todo))
        per = -(-len(todo) // 4) if todo else 0
        for k in range(4):
            plan += late[k:k + 1] + todo[k * per:(k + 1) * per]
    if cur:
        plan += [("sum", 2 * g), ("pv", 2 * g + 1)]
    if g == groups - 1:
        plan += [("sum", 2 * g + 1), ("out",)]
    return plan


def full_attention(sh, stage, heads=16, dh=64):
    nc, w, tag = sh.nc, sh.w(stage), f"s{stage}"
    G = heads // 4
    PAIRS, NV = heads // 2, 2 * TPC
    F32R = mybir.dt.float32r
    with ExitStack() as ctx:
        sb = lambda m, shape, dt=F32: ctx.enter_context(nc.sbuf_tensor(f"{tag}_{m}", shape, dt))
        sem = lambda m: sh.sem(f"{tag}_{m}")
        bank = lambda m: ctx.enter_context(nc.psum_tensor(f"{tag}_{m}", [P, S], F32))
        pj = [bank(f"odd_jobs{i}") for i in range(2)]
        p1 = [bank(f"for_max{i}") for i in range(2)]
        p2 = [bank(f"scores{i}") for i in range(2)]
        po, psm = bank("pv"), bank("sums")
        ln = LayerNorm(sh, ctx, tag, p1)
        qq = sb("q_hi_hi", [P, 2, 4, S], F32R)
        q2 = sb("q_lo_max", [dh + 2, 2, 4, S], F32R)
        kk = sb("k_hi_lo", [P, 2, 4, S], F32R)
        k2 = sb("k_hi_one", [P, 2, 4, S], F32R)
        ones = sb("ones", [P, dh])
        v = sb("v", [P, TPC, heads * dh])
        xc = sb("xnT_of_sequence", [P, S])
        negmax = sb("negmax", [P, 4, TPC])
        mparts = sb("max_parts", [P, TPC, 2, 4], F32R)
        mT = sb("maxT", [8, S], F32R)
        probs = sb("probs", [P, 2, 2, TPC, S])
        added = sb("probs_added", [P, 2, 2, S])
        acc = sb("probs_sum", [P, 2, 2, S])
        bo = sb("bo", [P, D])
        recip = sb("recip", [P, S])
        oT = sh.spare(ctx, f"{tag}_oT", stage, heads // 2 * S).rearrange("p (k n) -> p k n", n=S)
        s_one = sem("ones_made")
        s_proj, s_hi, s_lo, s_k2 = sem("qk_projected"), sem("hi_done"), sem("lo_done"), sem("k2_done")
        s_v, s_vs = sem("v_projected"), sem("v_in_sbuf")
        s_free = [sem(f"odd_bank_free{i}") for i in range(2)]
        s_max, s_neg, s_msplit = sem("scores_for_max"), sem("max_done"), sem("max_split_steps")
        s_maxT, s_mT, s_mw, s_mrow = sem("max_transposed"), sem("maxT_in_sbuf"), sem("maxT_stored"), sem("max_rows_loaded")
        s_sc, s_exp, s_pv = sem("scores_less_max"), sem("probs_ready"), sem("pv_done")
        s_added, s_acc, s_sum = sem("probs_added_up"), sem("probs_sum_ready"), sem("sums_ready")
        s_rec, s_norm, s_y, s_x = sem("recip_done"), sem("o_normalised"), sem("y_summed"), sem("x_updated")
        s_bias = sem("o_bias_added")
        scratch = nc.dram_tensor("scratch_max3", [G, 2, 4, S], F32, kind="Internal").ap()
        s_xc, s_bvo, s_bo = sem("xc_copied"), sem("bv_projected"), sem("bo_ready")
        plans = [(g, full_plan(g, G)) for g in range(-1, G)]
        fills = {}
        for g, plan in plans:
            for item in plan:
                if item[0] in ("q", "k"):
                    fills[item[0], 4 * (g + 1) + item[1]] = len(fills)
                elif item[0] == "v":
                    fills[item] = len(fills)
                elif item[0] == "maxT":
                    fills["maxT", g + 1] = len(fills)
        FILLS = len(fills) // 2
        assert len(fills) % 2 == 0
        block = ctx.enter_context(nc.Block())

        def freed(eng, key):
            eng.sem_inc(s_free[fills[key] % 2], 1)

        @block.sync
        def _(sp):
            sh.load_next(sp, stage)
            for c in range(B):
                sp.wait_ge(s_x, 1 + c)
                for g in range(G):
                    sp.wait_ge(s_mT, c * G + g + 1)
                    sp.dma_start(scratch[g].rearrange("k x n -> (k x) n"), mT[:, :].bitcast(F32)).then_inc(s_mw, 16)
                    sp.wait_ge(s_mw, (c * G + g + 1) * 16)
                    if g >= 2:
                        sp.wait_ge(s_sc, c * (4 * heads) + 16 * (g - 1))
                    sp.dma_start(q2[dh:dh + 2, g % 2, :, :].bitcast(F32), scratch[g]).then_inc(s_mrow, 16)

        @block.gpsimd
        def _(pool):
            nc.gpsimd.memset(ones[:, :], 1.0).then_inc(s_one, 1)
            pool.wait_ge(s_one, 1)
            nc.gpsimd.memset(k2[dh:P, :, :, :].bitcast(F32), 1.0).then_inc(s_one, 1)
            pool.wait_ge(s_one, 2)
            pool.wait_ge(sh.wsem[stage], 16)
            ln.gpsimd(pool)
            pool.wait_ge(ln.s_xn, NT)
            pool.wait_ge(s_bo, 1)
            for c in range(B):
                ts = slice(c * TPC, (c + 1) * TPC)
                nc.gpsimd.tensor_tensor(sh.x[:, ts, :], sh.x[:, ts, :],
                                        bo[:, :].unsqueeze(1).broadcast_to([P, TPC, D]), ALU.add).then_inc(s_bias, 1)
            with pool.Fori(0, B) as c:
                pool.wait_ge(s_x, 1 + c)
                for g, plan in plans:
                    for item in plan:
                        if item[0] == "exp" and item[1] % 2 and item[2] == 3:
                            p = 2 * g + item[1] // 2
                            if p:
                                pool.wait_ge(s_acc, c * PAIRS + p)
                            pool.wait_ge(s_exp, c * (4 * heads) + 8 * (p + 1))
                            nc.gpsimd.tensor_tensor(added[:, :, :, :], probs[:, p % 2, :, 0:2, :],
                                                    probs[:, p % 2, :, 2:4, :], ALU.add).then_inc(s_added, 1)
                            pool.wait_ge(s_added, c * PAIRS + p + 1)
                            if p >= 2:
                                pool.wait_ge(s_sum, c * PAIRS + p - 1)
                            nc.gpsimd.tensor_tensor(acc[:, p % 2, :, :], added[:, :, 0, :], added[:, :, 1, :],
                                                    ALU.add).then_inc(s_acc, 1)

        @block.tensor
        def _(pe):
            pe.sem_inc(s_free[0], 1)
            pe.sem_inc(s_free[1], 1)
            pe.wait_ge(sh.wsem[stage], 16)
            ln.tensor(pe)
            pe.wait_ge(ln.ready, B)
            pe.wait_ge(s_one, 2)
            for k in range(PAIRS):
                last = nc.tensor.matmul(psm[:, 0:D], w["bv"][:, k:k + 1].broadcast_to([P, P]),
                                        w["wo"][:, k * D:(k + 1) * D], start=(k == 0), stop=(k == PAIRS - 1))
            last.then_inc(s_bvo, 1)
            pe.wait_ge(s_bo, 1)
            with pe.Fori(0, B) as c:
                pe.wait_ge(s_x, 1 + c)

                def odd_bank(key):
                    k = fills[key]
                    pe.wait_ge(s_free[k % 2], c * FILLS + k // 2 + 1)
                    return pj[k % 2]

                for g, plan in plans:
                    for item in plan:
                        what = item[0]
                        if what in ("q", "k"):
                            h = 4 * (g + 1) + item[1]
                            ps = odd_bank((what, h))
                            for rows in (slice(0, dh), slice(dh, P)):
                                last = nc.tensor.matmul(ps[rows, :], w["w" + what][:, h * dh:(h + 1) * dh],
                                                        xc[:, :], start=True, stop=True)
                            last.then_inc(s_proj, 1)
                        elif what == "v":
                            i, half = divmod(item[1], 2)
                            ps = odd_bank(item)
                            pe.wait_ge(s_xc, c + 1)
                            nc.tensor.matmul(ps[:, :], xc[:, i * P:(i + 1) * P], w["wv"][:, half * S:(half + 1) * S],
                                             start=True, stop=True).then_inc(s_v, 1)
                        elif what == "max":
                            _, x, i = item
                            n, b = 4 * (g + 1) + x, (g + 1) % 2
                            m = 4 * n + i
                            if i == 0:
                                pe.wait_ge(s_hi, c * (2 * heads) + 2 * (n + 1))
                            if m >= 2:
                                pe.wait_ge(s_neg, c * (4 * heads) + m - 1)
                            nc.tensor.matmul(p1[m % 2][:, :], qq[0:dh, b, x, i * P:(i + 1) * P], kk[0:dh, b, x, :],
                                             start=True, stop=True).then_inc(s_max, 1)
                        elif what == "maxT":
                            ps = odd_bank(("maxT", g + 1))
                            pe.wait_ge(s_msplit, c * (2 * G) + 2 * (g + 2))
                            for i in range(TPC):
                                last = nc.tensor.transpose(ps[0:8, i * P:(i + 1) * P],
                                                           mparts[:, i, :, :].rearrange("p k x -> p (k x)").bitcast(F32),
                                                           sh.ident[:, :])
                            last.then_inc(s_maxT, 1)
                        elif what == "exp":
                            _, x, j = item
                            n, b = 4 * g + x, g % 2
                            m = 4 * n + j
                            if j == 0:
                                pe.wait_ge(s_lo, c * (2 * heads) + 2 * (n + 1))
                                pe.wait_ge(s_k2, c * heads + n + 1)
                                pe.wait_ge(s_mrow, (c * G + g + 1) * 16)
                            if m >= 2:
                                pe.wait_ge(s_exp, c * (4 * heads) + m - 1)
                            nc.tensor.matmul(p2[m % 2][:, :], kk[:, b, x, j * P:(j + 1) * P], qq[:, b, x, :],
                                             start=True, stop=False)
                            nc.tensor.matmul(p2[m % 2][:, :], k2[0:dh + 2, b, x, j * P:(j + 1) * P], q2[:, b, x, :],
                                             start=False, stop=True).then_inc(s_sc, 1)
                        elif what == "pv":
                            p = item[1]
                            pe.wait_ge(s_exp, c * (4 * heads) + 8 * (p + 1))
                            if p == 0:
                                pe.wait_ge(s_vs, c * NV + NV)
                            else:
                                pe.wait_ge(s_norm, c * PAIRS + p)
                            for j in range(TPC):
                                for x in range(2):
                                    last = nc.tensor.matmul(po[x * dh:(x + 1) * dh, :],
                                                            v[:, j, (2 * p + x) * dh:(2 * p + x + 1) * dh],
                                                            probs[:, p % 2, x, j, :], start=(j == 0), stop=(j == TPC - 1))
                            last.then_inc(s_pv, 1)
                        elif what == "sum":
                            p = item[1]
                            pe.wait_ge(s_acc, c * PAIRS + p + 1)
                            if p:
                                pe.wait_ge(s_norm, c * PAIRS + p)
                            for x in range(2):
                                last = nc.tensor.matmul(psm[x * dh:(x + 1) * dh, :], ones[:, :], acc[:, p % 2, x, :],
                                                        start=True, stop=True)
                            last.then_inc(s_sum, 1)
                        elif what == "out":
                            pe.wait_ge(s_norm, c * PAIRS + PAIRS)
                            for p in range(PAIRS):
                                for i in range(TPC):
                                    last = nc.tensor.matmul(p1[0][:, i * P:(i + 1) * P], oT[:, p, i * P:(i + 1) * P],
                                                            w["wo"][:, p * D:(p + 1) * D], start=(p == 0 and i == 0),
                                                            stop=(p == PAIRS - 1), skip_group_check=True)
                            last.then_inc(s_y, 1)

        @block.scalar
        def _(act):
            act.wait_ge(sh.wsem[stage], 16)
            ln.scalar(act)
            act.wait_ge(ln.ready, B)
            with act.Fori(0, B) as c:
                act.wait_ge(s_x, 1 + c)
                nc.scalar.copy(xc[:, :], sh.xnT[:, cols(c)]).then_inc(s_xc, 1)
                for g, plan in plans:
                    for item in plan:
                        what = item[0]
                        if what in ("q", "k"):
                            b, x = (g + 1) % 2, item[1]
                            h = 4 * (g + 1) + x
                            act.wait_ge(s_proj, c * (2 * heads) + 2 * h + (what == "k") + 1)
                            if h >= 8:
                                act.wait_ge(s_sc, c * (4 * heads) + 4 * (h - 7))
                                if what == "k":
                                    act.wait_ge(s_k2, c * heads + h - 7)
                            nc.scalar.activation((qq if what == "q" else kk)[:, b, x, :], pj[fills[what, h] % 2][:, :],
                                                 ACT.Identity, bias=w["b" + what][:, h:h + 1]).then_inc(s_hi, 1)
                        elif what == "maxT":
                            act.wait_ge(s_maxT, c * G + g + 2)
                            if g >= 0:
                                act.wait_ge(s_mw, (c * G + g + 1) * 16)
                            nc.scalar.copy(mT[:, :], pj[fills["maxT", g + 1] % 2][0:8, :]).then_inc(s_mT, 1)
                            act.wait_ge(s_mT, c * G + g + 2)
                            freed(act, ("maxT", g + 1))
                        elif what == "exp":
                            _, x, j = item
                            m, p = 4 * (4 * g + x) + j, 2 * g + x // 2
                            act.wait_ge(s_sc, c * (4 * heads) + m + 1)
                            if x % 2 == 0 and j == 0 and p >= 2:
                                act.wait_ge(s_pv, c * PAIRS + p - 1)
                                act.wait_ge(s_added, c * PAIRS + p - 1)
                            nc.scalar.activation(probs[:, p % 2, x % 2, j, :], p2[m % 2][:, :], ACT.Exp,
                                                 scale=dh ** -0.5).then_inc(s_exp, 1)

        @block.vector
        def _(dve):
            dve.sem_inc(s_x, 1)
            dve.wait_ge(sh.wsem[stage], 16)
            ln.vector(dve)
            dve.wait_ge(s_bvo, 1)
            nc.vector.tensor_tensor(bo[:, :], psm[:, 0:D], w["bo"], ALU.add).then_inc(s_bo, 1)
            dve.wait_ge(s_bias, B)
            with dve.Fori(0, B) as c:
                for g, plan in plans:
                    for item in plan:
                        what = item[0]
                        if what in ("q", "k"):
                            b, x = (g + 1) % 2, item[1]
                            h = 4 * (g + 1) + x
                            m = 2 * h + (what == "k")
                            ps = pj[fills[what, h] % 2]
                            dve.wait_ge(s_hi, c * (2 * heads) + m + 1)
                            if what == "q":
                                rows, hi = slice(0, dh), qq[0:dh, b, x, :].bitcast(F32)
                                out = q2[0:dh, b, x, :]
                                if h >= 8:
                                    dve.wait_ge(s_sc, c * (4 * heads) + 4 * (h - 7))
                            else:
                                rows, hi = slice(dh, P), kk[dh:P, b, x, :].bitcast(F32)
                                out = kk[dh:P, b, x, :]
                            nc.vector.scalar_tensor_tensor(out=out, in0=ps[rows, :], scalar=w["b" + what][rows, h:h + 1],
                                                           in1=hi, op0=ALU.add, op1=ALU.subtract).then_inc(s_lo, 1)
                            dve.wait_ge(s_lo, c * (2 * heads) + m + 1)
                            freed(dve, (what, h))
                            if what == "k":
                                if h >= 8:
                                    dve.wait_ge(s_sc, c * (4 * heads) + 4 * (h - 7))
                                nc.vector.tensor_copy(k2[0:dh, b, x, :], kk[0:dh, b, x, :]).then_inc(s_k2, 1)
                        elif what == "v":
                            u = item[1]
                            i, half = divmod(u, 2)
                            dve.wait_ge(s_v, c * NV + u + 1)
                            nc.vector.tensor_copy(v[:, i, half * S:(half + 1) * S],
                                                  pj[fills[item] % 2][:, :]).then_inc(s_vs, 1)
                            dve.wait_ge(s_vs, c * NV + u + 1)
                            freed(dve, item)
                        elif what == "max":
                            _, x, i = item
                            m = 4 * (4 * (g + 1) + x) + i
                            dve.wait_ge(s_max, c * (4 * heads) + m + 1)
                            nc.vector.tensor_reduce(negmax[:, x, i:i + 1], p1[m % 2][:, :], AX.X, ALU.max,
                                                    negate=True).then_inc(s_neg, 1)
                        elif what == "maxT":
                            dve.wait_ge(s_neg, c * (4 * heads) + 16 * (g + 2))
                            if g >= 0:
                                dve.wait_ge(s_maxT, c * G + g + 1)
                            st = Steps(dve, s_msplit, c * (2 * G) + 2 * (g + 1), 2)
                            by_tile = negmax[:, :, :].rearrange("p x i -> p i x")
                            st.then(nc.vector.tensor_copy(mparts[:, :, 0, :], by_tile))
                            st.did(nc.vector.tensor_tensor(mparts[:, :, 1, :], by_tile, mparts[:, :, 0, :].bitcast(F32),
                                                           ALU.subtract))
                            st.end()
                        elif what == "sum":
                            p = item[1]
                            dve.wait_ge(s_sum, c * PAIRS + p + 1)
                            nc.vector.reciprocal(recip[:, :], psm[:, :]).then_inc(s_rec, 1)
                            dve.wait_ge(s_pv, c * PAIRS + p + 1)
                            dve.wait_ge(s_rec, c * PAIRS + p + 1)
                            nc.vector.tensor_tensor(oT[:, p, :], po[:, :], recip[:, :], ALU.mult).then_inc(s_norm, 1)
                        elif what == "out":
                            dve.wait_ge(s_y, c + 1)
                            nc.vector.tensor_tensor(sh.x[:, tiles(c), :], sh.x[:, tiles(c), :],
                                                    p1[0][:, :].rearrange("p (t d) -> p t d", t=TPC),
                                                    ALU.add).then_inc(s_x, 1)


def dispatched_ffn(sh, stage, n_exp=8, hid=512, top=2):
    nc, w, tag = sh.nc, sh.w(stage), f"s{stage}"
    cap = top * (-(-T // n_exp))
    slots = n_exp * cap
    U = top * NT
    n_up, n_slot = hid // P, cap // P
    assert cap == S
    GROUP = 4
    with ExitStack() as ctx:
        sb = lambda m, shape, dt=F32: ctx.enter_context(nc.sbuf_tensor(f"{tag}_{m}", shape, dt))
        sem = lambda m: sh.sem(f"{tag}_{m}")
        bank = lambda m: ctx.enter_context(nc.psum_tensor(f"{tag}_{m}", [P, S], F32))
        ps_t = [bank(f"turned{i}") for i in range(2)]
        ps_up = [bank(f"up{i}") for i in range(2)]
        ps_y = [bank(f"y{i}") for i in range(2)]
        ps_route, ps_count = bank("route"), bank("count")
        disp = nc.dram_tensor("dispatched", [slots + top * T, D], F32, kind="Internal").ap()
        outs = nc.dram_tensor("expert_rows", [slots, D], F32, kind="Internal").ap()
        xn = sb("xn", [P, NT, D])
        ln = LayerNorm(sh, ctx, tag, ps_t, keep=xn)
        zeros = sb("zeros", [P, 2 * S])
        tri = sb("tri", [P, P], BF16)
        ones = sb("ones", [P, P], BF16)
        before = sb("before", [P, n_exp, n_exp])
        base = sb("slot_base", [P, n_exp])
        spare_i = sb("spare_int", [P, U], mybir.dt.int32)
        spare = sb("spare", [P, U])
        probs = sb("probs", [P, NT, n_exp])
        stat = sb("stat", [P, NT])
        rank = sb("rank", [P, NT, n_exp])
        gt = sb("gt", [P, NT, n_exp, n_exp])
        eq = sb("eq", [P, NT, n_exp, n_exp])
        chosen = sb("chosen", [P, U, n_exp], BF16)
        picked = sb("picked", [P, U, n_exp])
        gate = sb("gate", [P, U])
        total = sb("gate_sum", [P, NT])
        upto = sb("counts_up_to", [P, 2, NT + U, n_exp])
        loc = sb("loc", [P, U])
        first = sb("first_slot", [P, U])
        valid = sb("valid", [P, U])
        where = sb("where", [P, 2, U])
        idx = sb("idx", [P, 2, U], U32)
        rows = sb("rows", [P, 2, n_slot, D])
        rowsT = sb("rowsT", [P, 2, S])
        hidden = sb("hidden", [P, 2, n_up, S])
        y = sb("y", [P, 2, n_slot, D])
        back = sb("back", [P, U, D])
        w1, w2 = sb("w1", [P, n_exp * hid]), sb("w2", [P, n_exp * hid])
        b2 = sb("b2", [P, n_exp * D])
        s_w1, s_w2 = sem("w1_loaded"), sem("w2_b2_loaded")
        s_const, s_zero, s_zeroed = sem("constants_made"), sem("zeros_made"), sem("slots_cleared")
        s_before, s_base = sem("before_made"), sem("base_made")
        s_logits, s_less, s_exp, s_chosen, s_count = (sem("logits_ready"), sem("logits_less_max"), sem("exp_done"),
                                                      sem("choices_ready"), sem("counts_ready"))
        s_route, s_idx = sem("route_steps"), sem("idx_ready")
        s_put, s_rows, s_turn, s_rowsT = sem("rows_put"), [sem(f"rows_loaded{i}") for i in range(2)], sem("rows_transposed"), sem("rowsT_ready")
        s_up, s_hidden, s_down, s_y = sem("up_done"), sem("hidden_ready"), sem("down_done"), sem("y_ready")
        s_out, s_x = [sem(f"y_stored{i}") for i in range(2)], sem("x_steps")
        s_back = [sem(f"rows_back{i}") for i in range(U // GROUP)]
        block = ctx.enter_context(nc.Block())

        @block.sync
        def _(sp):
            sh.load_next(sp, stage)
            n = n_exp * hid
            sp.dma_start(w1[:, :], sh.extra[stage][:, 0:n]).then_inc(s_w1, 16)
            sp.dma_start(w2[:, :], sh.extra[stage][:, n:2 * n]).then_inc(s_w2, 16)
            sp.dma_start(b2[:, :], sh.extra[stage][:, 2 * n:]).then_inc(s_w2, 16)
            sp.wait_ge(s_zero, 1)
            n = slots * D // (P * 2 * S)
            for k in range(n):
                sp.dma_start(disp[k * slots // n:(k + 1) * slots // n].rearrange("(p r) d -> p (r d)", p=P),
                             zeros[:, :]).then_inc(s_zeroed, 16)
            sp.wait_ge(s_put, 16 * U)
            for e in range(n_exp + 2):
                if e < n_exp:
                    if e >= 2:
                        sp.wait_ge(s_turn, e - 1)
                    sp.dma_start(rows[:, e % 2, :, :], disp[e * cap:(e + 1) * cap].rearrange(
                        "(t p) d -> p t d", p=P)).then_inc(s_rows[e % 2], 16)
                if e >= 2:
                    sp.wait_ge(s_y, e - 1)
                    sp.dma_start(outs[(e - 2) * cap:(e - 1) * cap].rearrange("(t p) d -> p t d", p=P),
                                 y[:, e % 2, :, :]).then_inc(s_out[e % 2], 16)

        @block.gpsimd
        def _(pool):
            nc.gpsimd.memset(zeros[:, :], 0.0).then_inc(s_zero, 1)
            make_before(nc, pool, before, n_exp, s_before)
            nc.gpsimd.memset(ones[:, :], 1.0).then_inc(s_const, 1)
            nc.gpsimd.memset(tri[:, :], 1.0).then_inc(s_const, 1)
            nc.gpsimd.memset(upto[:, :, :, :], 0.0).then_inc(s_const, 1)
            nc.gpsimd.iota(spare_i[:, :], pattern=[[P, U]], base=slots, channel_multiplier=1).then_inc(s_const, 1)
            pool.wait_ge(s_const, 4)
            nc.gpsimd.affine_select(out=tri[:, :], in_=tri[:, :], compare_op=ALU.is_gt, fill=0.0, base=0,
                                    pattern=[[1, P]], channel_multiplier=-1).then_inc(s_const, 1)
            ln.gpsimd(pool)
            pool.wait_ge(s_idx, 1)
            pool.wait_ge(s_zeroed, 16 * (slots * D // (P * 2 * S)))
            for u in range(U):
                nc.gpsimd.indirect_dma_start(disp, bass.IndirectOffsetOnAxis(ap=idx[:, 0, u:u + 1], axis=0),
                                             xn[:, u % NT, :], None).then_inc(s_put, 16)
            for half in s_out:
                pool.wait_ge(half, 16 * n_exp // 2)
            for u in range(U):
                nc.gpsimd.indirect_dma_start(back[:, u, :], None, outs,
                                             bass.IndirectOffsetOnAxis(ap=idx[:, 1, u:u + 1], axis=0)).then_inc(s_back[u // GROUP], 16)

        @block.tensor
        def _(pe):
            pe.wait_ge(sh.wsem[stage], 16)
            ln.tensor(pe)
            pe.wait_ge(ln.ready, B)
            logits = ps_route[:, 0:NT * n_exp].rearrange("p (t e) -> p t e", t=NT)
            for t in range(NT):
                last = nc.tensor.matmul(logits[:, t, :], sh.xnT[:, t * P:(t + 1) * P], w["wg"],
                                        start=True, stop=True)
            last.then_inc(s_logits, 1)
            pe.wait_ge(s_const, 5)
            pe.wait_ge(s_chosen, 1)
            flat = chosen[:, :, :].rearrange("p u e -> p (u e)")
            nc.tensor.matmul(ps_count[:, 0:U * n_exp], tri[:, :], flat, start=True, stop=True)
            nc.tensor.matmul(ps_count[:, U * n_exp:], ones[:, :], flat, start=True, stop=True).then_inc(s_count, 1)

            def turn(e):
                pe.wait_ge(s_rows[e % 2], 16 * (e // 2 + 1))
                if e >= 2:
                    pe.wait_ge(s_rowsT, e - 1)
                for i in range(n_slot):
                    last = nc.tensor.transpose(ps_t[e % 2][:, i * P:(i + 1) * P], rows[:, e % 2, i, :], sh.ident[:, :])
                last.then_inc(s_turn, 1)

            def up(e):
                pe.wait_ge(s_rowsT, e + 1)
                for f in range(n_up):
                    m = e * n_up + f
                    if m >= 2:
                        pe.wait_ge(s_hidden, m - 1)
                    nc.tensor.matmul(ps_up[m % 2][:, :], w1[:, m * P:(m + 1) * P], rowsT[:, e % 2, :],
                                     start=True, stop=True).then_inc(s_up, 1)

            def down(e):
                pe.wait_ge(s_hidden, (e + 1) * n_up)
                if e >= 2:
                    pe.wait_ge(s_y, e - 1)
                for i in range(n_slot):
                    for f in range(n_up):
                        m = e * n_up + f
                        last = nc.tensor.matmul(ps_y[e % 2][:, i * P:(i + 1) * P], hidden[:, e % 2, f, i * P:(i + 1) * P],
                                                w2[:, m * D:(m + 1) * D], start=(f == 0 and i == 0),
                                                stop=(f == n_up - 1), skip_group_check=True)
                last.then_inc(s_down, 1)

            turn(0)
            pe.wait_ge(s_w1, 16)
            pe.wait_ge(s_w2, 32)
            for e in range(n_exp):
                up(e)
                if e + 1 < n_exp:
                    turn(e + 1)
                if e >= 1:
                    down(e - 1)
            down(n_exp - 1)

        @block.scalar
        def _(act):
            act.wait_ge(sh.wsem[stage], 16)
            ln.scalar(act)
            act.wait_ge(s_less, 1)
            nc.scalar.activation(probs[:, :, :], probs[:, :, :], ACT.Exp).then_inc(s_exp, 1)
            for e in range(n_exp):
                act.wait_ge(s_turn, e + 1)
                if e >= 2:
                    act.wait_ge(s_up, (e - 1) * n_up)
                nc.scalar.copy(rowsT[:, e % 2, :], ps_t[e % 2][:, :]).then_inc(s_rowsT, 1)
                for f in range(n_up):
                    m = e * n_up + f
                    act.wait_ge(s_up, m + 1)
                    if e >= 2 and f == 0:
                        act.wait_ge(s_down, e - 1)
                    nc.scalar.activation(hidden[:, e % 2, f, :], ps_up[m % 2][:, :], ACT.Relu,
                                         bias=w["b1"][:, m:m + 1]).then_inc(s_hidden, 1)

        @block.vector
        def _(dve):
            for e in range(n_exp):
                last = nc.vector.memset(base[:, e:e + 1], float(e * cap))
            last.then_inc(s_base, 1)
            ln.vector(dve)
            st = Steps(dve, s_route, 0, ROUTE_DISPATCH_STEPS)
            logits = ps_route[:, 0:NT * n_exp].rearrange("p (t e) -> p t e", t=NT)
            wide = lambda a: a.unsqueeze(2).broadcast_to([P, a.shape[1], n_exp])
            per_e = lambda a: a.unsqueeze(1).broadcast_to([P, U, n_exp])
            twice = lambda a: a.unsqueeze(1).broadcast_to([P, top] + a.shape[1:])
            by_choice = lambda a: a.rearrange("p (k t) e -> p k t e", k=top)
            dve.wait_ge(s_logits, 1)
            st.then(nc.vector.tensor_reduce(stat[:, :], logits, AX.X, ALU.max))
            nc.vector.tensor_tensor(probs[:, :, :], logits, wide(stat[:, :]), ALU.subtract).then_inc(s_less, 1)
            dve.wait_ge(s_exp, 1)
            st.then(nc.vector.tensor_reduce(stat[:, :], probs[:, :, :], AX.X, ALU.add))
            st.then(nc.vector.reciprocal(stat[:, :], stat[:, :]))
            st.then(nc.vector.tensor_tensor(probs[:, :, :], probs[:, :, :], wide(stat[:, :]), ALU.mult))
            dve.wait_ge(s_before, 2)
            dve.wait_ge(s_base, 1)
            ranks(nc, st, rank[:, :, :], probs[:, :, :], before[:, :, :], gt[:, :, :, :], eq[:, :, :, :])
            for k in range(top):
                last = nc.vector.tensor_scalar(chosen[:, k * NT:(k + 1) * NT, :], rank[:, :, :], float(k), None,
                                               ALU.is_equal)
                st.did(last)
            st.wait()
            dve.sem_inc(s_chosen, 1)
            for k in range(top):
                st.did(nc.vector.tensor_tensor(picked[:, k * NT:(k + 1) * NT, :], chosen[:, k * NT:(k + 1) * NT, :],
                                               probs[:, :, :], ALU.mult))
            st.wait()
            st.then(nc.vector.tensor_reduce(gate[:, :], picked[:, :, :], AX.X, ALU.add))
            st.then(nc.vector.tensor_tensor(total[:, :], gate[:, 0:NT], gate[:, NT:], ALU.add))
            st.then(nc.vector.reciprocal(total[:, :], total[:, :]))
            for k in range(top):
                st.did(nc.vector.tensor_tensor(gate[:, k * NT:(k + 1) * NT], gate[:, k * NT:(k + 1) * NT], total[:, :],
                                               ALU.mult))
            dve.wait_ge(s_count, 1)
            dve.wait_ge(s_const, 3)
            counts = ps_count[:, U * n_exp:].rearrange("p (u e) -> p u e", u=U)
            within = ps_count[:, 0:U * n_exp].rearrange("p (u e) -> p u e", u=U)
            st.then(nc.vector.tensor_copy(upto[:, 0, NT:, :], counts))
            shift, k = 1, 0
            while shift < U:
                st.then(nc.vector.tensor_tensor(upto[:, 1 - k, NT:, :], upto[:, k, NT:, :],
                                                upto[:, k, NT - shift:NT + U - shift, :], ALU.add))
                shift, k = 2 * shift, 1 - k
            st.then(nc.vector.tensor_tensor(picked[:, :, :], within, upto[:, k, NT - 1:NT + U - 1, :], ALU.add))
            st.then(nc.vector.tensor_tensor(picked[:, :, :], picked[:, :, :], chosen[:, :, :], ALU.mult))
            st.then(nc.vector.tensor_reduce(loc[:, :], picked[:, :, :], AX.X, ALU.add))
            st.then(nc.vector.tensor_tensor(picked[:, :, :], chosen[:, :, :], per_e(base[:, :]), ALU.mult))
            st.then(nc.vector.tensor_reduce(first[:, :], picked[:, :, :], AX.X, ALU.add))
            st.did(nc.vector.tensor_scalar(valid[:, :], loc[:, :], cap - 0.5, None, ALU.is_lt))
            st.did(nc.vector.tensor_copy(spare[:, :], spare_i[:, :]))
            st.then(nc.vector.scalar_tensor_tensor(out=where[:, 1, :], in0=loc[:, :], scalar=cap - 1.0, in1=first[:, :],
                                                   op0=ALU.min, op1=ALU.add))
            st.did(nc.vector.tensor_tensor(gate[:, :], gate[:, :], valid[:, :], ALU.mult))
            st.then(nc.vector.tensor_tensor(where[:, 0, :], where[:, 1, :], spare[:, :], ALU.subtract))
            st.then(nc.vector.tensor_tensor(where[:, 0, :], where[:, 0, :], valid[:, :], ALU.mult))
            st.then(nc.vector.tensor_tensor(where[:, 0, :], where[:, 0, :], spare[:, :], ALU.add))
            st.end()
            nc.vector.tensor_copy(idx[:, :, :], where[:, :, :]).then_inc(s_idx, 1)
            dve.wait_ge(s_w2, 32)
            for e in range(n_exp):
                dve.wait_ge(s_down, e + 1)
                if e >= 2:
                    dve.wait_ge(s_out[e % 2], 16 * (e // 2))
                nc.vector.tensor_tensor(y[:, e % 2, :, :], ps_y[e % 2][:, :].rearrange("p (t d) -> p t d", t=n_slot),
                                        b2[:, e * D:(e + 1) * D].unsqueeze(1).broadcast_to([P, n_slot, D]),
                                        ALU.add).then_inc(s_y, 1)
            for u in range(U):
                if u % GROUP == 0:
                    dve.wait_ge(s_back[u // GROUP], 16 * GROUP)
                if u >= NT:
                    dve.wait_ge(s_x, u - NT + 1)
                nc.vector.scalar_tensor_tensor(out=sh.x[:, u % NT, :], in0=back[:, u, :], scalar=gate[:, u:u + 1],
                                               in1=sh.x[:, u % NT, :], op0=ALU.mult, op1=ALU.add).then_inc(s_x, 1)


ROUTE_DISPATCH_STEPS = 36


def program(nc, x_in, weights, extra, out):
    with ExitStack() as ctx:
        sh = Shared(nc, ctx, weights, extra)
        sem = lambda n: ctx.enter_context(nc.semaphore(n))
        s_x, s_zero, s_id, s_half, s_out = (sem("x_loaded"), sem("ident_cleared"), sem("ident_made"),
                                            sem("mhalf_made"), sem("x_stored"))
        with nc.Block() as block:
            @block.sync
            def _(sp):
                for c in range(B):
                    sp.dma_start(sh.x[:, c * TPC:(c + 1) * TPC, :],
                                 x_in[c].rearrange("(t p) d -> p t d", p=P)).then_inc(s_x, 16)
                sh.load_weights(sp, list(weights)[0])
                sp.wait_ge(s_x, 16 * B)

            @block.gpsimd
            def _(pool):
                nc.gpsimd.memset(sh.mhalf[:, :], -0.5).then_inc(s_half, 1)
                for n, m in enumerate((sh.ident, sh.identb)):
                    nc.gpsimd.memset(m[:, :], 0.0).then_inc(s_zero, 1)
                    pool.wait_ge(s_zero, n + 1)
                    nc.gpsimd.affine_select(out=m[:, :], in_=m[:, :], compare_op=ALU.not_equal, fill=1.0,
                                            base=0, pattern=[[-1, P]], channel_multiplier=1).then_inc(s_id, 1)
        for stage in weights:
            RUN[stage](sh, stage)
            sh.stage_over()
        with nc.Block() as block:
            @block.sync
            def _(sp):
                for c in range(B):
                    sp.dma_start(out[c].rearrange("(t p) d -> p t d", p=P),
                                 sh.x[:, c * TPC:(c + 1) * TPC, :]).then_inc(s_out, 16)
                sp.wait_ge(s_out, 16 * B)
        sh.old_sems.close()


RUN = {
    0: gated_linear_attention,
    1: lambda sh, s: routed_ffn(sh, s, 16, 64, 128, ACT.Sigmoid, route_groups, ROUTE_GROUPS_STEPS),
    3: lambda sh, s: routed_ffn(sh, s, 8, 256, 256, ACT.Copy, route_top1, ROUTE_TOP1_STEPS),
    2: low_rank_attention,
    4: generated_block,
    5: ternary_ffn,
    6: full_attention,
    7: dispatched_ffn,
}


def _t(a):
    import numpy as np
    return np.moveaxis(a, -1, 0).reshape(a.shape[-1], -1)


def _fold(a):
    k = a.shape[0] // P
    return a.reshape(k, P, -1).transpose(1, 0, 2).reshape(P, -1)


def _col(v):
    return v.reshape(-1, P).T


def _rows(v):
    import numpy as np
    return np.broadcast_to(v.reshape(1, -1), (P, v.size))


def _layout(stage, a):
    import numpy as np
    cat = lambda *parts: np.concatenate(parts, axis=1)
    if stage == 0:
        return [("wq", _t(a["Wq"])), ("wk", _t(a["Wk"])), ("wgk1", _t(a["Wgk1"])), ("wgk2", _t(a["Wgk2"])),
                ("wvg", cat(_t(a["Wv"]), _t(a["Wg"]))), ("wout", _fold(_t(a["Wout"]))),
                ("bgk2", _rows(a["bgk2"])), ("rms_w", _rows(a["rms_w"]))]
    if stage == 1:
        down = cat(_fold(_t(a["w2_s"])), _fold(a["w2_e"].transpose(0, 2, 1).reshape(-1, D)))
        return [("router", _t(a["w_gate"])), ("gate", cat(_t(a["w1_s"]), _t(a["w1_e"]))),
                ("up", cat(_t(a["w3_s"]), _t(a["w3_e"]))), ("down", down)]
    if stage == 2:
        factor = np.concatenate([a["q_a"].transpose(2, 0, 1).reshape(64, -1), a["k_a"].transpose(2, 0, 1).reshape(64, -1)])
        other = np.concatenate([a["q_b"].transpose(1, 0, 2).reshape(64, -1), a["k_b"].transpose(1, 0, 2).reshape(64, -1)])
        return [("a", factor), ("b", other), ("v", _t(a["v_w"])), ("o", _t(a["o_w"])), ("v_b", _rows(a["v_b"])),
                ("o_b", _rows(a["o_b"]))]
    if stage == 3:
        down = cat(_fold(_t(a["w_down_s"])), _fold(a["down"].transpose(0, 2, 1).reshape(-1, D)))
        return [("router", _t(a["router"])), ("gate", cat(_t(a["w_gate_s"]), _t(a["gate"]))),
                ("up", cat(_t(a["w_up_s"]), _t(a["up"]))), ("down", down)]
    if stage == 4:
        def column(p):
            ca_b, cf_b = a["ca_" + p + "_b"], a["cf_" + p + "_b"]
            return cat(_t(a["ca_" + p + "_w"]), _t(a["cp_" + p + "_w"]), _t(a["cf_" + p + "_w"]),
                       _fold(_t(a["cm_" + p + "_w"])), _col(ca_b[:2 * D]), _rows(ca_b[2 * D:]),
                       _rows(a["cp_" + p + "_b"]), _col(cf_b), _rows(a["cm_" + p + "_b"]))
        subs = {}
        for k in range(2):
            for m in ("ca", "cp", "cf", "cm"):
                for p in "wb":
                    subs[f"{m}_{k}_{p}"] = a[f"{m}_sub_{p}"][k]
        a = dict(a, **subs)
        mix = cat(*[_rows(a[f"{m}_Wl_{p}"]) for p in "wb" for m in ("ca", "cp", "cf", "cm")])
        return [("sub0", column("0")), ("a", mix)] + \
            [(f"ln{i}_{p}", _col(a[f"ln{i}_{p}"])) for i in (1, 2) for p in "gb"] + \
            [("extra", cat(column("1"), column("W"), column("B")))]
    if stage == 6:
        double = lambda b: np.tile(b.reshape(16, 64).T, (2, 1))
        return [("wq", _t(a["Wq"])), ("wk", _t(a["Wk"])), ("wv", _t(a["Wv"])),
                ("wo", _fold(_t(a["Wo"]))), ("bq", double(a["bq"])), ("bk", double(a["bk"])),
                ("bv", _col(a["bv"])), ("bo", _rows(a["bo"]))]
    if stage == 7:
        down = a["w2"].reshape(8, 4, P, D).transpose(2, 0, 1, 3).reshape(P, -1)
        return [("wg", a["wg"]), ("b1", a["b1"].reshape(-1, P).T),
                ("extra", cat(a["w1"].transpose(1, 0, 2).reshape(D, -1), down, _rows(a["b2"])))]
    if stage == 5:
        return [("w1", _t(a["w1_w"])), ("w2", _t(a["w2_w"])), ("h1", _fold(_t(a["h1_w"]))),
                ("h2", _fold(_t(a["h2_w"]))), ("w3", _fold(_t(a["w3_w"]))), ("w1_s", _col(a["w1_s"])),
                ("w2_s", _col(a["w2_s"])), ("h1_s", _col(a["h1_s"])), ("h2_s", _col(a["h2_s"])),
                ("w3_s", _rows(a["w3_s"]))]


_NAMES = ["L0_attn", "L0_ffn", "L1_attn", "L1_ffn", "L2_attn", "L2_ffn", "L3_attn", "L3_ffn"]


def kernel(**inputs):
    import numpy as np
    import concourse.bacc as bacc
    from concourse.bass_utils import run_bass_kernel_spmd

    nc = bacc.Bacc("TRN2", target_bir_lowering=False, num_devices=1)
    arrays, weights = {"x_in": np.ascontiguousarray(inputs["L0_attn_x"])}, {}
    x_in = nc.dram_tensor("x_in", [B, S, D], F32, kind="ExternalInput").ap()
    extra = {}
    for stage in STAGES:
        mine = {k[len(_NAMES[stage]) + 1:]: np.asarray(v) for k, v in inputs.items()
                if k.startswith(_NAMES[stage] + "_")}
        parts = _layout(stage, mine)
        if parts[-1][0] == "extra":
            late = np.ascontiguousarray(parts.pop()[1])
            arrays[f"extra{stage}"] = late
            extra[stage] = nc.dram_tensor(f"extra{stage}", list(late.shape), F32, kind="ExternalInput").ap()
        packed = np.zeros((P, sum(v.shape[1] for _, v in parts)), np.float32)
        at, table = 0, []
        for name, v in parts:
            packed[:v.shape[0], at:at + v.shape[1]] = v
            at += v.shape[1]
            table.append((name, v.shape[0], v.shape[1]))
        arrays[f"w{stage}"] = packed
        weights[stage] = (nc.dram_tensor(f"w{stage}", list(packed.shape), F32, kind="ExternalInput").ap(), table)
    out = nc.dram_tensor("out", [B, S, D], F32, kind="ExternalOutput").ap()
    program(nc, x_in, weights, extra, out)
    return run_bass_kernel_spmd(nc, [arrays], core_ids=[0]).results[0]["out"]
```

```python
from contextlib import ExitStack

import concourse.bass as bass
from concourse import mybir

STAGES = (0, 1, 2, 3, 4, 5, 6, 7)

ALU = mybir.AluOpType
ACT = mybir.ActivationFunctionType
AX = mybir.AxisListType
F32 = mybir.dt.float32
BF16 = mybir.dt.bfloat16
U32 = mybir.dt.uint32

P = 128
B, S, D = 4, 512, 128
TPC = S // P
NT = B * TPC
T = B * S
H8, HD8 = 16, 8
LN_EPS = 1e-5
NEG = -1.0e30


def tiles(c, n=TPC):
    return bass.ds(c * n, n)


def cols(c, n=S):
    return bass.ds(c * n, n)


class Steps:

    def __init__(self, eng, sem, base, total):
        self.eng, self.sem, self.base, self.total, self.n = eng, sem, base, total, 0

    def did(self, ins):
        self.n += 1
        ins.then_inc(self.sem, 1)
        return self.n

    def wait(self, n=None):
        self.eng.wait_ge(self.sem, self.base + (self.n if n is None else n))

    def then(self, ins):
        self.did(ins)
        self.wait()

    def end(self):
        assert self.n == self.total, (self.sem, self.n, self.total)


class Shared:

    def __init__(self, nc, ctx, weights, extra):
        self.nc, self.weights, self.extra = nc, weights, extra
        self.x = ctx.enter_context(nc.sbuf_tensor("x_resid", [P, NT, D], F32))
        self.xnT = ctx.enter_context(nc.sbuf_tensor("xnT", [P, T], F32))
        self.ident = ctx.enter_context(nc.sbuf_tensor("ident", [P, P], F32))
        self.identb = ctx.enter_context(nc.sbuf_tensor("identb", [P, P], BF16))
        self.scratch_qk = nc.dram_tensor("scratch_qk", [B, 2, H8, 3, HD8, S], BF16, kind="Internal").ap()
        self.scratch_max = nc.dram_tensor("scratch_max", [B, 3 * H8, S], BF16, kind="Internal").ap()
        self.mhalf = ctx.enter_context(nc.sbuf_tensor("mhalf", [P, NT], F32))
        self.sems, self.old_sems, self.fresh, self.stale = ExitStack(), ExitStack(), [], []
        order = list(weights.values())
        width = [max([w.shape[1] for w, _ in order[i::2]] or [1]) for i in range(2)]
        self.wbuf = [ctx.enter_context(nc.sbuf_tensor(f"wbuf{i}", [P, width[i]], F32)) for i in range(2)]
        self.wsem = {s: ctx.enter_context(nc.semaphore(f"weights_loaded_{s}")) for s in weights}

    def sem(self, name):
        s = self.sems.enter_context(self.nc.semaphore(name))
        self.fresh.append(s)
        return s

    def stage_over(self):
        self.old_sems.close()
        self.old_sems, self.sems = self.sems, ExitStack()
        self.stale, self.fresh = self.fresh, []

    def w(self, stage):
        buf = self.wbuf[list(self.weights).index(stage) % 2]
        out, at = {}, 0
        for name, rows, n in self.weights[stage][1]:
            out[name] = buf[0:rows, at:at + n]
            at += n
        return out

    def spare(self, ctx, name, stage, n):
        order = list(self.weights)
        at = order.index(stage) + 1
        used = self.weights[order[at]][0].shape[1] if at < len(order) else 0
        buf = self.wbuf[at % 2]
        if buf.shape[1] - used >= n:
            return buf[:, buf.shape[1] - n:]
        return ctx.enter_context(self.nc.sbuf_tensor(name, [P, n], F32))[:, :]

    def gen(self, w):
        out, at = {}, 0
        for name, n in L2_SEGMENTS:
            out[name] = w["sub0"][:, at:at + n]
            at += n
        return out

    def load_weights(self, eng, stage):
        buf = self.wbuf[list(self.weights).index(stage) % 2]
        src = self.weights[stage][0]
        eng.dma_start(buf[:, 0:src.shape[1]], src).then_inc(self.wsem[stage], 16)

    def load_next(self, eng, stage):
        for s in self.stale:
            eng.sem_clear(s)
        order = list(self.weights)
        at = order.index(stage) + 1
        if at < len(order):
            self.load_weights(eng, order[at])


class LayerNorm:

    def __init__(self, sh, ctx, tag, ps=None, src=None, keep=None, affine=None):
        nc = sh.nc
        self.sh, self.ps, self.keep, self.affine = sh, ps, keep, affine
        self.src = sh.x if src is None else src
        sb = lambda n, shape: ctx.enter_context(nc.sbuf_tensor(f"{tag}_{n}", shape, F32))
        sem = lambda n: sh.sem(f"{tag}_{n}")
        self.stats = sb("ln_stats", [P, NT, 6])
        self.mv = sb("ln_mv", [P, NT, 2])
        self.rstd = sb("ln_rstd", [P, NT])
        self.xn = keep if keep is not None else sb("ln_xn", [P, 2, TPC, D])
        self.s_stats, self.s_mv = sem("ln_stats_done"), sem("ln_moments_done")
        self.s_eps, self.s_rstd = sem("ln_eps_added"), sem("ln_rstd_done")
        self.s_xn, self.s_T, self.ready = sem("ln_scaled"), sem("ln_transposed"), sem("xnT_ready")

    def xn_tile(self, c, i):
        return self.xn[:, c * TPC + i, :] if self.keep is not None else self.xn[:, c % 2, i, :]

    def vector(self, dve):
        nc = self.sh.nc
        for t in range(NT):
            nc.vector.bn_stats(self.stats[:, t, :], self.src[:, t, :]).then_inc(self.s_stats, 1)
            if t >= 1:
                dve.wait_ge(self.s_stats, t)
                nc.vector.bn_aggr(self.mv[:, t - 1, :], self.stats[:, t - 1, :]).then_inc(self.s_mv, 1)
        dve.wait_ge(self.s_stats, NT)
        nc.vector.bn_aggr(self.mv[:, NT - 1, :], self.stats[:, NT - 1, :]).then_inc(self.s_mv, 1)
        for t in range(NT):
            c, i = divmod(t, TPC)
            if i == 0:
                dve.wait_ge(self.s_rstd, c + 1)
                if c >= 2 and self.keep is None:
                    dve.wait_ge(self.s_T, c - 1)
            nc.vector.tensor_scalar(self.xn_tile(c, i), self.src[:, t, :], self.mv[:, t, 0:1],
                                    self.rstd[:, t:t + 1], ALU.subtract, ALU.mult).then_inc(self.s_xn, 1)

    def gpsimd(self, pool):
        nc = self.sh.nc
        for c in range(B):
            ts = slice(c * TPC, (c + 1) * TPC)
            pool.wait_ge(self.s_mv, (c + 1) * TPC)
            nc.gpsimd.tensor_scalar(self.rstd[:, ts], self.mv[:, ts, 1], LN_EPS, 1.0,
                                    ALU.add, ALU.mult).then_inc(self.s_eps, 1)
            pool.wait_ge(self.s_eps, c + 1)
            nc.gpsimd.tensor_tensor(self.rstd[:, ts], self.rstd[:, ts], self.sh.mhalf[:, ts],
                                    ALU.pow).then_inc(self.s_rstd, 1)

    def tensor(self, pe):
        nc = self.sh.nc
        for c in range(B):
            if c >= 2:
                pe.wait_ge(self.ready, c - 1)
            for i in range(TPC):
                pe.wait_ge(self.s_xn, c * TPC + i + 1)
                last = nc.tensor.transpose(self.ps[c % 2][:, i * P:(i + 1) * P], self.xn_tile(c, i),
                                           self.sh.ident[:, :])
            last.then_inc(self.s_T, 1)

    def scalar(self, act):
        nc = self.sh.nc
        for c in range(B):
            act.wait_ge(self.s_T, c + 1)
            dst, ps = self.sh.xnT[:, c * S:(c + 1) * S], self.ps[c % 2][:, :]
            if self.affine:
                last = nc.scalar.activation(dst, ps, ACT.Identity, bias=self.affine[1], scale=self.affine[0])
            else:
                last = nc.scalar.copy(dst, ps)
            last.then_inc(self.ready, 1)


def ranks(nc, st, rank, s, before, gt, eq):
    n, e = s.shape[1], s.shape[2]
    mine = s.unsqueeze(3).broadcast_to([P, n, e, e])
    other = s.unsqueeze(2).broadcast_to([P, n, e, e])
    st.did(nc.vector.tensor_tensor(gt, other, mine, ALU.is_gt))
    st.then(nc.vector.tensor_tensor(eq, other, mine, ALU.is_equal))
    st.then(nc.vector.tensor_tensor(eq, eq, before.unsqueeze(1).broadcast_to([P, n, e, e]), ALU.mult))
    st.then(nc.vector.tensor_tensor(gt, gt, eq, ALU.add))
    st.then(nc.vector.tensor_reduce(rank, gt, AX.X, ALU.add))


def make_before(nc, pool, before, e, sem):
    nc.gpsimd.memset(before[:, :, :], 1.0).then_inc(sem, 1)
    pool.wait_ge(sem, 1)
    nc.gpsimd.affine_select(out=before[:, :, :], in_=before[:, :, :], compare_op=ALU.is_gt, fill=0.0,
                            base=0, pattern=[[1, e], [-1, e]], channel_multiplier=0).then_inc(sem, 1)


def split3(ops, st, parts, src, rest):
    st.then(ops.tensor_copy(parts[0], src))
    st.then(ops.tensor_tensor(rest[0], src, parts[0], ALU.subtract))
    st.then(ops.tensor_copy(parts[1], rest[0]))
    st.then(ops.tensor_tensor(rest[1], rest[0], parts[1], ALU.subtract))
    st.then(ops.tensor_copy(parts[2], rest[1]))


GLA_LEVELS = (64, 32, 16, 8, 4, 2, 1)
GLA_STEPS = 28


def gated_linear_attention(sh, stage, heads=4, dk=32, dv=64, rank=32, gate_norm=32.0, rms_eps=1e-5):
    nc, w, tag = sh.nc, sh.w(stage), f"s{stage}"
    E, W = heads * dv, P // TPC
    NL = len(GLA_LEVELS)
    F_LAST, F_ALL = NL, NL + 1
    MUL, ADD, SUB = ALU.mult, ALU.add, ALU.subtract
    with ExitStack() as ctx:
        sb = lambda m, shape, dt=F32: ctx.enter_context(nc.sbuf_tensor(f"{tag}_{m}", shape, dt))
        sem = lambda m: sh.sem(f"{tag}_{m}")
        bank = lambda m, n=1: ctx.enter_context(nc.psum_tensor(f"{tag}_{m}", [P, n, S], F32))
        odd = [bank(f"odd_jobs{i}")[:, 0, :] for i in range(2)]
        ps_a, ps_o = bank("pair_products", heads), bank("o", 2)
        ln = LayerNorm(sh, ctx, tag, odd)
        xc = sb("xnT_of_sequence", [P, S])
        qT, kT, gk = sb("qT", [P, S]), sb("kT", [P, S]), sb("gk", [rank, S])
        z, soft, g = sb("z", [P, S]), sb("softplus", [P, S]), sb("log_decay", [P, S])
        v, gate = sb("v", [P, TPC, E]), sb("gate", [P, TPC, E])
        b = sb("decay_sums", [P, S])
        expo, fac = sb("exponents", [P, NL + 2, S]), sb("factors", [P, NL + 2, S])
        zkq = sb("scaled_kq", [P, NL + 2, S])
        near = sb("near_pairs", [P, heads, TPC, W])
        pairs = sb("pairs", [P, heads, TPC, P])
        kdec = sb("k_to_end", [P, TPC, P])
        state = sb("state", [P, E])
        sq, ss, rrms = sb("o_squared", [P, TPC, E]), sb("o_square_sums", [P, TPC * heads]), sb("rrms", [P, TPC * heads])
        og, ogT = sb("o_gated", [P, TPC, E]), sb("o_gatedT", [P, 2, S])
        tri = sb("tri", [P, P])
        it, ij = sb("iota_t", [P, W], mybir.dt.int32), sb("iota_j", [P, W], mybir.dt.int32)
        ix = sb("iota_xor", [P, W], mybir.dt.int32)
        ft, fj, fx = sb("query_no", [P, W]), sb("key_no", [P, W]), sb("xor", [P, W])
        later, below = sb("later", [P, W]), sb("below", [P, W])
        low = [m for m in GLA_LEVELS if m < W]
        turn = sb("wait_carrier", [P, 1])
        masks = sb("masks", [P, len(low) + 1, W])
        s_const, s_mask = sem("constants_made"), sem("mask_steps")
        s_xc, s_proj, s_gk, s_qk = sem("xc_copied"), sem("projected"), sem("gk_ready"), sem("qk_ready")
        s_z, s_vg, s_vgs = sem("z_ready"), sem("v_gate_projected"), sem("v_done")
        s_gates = sem("gate_done")
        s_st, s_e, s_l = sem("vector_steps"), sem("exp_done"), sem("log_done")
        s_b, s_bs, s_expo, s_fac = sem("sums_ready"), sem("sums_in_sbuf"), sem("exponents_done"), sem("factors_ready")
        s_zkq, s_round, s_taken, s_rect = sem("scaled_ready"), sem("pairs_round"), sem("round_taken"), sem("rects_copied")
        s_near, s_win = sem("near_done"), sem("windows_copied")
        s_kdT, s_kd = sem("k_to_end_turned"), sem("k_to_end_ready")
        s_inc, s_state, s_o = sem("state_added"), sem("state_ready"), sem("o_ready")
        s_sq, s_ss, s_rms = sem("squares_done"), sem("square_sums_done"), sem("rrms_done")
        s_gw = sem("gate_weighted")
        s_og, s_ogT, s_ogTs, s_y, s_x = sem("o_gated_ready"), sem("og_turned"), sem("ogT_ready"), sem("y_ready"), sem("x_updated")
        s_free = [sem(f"odd_bank_free{i}") for i in range(2)]
        jobs = ["gk", "q", "k", "z"] + [("vg", i) for i in range(TPC)] + ["b", "kd"] + \
            [("S", i) for i in range(TPC - 1)] + ["y"]
        job = {name: n for n, name in enumerate(jobs)}
        JOBS = len(jobs) // 2
        assert len(jobs) % 2 == 0
        rounds = [(0,), (64, 32, 16), (8, 4, 2, 1)]
        place = {0: 0, 64: 0, 32: 256, 16: 384, 8: 0, 4: 128, 2: 256, 1: 384}
        blocks = lambda a, m: a.rearrange("p (n u) -> p n u", u=2 * m)
        by_chunk = lambda a: a.rearrange("p (i t) -> p i t", i=TPC)
        block = ctx.enter_context(nc.Block())

        @block.sync
        def _(sp):
            sh.load_next(sp, stage)

        def freed(eng, name):
            eng.sem_inc(s_free[job[name] % 2], 1)

        @block.gpsimd
        def _(pool):
            nc.gpsimd.iota(it[:, :], pattern=[[1, W]], base=0, channel_multiplier=0).then_inc(s_const, 1)
            nc.gpsimd.iota(ij[:, :], pattern=[[0, W]], base=0, channel_multiplier=1).then_inc(s_const, 1)
            nc.gpsimd.memset(tri[:, :], 1.0 / gate_norm).then_inc(s_const, 1)
            nc.gpsimd.memset(pairs[:, :, :, :], 0.0).then_inc(s_const, 1)
            nc.gpsimd.memset(state[:, :], 0.0).then_inc(s_const, 1)
            pool.wait_ge(s_const, 5)
            nc.gpsimd.affine_select(out=tri[:, :], in_=tri[:, :], compare_op=ALU.is_ge, fill=0.0, base=0,
                                    pattern=[[1, P]], channel_multiplier=-1).then_inc(s_const, 1)
            ln.gpsimd(pool)
            pool.wait_ge(sh.wsem[stage], 16)
            with pool.Fori(0, B) as c:
                pool.wait_ge(s_x, 1 + c)
                pool.wait_ge(s_bs, c + 1)
                for n, m in enumerate(GLA_LEVELS):
                    src, dst = blocks(b[:, :], m), blocks(expo[:, n, :], m)
                    mid = src[:, :, m - 1:m].broadcast_to([P, S // (2 * m), m])
                    nc.gpsimd.tensor_tensor(dst[:, :, 0:m], mid, src[:, :, 0:m], SUB).then_inc(s_expo, 1)
                    nc.gpsimd.tensor_tensor(dst[:, :, m:], src[:, :, m:], mid, SUB).then_inc(s_expo, 1)
                nc.gpsimd.tensor_tensor(by_chunk(expo[:, F_LAST, :]),
                                        by_chunk(b[:, :])[:, :, P - 1:P].broadcast_to([P, TPC, P]),
                                        by_chunk(b[:, :]), SUB).then_inc(s_expo, 1)
                pool.wait_ge(s_gates, (c + 1) * TPC)
                nc.gpsimd.tensor_tensor(gate[:, :, :].rearrange("p i (h e) -> p (i h) e", h=heads),
                                        gate[:, :, :].rearrange("p i (h e) -> p (i h) e", h=heads),
                                        w["rms_w"].unsqueeze(1).broadcast_to([P, TPC * heads, dv]), MUL).then_inc(s_gw, 1)
                pool.wait_ge(s_ss, c + 1)
                nc.gpsimd.tensor_tensor(rrms[:, :], ss[:, :], sh.mhalf[:, 0:TPC * heads], ALU.pow).then_inc(s_rms, 1)

        @block.tensor
        def _(pe):
            pe.sem_inc(s_free[0], 1)
            pe.sem_inc(s_free[1], 1)
            pe.wait_ge(sh.wsem[stage], 16)
            ln.tensor(pe)
            pe.wait_ge(ln.ready, B)
            pe.wait_ge(s_const, 6)
            with pe.Fori(0, B) as c:
                pe.wait_ge(s_x, 1 + c)

                def take(name):
                    k = job[name]
                    pe.wait_ge(s_free[k % 2], c * JOBS + k // 2 + 1)
                    return odd[k % 2]

                ps = take("gk")
                nc.tensor.matmul(ps[0:rank, :], w["wgk1"], sh.xnT[:, cols(c)], start=True, stop=True).then_inc(s_proj, 1)
                for name in "qk":
                    ps = take(name)
                    nc.tensor.matmul(ps, w["w" + name], sh.xnT[:, cols(c)], start=True, stop=True).then_inc(s_proj, 1)
                ps = take("z")
                pe.wait_ge(s_gk, c + 1)
                for i in range(TPC):
                    last = nc.tensor.matmul(ps[:, i * P:(i + 1) * P], gk[:, i * P:(i + 1) * P], w["wgk2"],
                                            start=True, stop=True)
                last.then_inc(s_z, 1)
                pe.wait_ge(s_xc, c + 1)
                for i in range(TPC):
                    ps = take(("vg", i))
                    nc.tensor.matmul(ps, xc[:, i * P:(i + 1) * P], w["wvg"], start=True, stop=True).then_inc(s_vg, 1)
                ps = take("b")
                pe.wait_ge(s_st, c * GLA_STEPS + 3)
                pe.wait_ge(s_qk, (c + 1) * 2)
                for i in range(TPC):
                    last = nc.tensor.matmul(ps[:, i * P:(i + 1) * P], g[:, i * P:(i + 1) * P], tri[:, :],
                                            start=True, stop=True)
                last.then_inc(s_b, 1)
                for r, levels in enumerate(rounds):
                    if r:
                        pe.wait_ge(s_zkq, c * (NL + 2) + GLA_LEVELS.index(levels[-1]) + 1)
                        pe.wait_ge(s_taken, c * 3 + r)
                    if r == 2:
                        ps = take("kd")
                        pe.wait_ge(s_zkq, c * (NL + 2) + NL + 1)
                        for i in range(TPC):
                            last = nc.tensor.transpose(ps[:, i * P:(i + 1) * P], zkq[:, F_LAST, i * P:(i + 1) * P],
                                                       sh.ident[:, :])
                        last.then_inc(s_kdT, 1)
                    for m in levels:
                        n = GLA_LEVELS.index(m) if m else 0
                        keys, queries = (zkq[:, n, :],) * 2 if m else (kT, qT)
                        for i in range(TPC):
                            at = i * P
                            for h in range(heads):
                                rows = slice(h * dk, (h + 1) * dk)
                                if m == 64:
                                    to = place[m] + i * m
                                    last = nc.tensor.matmul(ps_a[0:m, h, to:to + m], keys[rows, at:at + m],
                                                            queries[rows, at + m:at + 2 * m], start=True, stop=True)
                                elif m == 32:
                                    to = place[m] + i * m
                                    for k in (0, 64):
                                        last = nc.tensor.matmul(ps_a[k:k + m, h, to:to + m], keys[rows, at + k:at + k + m],
                                                                queries[rows, at + k + m:at + k + 2 * m],
                                                                start=True, stop=True)
                                else:
                                    to = place[m] + i * W
                                    for k in range(0, P, W):
                                        last = nc.tensor.matmul(ps_a[k:k + W, h, to:to + W], keys[rows, at + k:at + k + W],
                                                                queries[rows, at + k:at + k + W], start=True, stop=True)
                    last.then_inc(s_round, 1)
                pe.wait_ge(s_zkq, (c + 1) * (NL + 2))
                pe.wait_ge(s_win, (c + 1) * TPC)
                pe.wait_ge(s_vgs, (c + 1) * TPC)
                for i in range(TPC):
                    half = ps_o[:, i // 2, (i % 2) * E:(i % 2 + 1) * E]
                    for h in range(heads):
                        last = nc.tensor.matmul(half[:, h * dv:(h + 1) * dv], pairs[:, h, i, :], v[:, i, h * dv:(h + 1) * dv],
                                                start=(i % 2 == 0 and h == 0), stop=False, skip_group_check=True)
                    if i < TPC - 1:
                        ps = take(("S", i))
                        pe.wait_ge(s_kd, c + 1)
                        nc.tensor.matmul(ps[:, 0:E], kdec[:, i, :], v[:, i, :], start=True, stop=True).then_inc(s_inc, 1)
                    if i:
                        pe.wait_ge(s_state, c * (TPC - 1) + i)
                        last = nc.tensor.matmul(half, zkq[:, F_ALL, i * P:(i + 1) * P], state[:, :],
                                                start=False, stop=True, skip_group_check=True)
                    last.then_inc(s_o, 1)
                pe.wait_ge(s_og, c + 1)
                for i in range(TPC):
                    for k in range(2):
                        last = nc.tensor.transpose(ps_a[:, k, i * P:(i + 1) * P], og[:, i, k * P:(k + 1) * P], sh.ident[:, :])
                last.then_inc(s_ogT, 1)
                ps = take("y")
                pe.wait_ge(s_ogTs, (c + 1) * 2)
                for i in range(TPC):
                    for k in range(2):
                        last = nc.tensor.matmul(ps[:, i * P:(i + 1) * P], ogT[:, k, i * P:(i + 1) * P],
                                                w["wout"][:, k * D:(k + 1) * D], start=(i == 0 and k == 0), stop=(k == 1),
                                                skip_group_check=True)
                last.then_inc(s_y, 1)

        @block.scalar
        def _(act):
            ln.scalar(act)
            act.wait_ge(ln.ready, B)
            with act.Fori(0, B) as c:
                act.wait_ge(s_x, 1 + c)
                nc.scalar.copy(xc[:, :], sh.xnT[:, cols(c)]).then_inc(s_xc, 1)
                act.wait_ge(s_proj, c * 3 + 1)
                nc.scalar.copy(gk[:, :], odd[job["gk"] % 2][0:rank, :]).then_inc(s_gk, 1)
                act.wait_ge(s_gk, c + 1)
                freed(act, "gk")
                for n, (name, dst) in enumerate((("q", qT), ("k", kT))):
                    act.wait_ge(s_proj, c * 3 + n + 2)
                    nc.scalar.activation(dst[:, :], odd[job[name] % 2], ACT.Copy,
                                         scale=dk ** -0.5 if name == "q" else 1.0).then_inc(s_qk, 1)
                    act.wait_ge(s_qk, c * 2 + n + 1)
                    freed(act, name)
                act.wait_ge(s_st, c * GLA_STEPS + 2)
                nc.scalar.activation(soft[:, :], soft[:, :], ACT.Exp, scale=-1.0).then_inc(s_e, 1)
                act.wait_ge(s_e, c + 1)
                nc.scalar.activation(soft[:, :], soft[:, :], ACT.Ln, bias=1.0).then_inc(s_l, 1)
                for i in range(TPC):
                    act.wait_ge(s_vg, c * TPC + i + 1)
                    nc.scalar.activation(gate[:, i, :], odd[job["vg", i] % 2][:, E:2 * E], ACT.Silu).then_inc(s_gates, 1)
                act.wait_ge(s_b, c + 1)
                nc.scalar.copy(b[:, :], odd[job["b"] % 2]).then_inc(s_bs, 1)
                act.wait_ge(s_bs, c + 1)
                freed(act, "b")
                nc.scalar.activation(fac[:, F_ALL, :], b[:, :], ACT.Exp).then_inc(s_fac, 1)
                for n in range(NL + 1):
                    act.wait_ge(s_expo, c * (2 * NL + 1) + min(2 * n + 2, 2 * NL + 1))
                    nc.scalar.activation(fac[:, n, :], expo[:, n, :], ACT.Exp).then_inc(s_fac, 1)
                act.wait_ge(s_round, c * 3 + 2)
                cut = lambda k, m, at: ps_a[k:k + m, :, at:at + TPC * m].rearrange("p h (i t) -> p h i t", i=TPC)
                nc.scalar.copy(pairs[0:64, :, :, 64:P], cut(0, 64, place[64])).then_inc(s_rect, 1)
                for k in (0, 64):
                    nc.scalar.copy(pairs[k:k + 32, :, :, k + 32:k + 64], cut(k, 32, place[32])).then_inc(s_rect, 1)
                act.wait_ge(s_kdT, c + 1)
                nc.scalar.copy(kdec[:, :, :].rearrange("p i d -> p (i d)"), odd[job["kd"] % 2]).then_inc(s_kd, 1)
                act.wait_ge(s_kd, c + 1)
                freed(act, "kd")
                act.wait_ge(s_near, c + 1)
                for k in range(TPC):
                    r = slice(k * W, (k + 1) * W)
                    nc.scalar.copy(pairs[r, :, :, r], near[r, :, :, :]).then_inc(s_win, 1)
                for k in range(2):
                    act.wait_ge(s_o, c * TPC + 2 * k + 2)
                    nc.scalar.activation(sq[:, 2 * k:2 * k + 2, :].rearrange("p i e -> p (i e)"), ps_o[:, k, :],
                                         ACT.Square).then_inc(s_sq, 1)
                act.wait_ge(s_ogT, c + 1)
                for k in range(2):
                    nc.scalar.copy(ogT[:, k, :], ps_a[:, k, :]).then_inc(s_ogTs, 1)

        @block.vector
        def _(dve):
            dve.sem_inc(s_x, 1)
            mk = Steps(dve, s_mask, 0, 7 + 3 * len(low))
            dve.wait_ge(s_const, 2)
            mk.then(nc.vector.tensor_scalar(ij[:, :], ij[:, :], W - 1, None, ALU.bitwise_and))
            mk.then(nc.vector.tensor_tensor(ix[:, :], it[:, :], ij[:, :], ALU.bitwise_xor))
            mk.did(nc.vector.tensor_copy(ft[:, :], it[:, :]))
            mk.did(nc.vector.tensor_copy(fj[:, :], ij[:, :]))
            mk.then(nc.vector.tensor_copy(fx[:, :], ix[:, :]))
            mk.did(nc.vector.tensor_tensor(later[:, :], ft[:, :], fj[:, :], ALU.is_gt))
            mk.then(nc.vector.tensor_tensor(masks[:, len(low), :], ft[:, :], fj[:, :], ALU.is_equal))
            for n, m in enumerate(low):
                mk.did(nc.vector.tensor_scalar(below[:, :], fx[:, :], 2 * m - 0.5, None, ALU.is_lt))
                mk.then(nc.vector.scalar_tensor_tensor(out=masks[:, n, :], in0=fx[:, :], scalar=m - 0.5, in1=later[:, :],
                                                       op0=ALU.is_gt, op1=MUL))
                mk.then(nc.vector.tensor_tensor(masks[:, n, :], masks[:, n, :], below[:, :], MUL))
            mk.end()
            dve.wait_ge(sh.wsem[stage], 16)
            ln.vector(dve)
            dve.wait_ge(s_const, 5)
            with dve.Fori(0, B) as c:
                st = Steps(dve, s_st, c * GLA_STEPS, GLA_STEPS)
                dve.wait_ge(s_z, c + 1)
                st.then(nc.vector.tensor_tensor(by_chunk(z[:, :]), by_chunk(odd[job["z"] % 2]),
                                                w["bgk2"].unsqueeze(1).broadcast_to([P, TPC, P]), ADD))
                freed(dve, "z")
                st.did(nc.vector.scalar_tensor_tensor(out=soft[:, :], in0=z[:, :], scalar=-1.0, in1=z[:, :],
                                                      op0=MUL, op1=ALU.max))
                dve.wait_ge(s_l, c + 1)
                st.did(nc.vector.scalar_tensor_tensor(out=g[:, :], in0=z[:, :], scalar=0.0, in1=soft[:, :],
                                                      op0=ALU.min, op1=SUB))
                for i in range(TPC):
                    dve.wait_ge(s_gates, c * TPC + i + 1)
                    nc.vector.tensor_copy(v[:, i, :], odd[job["vg", i] % 2][:, 0:E]).then_inc(s_vgs, 1)
                    dve.wait_ge(s_vgs, c * TPC + i + 1)
                    freed(dve, ("vg", i))
                dve.wait_ge(s_round, c * 3 + 1)
                low_round = lambda m: ps_a[:, :, place[m]:place[m] + TPC * W].rearrange("p h (i t) -> p h i t", i=TPC)
                wide = lambda n: masks[:, n, :].unsqueeze(1).unsqueeze(1).broadcast_to([P, heads, TPC, W])
                st.then(nc.vector.tensor_tensor(near[:, :, :, :], low_round(0), wide(len(low)), MUL))
                dve.sem_inc(s_taken, 1)
                for n, m in enumerate(GLA_LEVELS):
                    if n == 0:
                        dve.wait_ge(s_qk, (c + 1) * 2)
                    dve.wait_ge(s_fac, c * (NL + 2) + n + 2)
                    for src, half in ((kT, slice(0, m)), (qT, slice(m, 2 * m))):
                        last = nc.vector.tensor_tensor(blocks(zkq[:, n, :], m)[:, :, half], blocks(fac[:, n, :], m)[:, :, half],
                                                       blocks(src[:, :], m)[:, :, half], MUL)
                    last.then_inc(s_zkq, 1)
                dve.wait_ge(s_fac, (c + 1) * (NL + 2))
                nc.vector.tensor_tensor(zkq[:, F_LAST, :], fac[:, F_LAST, :], kT[:, :], MUL).then_inc(s_zkq, 1)
                nc.vector.tensor_tensor(zkq[:, F_ALL, :], fac[:, F_ALL, :], qT[:, :], MUL).then_inc(s_zkq, 1)
                for r, levels in enumerate(rounds):
                    if r:
                        dve.wait_ge(s_round, c * 3 + r + 1)
                        if r == 1:
                            dve.wait_ge(s_rect, c * 3 + 3)
                        for m in levels:
                            if m < W:
                                st.did(nc.vector.memset(turn[:, :], 0.0))
                                st.then(nc.vector.copy_predicated(near[:, :, :, :], wide(low.index(m)).bitcast(U32),
                                                                  low_round(m)))
                        dve.sem_inc(s_taken, 1)
                dve.sem_inc(s_near, 1)
                for i in range(TPC - 1):
                    dve.wait_ge(s_inc, c * (TPC - 1) + i + 1)
                    if i:
                        dve.wait_ge(s_o, c * TPC + i + 1)
                    for h in range(heads):
                        r, e = slice(h * dk, (h + 1) * dk), slice(h * dv, (h + 1) * dv)
                        if i == 0:
                            st.did(nc.vector.tensor_copy(state[r, e], odd[job["S", i] % 2][r, e]))
                        else:
                            at = (i + 1) * P - 1
                            st.did(nc.vector.scalar_tensor_tensor(out=state[r, e], in0=state[r, e],
                                                                  scalar=fac[r, F_ALL, at:at + 1],
                                                                  in1=odd[job["S", i] % 2][r, e], op0=MUL, op1=ADD))
                    st.wait()
                    freed(dve, ("S", i))
                    dve.sem_inc(s_state, 1)
                by_head = lambda a: a.rearrange("p i (h e) -> p (i h) e", h=heads)
                dve.wait_ge(s_sq, (c + 1) * 2)
                st.then(nc.vector.tensor_reduce(ss[:, :], by_head(sq[:, :, :]), AX.X, ADD))
                nc.vector.tensor_scalar(ss[:, :], ss[:, :], 1.0 / dv, rms_eps, MUL, ADD).then_inc(s_ss, 1)
                dve.wait_ge(s_rms, c + 1)
                st.then(nc.vector.tensor_tensor(by_head(og[:, :, :]),
                                                ps_o[:, :, :].rearrange("p k (i h e) -> p (k i h) e", h=heads, e=dv),
                                                rrms[:, :].unsqueeze(2).broadcast_to([P, TPC * heads, dv]), MUL))
                dve.wait_ge(s_gw, c + 1)
                nc.vector.tensor_tensor(og[:, :, :], og[:, :, :], gate[:, :, :], MUL).then_inc(s_og, 1)
                dve.wait_ge(s_y, c + 1)
                st.end()
                nc.vector.tensor_tensor(sh.x[:, tiles(c), :], sh.x[:, tiles(c), :],
                                        odd[job["y"] % 2].rearrange("p (t d) -> p t d", t=TPC), ADD).then_inc(s_x, 1)
                dve.wait_ge(s_x, c + 2)
                freed(dve, "y")


def route_top1(nc, st, s, comb, before, gt, eq, small):
    rank = small[:, 0, :].rearrange("p (t e) -> p t e", t=TPC)
    ranks(nc, st, rank, s, before[:, :, :], gt[:, :, :, :], eq[:, :, :, :])
    st.then(nc.vector.tensor_scalar(comb, rank, 0.5, None, ALU.is_lt))


def route_groups(nc, st, s, comb, before, gt, eq, small, groups=4, top_groups=2, top=4):
    e = s.shape[2]
    g = e // groups
    n = TPC * groups
    assert g == 4
    by_group = lambda a: a.rearrange("p t (h k) -> p (t h) k", h=groups)
    region = lambda k, m: small[:, k, 0:TPC * m].rearrange("p (t m) -> p t m", t=TPC)
    s4 = by_group(s).rearrange("p n (a b) -> p n a b", a=2)
    pmax, psum = (small[:, k, 0:2 * n].rearrange("p (n a) -> p n a", a=2) for k in (0, 1))
    best, pair, grank, allowed = (small[:, k, 0:n] for k in (2, 3, 4, 5))
    masked, rank, total = region(0, e), region(1, e), region(2, 1)
    per_tile = lambda a: a.rearrange("p (t h) -> p t h", t=TPC)
    st.did(nc.vector.tensor_tensor(pmax, s4[:, :, :, 0], s4[:, :, :, 1], ALU.max))
    st.then(nc.vector.tensor_tensor(psum, s4[:, :, :, 0], s4[:, :, :, 1], ALU.add))
    st.did(nc.vector.tensor_tensor(best, pmax[:, :, 0], pmax[:, :, 1], ALU.add))
    st.then(nc.vector.tensor_tensor(pair, psum[:, :, 0], psum[:, :, 1], ALU.max))
    st.then(nc.vector.tensor_tensor(best, best, pair, ALU.max))
    ranks(nc, st, per_tile(grank), per_tile(best), before[:, 0:groups, 0:groups],
          gt[:, :, 0:groups, 0:groups], eq[:, :, 0:groups, 0:groups])
    st.then(nc.vector.tensor_scalar(allowed, grank, top_groups - 0.5, None, ALU.is_lt))
    wide = allowed.unsqueeze(2).broadcast_to([P, n, g])
    st.then(nc.vector.tensor_tensor(by_group(masked), by_group(s), wide, ALU.mult))
    st.then(nc.vector.scalar_tensor_tensor(out=by_group(masked), in0=wide, scalar=-1.0, in1=by_group(masked),
                                           op0=ALU.add, op1=ALU.add))
    ranks(nc, st, rank, masked, before[:, :, :], gt[:, :, :, :], eq[:, :, :, :])
    st.then(nc.vector.scalar_tensor_tensor(out=masked, in0=rank, scalar=top - 0.5, in1=s,
                                           op0=ALU.is_lt, op1=ALU.mult))
    st.then(nc.vector.tensor_reduce(total, masked, AX.X, ALU.add))
    st.then(nc.vector.tensor_scalar(total, total, 1e-6, None, ALU.add))
    st.then(nc.vector.reciprocal(total, total))
    st.then(nc.vector.tensor_tensor(comb, masked, total.broadcast_to([P, TPC, e]), ALU.mult))


ROUTE_TOP1_STEPS = 11
ROUTE_GROUPS_STEPS = 28


def routed_ffn(sh, stage, n_exp, f_exp, f_shared, score_func, route, route_steps):
    nc, w, tag = sh.nc, sh.w(stage), f"s{stage}"
    n_shared = f_shared // P
    units = n_exp * f_exp // P + n_shared
    K = 3 * n_exp
    with ExitStack() as ctx:
        sb = lambda n, shape, dt=F32: ctx.enter_context(nc.sbuf_tensor(f"{tag}_{n}", shape, dt))
        sem = lambda n: sh.sem(f"{tag}_{n}")
        bank = lambda n, shape=(P, S), dt=F32: ctx.enter_context(nc.psum_tensor(f"{tag}_{n}", list(shape), dt))
        ps_gate = [bank(f"gate{i}") for i in range(2)]
        ps_up = [bank(f"up{i}") for i in range(2)]
        ps_comb = [bank(f"comb{i}") for i in range(2)]
        ps_y = bank("y", (P, TPC, D))
        ps_route = bank("route")
        ps_logits = ps_route[:, 0:NT * n_exp].rearrange("p (t e) -> p t e", t=NT)
        ps_combT = ps_route[:, 256:512].bitcast(BF16)
        ln = LayerNorm(sh, ctx, tag, [ps_route, ps_y[:, :, :].rearrange("p t d -> p (t d)")])
        silu = sb("silu", [P, 2, S])
        gated = sb("gated", [P, 2, S])
        hidden = sb("hidden", [P, 2, S])
        comb = sb("comb", [P, TPC, n_exp])
        parts_wide = sb("comb_parts", [P, TPC, P], BF16)
        parts = parts_wide[:, :, 0:K].rearrange("p t (a e) -> p t a e", a=3)
        rest = sb("comb_rest", [P, 2, TPC, n_exp])
        combT = sb("combT", [K, S], BF16)
        scores = sb("scores", [P, NT, n_exp])
        small = sb("small", [P, 6, TPC * n_exp])
        sel = sb("sel", [K, units - n_shared, P], BF16)
        before = sb("before", [P, n_exp, n_exp])
        gt = sb("gt", [P, TPC, n_exp, n_exp])
        eq = sb("eq", [P, TPC, n_exp, n_exp])
        s_sel, s_before, s_zero = sem("sel_made"), sem("before_made"), sem("parts_cleared")
        s_logits, s_scores = sem("logits_ready"), sem("scores_ready")
        s_route = sem("route_steps")
        s_partsT, s_combT = sem("parts_transposed"), sem("combT_ready")
        s_up, s_silu = sem("gate_up_ready"), sem("silu_ready")
        s_gated, s_hidden = sem("gated_done"), sem("hidden_ready")
        s_down, s_x = sem("down_done"), sem("x_updated")
        block = ctx.enter_context(nc.Block())

        @block.sync
        def _(sp):
            sh.load_next(sp, stage)

        @block.gpsimd
        def _(pool):
            make_before(nc, pool, before, n_exp, s_before)
            nc.gpsimd.memset(sel[:, :, :], 0.0).then_inc(s_sel, 1)
            pool.wait_ge(s_sel, 1)
            n = 1
            for part in range(3):
                if f_exp >= P:
                    k = f_exp // P
                    view = sel[:, :, :].rearrange("r (e k) f -> r e (k f)", k=k)
                    pattern = [[-1, n_exp], [0, k * P]]
                else:
                    view = sel[:, :, :].rearrange("r u (e f) -> r (u e) f", f=f_exp)
                    pattern = [[-1, n_exp], [0, f_exp]]
                nc.gpsimd.affine_select(out=view, in_=view, compare_op=ALU.not_equal, fill=1.0,
                                        base=-part * n_exp, pattern=pattern,
                                        channel_multiplier=1).then_inc(s_sel, 1)
                n += 1
                pool.wait_ge(s_sel, n)
            ln.gpsimd(pool)

        @block.tensor
        def _(pe):
            pe.sem_inc(s_down, 1)
            pe.wait_ge(sh.wsem[stage], 16)
            ln.tensor(pe)
            pe.wait_ge(s_sel, 4)
            pe.wait_ge(ln.ready, B)
            for t in range(NT):
                last = nc.tensor.matmul(ps_logits[:, t, :], sh.xnT[:, t * P:(t + 1) * P], w["router"],
                                        start=True, stop=True)
            last.then_inc(s_logits, 1)
            pe.wait_ge(s_scores, 1)
            with pe.Fori(0, B) as c:
                def gate_up(u):
                    pe.wait_ge(s_hidden, 1 + c * units + (u - 1 if u else 0))
                    nc.tensor.matmul(ps_gate[u % 2][:, :], w["gate"][:, u * P:(u + 1) * P],
                                     sh.xnT[:, cols(c)], start=True, stop=True)
                    last = nc.tensor.matmul(ps_up[u % 2][:, :], w["up"][:, u * P:(u + 1) * P],
                                            sh.xnT[:, cols(c)], start=True, stop=True)
                    if u >= n_shared:
                        pe.wait_ge(s_combT, c + 1)
                        last = nc.tensor.matmul(ps_comb[u % 2][:, :], sel[:, u - n_shared, :], combT[:, :],
                                                start=True, stop=True)
                    last.then_inc(s_up, 1)

                def down(u):
                    pe.wait_ge(s_hidden, 1 + c * units + u + 1)
                    if u == 0:
                        pe.wait_ge(s_x, 1 + c)
                    for i in range(TPC):
                        last = nc.tensor.matmul(ps_y[:, i, :], hidden[:, u % 2, i * P:(i + 1) * P],
                                                w["down"][:, u * P:(u + 1) * P],
                                                start=(u == 0 and i == 0), stop=(u == units - 1),
                                                skip_group_check=True)
                    last.then_inc(s_down, 1)

                for u in range(units):
                    gate_up(u)
                    if u == n_shared - 1:
                        pe.wait_ge(s_route, (c + 1) * route_steps)
                        for i in range(TPC):
                            last = nc.tensor.transpose(ps_combT[:, i * P:(i + 1) * P], parts_wide[:, i, :],
                                                       sh.identb[:, :])
                        last.then_inc(s_partsT, 1)
                    if u:
                        down(u - 1)
                down(units - 1)

        @block.scalar
        def _(act):
            ln.scalar(act)
            act.wait_ge(s_logits, 1)
            nc.scalar.activation(scores[:, :, :], ps_logits, score_func).then_inc(s_scores, 1)
            with act.Fori(0, B) as c:
                for u in range(units):
                    act.wait_ge(s_up, c * units + u + 1)
                    nc.scalar.activation(silu[:, u % 2, :], ps_gate[u % 2][:, :], ACT.Silu).then_inc(s_silu, 1)

        @block.vector
        def _(dve):
            dve.sem_inc(s_hidden, 1)
            dve.sem_inc(s_x, 1)
            nc.vector.memset(parts_wide[:, :, :], 0.0).then_inc(s_zero, 1)
            ln.vector(dve)
            dve.wait_ge(s_zero, 1)
            dve.wait_ge(s_before, 2)
            dve.wait_ge(s_scores, 1)
            with dve.Fori(0, B) as c:
                st = Steps(dve, s_route, c * route_steps, route_steps)
                route(nc, st, scores[:, tiles(c), :], comb[:, :, :], before, gt, eq, small)
                split3(nc.vector, st, [parts[:, :, k, :] for k in range(3)], comb[:, :, :],
                       [rest[:, k, :, :] for k in range(2)])
                st.end()
                for u in range(units):
                    if u == n_shared:
                        dve.wait_ge(s_partsT, c + 1)
                        nc.vector.tensor_copy(combT[:, :], ps_combT[0:K, :]).then_inc(s_combT, 1)
                    dve.wait_ge(s_silu, c * units + u + 1)
                    dve.wait_ge(s_down, 1 + c * units + (u - 1 if u else 0))
                    if u < n_shared:
                        nc.vector.tensor_tensor(hidden[:, u % 2, :], silu[:, u % 2, :], ps_up[u % 2][:, :],
                                                ALU.mult).then_inc(s_hidden, 1)
                    else:
                        nc.vector.tensor_tensor(gated[:, u % 2, :], silu[:, u % 2, :], ps_up[u % 2][:, :],
                                                ALU.mult).then_inc(s_gated, 1)
                        dve.wait_ge(s_gated, c * (units - n_shared) + u - n_shared + 1)
                        nc.vector.tensor_tensor(hidden[:, u % 2, :], gated[:, u % 2, :], ps_comb[u % 2][:, :],
                                                ALU.mult).then_inc(s_hidden, 1)
                dve.wait_ge(s_down, 1 + (c + 1) * units)
                nc.vector.tensor_tensor(sh.x[:, tiles(c), :], sh.x[:, tiles(c), :], ps_y[:, :, :],
                                        ALU.add).then_inc(s_x, 1)


def ternary_ffn(sh, stage, hid=512):
    nc, w, tag = sh.nc, sh.w(stage), f"s{stage}"
    n = hid // P
    with ExitStack() as ctx:
        sb = lambda m, shape, dt=F32: ctx.enter_context(nc.sbuf_tensor(f"{tag}_{m}", shape, dt))
        sem = lambda m: sh.sem(f"{tag}_{m}")
        bank = lambda m, shape=(P, S): ctx.enter_context(nc.psum_tensor(f"{tag}_{m}", list(shape), F32))
        ps_a = [bank(f"a{i}") for i in range(2)]
        ps_b = [bank(f"b{i}") for i in range(2)]
        ps_y = [bank(f"y{i}", (P, TPC, D)) for i in range(2)]
        ps_t = [bank(f"t{i}") for i in range(2)]
        ln = LayerNorm(sh, ctx, tag, ps_t)
        silu = sb("silu", [P, 2, S])
        h0 = sb("h0", [P, n, S])
        h1 = sb("h1", [P, n, S])
        h2 = sb("h2", [P, n, S])
        w3s = sb("w3_scaled", [P, n, D])
        s_w3 = sem("w3_scaled_done")
        s_up, s_silu, s_h0 = sem("gate_up_ready"), sem("silu_ready"), sem("h0_ready")
        s_p1, s_h1, s_p2, s_h2 = sem("h1_summed"), sem("h1_ready"), sem("h2_summed"), sem("h2_ready")
        s_y, s_x = sem("y_summed"), sem("x_updated")
        block = ctx.enter_context(nc.Block())

        @block.sync
        def _(sp):
            sh.load_next(sp, stage)

        @block.gpsimd
        def _(pool):
            ln.gpsimd(pool)

        @block.tensor
        def _(pe):
            pe.sem_inc(s_p1, 1)
            pe.sem_inc(s_y, 1)
            pe.wait_ge(sh.wsem[stage], 16)
            ln.tensor(pe)
            pe.wait_ge(ln.ready, B)
            pe.wait_ge(s_w3, n)
            with pe.Fori(0, B) as c:
                for f in range(n):
                    pe.wait_ge(s_h0, 1 + c * n + (f - 1 if f else 0))
                    nc.tensor.matmul(ps_a[f % 2][:, :], w["w1"][:, f * P:(f + 1) * P], sh.xnT[:, cols(c)],
                                     start=True, stop=True)
                    nc.tensor.matmul(ps_b[f % 2][:, :], w["w2"][:, f * P:(f + 1) * P], sh.xnT[:, cols(c)],
                                     start=True, stop=True).then_inc(s_up, 1)
                for name, src, s_src, first, ps, s_free, s_done in (("h1", h0, s_h0, 1, ps_a, s_h1, s_p1),
                                                                    ("h2", h1, s_h1, 0, ps_b, s_h2, s_p2)):
                    wt = w[name].rearrange("p (k o) -> p k o", k=n)
                    for f in range(n):
                        if f < 2:
                            pe.wait_ge(s_h0, 1 + (c + 1) * n)
                        else:
                            pe.wait_ge(s_free, c * n + f - 1)
                        for k in range(n):
                            if f == 0:
                                pe.wait_ge(s_src, first + c * n + k + 1)
                            last = nc.tensor.matmul(ps[f % 2][:, :], wt[:, k, f * P:(f + 1) * P], src[:, k, :],
                                                    start=(k == 0), stop=(k == n - 1))
                        last.then_inc(s_done, 1)
                pe.wait_ge(s_x, 1 + c)
                for k in range(n):
                    pe.wait_ge(s_h2, c * n + k + 1)
                    for i in range(TPC):
                        last = nc.tensor.matmul(ps_y[0][:, i, :], h2[:, k, i * P:(i + 1) * P], w3s[:, k, :],
                                                start=(k == 0 and i == 0), stop=(k == n - 1),
                                                skip_group_check=True)
                last.then_inc(s_y, 1)

        @block.scalar
        def _(act):
            ln.scalar(act)
            act.wait_ge(sh.wsem[stage], 16)
            with act.Fori(0, B) as c:
                for f in range(n):
                    act.wait_ge(s_up, c * n + f + 1)
                    nc.scalar.activation(silu[:, f % 2, :], ps_a[f % 2][:, :], ACT.Silu,
                                         scale=w["w1_s"][:, f:f + 1]).then_inc(s_silu, 1)
                for s_sum, first, ps, out, scale, s_out in ((s_p1, 1, ps_a, h1, w["h1_s"], s_h1),
                                                            (s_p2, 0, ps_b, h2, w["h2_s"], s_h2)):
                    for f in range(n):
                        act.wait_ge(s_sum, first + c * n + f + 1)
                        if s_out is s_h2 and f == 0:
                            act.wait_ge(s_y, 1 + c)
                        nc.scalar.activation(out[:, f, :], ps[f % 2][:, :], ACT.Gelu,
                                             scale=scale[:, f:f + 1]).then_inc(s_out, 1)

        @block.vector
        def _(dve):
            dve.sem_inc(s_h0, 1)
            dve.sem_inc(s_x, 1)
            dve.wait_ge(sh.wsem[stage], 16)
            for k in range(n):
                nc.vector.tensor_tensor(w3s[:, k, :], w["w3"][:, k * D:(k + 1) * D], w["w3_s"],
                                        ALU.mult).then_inc(s_w3, 1)
            ln.vector(dve)
            with dve.Fori(0, B) as c:
                for f in range(n):
                    dve.wait_ge(s_silu, c * n + f + 1)
                    if f == 0:
                        dve.wait_ge(s_p1, 1 + c * n)
                    nc.vector.scalar_tensor_tensor(out=h0[:, f, :], in0=ps_b[f % 2][:, :],
                                                   scalar=w["w2_s"][:, f:f + 1], in1=silu[:, f % 2, :],
                                                   op0=ALU.mult, op1=ALU.mult).then_inc(s_h0, 1)
                dve.wait_ge(s_y, 1 + c + 1)
                nc.vector.tensor_tensor(sh.x[:, tiles(c), :], sh.x[:, tiles(c), :], ps_y[0][:, :, :],
                                        ALU.add).then_inc(s_x, 1)


QUADS = H8 // 4


def causal_plan(q):
    per_bank = {0: 4, 1: 2, 2: 1, 3: 1}
    first = lambda d: [("max", d, n, i, 4 * (d % QUADS) + h, per_bank[i]) for n, (i, h) in
                       enumerate((i, h) for i in range(TPC) for h in range(0, 4, per_bank[i]))]
    fetch = lambda c: [("q", c), ("k", c), ("split", c)]
    if q == -2:
        return fetch(0) + first(0)
    if q == -1:
        return fetch(1) + first(1) + [("maxsplit", 0), ("maxT", 0)]
    c, g = divmod(q, QUADS)
    units = first(q + 2) if q + 2 < B * QUADS else []
    plan = []
    for r in range(5):
        plan += units[2 * r:2 * r + 1]
        if c < B:
            plan.append(("exp", q, r))
        plan += units[2 * r + 1:2 * r + 2] + units[10:] * (r == 4)
        if r in (0, 1) and q + 1 < B * QUADS:
            plan.append(("maxT" if r else "maxsplit", q + 1))
        if r == 1 and q:
            plan.append(("pv", q - 1))
        if r == 2 and g == 0 and c < B:
            plan.append(("v", c))
        if r == 3 and q:
            plan.append(("turn", q - 1))
        if r == 4 and g == 0 and q:
            plan.append(("oT", c - 1))
            if c == B:
                plan.append(("y", c - 1))
        if r == 0 and g == 1 and c:
            plan.append(("y", c - 1))
        if g == 2 and r >= 2 and c + 2 < B:
            plan.append(fetch(c + 2)[r - 2])
    return plan


def causal_attention(sh, stage, ctx, ln, pa, p1, p2, po, pm, wq, wk, wv, wo, qk_bias, v_bias, o_bias, scale,
                     before_scalar, before_vector, before_tensor, before_gpsimd, hs=None, extra=None):
    nc, tag = sh.nc, f"s{stage}"
    W = 3 * HD8
    R = 9 * HD8
    sb = lambda m, shape, dt=F32: ctx.enter_context(nc.sbuf_tensor(f"{tag}_{m}", shape, dt))
    sem = lambda m: sh.sem(f"{tag}_{m}")
    qkf = sb("qk_f32", [P, 2, S])
    parts = sb("qk_parts", [P, 3, 2, S], BF16)
    rest = sb("qk_rest", [P, 2, S])
    qs = sb("q_stack", [R + 3, 2, H8, S], BF16)
    ks = sb("k_stack", [P, 2, H8, S], BF16)
    v32 = sb("v_and_one", [P, TPC, H8, 32])
    mask_qk = sb("mask_qk", [P, P], BF16)
    mask_kq = sb("mask_kq", [P, P], BF16)
    negmax = sb("negmax", [P, TPC, H8])
    mparts = sb("max_parts", [P, QUADS, TPC, 3, 4], BF16)
    mrest = sb("max_rest", [P, 2, TPC, H8])
    mT = sb("maxT", [3 * 4, S], BF16)
    pb = sb("probs_b", [P, 2, 4, 256])
    oq = sb("o_quad", [P, S])
    recip = sb("recip", [P, TPC, 4])
    o = sb("o", [P, TPC, D])
    oT = ln.xn[:, 0, :, :].rearrange("p i d -> p (i d)")
    s_mask, s_ones = sem("masks_made"), sem("ones_made")
    s_q, s_qf = sem("qk_projected"), sem("qk_in_sbuf")
    s_v, s_v32 = sem("v_projected"), sem("v_in_sbuf")
    s_split, s_wrote = sem("qk_split_steps"), sem("qk_parts_stored")
    s_stack = [sem(f"stack_loaded{i}") for i in range(2)]
    s_max, s_neg, s_msplit = sem("scores_for_max"), sem("max_done"), sem("max_split_steps")
    s_maxT, s_mT, s_mwrote = sem("max_transposed"), sem("maxT_in_sbuf"), sem("maxT_stored")
    s_mrow = [sem(f"max_rows_loaded{i}") for i in range(2)]
    s_split0 = sem("first_qk_split_steps")
    s_sc, s_exp, s_pv = sem("scores_less_max"), sem("probs_ready"), sem("pv_done")
    s_oq, s_turn = sem("o_quad_in_sbuf"), sem("o_quad_transposed")
    s_rec, s_norm = sem("recip_done"), sem("o_normalised")
    s_oT, s_oTs, s_y, s_x = sem("o_transposed"), sem("oT_in_sbuf"), sem("y_ready"), sem("x_updated")
    s_bias = sem("o_bias_added")
    s_used = sem("misc_bank_free")
    UNITS = 11
    EXPS = 5
    plan = [item for q in range(-2, B * QUADS + 1) for item in causal_plan(q)]
    fills = {}
    for item in plan:
        if item[0] in ("q", "k", "maxT", "v", "turn", "oT", "y"):
            fills[item] = len(fills)
    block = ctx.enter_context(nc.Block())

    @block.sync
    def _(sp):
        if extra:
            sp.dma_start(extra[0], extra[1]).then_inc(extra[2], 16)
        sh.load_next(sp, stage)

        def store(c):
            if c:
                sp.wait_ge(s_split, 5 * c)
            else:
                sp.wait_ge(s_split0, 5)
            for qk in range(2):
                for k in range(3):
                    sp.dma_start(sh.scratch_qk[c, qk, :, k], parts[:, k, qk, :]).then_inc(s_wrote, 16)

        def stack(c):
            b = c % 2
            sp.wait_ge(s_wrote, 16 * 6 * (c + 1))
            if c >= 2:
                sp.wait_ge(s_sc, EXPS * QUADS * (c - 1))
            rows = lambda qk, k0, k1: sh.scratch_qk[c, qk, :, k0:k1].rearrange("h k d n -> (k d) h n")
            for a in range(3):
                sp.dma_start(ks[a * W:(a + 1) * W, b, :, :], rows(1, 0, 3)).then_inc(s_stack[b], 16)
                n = 3 - a
                sp.dma_start(qs[a * W:a * W + n * HD8, b, :, :], rows(0, a, 3)).then_inc(s_stack[b], 16)
                if a:
                    sp.dma_start(qs[a * W + n * HD8:(a + 1) * W, b, :, :], rows(0, 0, a)).then_inc(s_stack[b], 16)

        def max_rows(q):
            c, g = divmod(q, QUADS)
            sp.wait_ge(s_mT, q + 1)
            sp.dma_start(sh.scratch_max[c, 12 * g:12 * g + 12], mT[:, :]).then_inc(s_mwrote, 16)
            sp.wait_ge(s_mwrote, 16 * (q + 1))
            sp.dma_start(qs[R:R + 3, c % 2, 4 * g:4 * g + 4, :],
                         sh.scratch_max[c, 12 * g:12 * g + 12].rearrange("(k h) n -> k h n", k=3)).then_inc(s_mrow[q % 2], 16)

        sp.wait_ge(s_ones, 1)
        store(0)
        stack(0)
        for q in range(B * QUADS):
            max_rows(q)
            c, g = divmod(q, QUADS)
            if g == 1 and c < B - 1:
                store(c + 1)
                stack(c + 1)

    @block.gpsimd
    def _(pool):
        nc.gpsimd.memset(ks[64:96, :, :, :], 1.0).then_inc(s_ones, 1)
        pool.wait_ge(s_ones, 1)
        nc.gpsimd.memset(v32[:, :, :, HD8:32], 0.0).then_inc(s_ones, 1)
        pool.wait_ge(s_ones, 2)
        nc.gpsimd.memset(v32[:, :, :, HD8:HD8 + 1], 1.0).then_inc(s_ones, 1)
        nc.gpsimd.memset(mask_qk[:, :], 0.0).then_inc(s_mask, 1)
        nc.gpsimd.memset(mask_kq[:, :], 0.0).then_inc(s_mask, 1)
        pool.wait_ge(s_mask, 2)
        nc.gpsimd.affine_select(out=mask_qk[:, :], in_=mask_qk[:, :], compare_op=ALU.is_ge, fill=NEG,
                                base=0, pattern=[[-1, P]], channel_multiplier=1).then_inc(s_mask, 1)
        nc.gpsimd.affine_select(out=mask_kq[:, :], in_=mask_kq[:, :], compare_op=ALU.is_ge, fill=NEG,
                                base=0, pattern=[[1, P]], channel_multiplier=-1).then_inc(s_mask, 1)
        before_gpsimd(pool)

        resid = sh.x if hs is None else hs
        pool.wait_ge(ln.s_xn, NT)
        for c in range(B):
            ts = slice(c * TPC, (c + 1) * TPC)
            nc.gpsimd.tensor_tensor(resid[:, ts, :], resid[:, ts, :],
                                    o_bias.unsqueeze(1).broadcast_to([P, TPC, D]), ALU.add).then_inc(s_bias, 1)
        for c in range(1, B):
            if c >= 2:
                pool.wait_ge(s_wrote, 16 * 6 * c)
            else:
                pool.wait_ge(s_split0, 5)
                pool.wait_ge(s_wrote, 16 * 6)
            pool.wait_ge(s_qf, 2 * (c + 1))
            st = Steps(pool, s_split, 5 * (c - 1), 5)
            split3(nc.gpsimd, st, [parts[:, k] for k in range(3)], qkf[:, :, :], [rest[:, :, :], qkf[:, :, :]])
            st.end()
        if hs is not None:
            for c in range(B):
                ts = slice(c * TPC, (c + 1) * TPC)
                pool.wait_ge(s_x, c + 1)
                nc.gpsimd.tensor_tensor(sh.x[:, ts, :], sh.x[:, ts, :], hs[:, ts, :], ALU.add)

    @block.tensor
    def _(pe):
        pe.wait_ge(sh.wsem[stage], 16)
        before_tensor(pe)
        ln.tensor(pe)
        pe.wait_ge(ln.ready, B)
        pe.wait_ge(s_mask, 4)
        pe.wait_ge(s_ones, 3)

        def project(c, name):
            pe.wait_ge(s_used, fills[name, c]) if fills[name, c] else None
            x = sh.xnT[:, c * S:(c + 1) * S]
            if name == "v":
                for i in range(TPC):
                    last = nc.tensor.matmul(pm[:, i * P:(i + 1) * P], x[:, i * P:(i + 1) * P], wv,
                                            start=True, stop=True)
                last.then_inc(s_v, 1)
            else:
                nc.tensor.matmul(pm[:, :], wq if name == "q" else wk, x, start=True, stop=True).then_inc(s_q, 1)

        def scores_for_max(q, k, i, h0, n):
            c = q // QUADS
            k += UNITS * q
            if k >= 2:
                pe.wait_ge(s_neg, k - 1)
            m = (i + 1) * P
            for x in range(n):
                out = p1[k % 2][:, x * m:(x + 1) * m]
                nc.tensor.matmul(out, qs[0:R, c % 2, h0 + x, i * P:(i + 1) * P], ks[0:R, c % 2, h0 + x, 0:m],
                                 start=True, stop=False)
                last = nc.tensor.matmul(out[:, i * P:m], sh.identb[:, :], mask_qk[:, :], start=False, stop=True)
            last.then_inc(s_max, 1)

        def scores_less_max(q, r):
            c, g = divmod(q, QUADS)
            n = EXPS * q + r
            if n >= 2:
                pe.wait_ge(s_exp, n - 1)
            ps = p2[n % 2]
            blocks = [(0, 0, 4 * g + r), (1, 512, 4 * g + r), (3, 896, 4 * g + r)] if r < 4 else \
                     [(2, 256 * x, 4 * g + x) for x in range(4)]
            for j, at, h in blocks:
                n = S - j * P
                nc.tensor.matmul(ps[:, at:at + n], ks[0:R + 3, c % 2, h, j * P:(j + 1) * P],
                                 qs[0:R + 3, c % 2, h, j * P:S], start=True, stop=False)
                last = nc.tensor.matmul(ps[:, at:at + P], sh.identb[:, :], mask_kq[:, :], start=False, stop=True)
            last.then_inc(s_sc, 1)

        def values(q):
            c, g = divmod(q, QUADS)
            pe.wait_ge(s_exp, EXPS * (q + 1))
            if g == 0:
                pe.wait_ge(s_v32, c + 1)
            if q:
                pe.wait_ge(s_oq, q)
            for j in range(TPC):
                at, n = {0: 0, 1: 512, 3: 896}.get(j), S - j * P
                for x in range(4):
                    prob = pb[:, q % 2, x, :] if j == 2 else pa[:, q % 2, x, at:at + n]
                    last = nc.tensor.matmul(po[32 * x:32 * x + 32, j * P:S], v32[:, j, 4 * g + x, :], prob,
                                            start=(j == 0), stop=(j == TPC - 1), skip_group_check=True)
            last.then_inc(s_pv, 1)

        def turn(q):
            pe.wait_ge(s_oq, q + 1)
            pe.wait_ge(s_used, fills["turn", q])
            for i in range(TPC):
                last = nc.tensor.transpose(pm[:, i * P:(i + 1) * P], oq[:, i * P:(i + 1) * P], sh.ident[:, :])
            last.then_inc(s_turn, 1)

        def max_transposes(q):
            pe.wait_ge(s_msplit, 5 * (q + 1))
            pe.wait_ge(s_used, fills["maxT", q])
            out = pm[:, 0:S // 2].bitcast(BF16)
            for i in range(TPC):
                last = nc.tensor.transpose(out[0:12, i * P:(i + 1) * P],
                                           mparts[:, q % QUADS, i, :, :].rearrange("p k h -> p (k h)"), sh.identb[:, :])
            last.then_inc(s_maxT, 1)

        def turn_out(c):
            pe.wait_ge(s_norm, 4 * (c + 1))
            pe.wait_ge(s_used, fills["oT", c])
            for i in range(TPC):
                last = nc.tensor.transpose(pm[:, i * P:(i + 1) * P], o[:, i, :], sh.ident[:, :])
            last.then_inc(s_oT, 1)

        def project_out(c):
            pe.wait_ge(s_used, fills["y", c])
            for i in range(TPC):
                last = nc.tensor.matmul(pm[:, i * P:(i + 1) * P], oT[:, i * P:(i + 1) * P], wo, start=True, stop=True)
            last.then_inc(s_y, 1)

        for item in plan:
            if item[0] in ("q", "k", "v"):
                project(item[1], item[0])
            elif item[0] == "max":
                c, g = divmod(item[1], QUADS)
                if g == 0 and item[2] == 0:
                    pe.wait_ge(s_stack[c % 2], 16 * 8 * (c // 2 + 1))
                scores_for_max(*item[1:])
            elif item[0] == "maxT":
                max_transposes(item[1])
            elif item[0] == "exp":
                if item[2] == 0:
                    pe.wait_ge(s_mrow[item[1] % 2], 16 * (item[1] // 2 + 1))
                scores_less_max(*item[1:])
            elif item[0] == "pv":
                values(item[1])
            elif item[0] == "turn":
                turn(item[1])
            elif item[0] == "oT":
                turn_out(item[1])
            elif item[0] == "y":
                project_out(item[1])

    @block.scalar
    def _(act):
        before_scalar(act)
        ln.scalar(act)
        for item in plan:
            if item[0] in ("q", "k"):
                d, k = item[1], "qk".index(item[0])
                if d == 1:
                    act.wait_ge(s_split0, 5)
                elif d:
                    act.wait_ge(s_split, 5 * (d - 1))
                act.wait_ge(s_q, 2 * d + k + 1)
                nc.scalar.activation(qkf[:, k, :], pm[:, :], ACT.Identity,
                                     bias=qk_bias[k] if qk_bias else 0.0).then_inc(s_qf, 1)
                act.wait_ge(s_qf, 2 * d + k + 1)
                act.sem_inc(s_used, 1)
            elif item[0] == "maxT":
                q = item[1]
                act.wait_ge(s_maxT, q + 1)
                if q:
                    act.wait_ge(s_mwrote, 16 * q)
                nc.scalar.copy(mT[:, :], pm[0:12, 0:S // 2].bitcast(BF16)).then_inc(s_mT, 1)
                act.wait_ge(s_mT, q + 1)
                act.sem_inc(s_used, 1)
            elif item[0] == "exp":
                _, q, r = item
                n = EXPS * q + r
                act.wait_ge(s_sc, n + 1)
                if r == 0 and q >= 2:
                    act.wait_ge(s_pv, q - 1)
                out = pa[:, q % 2, r, :] if r < 4 else pb[:, q % 2, :, :].rearrange("p x n -> p (x n)")
                nc.scalar.activation(out, p2[n % 2][:, :], ACT.Exp, scale=scale).then_inc(s_exp, 1)
            elif item[0] == "pv":
                q = item[1]
                act.wait_ge(s_pv, q + 1)
                if q:
                    act.wait_ge(s_turn, q)
                nc.scalar.copy(oq[:, :], po[:, :]).then_inc(s_oq, 1)
            elif item[0] == "oT":
                act.wait_ge(s_oT, item[1] + 1)
                nc.scalar.copy(oT, pm[:, :]).then_inc(s_oTs, 1)
                act.wait_ge(s_oTs, item[1] + 1)
                act.sem_inc(s_used, 1)

    @block.vector
    def _(dve):
        before_vector(dve)
        ln.vector(dve)
        resid = sh.x if hs is None else hs
        for item in plan:
            if item[0] == "v":
                c = item[1]
                dve.wait_ge(s_v, c + 1)
                if c == 0:
                    dve.wait_ge(s_ones, 3)
                else:
                    dve.wait_ge(s_pv, 4 * c)
                for i in range(TPC):
                    last = nc.vector.tensor_tensor(v32[:, i, :, 0:HD8],
                                                   pm[:, i * P:(i + 1) * P].rearrange("p (h d) -> p h d", h=H8),
                                                   v_bias.rearrange("p (h d) -> p h d", h=H8), ALU.add)
                last.then_inc(s_v32, 1)
                dve.wait_ge(s_v32, c + 1)
                dve.sem_inc(s_used, 1)
            elif item == ("split", 0):
                dve.wait_ge(s_qf, 2)
                st = Steps(dve, s_split0, 0, 5)
                split3(nc.vector, st, [parts[:, k] for k in range(3)], qkf[:, :, :],
                       [rest[:, :, :], qkf[:, :, :]])
                st.end()
            elif item[0] == "max":
                _, q, k, i, h0, n = item
                k += UNITS * q
                m = (i + 1) * P
                dve.wait_ge(s_max, k + 1)
                nc.vector.tensor_reduce(negmax[:, i, h0:h0 + n],
                                        p1[k % 2][:, 0:n * m].rearrange("p (n m) -> p n m", n=n),
                                        AX.X, ALU.max, negate=True).then_inc(s_neg, 1)
            elif item[0] == "maxsplit":
                q = item[1]
                g = q % QUADS
                dve.wait_ge(s_neg, UNITS * (q + 1))
                if q >= QUADS:
                    dve.wait_ge(s_maxT, q - QUADS + 1)
                st = Steps(dve, s_msplit, 5 * q, 5)
                split3(nc.vector, st, [mparts[:, g, :, k, :] for k in range(3)], negmax[:, :, 4 * g:4 * g + 4],
                       [mrest[:, k, :, 4 * g:4 * g + 4] for k in range(2)])
                st.end()
            elif item[0] == "turn":
                q = item[1]
                c, g = divmod(q, QUADS)
                quad = pm[:, :].rearrange("p (t x d) -> p t x d", t=TPC, x=4)
                dve.wait_ge(s_turn, q + 1)
                nc.vector.reciprocal(recip[:, :, :], quad[:, :, :, HD8]).then_inc(s_rec, 1)
                dve.wait_ge(s_rec, q + 1)
                if g == 0 and c >= 1:
                    dve.wait_ge(s_oT, c)
                nc.vector.tensor_tensor(
                    o[:, :, 32 * g:32 * g + 32].rearrange("p t (x d) -> p t x d", x=4), quad[:, :, :, 0:HD8],
                    recip[:, :, :].unsqueeze(3).broadcast_to([P, TPC, 4, HD8]), ALU.mult).then_inc(s_norm, 1)
                dve.wait_ge(s_norm, q + 1)
                dve.sem_inc(s_used, 1)
            elif item[0] == "y":
                d = item[1]
                dve.wait_ge(s_y, d + 1)
                dve.wait_ge(s_bias, d + 1)
                ts = slice(d * TPC, (d + 1) * TPC)
                nc.vector.tensor_tensor(resid[:, ts, :], resid[:, ts, :],
                                        pm[:, :].rearrange("p (t d) -> p t d", t=TPC), ALU.add).then_inc(s_x, 1)
                dve.wait_ge(s_x, d + 1)
                dve.sem_inc(s_used, 1)


def low_rank_attention(sh, stage):
    nc, w, tag = sh.nc, sh.w(stage), f"s{stage}"
    R = 64
    with ExitStack() as ctx:
        bank = lambda m, shape=(P, S): ctx.enter_context(nc.psum_tensor(f"{tag}_{m}", list(shape), F32))
        p1 = [bank(f"for_max{i}") for i in range(2)]
        p2 = [bank(f"scores{i}", (P, 1024)) for i in range(2)]
        po, pm = bank("pv"), bank("odd_jobs")
        weff = ctx.enter_context(nc.sbuf_tensor(f"{tag}_weff", [P, 2, D], F32))
        s_prod, s_weff = (sh.sem(f"{tag}_{m}") for m in ("factors_multiplied", "weff_ready"))
        ln = LayerNorm(sh, ctx, tag, p1)
        pa = ctx.enter_context(nc.sbuf_tensor(f"{tag}_probs_a", [P, 2, 4, 1024], F32))

        def factors_tensor(pe):
            for k in range(2):
                rows = slice(k * R, (k + 1) * R)
                for h in range(H8):
                    last = nc.tensor.matmul(p2[k][:, h * HD8:(h + 1) * HD8],
                                            w["a"][rows, h * D:(h + 1) * D], w["b"][rows, h * HD8:(h + 1) * HD8],
                                            start=True, stop=True)
                last.then_inc(s_prod, 1)
            pe.wait_ge(s_weff, 2)

        def factors_scalar(act):
            for k in range(2):
                act.wait_ge(s_prod, k + 1)
                nc.scalar.copy(weff[:, k, :], p2[k][:, 0:D]).then_inc(s_weff, 1)

        def weights_vector(dve):
            dve.wait_ge(sh.wsem[stage], 16)

        def weights_gpsimd(pool):
            ln.gpsimd(pool)
            pool.wait_ge(sh.wsem[stage], 16)

        causal_attention(sh, stage, ctx, ln, pa, p1, p2, po, pm, weff[:, 0, :], weff[:, 1, :], w["v"], w["o"], None,
                         w["v_b"], w["o_b"], HD8 ** -0.5, factors_scalar, weights_vector, factors_tensor,
                         weights_gpsimd)


L2_SEGMENTS = [("ca_w", 3 * D), ("cp_w", D), ("cf_w", 512), ("cm_w", 512), ("ca_b", 2 + D), ("cp_b", D),
               ("cf_b", 4), ("cm_b", D)]


def generated_attention(sh, stage):
    nc, w, tag = sh.nc, sh.w(stage), f"s{stage}"
    width = sum(n for _, n in L2_SEGMENTS)
    with ExitStack() as ctx:
        bank = lambda m, shape=(P, S): ctx.enter_context(nc.psum_tensor(f"{tag}_{m}", list(shape), F32))
        sem = lambda m: sh.sem(f"{tag}_{m}")
        p1 = [bank(f"for_max{i}") for i in range(2)]
        p2 = [bank(f"scores{i}", (P, 1024)) for i in range(2)]
        po, pm = bank("pv"), bank("odd_jobs")
        s_mix, s_tanh, s_gen = sem("subs_mixed"), sem("tanh_done"), sem("params_steps")
        n = len(L2_SEGMENTS)
        outer = LayerNorm(sh, ctx, tag + "a", keep=sh.hs)
        ln = LayerNorm(sh, ctx, tag, p1, src=sh.hs, affine=(w["ln1_g"], w["ln1_b"]))
        gen = sh.gen(w)
        pa = ctx.enter_context(nc.sbuf_tensor(f"{tag}_probs_a", [P, 2, 4, 1024], F32))
        s_extra = sem("generators_loaded")
        flat = pa[:, :, :, :].rearrange("p a x n -> p (a x n)")
        sub1, W, bias = (flat[:, k * width:(k + 1) * width] for k in range(3))

        def params_vector(dve):
            dve.wait_ge(sh.wsem[stage], 16)
            outer.vector(dve)
            dve.wait_ge(outer.s_xn, NT)
            dve.wait_ge(s_extra, 16)
            at = 0
            for k, (name, m) in enumerate(L2_SEGMENTS):
                c = slice(at, at + m)
                nc.vector.tensor_scalar(w["sub0"][:, c], w["sub0"][:, c], w["a"][:, 2 * k:2 * k + 1], None,
                                        ALU.mult).then_inc(s_mix, 1)
                dve.wait_ge(s_mix, 2 * k + 1)
                nc.vector.scalar_tensor_tensor(out=w["sub0"][:, c], in0=sub1[:, c],
                                               scalar=w["a"][:, 2 * k + 1:2 * k + 2], in1=w["sub0"][:, c],
                                               op0=ALU.mult, op1=ALU.add).then_inc(s_mix, 1)
                at += m
            dve.wait_ge(s_tanh, 1)
            nc.vector.tensor_tensor(w["sub0"], w["sub0"], W, ALU.mult).then_inc(s_gen, 1)
            dve.wait_ge(s_gen, 1)
            nc.vector.tensor_tensor(w["sub0"], w["sub0"], bias, ALU.add).then_inc(s_gen, 1)

        def tanh_scalar(act):
            act.wait_ge(s_mix, 2 * n)
            nc.scalar.activation(w["sub0"], w["sub0"], ACT.Tanh).then_inc(s_tanh, 1)
            act.wait_ge(s_gen, 2)

        def wait_tensor(pe):
            pe.wait_ge(s_gen, 2)

        def norms_gpsimd(pool):
            pool.wait_ge(sh.wsem[stage], 16)
            outer.gpsimd(pool)
            ln.gpsimd(pool)
            pool.wait_ge(s_gen, 2)

        ca, cab = gen["ca_w"], gen["ca_b"]
        causal_attention(sh, stage, ctx, ln, pa, p1, p2, po, pm, ca[:, 0:D], ca[:, D:2 * D], ca[:, 2 * D:3 * D],
                         gen["cp_w"], (cab[:, 0:1], cab[:, 1:2]), cab[:, 2:2 + D], gen["cp_b"], HD8 ** -0.5,
                         tanh_scalar, params_vector, wait_tensor, norms_gpsimd, hs=sh.hs,
                         extra=(flat[:, 0:3 * width], sh.extra[stage], s_extra))


def generated_mlp(sh, stage, hid=512):
    nc, w, tag = sh.nc, sh.w(stage), f"s{stage}b"
    n = hid // P
    gen = sh.gen(w)
    with ExitStack() as ctx:
        sb = lambda m, shape, dt=F32: ctx.enter_context(nc.sbuf_tensor(f"{tag}_{m}", shape, dt))
        sem = lambda m: sh.sem(f"{tag}_{m}")
        bank = lambda m, shape=(P, S): ctx.enter_context(nc.psum_tensor(f"{tag}_{m}", list(shape), F32))
        ps_h = [bank(f"h{i}") for i in range(4)]
        ps_y = [bank(f"y{i}", (P, TPC, D)) for i in range(2)]
        ps_t = [bank(f"t{i}") for i in range(2)]
        ln = LayerNorm(sh, ctx, tag, ps_t, src=sh.hs, affine=(w["ln2_g"], w["ln2_b"]))
        h = sb("h", [P, 4, S])
        s_h, s_gelu, s_y, s_x, s_bias = (sem("h_summed"), sem("h_ready"), sem("y_summed"), sem("x_updated"),
                                         sem("bias_added"))
        block = ctx.enter_context(nc.Block())

        @block.gpsimd
        def _(pool):
            ln.gpsimd(pool)
            for c in range(B):
                ts = slice(c * TPC, (c + 1) * TPC)
                nc.gpsimd.tensor_tensor(sh.x[:, ts, :], sh.x[:, ts, :],
                                        gen["cm_b"].unsqueeze(1).broadcast_to([P, TPC, D]), ALU.add).then_inc(s_bias, 1)

        @block.tensor
        def _(pe):
            pe.sem_inc(s_y, 1)
            ln.tensor(pe)
            pe.wait_ge(ln.ready, B)
            with pe.Fori(0, B) as c:
                for f in range(n):
                    pe.wait_ge(s_gelu, 1 + c * n + f)
                    nc.tensor.matmul(ps_h[f][:, :], gen["cf_w"][:, f * P:(f + 1) * P], sh.xnT[:, cols(c)],
                                     start=True, stop=True).then_inc(s_h, 1)
                pe.wait_ge(s_x, 1 + c)
                for k in range(n):
                    pe.wait_ge(s_gelu, 4 + c * n + k + 1)
                    for i in range(TPC):
                        last = nc.tensor.matmul(ps_y[0][:, i, :], h[:, k, i * P:(i + 1) * P],
                                                gen["cm_w"][:, k * D:(k + 1) * D], start=(k == 0 and i == 0),
                                                stop=(k == n - 1), skip_group_check=True)
                last.then_inc(s_y, 1)

        @block.scalar
        def _(act):
            act.sem_inc(s_gelu, 4)
            ln.scalar(act)
            with act.Fori(0, B) as c:
                for f in range(n):
                    act.wait_ge(s_h, c * n + f + 1)
                    if f == 0:
                        act.wait_ge(s_y, 1 + c)
                    nc.scalar.activation(h[:, f, :], ps_h[f][:, :], ACT.Gelu_apprx_tanh,
                                         bias=gen["cf_b"][:, f:f + 1]).then_inc(s_gelu, 1)

        @block.vector
        def _(dve):
            dve.sem_inc(s_x, 1)
            ln.vector(dve)
            dve.wait_ge(s_bias, B)
            with dve.Fori(0, B) as c:
                dve.wait_ge(s_y, 1 + c + 1)
                nc.vector.tensor_tensor(sh.x[:, tiles(c), :], sh.x[:, tiles(c), :], ps_y[0][:, :, :],
                                        ALU.add).then_inc(s_x, 1)


def generated_block(sh, stage):
    nc = sh.nc
    with ExitStack() as ctx:
        sh.hs = ctx.enter_context(nc.sbuf_tensor("hs", [P, NT, D], F32))
        generated_attention(sh, stage)
        generated_mlp(sh, stage)


def full_start():
    plan = [("xc", 0)]
    plan += [("proj", n, x, k) for n in range(2) for x in range(2) for k in range(2)]
    plan += [("max", 0, x, j) for x in range(2) for j in range(TPC)]
    return plan + [("v", -1, u) for u in range(2 * TPC)] + [("maxT", 0, 0)]


def full_sequence(pairs, more):
    plan = []
    for s in range(pairs):
        if s == pairs - 2 and more:
            plan.append(("xc", 1))
        for u in range(2 * TPC):
            x, j = divmod(u, TPC)
            plan.append(("exp", s, x, j))
            if s + 1 < pairs or more:
                plan.append(("max", s + 1, x, j))
            if u < 4 and (s + 2 < pairs or more):
                plan.append(("proj", s + 2) + divmod(u, 2))
            if u == 1:
                plan.append(("maxT", s, 1))
            if u == 6 and (s + 1 < pairs or more):
                plan.append(("maxT", s + 1, 0))
            if u == 3 and s:
                plan.append(("sum", s - 1))
            if u >= 4 and s:
                plan.append(("pv", s - 1, u - 4))
                plan.append(("recip", s - 1, u - 4))
            if u == 0 and s > 1:
                plan.append(("norm", s - 2))
    plan.append(("norm", pairs - 2))
    plan += [("pv", pairs - 1, j) for j in range(TPC)]
    v = [("v", 0, u) for u in range(2 * TPC)] if more else []
    plan += v[:TPC] + [("sum", pairs - 1)] + [("recip", pairs - 1, j) for j in range(TPC)] + v[TPC:]
    return plan + [("norm", pairs - 1), ("out",)]


def full_attention(sh, stage, heads=16, dh=64):
    nc, w, tag = sh.nc, sh.w(stage), f"s{stage}"
    PAIRS, NV = heads // 2, 2 * TPC
    TILES = 2 * TPC
    SLOTS = 4
    F32R = mybir.dt.float32r
    with ExitStack() as ctx:
        sb = lambda m, shape, dt=F32: ctx.enter_context(nc.sbuf_tensor(f"{tag}_{m}", shape, dt))
        sem = lambda m: sh.sem(f"{tag}_{m}")
        bank = lambda m: ctx.enter_context(nc.psum_tensor(f"{tag}_{m}", [P, S], F32))
        pj = [bank(f"odd_jobs{i}") for i in range(2)]
        p1 = [bank(f"for_max{i}") for i in range(2)]
        p2 = [bank(f"scores{i}") for i in range(2)]
        po, psm = bank("pv"), bank("sums")
        ln = LayerNorm(sh, ctx, tag, p1)
        qq = sb("q_hi_hi", [P, SLOTS, 2, S], F32R)
        q2 = sb("q_lo_max", [dh + 2, SLOTS, 2, S], F32R)
        kk = sb("k_hi_lo", [P, SLOTS, 2, S], F32R)
        k2 = sb("k_hi_one", [P, SLOTS, 2, S], F32R)
        ones = sb("ones", [P, dh])
        v = sb("v", [P, TPC, heads * dh])
        xc = sb("xnT_of_sequence", [P, S])
        negmax = sb("negmax", [P, 2, TPC])
        mparts = sb("max_parts", [P, 2, TPC, 2], BF16)
        probs = sb("probs", [P, 2, 2, TPC, S])
        added = sb("probs_added", [P, 2, S])
        acc = sb("probs_sum", [P, 2, 2, S])
        bo = sb("bo", [P, D])
        recip = sb("recip", [P, S])
        oT = sh.spare(ctx, f"{tag}_oT", stage, heads // 2 * S).rearrange("p (k n) -> p k n", n=S)
        s_one = sem("ones_made")
        s_proj, s_hi, s_lo, s_k2 = sem("qk_projected"), sem("hi_done"), sem("lo_done"), sem("k2_done")
        s_v, s_vs = sem("v_projected"), sem("v_in_sbuf")
        s_free = [sem(f"odd_bank_free{i}") for i in range(2)]
        s_max, s_neg, s_split = sem("scores_for_max"), sem("max_done"), sem("max_split_steps")
        s_maxT, s_mrow = sem("max_transposed"), sem("max_rows_ready")
        s_sc, s_exp, s_pv = sem("scores_less_max"), sem("probs_ready"), sem("pv_done")
        s_added, s_acc, s_sum = sem("probs_added_up"), sem("probs_sum_ready"), sem("sums_ready")
        s_rec, s_norm, s_y, s_x = sem("recip_done"), sem("o_normalised"), sem("y_summed"), sem("x_updated")
        s_bias, s_xc, s_bvo, s_bo = sem("o_bias_added"), sem("xc_copied"), sem("bv_projected"), sem("bo_ready")
        start, middle, end = full_start(), full_sequence(PAIRS, True), full_sequence(PAIRS, False)
        odd = lambda plan: [item for item in plan if item[0] in ("proj", "maxT", "v")]
        FILLS = len(odd(middle))
        assert FILLS % 2 == 0 and PAIRS % SLOTS == 0
        fills = {}
        for item in odd(start) + odd(middle):
            fills[item] = len(fills)
        late = {item: len(odd(start)) + n for n, item in enumerate(odd(end))}
        block = ctx.enter_context(nc.Block())
        EXP0, PV0, ACC0, X0 = 2, 2, 4, 1

        def run(eng, emit):
            for item in start:
                emit(0, item, fills)
            with eng.Fori(0, B - 1) as c:
                for item in middle:
                    emit(c, item, fills)
            for item in end:
                emit(B - 1, item, late)

        def freed(eng, n):
            eng.sem_inc(s_free[n % 2], 1)

        @block.sync
        def _(sp):
            sh.load_next(sp, stage)

        @block.gpsimd
        def _(pool):
            pool.sem_inc(s_acc, ACC0)
            nc.gpsimd.memset(ones[:, :], 1.0).then_inc(s_one, 1)
            pool.wait_ge(s_one, 1)
            nc.gpsimd.memset(k2[dh:P, :, :, :].bitcast(F32), 1.0).then_inc(s_one, 1)
            pool.wait_ge(s_one, 2)
            pool.wait_ge(sh.wsem[stage], 16)
            ln.gpsimd(pool)
            pool.wait_ge(ln.s_xn, NT)
            pool.wait_ge(s_bo, 1)
            for c in range(B):
                ts = slice(c * TPC, (c + 1) * TPC)
                nc.gpsimd.tensor_tensor(sh.x[:, ts, :], sh.x[:, ts, :],
                                        bo[:, :].unsqueeze(1).broadcast_to([P, TPC, D]), ALU.add).then_inc(s_bias, 1)

            def emit(c, item, fills):
                if item[0] == "exp" and item[3] == TPC - 1:
                    _, n, x, j = item
                    h = 2 * n + x
                    pool.wait_ge(s_acc, c * heads + h + ACC0)
                    pool.wait_ge(s_exp, c * (heads * TPC) + TPC * (h + 1) + EXP0)
                    nc.gpsimd.tensor_tensor(added[:, :, :], probs[:, n % 2, x, 0:2, :], probs[:, n % 2, x, 2:4, :],
                                            ALU.add).then_inc(s_added, 1)
                    pool.wait_ge(s_added, c * heads + h + 1)
                    nc.gpsimd.tensor_tensor(acc[:, n % 2, x, :], added[:, 0, :], added[:, 1, :],
                                            ALU.add).then_inc(s_acc, 1)
            run(pool, emit)

        @block.tensor
        def _(pe):
            pe.sem_inc(s_pv, PV0)
            pe.wait_ge(sh.wsem[stage], 16)
            ln.tensor(pe)
            pe.wait_ge(ln.ready, B)
            pe.wait_ge(s_one, 2)
            for k in range(PAIRS):
                last = nc.tensor.matmul(psm[:, 0:D], w["bv"][:, k:k + 1].broadcast_to([P, P]),
                                        w["wo"][:, k * D:(k + 1) * D], start=(k == 0), stop=(k == PAIRS - 1))
            last.then_inc(s_bvo, 1)
            pe.wait_ge(s_bo, 1)

            def odd_bank(c, item, fills):
                k = fills[item]
                if k >= 2:
                    pe.wait_ge(s_free[k % 2], c * (FILLS // 2) + k // 2)
                return pj[k % 2]

            def emit(c, item, fills):
                what = item[0]
                if what == "proj":
                    _, n, x, k = item
                    h = (2 * n + x) % heads
                    ps = odd_bank(c, item, fills)
                    if (n, x, k) in ((0, 0, 0), (PAIRS, 0, 0)):
                        pe.wait_ge(s_xc, c + 1 + (n > 0))
                    for rows in (slice(0, dh), slice(dh, P)):
                        last = nc.tensor.matmul(ps[rows, :], w["w" + "qk"[k]][:, h * dh:(h + 1) * dh], xc[:, :],
                                                start=True, stop=True)
                    last.then_inc(s_proj, 1)
                elif what == "v":
                    i, half = divmod(item[2], 2)
                    ps = odd_bank(c, item, fills)
                    nc.tensor.matmul(ps[:, :], xc[:, i * P:(i + 1) * P], w["wv"][:, half * S:(half + 1) * S],
                                     start=True, stop=True).then_inc(s_v, 1)
                elif what == "max":
                    _, n, x, j = item
                    m = TILES * n + TPC * x + j
                    if j == 0:
                        pe.wait_ge(s_hi, c * (2 * heads) + 4 * n + 2 * x + 2)
                    if m >= 2:
                        pe.wait_ge(s_neg, c * (heads * TPC) + m - 1)
                    nc.tensor.matmul(p1[m % 2][:, :], qq[0:dh, n % SLOTS, x, j * P:(j + 1) * P],
                                     kk[0:dh, n % SLOTS, x, :], start=True, stop=True).then_inc(s_max, 1)
                elif what == "maxT":
                    _, n, x = item
                    ps = odd_bank(c, item, fills)
                    pe.wait_ge(s_split, c * (2 * heads) + 2 * (2 * n + x) + 2)
                    for i in range(TPC):
                        last = nc.tensor.matmul(ps[dh:dh + 2, i * P:(i + 1) * P], mparts[:, x, i, :], sh.identb[:, :],
                                                start=True, stop=True)
                    last.then_inc(s_maxT, 1)
                elif what == "exp":
                    _, n, x, j = item
                    m, slot = TILES * n + TPC * x + j, n % SLOTS
                    if j == 0:
                        pe.wait_ge(s_lo, c * (2 * heads) + 4 * n + 2 * x + 2)
                        pe.wait_ge(s_k2, c * heads + 2 * n + x + 1)
                        pe.wait_ge(s_mrow, c * heads + 2 * n + x + 1)
                    pe.wait_ge(s_exp, c * (heads * TPC) + m - 1 + EXP0)
                    nc.tensor.matmul(p2[m % 2][:, :], kk[:, slot, x, j * P:(j + 1) * P], qq[:, slot, x, :],
                                     start=True, stop=False)
                    nc.tensor.matmul(p2[m % 2][:, :], k2[0:dh + 2, slot, x, j * P:(j + 1) * P], q2[:, slot, x, :],
                                     start=False, stop=True).then_inc(s_sc, 1)
                elif what == "pv":
                    _, n, j = item
                    pe.wait_ge(s_exp, c * (heads * TPC) + TILES * n + TPC + j + 1 + EXP0)
                    if j == 0 and n == 0:
                        pe.wait_ge(s_vs, c * NV + NV)
                        pe.wait_ge(s_x, c + X0)
                    elif j == 0:
                        pe.wait_ge(s_norm, c * PAIRS + n)
                    for x in range(2):
                        last = nc.tensor.matmul(po[x * dh:(x + 1) * dh, :], v[:, j, (2 * n + x) * dh:(2 * n + x + 1) * dh],
                                                probs[:, n % 2, x, j, :], start=(j == 0), stop=(j == TPC - 1))
                    if j == TPC - 1:
                        last.then_inc(s_pv, 1)
                elif what == "sum":
                    n = item[1]
                    pe.wait_ge(s_acc, c * heads + 2 * (n + 1) + ACC0)
                    if n:
                        pe.wait_ge(s_rec, c * (PAIRS * TPC) + n * TPC)
                    for x in range(2):
                        last = nc.tensor.matmul(psm[x * dh:(x + 1) * dh, :], ones[:, :], acc[:, n % 2, x, :],
                                                start=True, stop=True)
                    last.then_inc(s_sum, 1)
                elif what == "out":
                    pe.wait_ge(s_norm, c * PAIRS + PAIRS)
                    for p in range(PAIRS):
                        for i in range(TPC):
                            last = nc.tensor.matmul(po[:, i * P:(i + 1) * P], oT[:, p, i * P:(i + 1) * P],
                                                    w["wo"][:, p * D:(p + 1) * D], start=(p == 0 and i == 0),
                                                    stop=(p == PAIRS - 1), skip_group_check=True)
                    last.then_inc(s_y, 1)
            run(pe, emit)

        @block.scalar
        def _(act):
            act.sem_inc(s_exp, EXP0)
            act.wait_ge(sh.wsem[stage], 16)
            ln.scalar(act)
            act.wait_ge(ln.ready, B)

            def emit(c, item, fills):
                what = item[0]
                if what == "xc":
                    if item[1]:
                        act.wait_ge(s_proj, c * (2 * heads) + 2 * heads)
                    nc.scalar.copy(xc[:, :], sh.xnT[:, bass.ds(c * S + item[1] * S, S)]).then_inc(s_xc, 1)
                elif what == "proj":
                    _, n, x, k = item
                    h, slot = (2 * n + x) % heads, n % SLOTS
                    ps, bias = pj[fills[item] % 2], w["b" + "qk"[k]]
                    act.wait_ge(s_proj, c * (2 * heads) + 4 * n + 2 * x + k + 1)
                    if k:
                        nc.scalar.activation(k2[0:dh, slot, x, :], ps[0:dh, :], ACT.Identity,
                                             bias=bias[0:dh, h:h + 1]).then_inc(s_k2, 1)
                    nc.scalar.activation((kk if k else qq)[:, slot, x, :], ps[:, :], ACT.Identity,
                                         bias=bias[:, h:h + 1]).then_inc(s_hi, 1)
                elif what == "maxT":
                    _, n, x = item
                    act.wait_ge(s_maxT, c * heads + 2 * n + x + 1)
                    nc.scalar.copy(q2[dh:dh + 2, n % SLOTS, x, :], pj[fills[item] % 2][dh:dh + 2, :]).then_inc(s_mrow, 1)
                    act.wait_ge(s_mrow, c * heads + 2 * n + x + 1)
                    freed(act, fills[item])
                elif what == "v":
                    _, nxt, u = item
                    i, half = divmod(u, 2)
                    t = (nxt + 1) * NV + u + 1
                    act.wait_ge(s_v, c * NV + t)
                    if nxt == 0 and u == 0:
                        act.wait_ge(s_pv, c * PAIRS + PAIRS + PV0)
                    nc.scalar.copy(v[:, i, half * S:(half + 1) * S], pj[fills[item] % 2][:, :]).then_inc(s_vs, 1)
                    act.wait_ge(s_vs, c * NV + t)
                    freed(act, fills[item])
                elif what == "exp":
                    _, n, x, j = item
                    m = TILES * n + TPC * x + j
                    act.wait_ge(s_sc, c * (heads * TPC) + m + 1)
                    if x == 0 and j == 0:
                        act.wait_ge(s_pv, c * PAIRS + n - 1 + PV0)
                        act.wait_ge(s_acc, c * heads + 2 * (n - 1) + ACC0)
                    nc.scalar.activation(probs[:, n % 2, x, j, :], p2[m % 2][:, :], ACT.Exp,
                                         scale=dh ** -0.5).then_inc(s_exp, 1)
            run(act, emit)

        @block.vector
        def _(dve):
            dve.sem_inc(s_x, X0)
            dve.wait_ge(sh.wsem[stage], 16)
            ln.vector(dve)
            dve.wait_ge(s_bvo, 1)
            nc.vector.tensor_tensor(bo[:, :], psm[:, 0:D], w["bo"], ALU.add).then_inc(s_bo, 1)

            def emit(c, item, fills):
                what = item[0]
                if what == "proj":
                    _, n, x, k = item
                    h, slot = (2 * n + x) % heads, n % SLOTS
                    m = 4 * n + 2 * x + k
                    ps, bias = pj[fills[item] % 2], w["b" + "qk"[k]]
                    dve.wait_ge(s_hi, c * (2 * heads) + m + 1)
                    rows, hi = (slice(dh, P), kk) if k else (slice(0, dh), qq)
                    nc.vector.scalar_tensor_tensor(out=(kk if k else q2)[rows, slot, x, :], in0=ps[rows, :],
                                                   scalar=bias[rows, h:h + 1], in1=hi[rows, slot, x, :].bitcast(F32),
                                                   op0=ALU.add, op1=ALU.subtract).then_inc(s_lo, 1)
                    dve.wait_ge(s_lo, c * (2 * heads) + m + 1)
                    freed(dve, fills[item])
                elif what == "max":
                    _, n, x, j = item
                    m, h = TILES * n + TPC * x + j, 2 * n + x
                    if j == 0 and n:
                        dve.wait_ge(s_split, c * (2 * heads) + 2 * (h - 2) + 2)
                    dve.wait_ge(s_max, c * (heads * TPC) + m + 1)
                    nc.vector.tensor_reduce(negmax[:, x, j:j + 1], p1[m % 2][:, :], AX.X, ALU.max,
                                            negate=True).then_inc(s_neg, 1)
                    if j == TPC - 1:
                        dve.wait_ge(s_neg, c * (heads * TPC) + m + 1)
                        if n:
                            dve.wait_ge(s_maxT, c * heads + h - 1)
                        nc.vector.tensor_copy(mparts[:, x, :, 0], negmax[:, x, :]).then_inc(s_split, 1)
                        dve.wait_ge(s_split, c * (2 * heads) + 2 * h + 1)
                        nc.vector.tensor_tensor(mparts[:, x, :, 1], negmax[:, x, :], mparts[:, x, :, 0],
                                                ALU.subtract).then_inc(s_split, 1)
                elif what == "recip":
                    _, n, j = item
                    at = slice(j * P, (j + 1) * P)
                    dve.wait_ge(s_sum, c * PAIRS + n + 1)
                    if n:
                        dve.wait_ge(s_norm, c * PAIRS + n)
                    nc.vector.reciprocal(recip[:, at], psm[:, at]).then_inc(s_rec, 1)
                elif what == "norm":
                    n = item[1]
                    dve.wait_ge(s_pv, c * PAIRS + n + 1 + PV0)
                    dve.wait_ge(s_rec, c * (PAIRS * TPC) + (n + 1) * TPC)
                    nc.vector.tensor_tensor(oT[:, n, :], po[:, :], recip[:, :], ALU.mult).then_inc(s_norm, 1)
                elif what == "out":
                    dve.wait_ge(s_y, c + 1)
                    dve.wait_ge(s_bias, B)
                    nc.vector.tensor_tensor(sh.x[:, tiles(c), :], sh.x[:, tiles(c), :],
                                            po[:, :].rearrange("p (t d) -> p t d", t=TPC), ALU.add).then_inc(s_x, 1)
            run(dve, emit)


def dispatched_ffn(sh, stage, n_exp=8, hid=512, top=2):
    nc, w, tag = sh.nc, sh.w(stage), f"s{stage}"
    cap = top * (-(-T // n_exp))
    slots = n_exp * cap
    U = top * NT
    n_up, n_slot = hid // P, cap // P
    assert cap == S
    GROUP = 4
    with ExitStack() as ctx:
        sb = lambda m, shape, dt=F32: ctx.enter_context(nc.sbuf_tensor(f"{tag}_{m}", shape, dt))
        sem = lambda m: sh.sem(f"{tag}_{m}")
        bank = lambda m: ctx.enter_context(nc.psum_tensor(f"{tag}_{m}", [P, S], F32))
        ps_t = [bank(f"turned{i}") for i in range(2)]
        ps_up = [bank(f"up{i}") for i in range(2)]
        ps_y = [bank(f"y{i}") for i in range(2)]
        ps_route, ps_count = bank("route"), bank("count")
        disp = nc.dram_tensor("dispatched", [slots + top * T, D], F32, kind="Internal").ap()
        outs = nc.dram_tensor("expert_rows", [slots, D], F32, kind="Internal").ap()
        xn = sb("xn", [P, NT, D])
        ln = LayerNorm(sh, ctx, tag, ps_t, keep=xn)
        zeros = sb("zeros", [P, 2 * S])
        tri = sb("tri", [P, P], BF16)
        ones = sb("ones", [P, P], BF16)
        before = sb("before", [P, n_exp, n_exp])
        base = sb("slot_base", [P, n_exp])
        spare_i = sb("spare_int", [P, U], mybir.dt.int32)
        spare = sb("spare", [P, U])
        probs = sb("probs", [P, NT, n_exp])
        stat = sb("stat", [P, NT])
        rank = sb("rank", [P, NT, n_exp])
        gt = sb("gt", [P, NT, n_exp, n_exp])
        eq = sb("eq", [P, NT, n_exp, n_exp])
        chosen = sb("chosen", [P, U, n_exp], BF16)
        picked = sb("picked", [P, U, n_exp])
        gate = sb("gate", [P, U])
        total = sb("gate_sum", [P, NT])
        upto = sb("counts_up_to", [P, 2, NT + U, n_exp])
        loc = sb("loc", [P, U])
        first = sb("first_slot", [P, U])
        valid = sb("valid", [P, U])
        where = sb("where", [P, 2, U])
        idx = sb("idx", [P, 2, U], U32)
        rows = sb("rows", [P, 2, n_slot, D])
        rowsT = sb("rowsT", [P, 2, S])
        hidden = sb("hidden", [P, 2, n_up, S])
        y = sb("y", [P, 2, n_slot, D])
        back = sb("back", [P, U, D])
        w1, w2 = sb("w1", [P, n_exp * hid]), sb("w2", [P, n_exp * hid])
        b2 = sb("b2", [P, n_exp * D])
        s_w1, s_w2 = sem("w1_loaded"), sem("w2_b2_loaded")
        s_const, s_zero, s_zeroed = sem("constants_made"), sem("zeros_made"), sem("slots_cleared")
        s_before, s_base = sem("before_made"), sem("base_made")
        s_logits, s_less, s_exp, s_chosen, s_count = (sem("logits_ready"), sem("logits_less_max"), sem("exp_done"),
                                                      sem("choices_ready"), sem("counts_ready"))
        s_route, s_idx = sem("route_steps"), sem("idx_ready")
        s_put, s_rows, s_turn, s_rowsT = sem("rows_put"), [sem(f"rows_loaded{i}") for i in range(2)], sem("rows_transposed"), sem("rowsT_ready")
        s_up, s_hidden, s_down, s_y = sem("up_done"), sem("hidden_ready"), sem("down_done"), sem("y_ready")
        s_out, s_x = [sem(f"y_stored{i}") for i in range(2)], sem("x_steps")
        s_back = [sem(f"rows_back{i}") for i in range(U // GROUP)]
        block = ctx.enter_context(nc.Block())

        @block.sync
        def _(sp):
            sh.load_next(sp, stage)
            n = n_exp * hid
            sp.dma_start(w1[:, :], sh.extra[stage][:, 0:n]).then_inc(s_w1, 16)
            sp.dma_start(w2[:, :], sh.extra[stage][:, n:2 * n]).then_inc(s_w2, 16)
            sp.dma_start(b2[:, :], sh.extra[stage][:, 2 * n:]).then_inc(s_w2, 16)
            sp.wait_ge(s_zero, 1)
            n = slots * D // (P * 2 * S)
            for k in range(n):
                sp.dma_start(disp[k * slots // n:(k + 1) * slots // n].rearrange("(p r) d -> p (r d)", p=P),
                             zeros[:, :]).then_inc(s_zeroed, 16)
            sp.wait_ge(s_put, 16 * U)
            for e in range(n_exp + 2):
                if e < n_exp:
                    if e >= 2:
                        sp.wait_ge(s_turn, e - 1)
                    sp.dma_start(rows[:, e % 2, :, :], disp[e * cap:(e + 1) * cap].rearrange(
                        "(t p) d -> p t d", p=P)).then_inc(s_rows[e % 2], 16)
                if e >= 2:
                    sp.wait_ge(s_y, e - 1)
                    sp.dma_start(outs[(e - 2) * cap:(e - 1) * cap].rearrange("(t p) d -> p t d", p=P),
                                 y[:, e % 2, :, :]).then_inc(s_out[e % 2], 16)

        @block.gpsimd
        def _(pool):
            nc.gpsimd.memset(zeros[:, :], 0.0).then_inc(s_zero, 1)
            make_before(nc, pool, before, n_exp, s_before)
            nc.gpsimd.memset(ones[:, :], 1.0).then_inc(s_const, 1)
            nc.gpsimd.memset(tri[:, :], 1.0).then_inc(s_const, 1)
            nc.gpsimd.memset(upto[:, :, :, :], 0.0).then_inc(s_const, 1)
            nc.gpsimd.iota(spare_i[:, :], pattern=[[P, U]], base=slots, channel_multiplier=1).then_inc(s_const, 1)
            pool.wait_ge(s_const, 4)
            nc.gpsimd.affine_select(out=tri[:, :], in_=tri[:, :], compare_op=ALU.is_gt, fill=0.0, base=0,
                                    pattern=[[1, P]], channel_multiplier=-1).then_inc(s_const, 1)
            ln.gpsimd(pool)
            pool.wait_ge(s_idx, 1)
            pool.wait_ge(s_zeroed, 16 * (slots * D // (P * 2 * S)))
            for u in range(U):
                nc.gpsimd.indirect_dma_start(disp, bass.IndirectOffsetOnAxis(ap=idx[:, 0, u:u + 1], axis=0),
                                             xn[:, u % NT, :], None).then_inc(s_put, 16)
            for half in s_out:
                pool.wait_ge(half, 16 * n_exp // 2)
            for u in range(U):
                nc.gpsimd.indirect_dma_start(back[:, u, :], None, outs,
                                             bass.IndirectOffsetOnAxis(ap=idx[:, 1, u:u + 1], axis=0)).then_inc(s_back[u // GROUP], 16)

        @block.tensor
        def _(pe):
            pe.wait_ge(sh.wsem[stage], 16)
            ln.tensor(pe)
            pe.wait_ge(ln.ready, B)
            logits = ps_route[:, 0:NT * n_exp].rearrange("p (t e) -> p t e", t=NT)
            for t in range(NT):
                last = nc.tensor.matmul(logits[:, t, :], sh.xnT[:, t * P:(t + 1) * P], w["wg"],
                                        start=True, stop=True)
            last.then_inc(s_logits, 1)
            pe.wait_ge(s_const, 5)
            pe.wait_ge(s_chosen, 1)
            flat = chosen[:, :, :].rearrange("p u e -> p (u e)")
            nc.tensor.matmul(ps_count[:, 0:U * n_exp], tri[:, :], flat, start=True, stop=True)
            nc.tensor.matmul(ps_count[:, U * n_exp:], ones[:, :], flat, start=True, stop=True).then_inc(s_count, 1)

            def turn(e):
                pe.wait_ge(s_rows[e % 2], 16 * (e // 2 + 1))
                if e >= 2:
                    pe.wait_ge(s_rowsT, e - 1)
                for i in range(n_slot):
                    last = nc.tensor.transpose(ps_t[e % 2][:, i * P:(i + 1) * P], rows[:, e % 2, i, :], sh.ident[:, :])
                last.then_inc(s_turn, 1)

            def up(e):
                pe.wait_ge(s_rowsT, e + 1)
                for f in range(n_up):
                    m = e * n_up + f
                    if m >= 2:
                        pe.wait_ge(s_hidden, m - 1)
                    nc.tensor.matmul(ps_up[m % 2][:, :], w1[:, m * P:(m + 1) * P], rowsT[:, e % 2, :],
                                     start=True, stop=True).then_inc(s_up, 1)

            def down(e):
                pe.wait_ge(s_hidden, (e + 1) * n_up)
                if e >= 2:
                    pe.wait_ge(s_y, e - 1)
                for i in range(n_slot):
                    for f in range(n_up):
                        m = e * n_up + f
                        last = nc.tensor.matmul(ps_y[e % 2][:, i * P:(i + 1) * P], hidden[:, e % 2, f, i * P:(i + 1) * P],
                                                w2[:, m * D:(m + 1) * D], start=(f == 0 and i == 0),
                                                stop=(f == n_up - 1), skip_group_check=True)
                last.then_inc(s_down, 1)

            turn(0)
            pe.wait_ge(s_w1, 16)
            pe.wait_ge(s_w2, 32)
            for e in range(n_exp):
                up(e)
                if e + 1 < n_exp:
                    turn(e + 1)
                if e >= 1:
                    down(e - 1)
            down(n_exp - 1)

        @block.scalar
        def _(act):
            act.wait_ge(sh.wsem[stage], 16)
            ln.scalar(act)
            act.wait_ge(s_less, 1)
            nc.scalar.activation(probs[:, :, :], probs[:, :, :], ACT.Exp).then_inc(s_exp, 1)
            for e in range(n_exp):
                act.wait_ge(s_turn, e + 1)
                if e >= 2:
                    act.wait_ge(s_up, (e - 1) * n_up)
                nc.scalar.copy(rowsT[:, e % 2, :], ps_t[e % 2][:, :]).then_inc(s_rowsT, 1)
                for f in range(n_up):
                    m = e * n_up + f
                    act.wait_ge(s_up, m + 1)
                    if e >= 2 and f == 0:
                        act.wait_ge(s_down, e - 1)
                    nc.scalar.activation(hidden[:, e % 2, f, :], ps_up[m % 2][:, :], ACT.Relu,
                                         bias=w["b1"][:, m:m + 1]).then_inc(s_hidden, 1)

        @block.vector
        def _(dve):
            for e in range(n_exp):
                last = nc.vector.memset(base[:, e:e + 1], float(e * cap))
            last.then_inc(s_base, 1)
            ln.vector(dve)
            st = Steps(dve, s_route, 0, ROUTE_DISPATCH_STEPS)
            logits = ps_route[:, 0:NT * n_exp].rearrange("p (t e) -> p t e", t=NT)
            wide = lambda a: a.unsqueeze(2).broadcast_to([P, a.shape[1], n_exp])
            per_e = lambda a: a.unsqueeze(1).broadcast_to([P, U, n_exp])
            twice = lambda a: a.unsqueeze(1).broadcast_to([P, top] + a.shape[1:])
            by_choice = lambda a: a.rearrange("p (k t) e -> p k t e", k=top)
            dve.wait_ge(s_logits, 1)
            st.then(nc.vector.tensor_reduce(stat[:, :], logits, AX.X, ALU.max))
            nc.vector.tensor_tensor(probs[:, :, :], logits, wide(stat[:, :]), ALU.subtract).then_inc(s_less, 1)
            dve.wait_ge(s_exp, 1)
            st.then(nc.vector.tensor_reduce(stat[:, :], probs[:, :, :], AX.X, ALU.add))
            st.then(nc.vector.reciprocal(stat[:, :], stat[:, :]))
            st.then(nc.vector.tensor_tensor(probs[:, :, :], probs[:, :, :], wide(stat[:, :]), ALU.mult))
            dve.wait_ge(s_before, 2)
            dve.wait_ge(s_base, 1)
            ranks(nc, st, rank[:, :, :], probs[:, :, :], before[:, :, :], gt[:, :, :, :], eq[:, :, :, :])
            for k in range(top):
                last = nc.vector.tensor_scalar(chosen[:, k * NT:(k + 1) * NT, :], rank[:, :, :], float(k), None,
                                               ALU.is_equal)
                st.did(last)
            st.wait()
            dve.sem_inc(s_chosen, 1)
            for k in range(top):
                st.did(nc.vector.tensor_tensor(picked[:, k * NT:(k + 1) * NT, :], chosen[:, k * NT:(k + 1) * NT, :],
                                               probs[:, :, :], ALU.mult))
            st.wait()
            st.then(nc.vector.tensor_reduce(gate[:, :], picked[:, :, :], AX.X, ALU.add))
            st.then(nc.vector.tensor_tensor(total[:, :], gate[:, 0:NT], gate[:, NT:], ALU.add))
            st.then(nc.vector.reciprocal(total[:, :], total[:, :]))
            for k in range(top):
                st.did(nc.vector.tensor_tensor(gate[:, k * NT:(k + 1) * NT], gate[:, k * NT:(k + 1) * NT], total[:, :],
                                               ALU.mult))
            dve.wait_ge(s_count, 1)
            dve.wait_ge(s_const, 3)
            counts = ps_count[:, U * n_exp:].rearrange("p (u e) -> p u e", u=U)
            within = ps_count[:, 0:U * n_exp].rearrange("p (u e) -> p u e", u=U)
            st.then(nc.vector.tensor_copy(upto[:, 0, NT:, :], counts))
            shift, k = 1, 0
            while shift < U:
                st.then(nc.vector.tensor_tensor(upto[:, 1 - k, NT:, :], upto[:, k, NT:, :],
                                                upto[:, k, NT - shift:NT + U - shift, :], ALU.add))
                shift, k = 2 * shift, 1 - k
            st.then(nc.vector.tensor_tensor(picked[:, :, :], within, upto[:, k, NT - 1:NT + U - 1, :], ALU.add))
            st.then(nc.vector.tensor_tensor(picked[:, :, :], picked[:, :, :], chosen[:, :, :], ALU.mult))
            st.then(nc.vector.tensor_reduce(loc[:, :], picked[:, :, :], AX.X, ALU.add))
            st.then(nc.vector.tensor_tensor(picked[:, :, :], chosen[:, :, :], per_e(base[:, :]), ALU.mult))
            st.then(nc.vector.tensor_reduce(first[:, :], picked[:, :, :], AX.X, ALU.add))
            st.did(nc.vector.tensor_scalar(valid[:, :], loc[:, :], cap - 0.5, None, ALU.is_lt))
            st.did(nc.vector.tensor_copy(spare[:, :], spare_i[:, :]))
            st.then(nc.vector.scalar_tensor_tensor(out=where[:, 1, :], in0=loc[:, :], scalar=cap - 1.0, in1=first[:, :],
                                                   op0=ALU.min, op1=ALU.add))
            st.did(nc.vector.tensor_tensor(gate[:, :], gate[:, :], valid[:, :], ALU.mult))
            st.then(nc.vector.tensor_tensor(where[:, 0, :], where[:, 1, :], spare[:, :], ALU.subtract))
            st.then(nc.vector.tensor_tensor(where[:, 0, :], where[:, 0, :], valid[:, :], ALU.mult))
            st.then(nc.vector.tensor_tensor(where[:, 0, :], where[:, 0, :], spare[:, :], ALU.add))
            st.end()
            nc.vector.tensor_copy(idx[:, :, :], where[:, :, :]).then_inc(s_idx, 1)
            dve.wait_ge(s_w2, 32)
            for e in range(n_exp):
                dve.wait_ge(s_down, e + 1)
                if e >= 2:
                    dve.wait_ge(s_out[e % 2], 16 * (e // 2))
                nc.vector.tensor_tensor(y[:, e % 2, :, :], ps_y[e % 2][:, :].rearrange("p (t d) -> p t d", t=n_slot),
                                        b2[:, e * D:(e + 1) * D].unsqueeze(1).broadcast_to([P, n_slot, D]),
                                        ALU.add).then_inc(s_y, 1)
            for u in range(U):
                if u % GROUP == 0:
                    dve.wait_ge(s_back[u // GROUP], 16 * GROUP)
                if u >= NT:
                    dve.wait_ge(s_x, u - NT + 1)
                nc.vector.scalar_tensor_tensor(out=sh.x[:, u % NT, :], in0=back[:, u, :], scalar=gate[:, u:u + 1],
                                               in1=sh.x[:, u % NT, :], op0=ALU.mult, op1=ALU.add).then_inc(s_x, 1)


ROUTE_DISPATCH_STEPS = 36


def program(nc, x_in, weights, extra, out):
    with ExitStack() as ctx:
        sh = Shared(nc, ctx, weights, extra)
        sem = lambda n: ctx.enter_context(nc.semaphore(n))
        s_x, s_zero, s_id, s_half, s_out = (sem("x_loaded"), sem("ident_cleared"), sem("ident_made"),
                                            sem("mhalf_made"), sem("x_stored"))
        with nc.Block() as block:
            @block.sync
            def _(sp):
                for c in range(B):
                    sp.dma_start(sh.x[:, c * TPC:(c + 1) * TPC, :],
                                 x_in[c].rearrange("(t p) d -> p t d", p=P)).then_inc(s_x, 16)
                sh.load_weights(sp, list(weights)[0])
                sp.wait_ge(s_x, 16 * B)

            @block.gpsimd
            def _(pool):
                nc.gpsimd.memset(sh.mhalf[:, :], -0.5).then_inc(s_half, 1)
                for n, m in enumerate((sh.ident, sh.identb)):
                    nc.gpsimd.memset(m[:, :], 0.0).then_inc(s_zero, 1)
                    pool.wait_ge(s_zero, n + 1)
                    nc.gpsimd.affine_select(out=m[:, :], in_=m[:, :], compare_op=ALU.not_equal, fill=1.0,
                                            base=0, pattern=[[-1, P]], channel_multiplier=1).then_inc(s_id, 1)
        for stage in weights:
            RUN[stage](sh, stage)
            sh.stage_over()
        with nc.Block() as block:
            @block.sync
            def _(sp):
                for c in range(B):
                    sp.dma_start(out[c].rearrange("(t p) d -> p t d", p=P),
                                 sh.x[:, c * TPC:(c + 1) * TPC, :]).then_inc(s_out, 16)
                sp.wait_ge(s_out, 16 * B)
        sh.old_sems.close()


RUN = {
    0: gated_linear_attention,
    1: lambda sh, s: routed_ffn(sh, s, 16, 64, 128, ACT.Sigmoid, route_groups, ROUTE_GROUPS_STEPS),
    3: lambda sh, s: routed_ffn(sh, s, 8, 256, 256, ACT.Copy, route_top1, ROUTE_TOP1_STEPS),
    2: low_rank_attention,
    4: generated_block,
    5: ternary_ffn,
    6: full_attention,
    7: dispatched_ffn,
}


def _t(a):
    import numpy as np
    return np.moveaxis(a, -1, 0).reshape(a.shape[-1], -1)


def _fold(a):
    k = a.shape[0] // P
    return a.reshape(k, P, -1).transpose(1, 0, 2).reshape(P, -1)


def _col(v):
    return v.reshape(-1, P).T


def _rows(v):
    import numpy as np
    return np.broadcast_to(v.reshape(1, -1), (P, v.size))


def _layout(stage, a):
    import numpy as np
    cat = lambda *parts: np.concatenate(parts, axis=1)
    if stage == 0:
        return [("wq", _t(a["Wq"])), ("wk", _t(a["Wk"])), ("wgk1", _t(a["Wgk1"])), ("wgk2", _t(a["Wgk2"])),
                ("wvg", cat(_t(a["Wv"]), _t(a["Wg"]))), ("wout", _fold(_t(a["Wout"]))),
                ("bgk2", _rows(a["bgk2"])), ("rms_w", _rows(a["rms_w"]))]
    if stage == 1:
        down = cat(_fold(_t(a["w2_s"])), _fold(a["w2_e"].transpose(0, 2, 1).reshape(-1, D)))
        return [("router", _t(a["w_gate"])), ("gate", cat(_t(a["w1_s"]), _t(a["w1_e"]))),
                ("up", cat(_t(a["w3_s"]), _t(a["w3_e"]))), ("down", down)]
    if stage == 2:
        factor = np.concatenate([a["q_a"].transpose(2, 0, 1).reshape(64, -1), a["k_a"].transpose(2, 0, 1).reshape(64, -1)])
        other = np.concatenate([a["q_b"].transpose(1, 0, 2).reshape(64, -1), a["k_b"].transpose(1, 0, 2).reshape(64, -1)])
        return [("a", factor), ("b", other), ("v", _t(a["v_w"])), ("o", _t(a["o_w"])), ("v_b", _rows(a["v_b"])),
                ("o_b", _rows(a["o_b"]))]
    if stage == 3:
        down = cat(_fold(_t(a["w_down_s"])), _fold(a["down"].transpose(0, 2, 1).reshape(-1, D)))
        return [("router", _t(a["router"])), ("gate", cat(_t(a["w_gate_s"]), _t(a["gate"]))),
                ("up", cat(_t(a["w_up_s"]), _t(a["up"]))), ("down", down)]
    if stage == 4:
        def column(p):
            ca_b, cf_b = a["ca_" + p + "_b"], a["cf_" + p + "_b"]
            return cat(_t(a["ca_" + p + "_w"]), _t(a["cp_" + p + "_w"]), _t(a["cf_" + p + "_w"]),
                       _fold(_t(a["cm_" + p + "_w"])), _col(ca_b[:2 * D]), _rows(ca_b[2 * D:]),
                       _rows(a["cp_" + p + "_b"]), _col(cf_b), _rows(a["cm_" + p + "_b"]))
        subs = {}
        for k in range(2):
            for m in ("ca", "cp", "cf", "cm"):
                for p in "wb":
                    subs[f"{m}_{k}_{p}"] = a[f"{m}_sub_{p}"][k]
        a = dict(a, **subs)
        mix = cat(*[_rows(a[f"{m}_Wl_{p}"]) for p in "wb" for m in ("ca", "cp", "cf", "cm")])
        return [("sub0", column("0")), ("a", mix)] + \
            [(f"ln{i}_{p}", _col(a[f"ln{i}_{p}"])) for i in (1, 2) for p in "gb"] + \
            [("extra", cat(column("1"), column("W"), column("B")))]
    if stage == 6:
        double = lambda b: np.tile(b.reshape(16, 64).T, (2, 1))
        return [("wq", _t(a["Wq"])), ("wk", _t(a["Wk"])), ("wv", _t(a["Wv"])),
                ("wo", _fold(_t(a["Wo"]))), ("bq", double(a["bq"])), ("bk", double(a["bk"])),
                ("bv", _col(a["bv"])), ("bo", _rows(a["bo"]))]
    if stage == 7:
        down = a["w2"].reshape(8, 4, P, D).transpose(2, 0, 1, 3).reshape(P, -1)
        return [("wg", a["wg"]), ("b1", a["b1"].reshape(-1, P).T),
                ("extra", cat(a["w1"].transpose(1, 0, 2).reshape(D, -1), down, _rows(a["b2"])))]
    if stage == 5:
        return [("w1", _t(a["w1_w"])), ("w2", _t(a["w2_w"])), ("h1", _fold(_t(a["h1_w"]))),
                ("h2", _fold(_t(a["h2_w"]))), ("w3", _fold(_t(a["w3_w"]))), ("w1_s", _col(a["w1_s"])),
                ("w2_s", _col(a["w2_s"])), ("h1_s", _col(a["h1_s"])), ("h2_s", _col(a["h2_s"])),
                ("w3_s", _rows(a["w3_s"]))]


_NAMES = ["L0_attn", "L0_ffn", "L1_attn", "L1_ffn", "L2_attn", "L2_ffn", "L3_attn", "L3_ffn"]


def kernel(**inputs):
    import numpy as np
    import concourse.bacc as bacc
    from concourse.bass_utils import run_bass_kernel_spmd

    nc = bacc.Bacc("TRN2", target_bir_lowering=False, num_devices=1)
    arrays, weights = {"x_in": np.ascontiguousarray(inputs["L0_attn_x"])}, {}
    x_in = nc.dram_tensor("x_in", [B, S, D], F32, kind="ExternalInput").ap()
    extra = {}
    for stage in STAGES:
        mine = {k[len(_NAMES[stage]) + 1:]: np.asarray(v) for k, v in inputs.items()
                if k.startswith(_NAMES[stage] + "_")}
        parts = _layout(stage, mine)
        if parts[-1][0] == "extra":
            late = np.ascontiguousarray(parts.pop()[1])
            arrays[f"extra{stage}"] = late
            extra[stage] = nc.dram_tensor(f"extra{stage}", list(late.shape), F32, kind="ExternalInput").ap()
        packed = np.zeros((P, sum(v.shape[1] for _, v in parts)), np.float32)
        at, table = 0, []
        for name, v in parts:
            packed[:v.shape[0], at:at + v.shape[1]] = v
            at += v.shape[1]
            table.append((name, v.shape[0], v.shape[1]))
        arrays[f"w{stage}"] = packed
        weights[stage] = (nc.dram_tensor(f"w{stage}", list(packed.shape), F32, kind="ExternalInput").ap(), table)
    out = nc.dram_tensor("out", [B, S, D], F32, kind="ExternalOutput").ap()
    program(nc, x_in, weights, extra, out)
    return run_bass_kernel_spmd(nc, [arrays], core_ids=[0]).results[0]["out"]
```

```python
from contextlib import ExitStack

import concourse.bass as bass
from concourse import mybir
import numpy as np

STAGES = (0, 1, 2, 3, 4, 5, 6, 7)

ALU = mybir.AluOpType
ACT = mybir.ActivationFunctionType
AX = mybir.AxisListType
F32 = mybir.dt.float32
F32R = mybir.dt.float32r
BF16 = mybir.dt.bfloat16
U32 = mybir.dt.uint32

P = 128
B, S, D = 4, 512, 128
TPC = S // P
NT = B * TPC
T = B * S
H8, HD8 = 16, 8
LN_EPS = 1e-5
NEG = -1.0e30


def tiles(c, n=TPC):
    return bass.ds(c * n, n)


def cols(c, n=S):
    return bass.ds(c * n, n)


class Steps:

    def __init__(self, eng, sem, base, total):
        self.eng, self.sem, self.base, self.total, self.n = eng, sem, base, total, 0

    def did(self, ins):
        self.n += 1
        ins.then_inc(self.sem, 1)
        return self.n

    def wait(self, n=None):
        self.eng.wait_ge(self.sem, self.base + (self.n if n is None else n))

    def then(self, ins):
        self.did(ins)
        self.wait()

    def end(self):
        assert self.n == self.total, (self.sem, self.n, self.total)


class Shared:

    def __init__(self, nc, ctx, weights, extra):
        self.nc, self.weights, self.extra = nc, weights, extra
        self.x = ctx.enter_context(nc.sbuf_tensor("x_resid", [P, NT, D], F32))
        self.xnT = ctx.enter_context(nc.sbuf_tensor("xnT", [P, T], F32))
        self.ident = ctx.enter_context(nc.sbuf_tensor("ident", [P, P], F32))
        self.identb = ctx.enter_context(nc.sbuf_tensor("identb", [P, P], BF16))
        self.scratch_qk = nc.dram_tensor("scratch_qk", [B, 2, H8, 3, HD8, S], BF16, kind="Internal").ap()
        self.scratch_max = nc.dram_tensor("scratch_max", [B, 3 * H8, S], BF16, kind="Internal").ap()
        self.mhalf = ctx.enter_context(nc.sbuf_tensor("mhalf", [P, NT], F32))
        self.sems, self.old_sems, self.fresh, self.stale = ExitStack(), ExitStack(), [], []
        order = list(weights.values())
        width = [max([w.shape[1] for w, _ in order[i::2]] or [1]) for i in range(2)]
        self.wbuf = [ctx.enter_context(nc.sbuf_tensor(f"wbuf{i}", [P, width[i]], F32)) for i in range(2)]
        self.wsem = {s: ctx.enter_context(nc.semaphore(f"weights_loaded_{s}")) for s in weights}

    def sem(self, name):
        s = self.sems.enter_context(self.nc.semaphore(name))
        self.fresh.append(s)
        return s

    def stage_over(self):
        self.old_sems.close()
        self.old_sems, self.sems = self.sems, ExitStack()
        self.stale, self.fresh = self.fresh, []

    def w(self, stage):
        buf = self.wbuf[list(self.weights).index(stage) % 2]
        out, at = {}, 0
        for name, rows, n in self.weights[stage][1]:
            out[name] = buf[0:rows, at:at + n]
            at += n
        return out

    def spare(self, ctx, name, stage, n):
        order = list(self.weights)
        at = order.index(stage) + 1
        used = self.weights[order[at]][0].shape[1] if at < len(order) else 0
        buf = self.wbuf[at % 2]
        if buf.shape[1] - used >= n:
            return buf[:, buf.shape[1] - n:]
        return ctx.enter_context(self.nc.sbuf_tensor(name, [P, n], F32))[:, :]

    def gen(self, w):
        out, at = {}, 0
        for name, n in L2_SEGMENTS:
            out[name] = w["sub0"][:, at:at + n]
            at += n
        return out

    def load_weights(self, eng, stage):
        buf = self.wbuf[list(self.weights).index(stage) % 2]
        src = self.weights[stage][0]
        eng.dma_start(buf[:, 0:src.shape[1]], src).then_inc(self.wsem[stage], 16)

    def load_next(self, eng, stage):
        for s in self.stale:
            eng.sem_clear(s)
        order = list(self.weights)
        at = order.index(stage) + 1
        if at < len(order):
            self.load_weights(eng, order[at])


class LayerNorm:

    def __init__(self, sh, ctx, tag, ps=None, src=None, keep=None, affine=None, split=False):
        nc = sh.nc
        self.split = split
        if split:
            self.hi, self.lo = (ctx.enter_context(nc.sbuf_tensor(f"{tag}_xnT_{m}", [P, T], F32R)) for m in ("hi", "lo"))
            self.s_hi, self.s_lo = sh.sem(f"{tag}_xnT_hi_ready"), sh.sem(f"{tag}_xnT_lo_ready")
        self.sh, self.ps, self.keep, self.affine = sh, ps, keep, affine
        self.src = sh.x if src is None else src
        sb = lambda n, shape: ctx.enter_context(nc.sbuf_tensor(f"{tag}_{n}", shape, F32))
        sem = lambda n: sh.sem(f"{tag}_{n}")
        self.stats = sb("ln_stats", [P, NT, 6])
        self.mv = sb("ln_mv", [P, NT, 2])
        self.rstd = sb("ln_rstd", [P, NT])
        self.xn = keep if keep is not None else sb("ln_xn", [P, 2, TPC, D])
        self.s_stats, self.s_mv = sem("ln_stats_done"), sem("ln_moments_done")
        self.s_eps, self.s_rstd = sem("ln_eps_added"), sem("ln_rstd_done")
        self.s_xn, self.s_T, self.ready = sem("ln_scaled"), sem("ln_transposed"), sem("xnT_ready")

    def xn_tile(self, c, i):
        return self.xn[:, c * TPC + i, :] if self.keep is not None else self.xn[:, c % 2, i, :]

    def vector(self, dve):
        nc = self.sh.nc
        for t in range(NT):
            nc.vector.bn_stats(self.stats[:, t, :], self.src[:, t, :]).then_inc(self.s_stats, 1)
            if t >= 1:
                dve.wait_ge(self.s_stats, t)
                nc.vector.bn_aggr(self.mv[:, t - 1, :], self.stats[:, t - 1, :]).then_inc(self.s_mv, 1)
        dve.wait_ge(self.s_stats, NT)
        nc.vector.bn_aggr(self.mv[:, NT - 1, :], self.stats[:, NT - 1, :]).then_inc(self.s_mv, 1)
        for t in range(NT):
            c, i = divmod(t, TPC)
            if i == 0:
                dve.wait_ge(self.s_rstd, c + 1)
                if c >= 2 and self.keep is None:
                    dve.wait_ge(self.s_T, c - 1)
            nc.vector.tensor_scalar(self.xn_tile(c, i), self.src[:, t, :], self.mv[:, t, 0:1],
                                    self.rstd[:, t:t + 1], ALU.subtract, ALU.mult).then_inc(self.s_xn, 1)

    def low_parts(self, dve):
        for c in range(B):
            cs = slice(c * S, (c + 1) * S)
            dve.wait_ge(self.ready, c + 1)
            dve.wait_ge(self.s_hi, c + 1)
            self.sh.nc.vector.tensor_tensor(self.lo[:, cs], self.sh.xnT[:, cs], self.hi[:, cs].bitcast(F32),
                                            ALU.subtract).then_inc(self.s_lo, 1)

    def gpsimd(self, pool, between=None):
        nc = self.sh.nc
        for c in range(B):
            ts = slice(c * TPC, (c + 1) * TPC)
            if between:
                between(c)
            pool.wait_ge(self.s_mv, (c + 1) * TPC)
            nc.gpsimd.tensor_scalar(self.rstd[:, ts], self.mv[:, ts, 1], LN_EPS, 1.0,
                                    ALU.add, ALU.mult).then_inc(self.s_eps, 1)
            pool.wait_ge(self.s_eps, c + 1)
            nc.gpsimd.tensor_tensor(self.rstd[:, ts], self.rstd[:, ts], self.sh.mhalf[:, ts],
                                    ALU.pow).then_inc(self.s_rstd, 1)

    def tensor(self, pe):
        nc = self.sh.nc
        for c in range(B):
            if c >= 2:
                pe.wait_ge(self.ready, c - 1)
            for i in range(TPC):
                pe.wait_ge(self.s_xn, c * TPC + i + 1)
                last = nc.tensor.transpose(self.ps[c % 2][:, i * P:(i + 1) * P], self.xn_tile(c, i),
                                           self.sh.ident[:, :])
            last.then_inc(self.s_T, 1)

    def scalar(self, act):
        nc = self.sh.nc
        for c in range(B):
            act.wait_ge(self.s_T, c + 1)
            dst, ps = self.sh.xnT[:, c * S:(c + 1) * S], self.ps[c % 2][:, :]
            if self.split:
                nc.scalar.copy(self.hi[:, c * S:(c + 1) * S], ps).then_inc(self.s_hi, 1)
            if self.affine:
                last = nc.scalar.activation(dst, ps, ACT.Identity, bias=self.affine[1], scale=self.affine[0])
            else:
                last = nc.scalar.copy(dst, ps)
            last.then_inc(self.ready, 1)


class SplitWeights:

    def __init__(self, sh, ctx, tag, pieces):
        self.nc, self.tag, self.pieces, self.parts = sh.nc, tag, pieces, []
        for n, piece in enumerate(pieces):
            self.parts.append([ctx.enter_context(sh.nc.sbuf_tensor(f"{tag}_w{n}_{m}", [P, piece.shape[1]], F32R))
                               for m in ("hi", "lo")])
        self.s_hi, self.s_lo = sh.sem(f"{tag}_w_hi_ready"), sh.sem(f"{tag}_w_lo_ready")

    def scalar(self):
        for n, piece in enumerate(self.pieces):
            self.nc.scalar.copy(self.parts[n][0][:, :], piece).then_inc(self.s_hi, 1)

    def gpsimd(self, pool, which):
        for n in which:
            pool.wait_ge(self.s_hi, n + 1)
            self.nc.gpsimd.tensor_tensor(self.parts[n][1][:, :], self.pieces[n], self.parts[n][0][:, :].bitcast(F32),
                                         ALU.subtract).then_inc(self.s_lo, 1)


def ranks(nc, st, rank, s, before, gt, eq, parts=(0, 1, 2)):
    n, e = s.shape[1], s.shape[2]
    mine = s.unsqueeze(3).broadcast_to([P, n, e, e])
    other = s.unsqueeze(2).broadcast_to([P, n, e, e])
    if 0 in parts:
        st.did(nc.vector.tensor_tensor(gt, other, mine, ALU.is_gt))
    if 1 in parts:
        st.then(nc.vector.tensor_tensor(eq, other, mine, ALU.is_equal))
        st.then(nc.vector.tensor_tensor(eq, eq, before.unsqueeze(1).broadcast_to([P, n, e, e]), ALU.mult))
    if 2 in parts:
        st.then(nc.vector.tensor_tensor(gt, gt, eq, ALU.add))
        st.then(nc.vector.tensor_reduce(rank, gt, AX.X, ALU.add))


def make_before(nc, pool, before, e, sem):
    nc.gpsimd.memset(before[:, :, :], 1.0).then_inc(sem, 1)
    pool.wait_ge(sem, 1)
    nc.gpsimd.affine_select(out=before[:, :, :], in_=before[:, :, :], compare_op=ALU.is_gt, fill=0.0,
                            base=0, pattern=[[1, e], [-1, e]], channel_multiplier=0).then_inc(sem, 1)


def split3(ops, st, parts, src, rest):
    st.then(ops.tensor_copy(parts[0], src))
    st.then(ops.tensor_tensor(rest[0], src, parts[0], ALU.subtract))
    st.then(ops.tensor_copy(parts[1], rest[0]))
    st.then(ops.tensor_tensor(rest[1], rest[0], parts[1], ALU.subtract))
    st.then(ops.tensor_copy(parts[2], rest[1]))


GLA_LEVELS = (64, 32, 16, 8, 4, 2, 1)


def gated_linear_attention(sh, stage, heads=4, dk=32, dv=64, rank=32, gate_norm=32.0, rms_eps=1e-5):
    nc, w, tag = sh.nc, sh.w(stage), f"s{stage}"
    E, W = heads * dv, P // TPC
    NL = len(GLA_LEVELS)
    F_LAST, F_ALL = NL, NL + 1
    IN_STEPS, OUT_STEPS = 14, 14
    MUL, ADD, SUB = ALU.mult, ALU.add, ALU.subtract
    with ExitStack() as ctx:
        sb = lambda m, shape, dt=F32: ctx.enter_context(nc.sbuf_tensor(f"{tag}_{m}", shape, dt))
        sem = lambda m: sh.sem(f"{tag}_{m}")
        bank = lambda m, n=1: ctx.enter_context(nc.psum_tensor(f"{tag}_{m}", [P, n, S], F32))
        odd = [bank(f"odd_jobs{i}")[:, 0, :] for i in range(2)]
        ps_a, ps_o = bank("pair_products", heads), bank("o", 2)
        ln = LayerNorm(sh, ctx, tag, odd)
        xc = sb("xnT_of_sequence", [P, S])
        qT, kT, gk = sb("qT", [P, S]), sb("kT", [P, S]), sb("gk", [rank, S])
        z, soft, g = sb("z", [P, S]), sb("softplus", [P, S]), sb("log_decay", [P, S])
        v, gate = sb("v", [P, TPC, E]), sb("gate", [P, TPC, E])
        b = sb("decay_sums", [P, S])
        expo, fac = sb("exponents", [P, NL + 2, S]), sb("factors", [P, NL + 2, S])
        zkq = sb("scaled_kq", [P, NL + 2, S])
        near = sb("near_pairs", [P, heads, TPC, W])
        pairs = sb("pairs", [P, heads, TPC, P])
        kdec = sb("k_to_end", [P, TPC, P])
        state = sb("state", [P, E])
        sq, ss, rrms = sb("o_squared", [P, TPC, E]), sb("o_square_sums", [P, TPC * heads]), sb("rrms", [P, TPC * heads])
        og, ogT = sb("o_gated", [P, TPC, E]), sb("o_gatedT", [P, 2, S])
        tri = sb("tri", [P, P])
        it, ij = sb("iota_t", [P, W], mybir.dt.int32), sb("iota_j", [P, W], mybir.dt.int32)
        ix = sb("iota_xor", [P, W], mybir.dt.int32)
        ft, fj, fx = sb("query_no", [P, W]), sb("key_no", [P, W]), sb("xor", [P, W])
        later, below = sb("later", [P, W]), sb("below", [P, W])
        low = [m for m in GLA_LEVELS if m < W]
        turn = sb("wait_carrier", [P, 1])
        masks = sb("masks", [P, len(low) + 1, W])
        s_const, s_mask = sem("constants_made"), sem("mask_steps")
        s_xc, s_proj, s_gk, s_qk = sem("xc_copied"), sem("projected"), sem("gk_ready"), sem("qk_ready")
        s_z, s_vg, s_vgs = sem("z_ready"), sem("v_gate_projected"), sem("v_done")
        s_gates = sem("gate_done")
        s_in, s_out, s_e, s_l = sem("vector_in_steps"), sem("vector_out_steps"), sem("exp_done"), sem("log_done")
        s_b, s_bs, s_expo, s_fac = sem("sums_ready"), sem("sums_in_sbuf"), sem("exponents_done"), sem("factors_ready")
        s_zkq, s_round, s_taken, s_rect = sem("scaled_ready"), sem("pairs_round"), sem("round_taken"), sem("rects_copied")
        s_near, s_win = sem("near_done"), sem("windows_copied")
        s_kdT, s_kd = sem("k_to_end_turned"), sem("k_to_end_ready")
        s_inc, s_state, s_o = sem("state_added"), sem("state_ready"), sem("o_ready")
        s_sq, s_ss, s_rms = sem("squares_done"), sem("square_sums_done"), sem("rrms_done")
        s_gw = sem("gate_weighted")
        s_og, s_ogT, s_ogTs, s_y, s_x = sem("o_gated_ready"), sem("og_turned"), sem("ogT_ready"), sem("y_ready"), sem("x_updated")
        s_free = [sem(f"odd_bank_free{i}") for i in range(2)]
        halves = ["gk", "q", "k", "z"], [("S", i) for i in range(TPC - 1)], ["b", "y"] + \
            [("vg", i) for i in range(TPC)] + ["kd"]
        first = [job for job in halves[0] + halves[2] if job != "y"]
        middle = sum(halves, [])
        last = halves[1] + ["y"]
        uses = {job: n for n, job in enumerate(first)}
        loop_uses = {job: len(first) + n for n, job in enumerate(middle)}
        end_uses = {job: len(first) + n for n, job in enumerate(last)}
        JOBS = len(middle) // 2
        assert len(first) % 2 == 0 and len(middle) % 2 == 0
        rounds = [(0,), (64, 32, 16), (8, 4, 2, 1)]
        place = {0: 0, 64: 0, 32: 256, 16: 384, 8: 0, 4: 128, 2: 256, 1: 384}
        blocks = lambda a, m: a.rearrange("p (n u) -> p n u", u=2 * m)
        by_chunk = lambda a: a.rearrange("p (i t) -> p i t", i=TPC)
        block = ctx.enter_context(nc.Block())

        @block.sync
        def _(sp):
            sh.load_next(sp, stage)

        def run(eng, steps_in, steps_out):
            for name in ("project", "decay", "rest"):
                steps_in[name](0, 0, uses)
            with eng.Fori(0, B - 1) as c:
                steps_in["project"](c + 1, c, loop_uses)
                steps_out["states"](c, c, loop_uses)
                steps_in["decay"](c + 1, c, loop_uses)
                steps_out["output"](c, c, loop_uses)
                steps_in["rest"](c + 1, c, loop_uses)
            steps_out["states"](B - 1, B - 1, end_uses)
            steps_out["output"](B - 1, B - 1, end_uses)

        def freed(eng, n):
            eng.sem_inc(s_free[n % 2], 1)

        nothing = lambda c, r, uses: None

        @block.gpsimd
        def _(pool):
            nc.gpsimd.iota(it[:, :], pattern=[[1, W]], base=0, channel_multiplier=0).then_inc(s_const, 1)
            nc.gpsimd.iota(ij[:, :], pattern=[[0, W]], base=0, channel_multiplier=1).then_inc(s_const, 1)
            nc.gpsimd.memset(tri[:, :], 1.0 / gate_norm).then_inc(s_const, 1)
            nc.gpsimd.memset(state[:, :], 0.0).then_inc(s_const, 1)
            pool.wait_ge(s_const, 4)
            nc.gpsimd.affine_select(out=tri[:, :], in_=tri[:, :], compare_op=ALU.is_ge, fill=0.0, base=0,
                                    pattern=[[1, P]], channel_multiplier=-1).then_inc(s_const, 1)
            ln.gpsimd(pool)
            nc.gpsimd.memset(pairs[:, :, :, :], 0.0).then_inc(s_const, 1)
            pool.wait_ge(sh.wsem[stage], 16)

            def exponents(c, r, uses):
                pool.wait_ge(s_bs, c + 1)
                for n, m in enumerate(GLA_LEVELS):
                    src, dst = blocks(b[:, :], m), blocks(expo[:, n, :], m)
                    mid = src[:, :, m - 1:m].broadcast_to([P, S // (2 * m), m])
                    nc.gpsimd.tensor_tensor(dst[:, :, 0:m], mid, src[:, :, 0:m], SUB).then_inc(s_expo, 1)
                    nc.gpsimd.tensor_tensor(dst[:, :, m:], src[:, :, m:], mid, SUB).then_inc(s_expo, 1)
                nc.gpsimd.tensor_tensor(by_chunk(expo[:, F_LAST, :]),
                                        by_chunk(b[:, :])[:, :, P - 1:P].broadcast_to([P, TPC, P]),
                                        by_chunk(b[:, :]), SUB).then_inc(s_expo, 1)

            def weigh_gate(c, r, uses):
                pool.wait_ge(s_gates, (c + 1) * TPC)
                nc.gpsimd.tensor_tensor(gate[:, :, :].rearrange("p i (h e) -> p (i h) e", h=heads),
                                        gate[:, :, :].rearrange("p i (h e) -> p (i h) e", h=heads),
                                        w["rms_w"].unsqueeze(1).broadcast_to([P, TPC * heads, dv]), MUL).then_inc(s_gw, 1)

            def rms(c, r, uses):
                pool.wait_ge(s_ss, c + 1)
                nc.gpsimd.tensor_tensor(rrms[:, :], ss[:, :], sh.mhalf[:, 0:TPC * heads], ALU.pow).then_inc(s_rms, 1)

            run(pool, {"project": nothing, "decay": exponents, "rest": weigh_gate},
                {"states": rms, "output": nothing})

        @block.tensor
        def _(pe):
            pe.wait_ge(sh.wsem[stage], 16)
            ln.tensor(pe)
            pe.wait_ge(ln.ready, B)
            pe.wait_ge(s_const, 6)

            def take(r, uses, job):
                k = uses[job]
                if k >= 2:
                    pe.wait_ge(s_free[k % 2], r * JOBS + k // 2)
                return odd[k % 2]

            def project(c, r, uses):
                pe.wait_ge(s_xc, c + 1)
                ps = take(r, uses, "gk")
                nc.tensor.matmul(ps[0:rank, :], w["wgk1"], xc[:, :], start=True, stop=True).then_inc(s_proj, 1)
                for name in "qk":
                    ps = take(r, uses, name)
                    nc.tensor.matmul(ps, w["w" + name], xc[:, :], start=True, stop=True).then_inc(s_proj, 1)
                ps = take(r, uses, "z")
                pe.wait_ge(s_gk, c + 1)
                for i in range(TPC):
                    last = nc.tensor.matmul(ps[:, i * P:(i + 1) * P], gk[:, i * P:(i + 1) * P], w["wgk2"],
                                            start=True, stop=True)
                last.then_inc(s_z, 1)

            def states(c, r, uses):
                pe.wait_ge(s_zkq, (c + 1) * (NL + 2))
                pe.wait_ge(s_win, (c + 1) * TPC)
                pe.wait_ge(s_vgs, (c + 1) * TPC)
                for i in range(TPC):
                    half = ps_o[:, i // 2, (i % 2) * E:(i % 2 + 1) * E]
                    for h in range(heads):
                        last = nc.tensor.matmul(half[:, h * dv:(h + 1) * dv], pairs[:, h, i, :], v[:, i, h * dv:(h + 1) * dv],
                                                start=(i % 2 == 0 and h == 0), stop=False, skip_group_check=True)
                    if i < TPC - 1:
                        ps = take(r, uses, ("S", i))
                        pe.wait_ge(s_kd, c + 1)
                        nc.tensor.matmul(ps[:, 0:E], kdec[:, i, :], v[:, i, :], start=True, stop=True).then_inc(s_inc, 1)
                    if i:
                        pe.wait_ge(s_state, c * (TPC - 1) + i)
                        last = nc.tensor.matmul(half, zkq[:, F_ALL, i * P:(i + 1) * P], state[:, :],
                                                start=False, stop=True, skip_group_check=True)
                    last.then_inc(s_o, 1)

            def pair_round(c, n):
                for m in rounds[n]:
                    level = GLA_LEVELS.index(m) if m else 0
                    keys, queries = (zkq[:, level, :],) * 2 if m else (kT, qT)
                    for i in range(TPC):
                        at = i * P
                        for h in range(heads):
                            rows = slice(h * dk, (h + 1) * dk)
                            if m == 64:
                                to = place[m] + i * m
                                last = nc.tensor.matmul(ps_a[0:m, h, to:to + m], keys[rows, at:at + m],
                                                        queries[rows, at + m:at + 2 * m], start=True, stop=True)
                            elif m == 32:
                                to = place[m] + i * m
                                for k in (0, 64):
                                    last = nc.tensor.matmul(ps_a[k:k + m, h, to:to + m], keys[rows, at + k:at + k + m],
                                                            queries[rows, at + k + m:at + k + 2 * m],
                                                            start=True, stop=True)
                            else:
                                to = place[m] + i * W
                                for k in range(0, P, W):
                                    last = nc.tensor.matmul(ps_a[k:k + W, h, to:to + W], keys[rows, at + k:at + k + W],
                                                            queries[rows, at + k:at + k + W], start=True, stop=True)
                last.then_inc(s_round, 1)

            def decay(c, r, uses):
                ps = take(r, uses, "b")
                pe.wait_ge(s_in, c * IN_STEPS + 3)
                pe.wait_ge(s_qk, (c + 1) * 2)
                for i in range(TPC):
                    last = nc.tensor.matmul(ps[:, i * P:(i + 1) * P], g[:, i * P:(i + 1) * P], tri[:, :],
                                            start=True, stop=True)
                last.then_inc(s_b, 1)
                pair_round(c, 0)

            def rest(c, r, uses):
                for i in range(TPC):
                    ps = take(r, uses, ("vg", i))
                    nc.tensor.matmul(ps, xc[:, i * P:(i + 1) * P], w["wvg"], start=True, stop=True).then_inc(s_vg, 1)
                for n in (1, 2):
                    pe.wait_ge(s_zkq, c * (NL + 2) + GLA_LEVELS.index(rounds[n][-1]) + 1)
                    pe.wait_ge(s_taken, c * 3 + n)
                    if n == 2:
                        ps = take(r, uses, "kd")
                        pe.wait_ge(s_zkq, c * (NL + 2) + NL + 1)
                        for i in range(TPC):
                            last = nc.tensor.transpose(ps[:, i * P:(i + 1) * P], zkq[:, F_LAST, i * P:(i + 1) * P],
                                                       sh.ident[:, :])
                        last.then_inc(s_kdT, 1)
                    pair_round(c, n)

            def output(c, r, uses):
                pe.wait_ge(s_og, c + 1)
                for i in range(TPC):
                    for k in range(2):
                        last = nc.tensor.transpose(ps_o[:, k, i * P:(i + 1) * P], og[:, i, k * P:(k + 1) * P], sh.ident[:, :])
                last.then_inc(s_ogT, 1)
                ps = take(r, uses, "y")
                pe.wait_ge(s_ogTs, (c + 1) * 2)
                for i in range(TPC):
                    for k in range(2):
                        last = nc.tensor.matmul(ps[:, i * P:(i + 1) * P], ogT[:, k, i * P:(i + 1) * P],
                                                w["wout"][:, k * D:(k + 1) * D], start=(i == 0 and k == 0), stop=(k == 1),
                                                skip_group_check=True)
                last.then_inc(s_y, 1)

            run(pe, {"project": project, "decay": decay, "rest": rest}, {"states": states, "output": output})

        @block.scalar
        def _(act):
            ln.scalar(act)
            act.wait_ge(ln.ready, B)
            act.wait_ge(sh.wsem[stage], 16)

            def exps(c, levels):
                for n in levels:
                    act.wait_ge(s_expo, c * (2 * NL + 1) + min(2 * n + 2, 2 * NL + 1))
                    nc.scalar.activation(fac[:, n, :], expo[:, n, :], ACT.Exp).then_inc(s_fac, 1)

            def project(c, r, uses):
                nc.scalar.copy(xc[:, :], sh.xnT[:, cols(c)]).then_inc(s_xc, 1)
                act.wait_ge(s_proj, c * 3 + 1)
                nc.scalar.copy(gk[:, :], odd[uses["gk"] % 2][0:rank, :]).then_inc(s_gk, 1)
                act.wait_ge(s_gk, c + 1)
                freed(act, uses["gk"])
                for n, (name, dst) in enumerate((("q", qT), ("k", kT))):
                    act.wait_ge(s_proj, c * 3 + n + 2)
                    nc.scalar.activation(dst[:, :], odd[uses[name] % 2], ACT.Copy,
                                         scale=dk ** -0.5 if name == "q" else 1.0).then_inc(s_qk, 1)
                    act.wait_ge(s_qk, c * 2 + n + 1)
                    freed(act, uses[name])
                act.wait_ge(s_in, c * IN_STEPS + 2)
                nc.scalar.activation(soft[:, :], soft[:, :], ACT.Exp, scale=-1.0).then_inc(s_e, 1)
                act.wait_ge(s_e, c + 1)
                nc.scalar.activation(soft[:, :], soft[:, :], ACT.Ln, bias=1.0).then_inc(s_l, 1)

            def states(c, r, uses):
                for k in range(2):
                    act.wait_ge(s_o, c * TPC + 2 * k + 2)
                    nc.scalar.activation(sq[:, 2 * k:2 * k + 2, :].rearrange("p i e -> p (i e)"), ps_o[:, k, :],
                                         ACT.Square).then_inc(s_sq, 1)

            def decay(c, r, uses):
                act.wait_ge(s_b, c + 1)
                nc.scalar.copy(b[:, :], odd[uses["b"] % 2]).then_inc(s_bs, 1)
                act.wait_ge(s_bs, c + 1)
                freed(act, uses["b"])
                nc.scalar.activation(fac[:, F_ALL, :], b[:, :], ACT.Exp).then_inc(s_fac, 1)
                exps(c, range(3))

            def output(c, r, uses):
                act.wait_ge(s_ogT, c + 1)
                for k in range(2):
                    nc.scalar.copy(ogT[:, k, :], ps_o[:, k, :]).then_inc(s_ogTs, 1)

            def rest(c, r, uses):
                for i in range(TPC):
                    act.wait_ge(s_vg, c * TPC + i + 1)
                    nc.scalar.activation(gate[:, i, :], odd[uses["vg", i] % 2][:, E:2 * E], ACT.Silu).then_inc(s_gates, 1)
                exps(c, range(3, NL + 1))
                act.wait_ge(s_round, c * 3 + 2)
                cut = lambda k, m, at: ps_a[k:k + m, :, at:at + TPC * m].rearrange("p h (i t) -> p h i t", i=TPC)
                nc.scalar.copy(pairs[0:64, :, :, 64:P], cut(0, 64, place[64])).then_inc(s_rect, 1)
                for k in (0, 64):
                    nc.scalar.copy(pairs[k:k + 32, :, :, k + 32:k + 64], cut(k, 32, place[32])).then_inc(s_rect, 1)
                act.wait_ge(s_kdT, c + 1)
                nc.scalar.copy(kdec[:, :, :].rearrange("p i d -> p (i d)"), odd[uses["kd"] % 2]).then_inc(s_kd, 1)
                act.wait_ge(s_kd, c + 1)
                freed(act, uses["kd"])
                act.wait_ge(s_near, c + 1)
                for k in range(TPC):
                    rows = slice(k * W, (k + 1) * W)
                    nc.scalar.copy(pairs[rows, :, :, rows], near[rows, :, :, :]).then_inc(s_win, 1)

            run(act, {"project": project, "decay": decay, "rest": rest}, {"states": states, "output": output})

        @block.vector
        def _(dve):
            mk = Steps(dve, s_mask, 0, 7 + 3 * len(low))
            dve.wait_ge(s_const, 2)
            mk.then(nc.vector.tensor_scalar(ij[:, :], ij[:, :], W - 1, None, ALU.bitwise_and))
            mk.then(nc.vector.tensor_tensor(ix[:, :], it[:, :], ij[:, :], ALU.bitwise_xor))
            mk.did(nc.vector.tensor_copy(ft[:, :], it[:, :]))
            mk.did(nc.vector.tensor_copy(fj[:, :], ij[:, :]))
            mk.then(nc.vector.tensor_copy(fx[:, :], ix[:, :]))
            mk.did(nc.vector.tensor_tensor(later[:, :], ft[:, :], fj[:, :], ALU.is_gt))
            mk.then(nc.vector.tensor_tensor(masks[:, len(low), :], ft[:, :], fj[:, :], ALU.is_equal))
            for n, m in enumerate(low):
                mk.did(nc.vector.tensor_scalar(below[:, :], fx[:, :], 2 * m - 0.5, None, ALU.is_lt))
                mk.then(nc.vector.scalar_tensor_tensor(out=masks[:, n, :], in0=fx[:, :], scalar=m - 0.5, in1=later[:, :],
                                                       op0=ALU.is_gt, op1=MUL))
                mk.then(nc.vector.tensor_tensor(masks[:, n, :], masks[:, n, :], below[:, :], MUL))
            mk.end()
            dve.wait_ge(sh.wsem[stage], 16)
            ln.vector(dve)
            dve.wait_ge(s_const, 5)
            wide = lambda n: masks[:, n, :].unsqueeze(1).unsqueeze(1).broadcast_to([P, heads, TPC, W])
            low_round = lambda m: ps_a[:, :, place[m]:place[m] + TPC * W].rearrange("p h (i t) -> p h i t", i=TPC)
            by_head = lambda a: a.rearrange("p i (h e) -> p (i h) e", h=heads)

            def steps(c, sem, total, at, end):
                st = Steps(dve, sem, c * total, end)
                st.n = at
                return st

            def project(c, r, uses):
                st = steps(c, s_in, IN_STEPS, 0, 3)
                dve.wait_ge(s_z, c + 1)
                st.then(nc.vector.tensor_tensor(by_chunk(z[:, :]), by_chunk(odd[uses["z"] % 2]),
                                                w["bgk2"].unsqueeze(1).broadcast_to([P, TPC, P]), ADD))
                freed(dve, uses["z"])
                st.did(nc.vector.scalar_tensor_tensor(out=soft[:, :], in0=z[:, :], scalar=-1.0, in1=z[:, :],
                                                      op0=MUL, op1=ALU.max))
                dve.wait_ge(s_l, c + 1)
                st.did(nc.vector.scalar_tensor_tensor(out=g[:, :], in0=z[:, :], scalar=0.0, in1=soft[:, :],
                                                      op0=ALU.min, op1=SUB))
                st.end()

            def states(c, r, uses):
                st = steps(c, s_out, OUT_STEPS, 0, 13)
                for i in range(TPC - 1):
                    dve.wait_ge(s_inc, c * (TPC - 1) + i + 1)
                    if i:
                        dve.wait_ge(s_o, c * TPC + i + 1)
                    for h in range(heads):
                        rows, e = slice(h * dk, (h + 1) * dk), slice(h * dv, (h + 1) * dv)
                        ps = odd[uses["S", i] % 2]
                        if i == 0:
                            st.did(nc.vector.tensor_copy(state[rows, e], ps[rows, e]))
                        else:
                            at = (i + 1) * P - 1
                            st.did(nc.vector.scalar_tensor_tensor(out=state[rows, e], in0=state[rows, e],
                                                                  scalar=fac[rows, F_ALL, at:at + 1],
                                                                  in1=ps[rows, e], op0=MUL, op1=ADD))
                    st.wait()
                    freed(dve, uses["S", i])
                    dve.sem_inc(s_state, 1)
                dve.wait_ge(s_sq, (c + 1) * 2)
                st.then(nc.vector.tensor_reduce(ss[:, :], by_head(sq[:, :, :]), AX.X, ADD))
                nc.vector.tensor_scalar(ss[:, :], ss[:, :], 1.0 / dv, rms_eps, MUL, ADD).then_inc(s_ss, 1)
                st.end()

            def decay(c, r, uses):
                st = steps(c, s_in, IN_STEPS, 3, 4)
                dve.wait_ge(s_round, c * 3 + 1)
                st.then(nc.vector.tensor_tensor(near[:, :, :, :], low_round(0), wide(len(low)), MUL))
                dve.sem_inc(s_taken, 1)
                st.end()

            def output(c, r, uses):
                st = steps(c, s_out, OUT_STEPS, 13, OUT_STEPS)
                dve.wait_ge(s_rms, c + 1)
                st.then(nc.vector.tensor_tensor(by_head(og[:, :, :]),
                                                ps_o[:, :, :].rearrange("p k (i h e) -> p (k i h) e", h=heads, e=dv),
                                                rrms[:, :].unsqueeze(2).broadcast_to([P, TPC * heads, dv]), MUL))
                dve.wait_ge(s_gw, c + 1)
                nc.vector.tensor_tensor(og[:, :, :], og[:, :, :], gate[:, :, :], MUL).then_inc(s_og, 1)
                dve.wait_ge(s_y, c + 1)
                nc.vector.tensor_tensor(sh.x[:, tiles(c), :], sh.x[:, tiles(c), :],
                                        odd[uses["y"] % 2].rearrange("p (t d) -> p t d", t=TPC), ADD).then_inc(s_x, 1)
                dve.wait_ge(s_x, c + 1)
                freed(dve, uses["y"])
                st.end()

            def rest(c, r, uses):
                st = steps(c, s_in, IN_STEPS, 4, IN_STEPS)
                for i in range(TPC):
                    dve.wait_ge(s_gates, c * TPC + i + 1)
                    nc.vector.tensor_copy(v[:, i, :], odd[uses["vg", i] % 2][:, 0:E]).then_inc(s_vgs, 1)
                    dve.wait_ge(s_vgs, c * TPC + i + 1)
                    freed(dve, uses["vg", i])
                for n, m in enumerate(GLA_LEVELS):
                    if n == 0:
                        dve.wait_ge(s_qk, (c + 1) * 2)
                    dve.wait_ge(s_fac, c * (NL + 2) + n + 2)
                    for src, half in ((kT, slice(0, m)), (qT, slice(m, 2 * m))):
                        last = nc.vector.tensor_tensor(blocks(zkq[:, n, :], m)[:, :, half], blocks(fac[:, n, :], m)[:, :, half],
                                                       blocks(src[:, :], m)[:, :, half], MUL)
                    last.then_inc(s_zkq, 1)
                dve.wait_ge(s_fac, (c + 1) * (NL + 2))
                nc.vector.tensor_tensor(zkq[:, F_LAST, :], fac[:, F_LAST, :], kT[:, :], MUL).then_inc(s_zkq, 1)
                nc.vector.tensor_tensor(zkq[:, F_ALL, :], fac[:, F_ALL, :], qT[:, :], MUL).then_inc(s_zkq, 1)
                for n in (1, 2):
                    dve.wait_ge(s_round, c * 3 + n + 1)
                    if n == 1:
                        dve.wait_ge(s_rect, c * 3 + 3)
                    for m in rounds[n]:
                        if m < W:
                            st.did(nc.vector.memset(turn[:, :], 0.0))
                            st.then(nc.vector.copy_predicated(near[:, :, :, :], wide(low.index(m)).bitcast(U32),
                                                              low_round(m)))
                    dve.sem_inc(s_taken, 1)
                dve.sem_inc(s_near, 1)
                st.end()

            run(dve, {"project": project, "decay": decay, "rest": rest}, {"states": states, "output": output})


def route_top1(nc, st, part, s, comb, before, gt, eq, small):
    rank = small[:, 0, :].rearrange("p (t e) -> p t e", t=TPC)
    ranks(nc, st, rank, s, before[:, :, :], gt[:, :, :, :], eq[:, :, :, :], (part,))
    if part == 3:
        st.then(nc.vector.tensor_scalar(comb, rank, 0.5, None, ALU.is_lt))


def route_groups(nc, st, part, s, comb, before, gt, eq, small, groups=4, top_groups=2, top=4):
    e = s.shape[2]
    g = e // groups
    n = TPC * groups
    assert g == 4
    by_group = lambda a: a.rearrange("p t (h k) -> p (t h) k", h=groups)
    region = lambda k, m: small[:, k, 0:TPC * m].rearrange("p (t m) -> p t m", t=TPC)
    s4 = by_group(s).rearrange("p n (a b) -> p n a b", a=2)
    pmax, psum = (small[:, k, 0:2 * n].rearrange("p (n a) -> p n a", a=2) for k in (0, 1))
    best, pair, grank, allowed = (small[:, k, 0:n] for k in (2, 3, 4, 5))
    masked, rank, total = region(0, e), region(1, e), region(2, 1)
    per_tile = lambda a: a.rearrange("p (t h) -> p t h", t=TPC)
    if part == 0:
        st.did(nc.vector.tensor_tensor(pmax, s4[:, :, :, 0], s4[:, :, :, 1], ALU.max))
        st.then(nc.vector.tensor_tensor(psum, s4[:, :, :, 0], s4[:, :, :, 1], ALU.add))
        st.did(nc.vector.tensor_tensor(best, pmax[:, :, 0], pmax[:, :, 1], ALU.add))
        st.then(nc.vector.tensor_tensor(pair, psum[:, :, 0], psum[:, :, 1], ALU.max))
        st.then(nc.vector.tensor_tensor(best, best, pair, ALU.max))
    if part == 1:
        ranks(nc, st, per_tile(grank), per_tile(best), before[:, 0:groups, 0:groups],
              gt[:, :, 0:groups, 0:groups], eq[:, :, 0:groups, 0:groups])
        st.then(nc.vector.tensor_scalar(allowed, grank, top_groups - 0.5, None, ALU.is_lt))
    if part == 2:
        wide = allowed.unsqueeze(2).broadcast_to([P, n, g])
        st.then(nc.vector.tensor_tensor(by_group(masked), by_group(s), wide, ALU.mult))
        st.then(nc.vector.scalar_tensor_tensor(out=by_group(masked), in0=wide, scalar=-1.0, in1=by_group(masked),
                                               op0=ALU.add, op1=ALU.add))
    if part in (2, 3, 4):
        ranks(nc, st, rank, masked, before[:, :, :], gt[:, :, :, :], eq[:, :, :, :], (part - 2,))
    if part == 5:
        st.then(nc.vector.scalar_tensor_tensor(out=masked, in0=rank, scalar=top - 0.5, in1=s,
                                               op0=ALU.is_lt, op1=ALU.mult))
        st.then(nc.vector.tensor_reduce(total, masked, AX.X, ALU.add))
        st.then(nc.vector.tensor_scalar(total, total, 1e-6, None, ALU.add))
        st.then(nc.vector.reciprocal(total, total))
        st.then(nc.vector.tensor_tensor(comb, masked, total.broadcast_to([P, TPC, e]), ALU.mult))


ROUTE_TOP1_STEPS = (1, 2, 2, 1, 5)
ROUTE_GROUPS_STEPS = (5, 6, 3, 2, 2, 5, 5)


def routed_ffn(sh, stage, n_exp, f_exp, f_shared, score_func, route, part_steps):
    nc, w, tag = sh.nc, sh.w(stage), f"s{stage}"
    n_shared = f_shared // P
    route_steps = sum(part_steps)
    units = n_exp * f_exp // P + n_shared
    K = 3 * n_exp
    with ExitStack() as ctx:
        sb = lambda n, shape, dt=F32: ctx.enter_context(nc.sbuf_tensor(f"{tag}_{n}", shape, dt))
        sem = lambda n: sh.sem(f"{tag}_{n}")
        bank = lambda n, shape=(P, S), dt=F32: ctx.enter_context(nc.psum_tensor(f"{tag}_{n}", list(shape), dt))
        ps_gate = [bank(f"gate{i}") for i in range(2)]
        ps_up = [bank(f"up{i}") for i in range(2)]
        ps_comb = [bank(f"comb{i}") for i in range(2)]
        ps_y = bank("y", (P, TPC, D))
        ps_route = bank("route")
        ps_logits = ps_route[:, 0:NT * n_exp].rearrange("p (t e) -> p t e", t=NT)
        ps_combT = ps_route[:, 256:512].bitcast(BF16)
        ln = LayerNorm(sh, ctx, tag, [ps_route, ps_y[:, :, :].rearrange("p t d -> p (t d)")], split=True)
        UPP = 2 if units % 2 == 0 else 3
        assert units % UPP == 0
        n_pieces = 2 * (units // UPP)
        split = SplitWeights(sh, ctx, tag, [w[m][:, u * P:(u + UPP) * P] for u in range(0, units, UPP)
                                            for m in ("gate", "up")])
        silu = sb("silu", [P, 2, S])
        gated = sb("gated", [P, 2, S])
        hidden = sb("hidden", [P, 2, S])
        comb = sb("comb", [P, TPC, n_exp])
        parts_wide = sb("comb_parts", [P, TPC, P], BF16)
        parts = parts_wide[:, :, 0:K].rearrange("p t (a e) -> p t a e", a=3)
        rest = sb("comb_rest", [P, 2, TPC, n_exp])
        combT = sb("combT", [K, S], BF16)
        scores = sb("scores", [P, NT + TPC, n_exp])
        small = sb("small", [P, 6, TPC * n_exp])
        sel = sb("sel", [K, units - n_shared, P], BF16)
        before = sb("before", [P, n_exp, n_exp], BF16)
        gt = sb("gt", [P, TPC, n_exp, n_exp], BF16)
        eq = sb("eq", [P, TPC, n_exp, n_exp], BF16)
        s_sel, s_before, s_zero = sem("sel_made"), sem("before_made"), sem("parts_cleared")
        s_logits, s_scores = sem("logits_ready"), sem("scores_ready")
        s_route = sem("route_steps")
        s_partsT, s_combT = sem("parts_transposed"), sem("combT_ready")
        s_up, s_silu = sem("gate_up_ready"), sem("silu_ready")
        s_gated, s_hidden = sem("gated_done"), sem("hidden_ready")
        s_down, s_x = sem("down_done"), sem("x_updated")
        block = ctx.enter_context(nc.Block())

        @block.sync
        def _(sp):
            sh.load_next(sp, stage)

        @block.gpsimd
        def _(pool):
            pool.wait_ge(sh.wsem[stage], 16)
            early = -(-n_pieces // 6)
            split.gpsimd(pool, range(early))
            make_before(nc, pool, before, n_exp, s_before)
            ln.gpsimd(pool, lambda c: split.gpsimd(pool, range(early * (c + 1), min(early * (c + 2), n_pieces))))
            nc.gpsimd.memset(sel[:, :, :], 0.0).then_inc(s_sel, 1)
            pool.wait_ge(s_sel, 1)
            n = 1
            for part in range(3):
                if f_exp >= P:
                    k = f_exp // P
                    view = sel[:, :, :].rearrange("r (e k) f -> r e (k f)", k=k)
                    pattern = [[-1, n_exp], [0, k * P]]
                else:
                    view = sel[:, :, :].rearrange("r u (e f) -> r (u e) f", f=f_exp)
                    pattern = [[-1, n_exp], [0, f_exp]]
                nc.gpsimd.affine_select(out=view, in_=view, compare_op=ALU.not_equal, fill=1.0,
                                        base=-part * n_exp, pattern=pattern,
                                        channel_multiplier=1).then_inc(s_sel, 1)
                n += 1
                pool.wait_ge(s_sel, n)
            split.gpsimd(pool, range(5 * early, n_pieces))

        @block.tensor
        def _(pe):
            pe.sem_inc(s_down, 1)
            pe.wait_ge(sh.wsem[stage], 16)
            ln.tensor(pe)
            pe.wait_ge(ln.ready, B)
            for t in range(NT):
                last = nc.tensor.matmul(ps_logits[:, t, :], sh.xnT[:, t * P:(t + 1) * P], w["router"],
                                        start=True, stop=True)
            last.then_inc(s_logits, 1)
            pe.wait_ge(s_scores, 1)
            with pe.Fori(0, B) as c:
                def gate_up(u):
                    pe.wait_ge(s_hidden, 1 + c * units + (u - 1 if u else 0))
                    if u == 0:
                        pe.wait_ge(ln.s_lo, c + 1)
                    us = slice(u % UPP * P, (u % UPP + 1) * P)
                    for m, ps in enumerate((ps_gate, ps_up)):
                        at = u // UPP * 2 + m
                        if u % UPP == 0:
                            pe.wait_ge(split.s_lo, at + 1)
                        w_hi, w_lo = split.parts[at]
                        nc.tensor.matmul(ps[u % 2][:, :], w_hi[:, us], ln.hi[:, cols(c)], start=True, stop=False)
                        nc.tensor.matmul(ps[u % 2][:, :], w_lo[:, us], ln.hi[:, cols(c)], start=False, stop=False)
                        last = nc.tensor.matmul(ps[u % 2][:, :], w_hi[:, us], ln.lo[:, cols(c)], start=False, stop=True)
                    if u >= n_shared:
                        if u == n_shared:
                            pe.wait_ge(s_sel, 4)
                        pe.wait_ge(s_combT, c + 1)
                        last = nc.tensor.matmul(ps_comb[u % 2][:, :], sel[:, u - n_shared, :], combT[:, :],
                                                start=True, stop=True)
                    last.then_inc(s_up, 1)

                def down(u):
                    pe.wait_ge(s_hidden, 1 + c * units + u + 1)
                    if u == 0:
                        pe.wait_ge(s_x, 1 + c)
                    for i in range(TPC):
                        last = nc.tensor.matmul(ps_y[:, i, :], hidden[:, u % 2, i * P:(i + 1) * P],
                                                w["down"][:, u * P:(u + 1) * P],
                                                start=(u == 0 and i == 0), stop=(u == units - 1),
                                                skip_group_check=True)
                    last.then_inc(s_down, 1)

                for u in range(units):
                    gate_up(u)
                    if u == n_shared - 1:
                        pe.wait_ge(s_route, (c + 1) * route_steps)
                        for i in range(TPC):
                            last = nc.tensor.transpose(ps_combT[:, i * P:(i + 1) * P], parts_wide[:, i, :],
                                                       sh.identb[:, :])
                        last.then_inc(s_partsT, 1)
                    if u:
                        down(u - 1)
                down(units - 1)

        @block.scalar
        def _(act):
            act.wait_ge(sh.wsem[stage], 16)
            split.scalar()
            ln.scalar(act)
            act.wait_ge(s_logits, 1)
            nc.scalar.activation(scores[:, 0:NT, :], ps_logits, score_func).then_inc(s_scores, 1)
            with act.Fori(0, B) as c:
                for u in range(units):
                    act.wait_ge(s_up, c * units + u + 1)
                    nc.scalar.activation(silu[:, u % 2, :], ps_gate[u % 2][:, :], ACT.Silu).then_inc(s_silu, 1)

        @block.vector
        def _(dve):
            dve.sem_inc(s_hidden, 1)
            dve.sem_inc(s_x, 1)
            nc.vector.memset(parts_wide[:, :, :], 0.0).then_inc(s_zero, 1)
            nc.vector.memset(scores[:, NT:, :], 0.0).then_inc(s_zero, 1)
            ln.vector(dve)
            ln.low_parts(dve)
            dve.wait_ge(s_zero, 2)
            dve.wait_ge(s_before, 2)
            dve.wait_ge(s_scores, 1)

            n_parts = len(part_steps)

            def route_part(c, part):
                st = Steps(dve, s_route, c * route_steps + sum(part_steps[:part]), part_steps[part])
                if part < n_parts - 1:
                    route(nc, st, part, scores[:, tiles(c), :], comb[:, :, :], before, gt, eq, small)
                else:
                    split3(nc.vector, st, [parts[:, :, k, :] for k in range(3)], comb[:, :, :],
                           [rest[:, k, :, :] for k in range(2)])
                st.end()

            for part in range(n_parts):
                route_part(0, part)
            with dve.Fori(0, B) as c:
                for u in range(units):
                    if u == n_shared:
                        dve.wait_ge(s_partsT, c + 1)
                        nc.vector.tensor_copy(combT[:, :], ps_combT[0:K, :]).then_inc(s_combT, 1)
                    dve.wait_ge(s_silu, c * units + u + 1)
                    dve.wait_ge(s_down, 1 + c * units + (u - 1 if u else 0))
                    if u < n_shared:
                        nc.vector.tensor_tensor(hidden[:, u % 2, :], silu[:, u % 2, :], ps_up[u % 2][:, :],
                                                ALU.mult).then_inc(s_hidden, 1)
                    else:
                        nc.vector.tensor_tensor(gated[:, u % 2, :], silu[:, u % 2, :], ps_up[u % 2][:, :],
                                                ALU.mult).then_inc(s_gated, 1)
                        dve.wait_ge(s_gated, c * (units - n_shared) + u - n_shared + 1)
                        nc.vector.tensor_tensor(hidden[:, u % 2, :], gated[:, u % 2, :], ps_comb[u % 2][:, :],
                                                ALU.mult).then_inc(s_hidden, 1)
                    if 1 <= u <= n_parts:
                        dve.wait_ge(s_route, c * route_steps + route_steps + sum(part_steps[:u - 1]))
                        route_part(c + 1, u - 1)
                dve.wait_ge(s_down, 1 + (c + 1) * units)
                nc.vector.tensor_tensor(sh.x[:, tiles(c), :], sh.x[:, tiles(c), :], ps_y[:, :, :],
                                        ALU.add).then_inc(s_x, 1)


def ternary_ffn(sh, stage, hid=512):
    nc, w, tag = sh.nc, sh.w(stage), f"s{stage}"
    n = hid // P
    with ExitStack() as ctx:
        sb = lambda m, shape, dt=F32: ctx.enter_context(nc.sbuf_tensor(f"{tag}_{m}", shape, dt))
        sem = lambda m: sh.sem(f"{tag}_{m}")
        bank = lambda m, shape=(P, S): ctx.enter_context(nc.psum_tensor(f"{tag}_{m}", list(shape), F32))
        ps_a = [bank(f"a{i}") for i in range(2)]
        ps_b = [bank(f"b{i}") for i in range(2)]
        ps_y = [bank(f"y{i}", (P, TPC, D)) for i in range(2)]
        ps_t = [bank(f"t{i}") for i in range(2)]
        ln = LayerNorm(sh, ctx, tag, ps_t, split=True)
        wt = [w[name].rearrange("p (k o) -> p k o", k=n) for name in ("h1", "h2")]
        split = SplitWeights(sh, ctx, tag, [w["w1"], w["w2"]] + [m[:, k, :] for m in wt for k in range(n)])
        silu = sb("silu", [P, 2, S])
        h0 = sb("h0", [P, n, S])
        h1 = sb("h1", [P, n, S])
        h2 = sb("h2", [P, n, S])
        w3s = sb("w3_scaled", [P, n, D])
        s_w3 = sem("w3_scaled_done")
        s_up, s_silu, s_h0 = sem("gate_up_ready"), sem("silu_ready"), sem("h0_ready")
        s_p1, s_h1, s_p2, s_h2 = sem("h1_summed"), sem("h1_ready"), sem("h2_summed"), sem("h2_ready")
        hi, lo = ([sb(f"h{i}_{m}", [P, n, S], F32R) for i in range(2)] for m in ("hi", "lo"))
        s_hi, s_lo = ([sem(f"h{i}_{m}_ready") for i in range(2)] for m in ("hi", "lo"))
        s_y, s_x = sem("y_summed"), sem("x_updated")
        block = ctx.enter_context(nc.Block())

        @block.sync
        def _(sp):
            sh.load_next(sp, stage)

        @block.gpsimd
        def _(pool):
            pool.wait_ge(sh.wsem[stage], 16)
            split.gpsimd(pool, range(2))
            ln.gpsimd(pool, lambda c: split.gpsimd(pool, [2 + c]))
            split.gpsimd(pool, range(2 + n, 2 + 2 * n))
            with pool.Fori(0, B) as c:
                for i, h in enumerate((h0, h1)):
                    for k in range(n):
                        pool.wait_ge(s_hi[i], c * n + k + 1)
                        nc.gpsimd.tensor_tensor(lo[i][:, k, :], h[:, k, :], hi[i][:, k, :].bitcast(F32),
                                                ALU.subtract).then_inc(s_lo[i], 1)

        @block.tensor
        def _(pe):
            pe.sem_inc(s_p1, 1)
            pe.sem_inc(s_y, 1)
            pe.wait_ge(sh.wsem[stage], 16)
            ln.tensor(pe)
            pe.wait_ge(split.s_lo, 2)
            with pe.Fori(0, B) as c:
                pe.wait_ge(ln.s_hi, c + 1)
                for f in range(n):
                    pe.wait_ge(s_h0, 1 + c * n + (f - 1 if f else 0))
                    if f == 0:
                        pe.wait_ge(ln.s_lo, c + 1)
                    fs = slice(f * P, (f + 1) * P)
                    for (w_hi, w_lo), ps in zip(split.parts[0:2], (ps_a, ps_b)):
                        nc.tensor.matmul(ps[f % 2][:, :], w_hi[:, fs], ln.hi[:, cols(c)], start=True, stop=False)
                        nc.tensor.matmul(ps[f % 2][:, :], w_lo[:, fs], ln.hi[:, cols(c)], start=False, stop=False)
                        last = nc.tensor.matmul(ps[f % 2][:, :], w_hi[:, fs], ln.lo[:, cols(c)], start=False, stop=True)
                    last.then_inc(s_up, 1)
                for i, ps, s_free, s_done in ((0, ps_a, s_h1, s_p1), (1, ps_b, s_h2, s_p2)):
                    layer = split.parts[2 + i * n:2 + (i + 1) * n]
                    for f in range(n):
                        fs = slice(f * P, (f + 1) * P)
                        if f < 2:
                            pe.wait_ge(s_h0, 1 + (c + 1) * n)
                        else:
                            pe.wait_ge(s_free, c * n + f - 1)
                        if f == 0:
                            pe.wait_ge(split.s_lo, 2 + (i + 1) * n)
                        for k in range(n):
                            if f == 0:
                                pe.wait_ge(s_hi[i], c * n + k + 1)
                            for part in layer[k]:
                                nc.tensor.matmul(ps[f % 2][:, :], part[:, fs], hi[i][:, k, :],
                                                 start=(k == 0 and part is layer[k][0]), stop=False)
                        for k in range(n):
                            if f == 0:
                                pe.wait_ge(s_lo[i], c * n + k + 1)
                            last = nc.tensor.matmul(ps[f % 2][:, :], layer[k][0][:, fs], lo[i][:, k, :],
                                                    start=False, stop=(k == n - 1))
                        last.then_inc(s_done, 1)
                pe.wait_ge(s_w3, n)
                pe.wait_ge(s_x, 1 + c)
                for k in range(n):
                    pe.wait_ge(s_h2, c * n + k + 1)
                    for i in range(TPC):
                        last = nc.tensor.matmul(ps_y[0][:, i, :], h2[:, k, i * P:(i + 1) * P], w3s[:, k, :],
                                                start=(k == 0 and i == 0), stop=(k == n - 1),
                                                skip_group_check=True)
                last.then_inc(s_y, 1)

        @block.scalar
        def _(act):
            act.wait_ge(sh.wsem[stage], 16)
            split.scalar()
            ln.scalar(act)
            with act.Fori(0, B) as c:
                for f in range(n):
                    act.wait_ge(s_up, c * n + f + 1)
                    nc.scalar.activation(silu[:, f % 2, :], ps_a[f % 2][:, :], ACT.Silu,
                                         scale=w["w1_s"][:, f:f + 1]).then_inc(s_silu, 1)
                for s_sum, first, ps, out, scale, s_out in ((s_p1, 1, ps_a, h1, w["h1_s"], s_h1),
                                                            (s_p2, 0, ps_b, h2, w["h2_s"], s_h2)):
                    for f in range(n):
                        act.wait_ge(s_sum, first + c * n + f + 1)
                        if s_out is s_h2 and f == 0:
                            act.wait_ge(s_y, 1 + c)
                        nc.scalar.activation(out[:, f, :], ps[f % 2][:, :], ACT.Gelu,
                                             scale=scale[:, f:f + 1]).then_inc(s_out, 1)

        @block.vector
        def _(dve):
            dve.sem_inc(s_h0, 1)
            dve.sem_inc(s_x, 1)
            ln.vector(dve)
            dve.wait_ge(sh.wsem[stage], 16)
            for k in range(n):
                nc.vector.tensor_tensor(w3s[:, k, :], w["w3"][:, k * D:(k + 1) * D], w["w3_s"],
                                        ALU.mult).then_inc(s_w3, 1)
            ln.low_parts(dve)

            def high(i, k):
                nc.vector.tensor_copy(hi[i][:, k, :], (h0, h1)[i][:, k, :]).then_inc(s_hi[i], 1)

            with dve.Fori(0, B) as c:
                for f in range(n):
                    dve.wait_ge(s_silu, c * n + f + 1)
                    if f == 0:
                        dve.wait_ge(s_p1, 1 + c * n)
                    nc.vector.scalar_tensor_tensor(out=h0[:, f, :], in0=ps_b[f % 2][:, :],
                                                   scalar=w["w2_s"][:, f:f + 1], in1=silu[:, f % 2, :],
                                                   op0=ALU.mult, op1=ALU.mult).then_inc(s_h0, 1)
                    dve.wait_ge(s_h0, 1 + c * n + f + 1)
                    high(0, f)
                for f in range(n):
                    dve.wait_ge(s_h1, c * n + f + 1)
                    high(1, f)
                dve.wait_ge(s_y, 1 + c + 1)
                nc.vector.tensor_tensor(sh.x[:, tiles(c), :], sh.x[:, tiles(c), :], ps_y[0][:, :, :],
                                        ALU.add).then_inc(s_x, 1)


QUADS = H8 // 4


def causal_plan(q):
    per_bank = {0: 4, 1: 2, 2: 1, 3: 1}
    first = lambda d: [("max", d, n, i, 4 * (d % QUADS) + h, per_bank[i]) for n, (i, h) in
                       enumerate((i, h) for i in range(TPC) for h in range(0, 4, per_bank[i]))]
    fetch = lambda c: [("q", c), ("k", c), ("split", c)]
    if q == -2:
        return fetch(0) + first(0)
    if q == -1:
        return fetch(1) + first(1) + [("maxsplit", 0), ("maxT", 0)]
    c, g = divmod(q, QUADS)
    units = first(q + 2) if q + 2 < B * QUADS else []
    plan = []
    for r in range(5):
        plan += units[2 * r:2 * r + 1]
        if c < B:
            plan.append(("exp", q, r))
        plan += units[2 * r + 1:2 * r + 2] + units[10:] * (r == 4)
        if r in (0, 1) and q + 1 < B * QUADS:
            plan.append(("maxT" if r else "maxsplit", q + 1))
        if r == 1 and q:
            plan.append(("pv", q - 1))
        if r == 2 and g == 0 and c < B:
            plan.append(("v", c))
        if r == 3 and q:
            plan.append(("turn", q - 1))
        if r == 4 and g == 0 and q:
            plan.append(("oT", c - 1))
            if c == B:
                plan.append(("y", c - 1))
        if r == 0 and g == 1 and c:
            plan.append(("y", c - 1))
        if g == 2 and r >= 2 and c + 2 < B:
            plan.append(fetch(c + 2)[r - 2])
    return plan


def causal_attention(sh, stage, ctx, ln, pa, p1, p2, po, pm, wq, wk, wv, wo, qk_bias, v_bias, o_bias, scale,
                     before_scalar, before_vector, before_tensor, norm_gpsimd, after_norm_gpsimd, hs=None, extra=None):
    nc, tag = sh.nc, f"s{stage}"
    W = 3 * HD8
    R = 9 * HD8
    sb = lambda m, shape, dt=F32: ctx.enter_context(nc.sbuf_tensor(f"{tag}_{m}", shape, dt))
    sem = lambda m: sh.sem(f"{tag}_{m}")
    qkf = sb("qk_f32", [P, 2, S])
    parts = sb("qk_parts", [P, 3, 2, S], BF16)
    rest = sb("qk_rest", [P, 2, S])
    qs = sb("q_stack", [R + 3, 2, H8, S], BF16)
    ks = sb("k_stack", [P, 2, H8, S], BF16)
    v32 = sb("v_and_one", [P, TPC, H8, 32])
    mask_qk = sb("mask_qk", [P, P], BF16)
    mask_kq = sb("mask_kq", [P, P], BF16)
    negmax = sb("negmax", [P, TPC, H8])
    mparts = sb("max_parts", [P, QUADS, TPC, 3, 4], BF16)
    mrest = sb("max_rest", [P, 2, TPC, H8])
    mT = sb("maxT", [3 * 4, S], BF16)
    pb = sb("probs_b", [P, 2, 4, 256])
    oq = sb("o_quad", [P, S])
    recip = sb("recip", [P, TPC, 4])
    o = sb("o", [P, TPC, D])
    oT = ln.xn[:, 0, :, :].rearrange("p i d -> p (i d)")
    s_mask, s_ones = sem("masks_made"), sem("ones_made")
    s_q, s_qf = sem("qk_projected"), sem("qk_in_sbuf")
    s_v, s_v32 = sem("v_projected"), sem("v_in_sbuf")
    s_split, s_wrote = sem("qk_split_steps"), sem("qk_parts_stored")
    s_stack = [sem(f"stack_loaded{i}") for i in range(2)]
    s_max, s_neg, s_msplit = sem("scores_for_max"), sem("max_done"), sem("max_split_steps")
    s_maxT, s_mT, s_mwrote = sem("max_transposed"), sem("maxT_in_sbuf"), sem("maxT_stored")
    s_mrow = [sem(f"max_rows_loaded{i}") for i in range(2)]
    s_split0 = sem("first_qk_split_steps")
    s_sc, s_exp, s_pv = sem("scores_less_max"), sem("probs_ready"), sem("pv_done")
    s_oq, s_turn = sem("o_quad_in_sbuf"), sem("o_quad_transposed")
    s_rec, s_norm = sem("recip_done"), sem("o_normalised")
    s_oT, s_oTs, s_y, s_x = sem("o_transposed"), sem("oT_in_sbuf"), sem("y_ready"), sem("x_updated")
    s_bias = sem("o_bias_added")
    s_used = sem("misc_bank_free")
    UNITS = 11
    EXPS = 5
    plan = [item for q in range(-2, B * QUADS + 1) for item in causal_plan(q)]
    fills = {}
    for item in plan:
        if item[0] in ("q", "k", "maxT", "v", "turn", "oT", "y"):
            fills[item] = len(fills)
    block = ctx.enter_context(nc.Block())

    @block.sync
    def _(sp):
        if extra:
            sp.dma_start(extra[0], extra[1]).then_inc(extra[2], 16)
        sh.load_next(sp, stage)

        def store(c):
            if c:
                sp.wait_ge(s_split, 5 * c)
            else:
                sp.wait_ge(s_split0, 5)
            for qk in range(2):
                for k in range(3):
                    sp.dma_start(sh.scratch_qk[c, qk, :, k], parts[:, k, qk, :]).then_inc(s_wrote, 16)

        def stack(c):
            b = c % 2
            sp.wait_ge(s_wrote, 16 * 6 * (c + 1))
            if c >= 2:
                sp.wait_ge(s_sc, EXPS * QUADS * (c - 1))
            rows = lambda qk, k0, k1: sh.scratch_qk[c, qk, :, k0:k1].rearrange("h k d n -> (k d) h n")
            for a in range(3):
                sp.dma_start(ks[a * W:(a + 1) * W, b, :, :], rows(1, 0, 3)).then_inc(s_stack[b], 16)
                n = 3 - a
                sp.dma_start(qs[a * W:a * W + n * HD8, b, :, :], rows(0, a, 3)).then_inc(s_stack[b], 16)
                if a:
                    sp.dma_start(qs[a * W + n * HD8:(a + 1) * W, b, :, :], rows(0, 0, a)).then_inc(s_stack[b], 16)

        def max_rows(q):
            c, g = divmod(q, QUADS)
            sp.wait_ge(s_mT, q + 1)
            sp.dma_start(sh.scratch_max[c, 12 * g:12 * g + 12], mT[:, :]).then_inc(s_mwrote, 16)
            sp.wait_ge(s_mwrote, 16 * (q + 1))
            sp.dma_start(qs[R:R + 3, c % 2, 4 * g:4 * g + 4, :],
                         sh.scratch_max[c, 12 * g:12 * g + 12].rearrange("(k h) n -> k h n", k=3)).then_inc(s_mrow[q % 2], 16)

        sp.wait_ge(s_ones, 1)
        store(0)
        stack(0)
        for q in range(B * QUADS):
            max_rows(q)
            c, g = divmod(q, QUADS)
            if g == 1 and c < B - 1:
                store(c + 1)
                stack(c + 1)

    @block.gpsimd
    def _(pool):
        norm_gpsimd(pool)
        pool.wait_ge(ln.s_rstd, B)
        pair_of_ones = float(np.array([0x3F803F80], np.uint32).view(np.float32)[0])
        nc.gpsimd.memset(ks[64:96, :, :, :].rearrange("p b h n -> p (b h n)").bitcast(F32),
                         pair_of_ones).then_inc(s_ones, 1)
        pool.wait_ge(s_ones, 1)
        nc.gpsimd.memset(v32[:, :, :, HD8:32], 0.0).then_inc(s_ones, 1)
        pool.wait_ge(s_ones, 2)
        nc.gpsimd.memset(v32[:, :, :, HD8:HD8 + 1], 1.0).then_inc(s_ones, 1)
        nc.gpsimd.memset(mask_qk[:, :], 0.0).then_inc(s_mask, 1)
        nc.gpsimd.memset(mask_kq[:, :], 0.0).then_inc(s_mask, 1)
        pool.wait_ge(s_mask, 2)
        nc.gpsimd.affine_select(out=mask_qk[:, :], in_=mask_qk[:, :], compare_op=ALU.is_ge, fill=NEG,
                                base=0, pattern=[[-1, P]], channel_multiplier=1).then_inc(s_mask, 1)
        nc.gpsimd.affine_select(out=mask_kq[:, :], in_=mask_kq[:, :], compare_op=ALU.is_ge, fill=NEG,
                                base=0, pattern=[[1, P]], channel_multiplier=-1).then_inc(s_mask, 1)
        after_norm_gpsimd(pool)
        resid = sh.x if hs is None else hs
        pool.wait_ge(ln.s_xn, NT)
        for c in range(B):
            ts = slice(c * TPC, (c + 1) * TPC)
            nc.gpsimd.tensor_tensor(resid[:, ts, :], resid[:, ts, :],
                                    o_bias.unsqueeze(1).broadcast_to([P, TPC, D]), ALU.add).then_inc(s_bias, 1)
        for c in range(1, B):
            if c >= 2:
                pool.wait_ge(s_wrote, 16 * 6 * c)
            else:
                pool.wait_ge(s_split0, 5)
                pool.wait_ge(s_wrote, 16 * 6)
            pool.wait_ge(s_qf, 2 * (c + 1))
            st = Steps(pool, s_split, 5 * (c - 1), 5)
            split3(nc.gpsimd, st, [parts[:, k] for k in range(3)], qkf[:, :, :], [rest[:, :, :], qkf[:, :, :]])
            st.end()
        if hs is not None:
            for c in range(B):
                ts = slice(c * TPC, (c + 1) * TPC)
                pool.wait_ge(s_x, c + 1)
                nc.gpsimd.tensor_tensor(sh.x[:, ts, :], sh.x[:, ts, :], hs[:, ts, :], ALU.add)

    @block.tensor
    def _(pe):
        pe.wait_ge(sh.wsem[stage], 16)
        before_tensor(pe)
        pe.wait_ge(ln.ready, B)
        pe.wait_ge(s_mask, 4)
        pe.wait_ge(s_ones, 3)

        def project(c, name):
            pe.wait_ge(s_used, fills[name, c]) if fills[name, c] else None
            x = sh.xnT[:, c * S:(c + 1) * S]
            if name == "v":
                for i in range(TPC):
                    last = nc.tensor.matmul(pm[:, i * P:(i + 1) * P], x[:, i * P:(i + 1) * P], wv,
                                            start=True, stop=True)
                last.then_inc(s_v, 1)
            else:
                nc.tensor.matmul(pm[:, :], wq if name == "q" else wk, x, start=True, stop=True).then_inc(s_q, 1)

        def scores_for_max(q, k, i, h0, n):
            c = q // QUADS
            k += UNITS * q
            if k >= 2:
                pe.wait_ge(s_neg, k - 1)
            m = (i + 1) * P
            for x in range(n):
                out = p1[k % 2][:, x * m:(x + 1) * m]
                nc.tensor.matmul(out, qs[0:R, c % 2, h0 + x, i * P:(i + 1) * P], ks[0:R, c % 2, h0 + x, 0:m],
                                 start=True, stop=False)
                last = nc.tensor.matmul(out[:, i * P:m], sh.identb[:, :], mask_qk[:, :], start=False, stop=True)
            last.then_inc(s_max, 1)

        def scores_less_max(q, r):
            c, g = divmod(q, QUADS)
            n = EXPS * q + r
            if n >= 2:
                pe.wait_ge(s_exp, n - 1)
            ps = p2[n % 2]
            blocks = [(0, 0, 4 * g + r), (1, 512, 4 * g + r), (3, 896, 4 * g + r)] if r < 4 else \
                     [(2, 256 * x, 4 * g + x) for x in range(4)]
            for j, at, h in blocks:
                n = S - j * P
                nc.tensor.matmul(ps[:, at:at + n], ks[0:R + 3, c % 2, h, j * P:(j + 1) * P],
                                 qs[0:R + 3, c % 2, h, j * P:S], start=True, stop=False)
                last = nc.tensor.matmul(ps[:, at:at + P], sh.identb[:, :], mask_kq[:, :], start=False, stop=True)
            last.then_inc(s_sc, 1)

        def values(q):
            c, g = divmod(q, QUADS)
            pe.wait_ge(s_exp, EXPS * (q + 1))
            if g == 0:
                pe.wait_ge(s_v32, c + 1)
            if q:
                pe.wait_ge(s_oq, q)
            for j in range(TPC):
                at, n = {0: 0, 1: 512, 3: 896}.get(j), S - j * P
                for x in range(4):
                    prob = pb[:, q % 2, x, :] if j == 2 else pa[:, q % 2, x, at:at + n]
                    last = nc.tensor.matmul(po[32 * x:32 * x + 32, j * P:S], v32[:, j, 4 * g + x, :], prob,
                                            start=(j == 0), stop=(j == TPC - 1), skip_group_check=True)
            last.then_inc(s_pv, 1)

        def turn(q):
            pe.wait_ge(s_oq, q + 1)
            pe.wait_ge(s_used, fills["turn", q])
            for i in range(TPC):
                last = nc.tensor.transpose(pm[:, i * P:(i + 1) * P], oq[:, i * P:(i + 1) * P], sh.ident[:, :])
            last.then_inc(s_turn, 1)

        def max_transposes(q):
            pe.wait_ge(s_msplit, 5 * (q + 1))
            pe.wait_ge(s_used, fills["maxT", q])
            out = pm[:, 0:S // 2].bitcast(BF16)
            for i in range(TPC):
                last = nc.tensor.transpose(out[0:12, i * P:(i + 1) * P],
                                           mparts[:, q % QUADS, i, :, :].rearrange("p k h -> p (k h)"), sh.identb[:, :])
            last.then_inc(s_maxT, 1)

        def turn_out(c):
            pe.wait_ge(s_norm, 4 * (c + 1))
            pe.wait_ge(s_used, fills["oT", c])
            for i in range(TPC):
                last = nc.tensor.transpose(pm[:, i * P:(i + 1) * P], o[:, i, :], sh.ident[:, :])
            last.then_inc(s_oT, 1)

        def project_out(c):
            pe.wait_ge(s_used, fills["y", c])
            for i in range(TPC):
                last = nc.tensor.matmul(pm[:, i * P:(i + 1) * P], oT[:, i * P:(i + 1) * P], wo, start=True, stop=True)
            last.then_inc(s_y, 1)

        for item in plan:
            if item[0] in ("q", "k", "v"):
                project(item[1], item[0])
            elif item[0] == "max":
                c, g = divmod(item[1], QUADS)
                if g == 0 and item[2] == 0:
                    pe.wait_ge(s_stack[c % 2], 16 * 8 * (c // 2 + 1))
                scores_for_max(*item[1:])
            elif item[0] == "maxT":
                max_transposes(item[1])
            elif item[0] == "exp":
                if item[2] == 0:
                    pe.wait_ge(s_mrow[item[1] % 2], 16 * (item[1] // 2 + 1))
                scores_less_max(*item[1:])
            elif item[0] == "pv":
                values(item[1])
            elif item[0] == "turn":
                turn(item[1])
            elif item[0] == "oT":
                turn_out(item[1])
            elif item[0] == "y":
                project_out(item[1])

    @block.scalar
    def _(act):
        before_scalar(act)
        for item in plan:
            if item[0] in ("q", "k"):
                d, k = item[1], "qk".index(item[0])
                if d == 1:
                    act.wait_ge(s_split0, 5)
                elif d:
                    act.wait_ge(s_split, 5 * (d - 1))
                act.wait_ge(s_q, 2 * d + k + 1)
                nc.scalar.activation(qkf[:, k, :], pm[:, :], ACT.Identity,
                                     bias=qk_bias[k] if qk_bias else 0.0).then_inc(s_qf, 1)
                act.wait_ge(s_qf, 2 * d + k + 1)
                act.sem_inc(s_used, 1)
            elif item[0] == "maxT":
                q = item[1]
                act.wait_ge(s_maxT, q + 1)
                if q:
                    act.wait_ge(s_mwrote, 16 * q)
                nc.scalar.copy(mT[:, :], pm[0:12, 0:S // 2].bitcast(BF16)).then_inc(s_mT, 1)
                act.wait_ge(s_mT, q + 1)
                act.sem_inc(s_used, 1)
            elif item[0] == "exp":
                _, q, r = item
                n = EXPS * q + r
                act.wait_ge(s_sc, n + 1)
                if r == 0 and q >= 2:
                    act.wait_ge(s_pv, q - 1)
                out = pa[:, q % 2, r, :] if r < 4 else pb[:, q % 2, :, :].rearrange("p x n -> p (x n)")
                nc.scalar.activation(out, p2[n % 2][:, :], ACT.Exp, scale=scale).then_inc(s_exp, 1)
            elif item[0] == "pv":
                q = item[1]
                act.wait_ge(s_pv, q + 1)
                if q:
                    act.wait_ge(s_turn, q)
                nc.scalar.copy(oq[:, :], po[:, :]).then_inc(s_oq, 1)
            elif item[0] == "oT":
                act.wait_ge(s_oT, item[1] + 1)
                nc.scalar.copy(oT, pm[:, :]).then_inc(s_oTs, 1)
                act.wait_ge(s_oTs, item[1] + 1)
                act.sem_inc(s_used, 1)

    @block.vector
    def _(dve):
        before_vector(dve)
        resid = sh.x if hs is None else hs
        for item in plan:
            if item[0] == "v":
                c = item[1]
                dve.wait_ge(s_v, c + 1)
                if c == 0:
                    dve.wait_ge(s_ones, 3)
                else:
                    dve.wait_ge(s_pv, 4 * c)
                for i in range(TPC):
                    last = nc.vector.tensor_tensor(v32[:, i, :, 0:HD8],
                                                   pm[:, i * P:(i + 1) * P].rearrange("p (h d) -> p h d", h=H8),
                                                   v_bias.rearrange("p (h d) -> p h d", h=H8), ALU.add)
                last.then_inc(s_v32, 1)
                dve.wait_ge(s_v32, c + 1)
                dve.sem_inc(s_used, 1)
            elif item == ("split", 0):
                dve.wait_ge(s_qf, 2)
                st = Steps(dve, s_split0, 0, 5)
                split3(nc.vector, st, [parts[:, k] for k in range(3)], qkf[:, :, :],
                       [rest[:, :, :], qkf[:, :, :]])
                st.end()
            elif item[0] == "max":
                _, q, k, i, h0, n = item
                k += UNITS * q
                m = (i + 1) * P
                dve.wait_ge(s_max, k + 1)
                nc.vector.tensor_reduce(negmax[:, i, h0:h0 + n],
                                        p1[k % 2][:, 0:n * m].rearrange("p (n m) -> p n m", n=n),
                                        AX.X, ALU.max, negate=True).then_inc(s_neg, 1)
            elif item[0] == "maxsplit":
                q = item[1]
                g = q % QUADS
                dve.wait_ge(s_neg, UNITS * (q + 1))
                if q >= QUADS:
                    dve.wait_ge(s_maxT, q - QUADS + 1)
                st = Steps(dve, s_msplit, 5 * q, 5)
                split3(nc.vector, st, [mparts[:, g, :, k, :] for k in range(3)], negmax[:, :, 4 * g:4 * g + 4],
                       [mrest[:, k, :, 4 * g:4 * g + 4] for k in range(2)])
                st.end()
            elif item[0] == "turn":
                q = item[1]
                c, g = divmod(q, QUADS)
                quad = pm[:, :].rearrange("p (t x d) -> p t x d", t=TPC, x=4)
                dve.wait_ge(s_turn, q + 1)
                nc.vector.reciprocal(recip[:, :, :], quad[:, :, :, HD8]).then_inc(s_rec, 1)
                dve.wait_ge(s_rec, q + 1)
                if g == 0 and c >= 1:
                    dve.wait_ge(s_oT, c)
                nc.vector.tensor_tensor(
                    o[:, :, 32 * g:32 * g + 32].rearrange("p t (x d) -> p t x d", x=4), quad[:, :, :, 0:HD8],
                    recip[:, :, :].unsqueeze(3).broadcast_to([P, TPC, 4, HD8]), ALU.mult).then_inc(s_norm, 1)
                dve.wait_ge(s_norm, q + 1)
                dve.sem_inc(s_used, 1)
            elif item[0] == "y":
                d = item[1]
                dve.wait_ge(s_y, d + 1)
                dve.wait_ge(s_bias, d + 1)
                ts = slice(d * TPC, (d + 1) * TPC)
                nc.vector.tensor_tensor(resid[:, ts, :], resid[:, ts, :],
                                        pm[:, :].rearrange("p (t d) -> p t d", t=TPC), ALU.add).then_inc(s_x, 1)
                dve.wait_ge(s_x, d + 1)
                dve.sem_inc(s_used, 1)


def low_rank_attention(sh, stage):
    nc, w, tag = sh.nc, sh.w(stage), f"s{stage}"
    R = 64
    with ExitStack() as ctx:
        bank = lambda m, shape=(P, S): ctx.enter_context(nc.psum_tensor(f"{tag}_{m}", list(shape), F32))
        p1 = [bank(f"for_max{i}") for i in range(2)]
        p2 = [bank(f"scores{i}", (P, 1024)) for i in range(2)]
        po, pm = bank("pv"), bank("odd_jobs")
        weff = ctx.enter_context(nc.sbuf_tensor(f"{tag}_weff", [P, 2, D], F32))
        s_prod, s_weff = (sh.sem(f"{tag}_{m}") for m in ("factors_multiplied", "weff_ready"))
        ln = LayerNorm(sh, ctx, tag, p1)
        pa = ctx.enter_context(nc.sbuf_tensor(f"{tag}_probs_a", [P, 2, 4, 1024], F32))

        def factors_tensor(pe):
            for k in range(2):
                rows = slice(k * R, (k + 1) * R)
                for h in range(H8):
                    last = nc.tensor.matmul(p2[k][:, h * HD8:(h + 1) * HD8],
                                            w["a"][rows, h * D:(h + 1) * D], w["b"][rows, h * HD8:(h + 1) * HD8],
                                            start=True, stop=True)
                last.then_inc(s_prod, 1)
            ln.tensor(pe)
            pe.wait_ge(s_weff, 2)

        def factors_scalar(act):
            for k in range(2):
                act.wait_ge(s_prod, k + 1)
                nc.scalar.copy(weff[:, k, :], p2[k][:, 0:D]).then_inc(s_weff, 1)
            ln.scalar(act)

        def weights_vector(dve):
            ln.vector(dve)
            dve.wait_ge(sh.wsem[stage], 16)

        def weights_gpsimd(pool):
            pool.wait_ge(sh.wsem[stage], 16)

        causal_attention(sh, stage, ctx, ln, pa, p1, p2, po, pm, weff[:, 0, :], weff[:, 1, :], w["v"], w["o"], None,
                         w["v_b"], w["o_b"], HD8 ** -0.5, factors_scalar, weights_vector, factors_tensor,
                         ln.gpsimd, weights_gpsimd)


L2_SEGMENTS = [("ca_w", 3 * D), ("cp_w", D), ("cf_w", 512), ("cm_w", 512), ("ca_b", 2 + D), ("cp_b", D),
               ("cf_b", 4), ("cm_b", D)]


def generated_attention(sh, stage):
    nc, w, tag = sh.nc, sh.w(stage), f"s{stage}"
    width = sum(n for _, n in L2_SEGMENTS)
    with ExitStack() as ctx:
        bank = lambda m, shape=(P, S): ctx.enter_context(nc.psum_tensor(f"{tag}_{m}", list(shape), F32))
        sem = lambda m: sh.sem(f"{tag}_{m}")
        p1 = [bank(f"for_max{i}") for i in range(2)]
        p2 = [bank(f"scores{i}", (P, 1024)) for i in range(2)]
        po, pm = bank("pv"), bank("odd_jobs")
        s_mix, s_mixed = sem("subs_scaled"), sem("subs_summed")
        s_tanh, s_gen = sem("tanh_done"), sem("params_steps")
        n = len(L2_SEGMENTS)
        outer = LayerNorm(sh, ctx, tag + "a", keep=sh.hs)
        ln = LayerNorm(sh, ctx, tag, p1, src=sh.hs, affine=(w["ln1_g"], w["ln1_b"]))
        gen = sh.gen(w)
        pa = ctx.enter_context(nc.sbuf_tensor(f"{tag}_probs_a", [P, 2, 4, 1024], F32))
        s_extra = sem("generators_loaded")
        flat = pa[:, :, :, :].rearrange("p a x n -> p (a x n)")
        sub1, W, bias = (flat[:, k * width:(k + 1) * width] for k in range(3))

        def params_vector(dve):
            outer.vector(dve)
            dve.wait_ge(outer.s_xn, NT)
            ln.vector(dve)
            dve.wait_ge(s_tanh, 1)
            nc.vector.tensor_tensor(w["sub0"], w["sub0"], W, ALU.mult).then_inc(s_gen, 1)
            dve.wait_ge(s_gen, 1)
            nc.vector.tensor_tensor(w["sub0"], w["sub0"], bias, ALU.add).then_inc(s_gen, 1)

        def tanh_scalar(act):
            act.wait_ge(sh.wsem[stage], 16)
            act.wait_ge(s_extra, 16)
            at = 0
            for k, (name, m) in enumerate(L2_SEGMENTS):
                for i, sub in enumerate((w["sub0"], sub1)):
                    nc.scalar.activation(sub[:, at:at + m], sub[:, at:at + m], ACT.Identity,
                                         scale=w["a"][:, 2 * k + i:2 * k + i + 1]).then_inc(s_mix, 1)
                at += m
            ln.scalar(act)
            act.wait_ge(s_mixed, 1)
            nc.scalar.activation(w["sub0"], w["sub0"], ACT.Tanh).then_inc(s_tanh, 1)
            act.wait_ge(s_gen, 2)

        def wait_tensor(pe):
            ln.tensor(pe)
            pe.wait_ge(s_gen, 2)

        def norms_gpsimd(pool):
            outer.gpsimd(pool)
            ln.gpsimd(pool)

        def params_gpsimd(pool):
            pool.wait_ge(s_mix, 2 * n)
            nc.gpsimd.tensor_tensor(w["sub0"], w["sub0"], sub1, ALU.add).then_inc(s_mixed, 1)
            pool.wait_ge(s_gen, 2)

        ca, cab = gen["ca_w"], gen["ca_b"]
        causal_attention(sh, stage, ctx, ln, pa, p1, p2, po, pm, ca[:, 0:D], ca[:, D:2 * D], ca[:, 2 * D:3 * D],
                         gen["cp_w"], (cab[:, 0:1], cab[:, 1:2]), cab[:, 2:2 + D], gen["cp_b"], HD8 ** -0.5,
                         tanh_scalar, params_vector, wait_tensor, norms_gpsimd, params_gpsimd, hs=sh.hs,
                         extra=(flat[:, 0:3 * width], sh.extra[stage], s_extra))


def generated_mlp(sh, stage, hid=512):
    nc, w, tag = sh.nc, sh.w(stage), f"s{stage}b"
    n = hid // P
    gen = sh.gen(w)
    with ExitStack() as ctx:
        sb = lambda m, shape, dt=F32: ctx.enter_context(nc.sbuf_tensor(f"{tag}_{m}", shape, dt))
        sem = lambda m: sh.sem(f"{tag}_{m}")
        bank = lambda m, shape=(P, S): ctx.enter_context(nc.psum_tensor(f"{tag}_{m}", list(shape), F32))
        ps_h = [bank(f"h{i}") for i in range(4)]
        ps_y = [bank(f"y{i}", (P, TPC, D)) for i in range(2)]
        ps_t = [bank(f"t{i}") for i in range(2)]
        ln = LayerNorm(sh, ctx, tag, ps_t, src=sh.hs, affine=(w["ln2_g"], w["ln2_b"]))
        h = sb("h", [P, 4, S])
        s_h, s_gelu, s_y, s_x, s_bias = (sem("h_summed"), sem("h_ready"), sem("y_summed"), sem("x_updated"),
                                         sem("bias_added"))
        block = ctx.enter_context(nc.Block())

        @block.gpsimd
        def _(pool):
            ln.gpsimd(pool)
            for c in range(B):
                ts = slice(c * TPC, (c + 1) * TPC)
                nc.gpsimd.tensor_tensor(sh.x[:, ts, :], sh.x[:, ts, :],
                                        gen["cm_b"].unsqueeze(1).broadcast_to([P, TPC, D]), ALU.add).then_inc(s_bias, 1)

        @block.tensor
        def _(pe):
            pe.sem_inc(s_y, 1)
            ln.tensor(pe)
            pe.wait_ge(ln.ready, B)
            with pe.Fori(0, B) as c:
                for f in range(n):
                    pe.wait_ge(s_gelu, 1 + c * n + f)
                    nc.tensor.matmul(ps_h[f][:, :], gen["cf_w"][:, f * P:(f + 1) * P], sh.xnT[:, cols(c)],
                                     start=True, stop=True).then_inc(s_h, 1)
                pe.wait_ge(s_x, 1 + c)
                for k in range(n):
                    pe.wait_ge(s_gelu, 4 + c * n + k + 1)
                    for i in range(TPC):
                        last = nc.tensor.matmul(ps_y[0][:, i, :], h[:, k, i * P:(i + 1) * P],
                                                gen["cm_w"][:, k * D:(k + 1) * D], start=(k == 0 and i == 0),
                                                stop=(k == n - 1), skip_group_check=True)
                last.then_inc(s_y, 1)

        @block.scalar
        def _(act):
            act.sem_inc(s_gelu, 4)
            ln.scalar(act)
            with act.Fori(0, B) as c:
                for f in range(n):
                    act.wait_ge(s_h, c * n + f + 1)
                    if f == 0:
                        act.wait_ge(s_y, 1 + c)
                    nc.scalar.activation(h[:, f, :], ps_h[f][:, :], ACT.Gelu_apprx_tanh,
                                         bias=gen["cf_b"][:, f:f + 1]).then_inc(s_gelu, 1)

        @block.vector
        def _(dve):
            dve.sem_inc(s_x, 1)
            ln.vector(dve)
            dve.wait_ge(s_bias, B)
            with dve.Fori(0, B) as c:
                dve.wait_ge(s_y, 1 + c + 1)
                nc.vector.tensor_tensor(sh.x[:, tiles(c), :], sh.x[:, tiles(c), :], ps_y[0][:, :, :],
                                        ALU.add).then_inc(s_x, 1)


def generated_block(sh, stage):
    nc = sh.nc
    with ExitStack() as ctx:
        sh.hs = ctx.enter_context(nc.sbuf_tensor("hs", [P, NT, D], F32))
        generated_attention(sh, stage)
        generated_mlp(sh, stage)


def full_start():
    plan = [("xc", 0)]
    for n in range(2):
        for k in range(2):
            plan += [("proj", n, k)] + [("parts", n, k, x) for x in range(2)]
    plan += [("max", 0, x, j) for x in range(2) for j in range(TPC)]
    return plan + [("v", -1, u) for u in range(2 * TPC)] + [("maxT", 0, 0)]


def full_sequence(pairs, more):
    plan = []
    for s in range(pairs):
        for u in range(2 * TPC):
            x, j = divmod(u, TPC)
            plan.append(("exp", s, x, j))
            if s == pairs - 3 and u == 5 and more:
                plan.append(("xc", 1))
            if u == 3:
                plan.append(("maxT", s, 1))
            if s + 1 < pairs or more:
                plan.append(("max", s + 1, x, j))
            if u < 4 and (s + 2 < pairs or more):
                k, x = divmod(u, 2)
                plan += [("proj", s + 2, k)] * (x == 0) + [("parts", s + 2, k, x)]
            if u == 6 and (s + 1 < pairs or more):
                plan.append(("maxT", s + 1, 0))
            if u == 3 and s:
                plan.append(("sum", s - 1))
            if u >= 4 and s:
                plan.append(("pv", s - 1, u - 4))
                plan.append(("recip", s - 1, u - 4))
            if u == 0 and s > 1:
                plan.append(("norm", s - 2))
    plan.append(("norm", pairs - 2))
    plan += [("pv", pairs - 1, j) for j in range(TPC)]
    v = [("v", 0, u) for u in range(2 * TPC)] if more else []
    plan += v[:TPC] + [("sum", pairs - 1)] + [("recip", pairs - 1, j) for j in range(TPC)] + v[TPC:]
    return plan + [("norm", pairs - 1), ("out",)]


def full_attention(sh, stage, heads=16, dh=64):
    nc, w, tag = sh.nc, sh.w(stage), f"s{stage}"
    PAIRS, NV = heads // 2, 2 * TPC
    TILES = 2 * TPC
    SLOTS = 4
    with ExitStack() as ctx:
        sb = lambda m, shape, dt=F32: ctx.enter_context(nc.sbuf_tensor(f"{tag}_{m}", shape, dt))
        sem = lambda m: sh.sem(f"{tag}_{m}")
        bank = lambda m: ctx.enter_context(nc.psum_tensor(f"{tag}_{m}", [P, S], F32))
        pj = [bank(f"odd_jobs{i}") for i in range(2)]
        p1 = [bank(f"for_max{i}") for i in range(2)]
        p2 = [bank(f"scores{i}") for i in range(2)]
        po, psm = bank("pv"), bank("sums")
        ln = LayerNorm(sh, ctx, tag, p1)
        qq = sb("q_hi_hi", [P, SLOTS, 2, S], F32R)
        q2 = sb("q_lo_max", [dh + 2, SLOTS, 2, S], F32R)
        kk = sb("k_hi_lo", [P, SLOTS, 2, S], F32R)
        k2 = sb("k_hi_one", [P, SLOTS, 2, S], F32R)
        ones = sb("ones", [P, dh])
        v = sb("v", [P, TPC, heads * dh])
        xc = sb("xnT_of_sequence", [P, S])
        negmax = sb("negmax", [P, 2, TPC])
        mparts = sb("max_parts", [P, 2, TPC, 2], BF16)
        probs = sb("probs", [P, 2, 2, TPC, S])
        added = sb("probs_added", [P, 2, S])
        acc = sb("probs_sum", [P, 2, 2, S])
        bo = sb("bo", [P, D])
        recip = sb("recip", [P, S])
        oT = sh.spare(ctx, f"{tag}_oT", stage, heads // 2 * S).rearrange("p (k n) -> p k n", n=S)
        s_one = sem("ones_made")
        s_proj, s_hi, s_lo, s_k2 = sem("qk_projected"), sem("hi_done"), sem("lo_done"), sem("k2_done")
        s_v, s_vs = sem("v_projected"), sem("v_in_sbuf")
        s_free = [sem(f"odd_bank_free{i}") for i in range(2)]
        s_max, s_neg, s_split = sem("scores_for_max"), sem("max_done"), sem("max_split_steps")
        s_maxT, s_mrow = sem("max_transposed"), sem("max_rows_ready")
        s_sc, s_exp, s_pv = sem("scores_less_max"), sem("probs_ready"), sem("pv_done")
        s_added, s_acc, s_sum = sem("probs_added_up"), sem("probs_sum_ready"), sem("sums_ready")
        s_rec, s_norm, s_y, s_x = sem("recip_done"), sem("o_normalised"), sem("y_summed"), sem("x_updated")
        s_bias, s_xc, s_bvo, s_bo = sem("o_bias_added"), sem("xc_copied"), sem("bv_projected"), sem("bo_ready")
        start, middle, end = full_start(), full_sequence(PAIRS, True), full_sequence(PAIRS, False)
        odd = lambda plan: [item for item in plan if item[0] in ("proj", "maxT", "v")]
        FILLS = len(odd(middle))
        assert FILLS % 2 == 0 and PAIRS % SLOTS == 0
        fills = {}
        for item in odd(start) + odd(middle):
            fills[item] = len(fills)
        late = {item: len(odd(start)) + n for n, item in enumerate(odd(end))}
        block = ctx.enter_context(nc.Block())
        EXP0, PV0, ACC0, X0 = 2, 2, 4, 1

        def run(eng, emit):
            for item in start:
                emit(0, item, fills)
            with eng.Fori(0, B - 1) as c:
                for item in middle:
                    emit(c, item, fills)
            for item in end:
                emit(B - 1, item, late)

        def freed(eng, n):
            eng.sem_inc(s_free[n % 2], 1)

        @block.sync
        def _(sp):
            sh.load_next(sp, stage)

        @block.gpsimd
        def _(pool):
            pool.sem_inc(s_acc, ACC0)
            nc.gpsimd.memset(ones[:, :], 1.0).then_inc(s_one, 1)
            pool.wait_ge(s_one, 1)
            nc.gpsimd.memset(k2[dh:P, :, :, :].bitcast(F32), 1.0).then_inc(s_one, 1)
            pool.wait_ge(s_one, 2)
            pool.wait_ge(sh.wsem[stage], 16)
            ln.gpsimd(pool)
            pool.wait_ge(ln.s_xn, NT)
            pool.wait_ge(s_bo, 1)
            for c in range(B):
                ts = slice(c * TPC, (c + 1) * TPC)
                nc.gpsimd.tensor_tensor(sh.x[:, ts, :], sh.x[:, ts, :],
                                        bo[:, :].unsqueeze(1).broadcast_to([P, TPC, D]), ALU.add).then_inc(s_bias, 1)

            def emit(c, item, fills):
                if item[0] == "exp" and item[3] == TPC - 1:
                    _, n, x, j = item
                    h = 2 * n + x
                    pool.wait_ge(s_acc, c * heads + h + ACC0)
                    pool.wait_ge(s_exp, c * (heads * TPC) + TPC * (h + 1) + EXP0)
                    nc.gpsimd.tensor_tensor(added[:, :, :], probs[:, n % 2, x, 0:2, :], probs[:, n % 2, x, 2:4, :],
                                            ALU.add).then_inc(s_added, 1)
                    pool.wait_ge(s_added, c * heads + h + 1)
                    nc.gpsimd.tensor_tensor(acc[:, n % 2, x, :], added[:, 0, :], added[:, 1, :],
                                            ALU.add).then_inc(s_acc, 1)
            run(pool, emit)

        @block.tensor
        def _(pe):
            pe.sem_inc(s_pv, PV0)
            pe.wait_ge(sh.wsem[stage], 16)
            ln.tensor(pe)
            pe.wait_ge(ln.ready, B)
            pe.wait_ge(s_one, 2)
            for k in range(PAIRS):
                last = nc.tensor.matmul(psm[:, 0:D], w["bv"][:, k:k + 1].broadcast_to([P, P]),
                                        w["wo"][:, k * D:(k + 1) * D], start=(k == 0), stop=(k == PAIRS - 1))
            last.then_inc(s_bvo, 1)
            pe.wait_ge(s_bo, 1)

            def odd_bank(c, item, fills):
                k = fills[item]
                if k >= 2:
                    pe.wait_ge(s_free[k % 2], c * (FILLS // 2) + k // 2)
                return pj[k % 2]

            def emit(c, item, fills):
                what = item[0]
                if what == "proj":
                    _, n, k = item
                    ps = odd_bank(c, item, fills)
                    if (n, k) in ((0, 0), (PAIRS, 0)):
                        pe.wait_ge(s_xc, c + 1 + (n > 0))
                    at = n % PAIRS * P
                    nc.tensor.matmul(ps[:, :], w["w" + "qk"[k]][:, at:at + P], xc[:, :],
                                     start=True, stop=True).then_inc(s_proj, 1)
                elif what == "v":
                    i, half = divmod(item[2], 2)
                    ps = odd_bank(c, item, fills)
                    nc.tensor.matmul(ps[:, :], xc[:, i * P:(i + 1) * P], w["wv"][:, half * S:(half + 1) * S],
                                     start=True, stop=True).then_inc(s_v, 1)
                elif what == "max":
                    _, n, x, j = item
                    m = TILES * n + TPC * x + j
                    if j == 0:
                        pe.wait_ge(s_hi, c * (2 * heads) + 4 * n + 2 + x + 1)
                    if m >= 2:
                        pe.wait_ge(s_neg, c * (heads * TPC) + m - 1)
                    nc.tensor.matmul(p1[m % 2][:, :], qq[0:dh, n % SLOTS, x, j * P:(j + 1) * P],
                                     kk[0:dh, n % SLOTS, x, :], start=True, stop=True).then_inc(s_max, 1)
                elif what == "maxT":
                    _, n, x = item
                    ps = odd_bank(c, item, fills)
                    pe.wait_ge(s_split, c * (2 * heads) + 2 * (2 * n + x) + 2)
                    for i in range(TPC):
                        last = nc.tensor.matmul(ps[dh:dh + 2, i * P:(i + 1) * P], mparts[:, x, i, :], sh.identb[:, :],
                                                start=True, stop=True)
                    last.then_inc(s_maxT, 1)
                elif what == "exp":
                    _, n, x, j = item
                    m, slot = TILES * n + TPC * x + j, n % SLOTS
                    if j == 0:
                        pe.wait_ge(s_lo, c * (2 * heads) + 4 * n + 2 + x + 1)
                    pe.wait_ge(s_exp, c * (heads * TPC) + m - 1 + EXP0)
                    nc.tensor.matmul(p2[m % 2][:, :], kk[:, slot, x, j * P:(j + 1) * P], qq[:, slot, x, :],
                                     start=True, stop=False)
                    if j == 0:
                        pe.wait_ge(s_k2, c * heads + 2 * n + x + 1)
                        pe.wait_ge(s_mrow, c * heads + 2 * n + x + 1)
                    nc.tensor.matmul(p2[m % 2][:, :], k2[0:dh + 2, slot, x, j * P:(j + 1) * P], q2[:, slot, x, :],
                                     start=False, stop=True).then_inc(s_sc, 1)
                elif what == "pv":
                    _, n, j = item
                    pe.wait_ge(s_exp, c * (heads * TPC) + TILES * n + TPC + j + 1 + EXP0)
                    if j == 0 and n == 0:
                        pe.wait_ge(s_vs, c * NV + NV)
                        pe.wait_ge(s_x, c + X0)
                    elif j == 0:
                        pe.wait_ge(s_norm, c * PAIRS + n)
                    for x in range(2):
                        last = nc.tensor.matmul(po[x * dh:(x + 1) * dh, :], v[:, j, (2 * n + x) * dh:(2 * n + x + 1) * dh],
                                                probs[:, n % 2, x, j, :], start=(j == 0), stop=(j == TPC - 1))
                    if j == TPC - 1:
                        last.then_inc(s_pv, 1)
                elif what == "sum":
                    n = item[1]
                    pe.wait_ge(s_acc, c * heads + 2 * (n + 1) + ACC0)
                    if n:
                        pe.wait_ge(s_rec, c * (PAIRS * TPC) + n * TPC)
                    for x in range(2):
                        last = nc.tensor.matmul(psm[x * dh:(x + 1) * dh, :], ones[:, :], acc[:, n % 2, x, :],
                                                start=True, stop=True)
                    last.then_inc(s_sum, 1)
                elif what == "out":
                    pe.wait_ge(s_norm, c * PAIRS + PAIRS)
                    for p in range(PAIRS):
                        for i in range(TPC):
                            last = nc.tensor.matmul(po[:, i * P:(i + 1) * P], oT[:, p, i * P:(i + 1) * P],
                                                    w["wo"][:, p * D:(p + 1) * D], start=(p == 0 and i == 0),
                                                    stop=(p == PAIRS - 1), skip_group_check=True)
                    last.then_inc(s_y, 1)
            run(pe, emit)

        @block.scalar
        def _(act):
            act.sem_inc(s_exp, EXP0)
            act.wait_ge(sh.wsem[stage], 16)
            ln.scalar(act)
            act.wait_ge(ln.ready, B)

            def emit(c, item, fills):
                what = item[0]
                if what == "xc":
                    if item[1]:
                        act.wait_ge(s_proj, c * heads + heads)
                    nc.scalar.copy(xc[:, :], sh.xnT[:, bass.ds(c * S + item[1] * S, S)]).then_inc(s_xc, 1)
                elif what == "parts":
                    _, n, k, x = item
                    h, slot, rows = (2 * n + x) % heads, n % SLOTS, slice(x * dh, (x + 1) * dh)
                    ps, bias = pj[fills[("proj", n, k)] % 2][rows, :], w["b" + "qk"[k]][rows, h:h + 1]
                    act.wait_ge(s_proj, c * heads + 2 * n + k + 1)
                    if k:
                        nc.scalar.activation(k2[0:dh, slot, x, :], ps, ACT.Identity, bias=bias).then_inc(s_k2, 1)
                    if x or not k:
                        nc.scalar.activation((kk if k else qq)[dh:P, slot, x, :], ps, ACT.Identity, bias=bias)
                    nc.scalar.activation((kk if k else qq)[0:dh, slot, x, :], ps, ACT.Identity,
                                         bias=bias).then_inc(s_hi, 1)
                elif what == "maxT":
                    _, n, x = item
                    act.wait_ge(s_maxT, c * heads + 2 * n + x + 1)
                    nc.scalar.copy(q2[dh:dh + 2, n % SLOTS, x, :], pj[fills[item] % 2][dh:dh + 2, :]).then_inc(s_mrow, 1)
                    act.wait_ge(s_mrow, c * heads + 2 * n + x + 1)
                    freed(act, fills[item])
                elif what == "v":
                    _, nxt, u = item
                    i, half = divmod(u, 2)
                    t = (nxt + 1) * NV + u + 1
                    act.wait_ge(s_v, c * NV + t)
                    if nxt == 0 and u == 0:
                        act.wait_ge(s_pv, c * PAIRS + PAIRS + PV0)
                    nc.scalar.copy(v[:, i, half * S:(half + 1) * S], pj[fills[item] % 2][:, :]).then_inc(s_vs, 1)
                    act.wait_ge(s_vs, c * NV + t)
                    freed(act, fills[item])
                elif what == "exp":
                    _, n, x, j = item
                    m = TILES * n + TPC * x + j
                    act.wait_ge(s_sc, c * (heads * TPC) + m + 1)
                    if x == 0 and j == 0:
                        act.wait_ge(s_pv, c * PAIRS + n - 1 + PV0)
                        act.wait_ge(s_acc, c * heads + 2 * (n - 1) + ACC0)
                    nc.scalar.activation(probs[:, n % 2, x, j, :], p2[m % 2][:, :], ACT.Exp,
                                         scale=dh ** -0.5).then_inc(s_exp, 1)
            run(act, emit)

        @block.vector
        def _(dve):
            dve.sem_inc(s_x, X0)
            dve.wait_ge(sh.wsem[stage], 16)
            ln.vector(dve)
            dve.wait_ge(s_bvo, 1)
            nc.vector.tensor_tensor(bo[:, :], psm[:, 0:D], w["bo"], ALU.add).then_inc(s_bo, 1)

            def emit(c, item, fills):
                what = item[0]
                if what == "parts":
                    _, n, k, x = item
                    h, slot, rows = (2 * n + x) % heads, n % SLOTS, slice(x * dh, (x + 1) * dh)
                    m = 4 * n + 2 * k + x
                    fill = fills[("proj", n, k)]
                    dve.wait_ge(s_hi, c * (2 * heads) + m + 1)
                    low, hi = (kk[dh:P, slot, x, :], kk) if k else (q2[0:dh, slot, x, :], qq)
                    nc.vector.scalar_tensor_tensor(out=low, in0=pj[fill % 2][rows, :],
                                                   scalar=w["b" + "qk"[k]][rows, h:h + 1],
                                                   in1=hi[rows, slot, x, :].bitcast(F32),
                                                   op0=ALU.add, op1=ALU.subtract).then_inc(s_lo, 1)
                    if x:
                        dve.wait_ge(s_lo, c * (2 * heads) + m + 1)
                        freed(dve, fill)
                elif what == "max":
                    _, n, x, j = item
                    m, h = TILES * n + TPC * x + j, 2 * n + x
                    if j == 0 and n:
                        dve.wait_ge(s_split, c * (2 * heads) + 2 * (h - 2) + 2)
                    dve.wait_ge(s_max, c * (heads * TPC) + m + 1)
                    nc.vector.tensor_reduce(negmax[:, x, j:j + 1], p1[m % 2][:, :], AX.X, ALU.max,
                                            negate=True).then_inc(s_neg, 1)
                    if j == TPC - 1:
                        dve.wait_ge(s_neg, c * (heads * TPC) + m + 1)
                        if n:
                            dve.wait_ge(s_maxT, c * heads + h - 1)
                        nc.vector.tensor_copy(mparts[:, x, :, 0], negmax[:, x, :]).then_inc(s_split, 1)
                        dve.wait_ge(s_split, c * (2 * heads) + 2 * h + 1)
                        nc.vector.tensor_tensor(mparts[:, x, :, 1], negmax[:, x, :], mparts[:, x, :, 0],
                                                ALU.subtract).then_inc(s_split, 1)
                elif what == "recip":
                    _, n, j = item
                    at = slice(j * P, (j + 1) * P)
                    dve.wait_ge(s_sum, c * PAIRS + n + 1)
                    if n:
                        dve.wait_ge(s_norm, c * PAIRS + n)
                    nc.vector.reciprocal(recip[:, at], psm[:, at]).then_inc(s_rec, 1)
                elif what == "norm":
                    n = item[1]
                    dve.wait_ge(s_pv, c * PAIRS + n + 1 + PV0)
                    dve.wait_ge(s_rec, c * (PAIRS * TPC) + (n + 1) * TPC)
                    nc.vector.tensor_tensor(oT[:, n, :], po[:, :], recip[:, :], ALU.mult).then_inc(s_norm, 1)
                elif what == "out":
                    dve.wait_ge(s_y, c + 1)
                    dve.wait_ge(s_bias, B)
                    nc.vector.tensor_tensor(sh.x[:, tiles(c), :], sh.x[:, tiles(c), :],
                                            po[:, :].rearrange("p (t d) -> p t d", t=TPC), ALU.add).then_inc(s_x, 1)
            run(dve, emit)


def dispatched_ffn(sh, stage, n_exp=8, hid=512, top=2):
    nc, w, tag = sh.nc, sh.w(stage), f"s{stage}"
    cap = top * (-(-T // n_exp))
    slots = n_exp * cap
    U = top * NT
    n_up, n_slot = hid // P, cap // P
    assert cap == S
    GROUP = 4
    with ExitStack() as ctx:
        sb = lambda m, shape, dt=F32: ctx.enter_context(nc.sbuf_tensor(f"{tag}_{m}", shape, dt))
        sem = lambda m: sh.sem(f"{tag}_{m}")
        bank = lambda m: ctx.enter_context(nc.psum_tensor(f"{tag}_{m}", [P, S], F32))
        ps_t = [bank(f"turned{i}") for i in range(2)]
        ps_up = [bank(f"up{i}") for i in range(2)]
        ps_y = [bank(f"y{i}") for i in range(2)]
        ps_route, ps_count = bank("route"), bank("count")
        ROW = D + 1
        disp = nc.dram_tensor("dispatched", [slots + top * T, ROW], F32, kind="Internal").ap()
        outs = nc.dram_tensor("expert_rows", [top * T + slots, D], F32, kind="Internal").ap()
        xn = sb("xn", [P, NT, ROW])
        ln = LayerNorm(sh, ctx, tag, ps_t, keep=xn[:, :, 0:D])
        token_i = sb("token_int", [P, NT], mybir.dt.int32)
        empty = sb("empty_slots", [P, slots // P, ROW])
        empty_i = sb("empty_int", [P, slots // P], mybir.dt.int32)
        slot_i = sb("slot_int", [P, n_slot], mybir.dt.int32)
        slot = sb("slot", [P, n_slot])
        second = sb("second_choice", [P, n_exp, n_slot])
        place = sb("place", [P, 2, n_slot])
        place_i = sb("place_int", [P, 2, n_slot], U32)
        tri = sb("tri", [P, P], BF16)
        ones = sb("ones", [P, P], BF16)
        before = sb("before", [P, n_exp, n_exp])
        base = sb("slot_base", [P, n_exp])
        spare_i = sb("spare_int", [P, U], mybir.dt.int32)
        spare = sb("spare", [P, U])
        probs = sb("probs", [P, NT, n_exp])
        stat = sb("stat", [P, NT])
        rank = sb("rank", [P, NT, n_exp])
        gt = sb("gt", [P, NT, n_exp, n_exp])
        eq = sb("eq", [P, NT, n_exp, n_exp])
        chosen = sb("chosen", [P, U, n_exp], BF16)
        picked = sb("picked", [P, U, n_exp])
        gate = sb("gate", [P, U])
        total = sb("gate_sum", [P, NT])
        upto = sb("counts_up_to", [P, 2, NT + U, n_exp])
        loc = sb("loc", [P, U])
        first = sb("first_slot", [P, U])
        valid = sb("valid", [P, U])
        where = sb("where", [P, U])
        idx = sb("idx", [P, U], U32)
        rows = sb("rows", [P, 3, n_slot, ROW])
        rowsT = sb("rowsT", [P, 2, S])
        hidden = sb("hidden", [P, 2, n_up, S])
        y = sb("y", [P, 2, n_slot, D])
        back = sb("back", [P, U, D])
        w1, w2 = sb("w1", [P, n_exp * hid]), sb("w2", [P, n_exp * hid])
        b2 = sb("b2", [P, n_exp * D])
        s_w1, s_w2 = sem("w1_loaded"), sem("w2_b2_loaded")
        s_const, s_zero, s_zeroed = sem("constants_made"), sem("zeros_made"), sem("slots_cleared")
        s_number, s_place, s_placed = sem("numbers_made"), sem("place_steps"), sem("places_ready")
        s_before, s_base = sem("before_made"), sem("base_made")
        s_logits, s_less, s_exp, s_chosen, s_count = (sem("logits_ready"), sem("logits_less_max"), sem("exp_done"),
                                                      sem("choices_ready"), sem("counts_ready"))
        s_route, s_idx = sem("route_steps"), sem("idx_ready")
        s_put, s_rows, s_turn, s_rowsT = sem("rows_put"), [sem(f"rows_loaded{i}") for i in range(3)], sem("rows_transposed"), sem("rowsT_ready")
        s_up, s_hidden, s_down, s_y = sem("up_done"), sem("hidden_ready"), sem("down_done"), sem("y_ready")
        s_out, s_x = [sem(f"y_stored{i}") for i in range(2)], sem("x_steps")
        s_back = [sem(f"rows_back{i}") for i in range(U // GROUP)]
        groups = [k * B + c for c in range(B) for k in range(top)]
        block = ctx.enter_context(nc.Block())

        @block.sync
        def _(sp):
            sh.load_next(sp, stage)
            n = n_exp * hid
            sp.dma_start(w1[:, :], sh.extra[stage][:, 0:n]).then_inc(s_w1, 16)
            sp.dma_start(w2[:, :], sh.extra[stage][:, n:2 * n]).then_inc(s_w2, 16)
            sp.dma_start(b2[:, :], sh.extra[stage][:, 2 * n:]).then_inc(s_w2, 16)
            sp.wait_ge(s_zero, 2)
            sp.dma_start(disp[0:slots].rearrange("(p r) d -> p r d", p=P), empty[:, :, :]).then_inc(s_zeroed, 16)
            sp.dma_start(outs[0:top * T].rearrange("(p r) d -> p r d", p=P),
                         empty[:, :, 0:D]).then_inc(s_zeroed, 16)
            sp.wait_ge(s_put, 16 * U)
            for e in range(n_exp):
                if e >= 3:
                    sp.wait_ge(s_turn, e - 2)
                    sp.wait_ge(s_placed, e - 2)
                sp.dma_start(rows[:, e % 3, :, :], disp[e * cap:(e + 1) * cap].rearrange(
                    "(t p) d -> p t d", p=P)).then_inc(s_rows[e % 3], 16)
            for half in s_out:
                sp.wait_ge(half, 16 * n_slot * n_exp // 2)
            for g in groups:
                at = g * GROUP
                sp.dma_start(back[:, at:at + GROUP, :], outs[at * P:(at + GROUP) * P].rearrange(
                    "(t p) d -> p t d", p=P)).then_inc(s_back[g], 16)

        @block.gpsimd
        def _(pool):
            nc.gpsimd.memset(ones[:, :], 1.0).then_inc(s_const, 1)
            nc.gpsimd.memset(tri[:, :], 1.0).then_inc(s_const, 1)
            nc.gpsimd.memset(upto[:, :, :, :], 0.0).then_inc(s_const, 1)
            nc.gpsimd.iota(spare_i[:, :], pattern=[[P, U]], base=slots, channel_multiplier=1).then_inc(s_const, 1)
            pool.wait_ge(s_const, 4)
            nc.gpsimd.affine_select(out=tri[:, :], in_=tri[:, :], compare_op=ALU.is_gt, fill=0.0, base=0,
                                    pattern=[[1, P]], channel_multiplier=-1).then_inc(s_const, 1)
            nc.gpsimd.iota(token_i[:, :], pattern=[[P, NT]], base=0, channel_multiplier=1).then_inc(s_number, 1)
            nc.gpsimd.iota(slot_i[:, :], pattern=[[P, n_slot]], base=0, channel_multiplier=1).then_inc(s_number, 1)
            nc.gpsimd.iota(empty_i[:, :], pattern=[[1, slots // P]], base=T,
                           channel_multiplier=slots // P).then_inc(s_number, 1)
            nc.gpsimd.memset(empty[:, :, 0:D], 0.0).then_inc(s_zero, 1)
            pool.wait_ge(s_number, 3)
            nc.gpsimd.tensor_copy(empty[:, :, D], empty_i[:, :]).then_inc(s_zero, 1)
            make_before(nc, pool, before, n_exp, s_before)
            ln.gpsimd(pool)
            pool.wait_ge(s_idx, 1)
            pool.wait_ge(s_zeroed, 32)
            for u in range(U):
                nc.gpsimd.indirect_dma_start(disp, bass.IndirectOffsetOnAxis(ap=idx[:, u:u + 1], axis=0),
                                             xn[:, u % NT, :], None).then_inc(s_put, 16)
            for e in range(n_exp):
                pool.wait_ge(s_placed, e + 1)
                pool.wait_ge(s_y, e + 1)
                for i in range(n_slot):
                    nc.gpsimd.indirect_dma_start(outs, bass.IndirectOffsetOnAxis(ap=place_i[:, e % 2, i:i + 1], axis=0),
                                                 y[:, e % 2, i, :], None).then_inc(s_out[e % 2], 16)

        @block.tensor
        def _(pe):
            pe.wait_ge(sh.wsem[stage], 16)
            ln.tensor(pe)
            pe.wait_ge(ln.ready, B)
            logits = ps_route[:, 0:NT * n_exp].rearrange("p (t e) -> p t e", t=NT)
            for t in range(NT):
                last = nc.tensor.matmul(logits[:, t, :], sh.xnT[:, t * P:(t + 1) * P], w["wg"],
                                        start=True, stop=True)
            last.then_inc(s_logits, 1)
            pe.wait_ge(s_const, 5)
            pe.wait_ge(s_chosen, 1)
            flat = chosen[:, :, :].rearrange("p u e -> p (u e)")
            nc.tensor.matmul(ps_count[:, 0:U * n_exp], tri[:, :], flat, start=True, stop=True)
            nc.tensor.matmul(ps_count[:, U * n_exp:], ones[:, :], flat, start=True, stop=True).then_inc(s_count, 1)

            def turn(e):
                pe.wait_ge(s_rows[e % 3], 16 * (e // 3 + 1))
                if e >= 2:
                    pe.wait_ge(s_rowsT, e - 1)
                for i in range(n_slot):
                    last = nc.tensor.transpose(ps_t[e % 2][:, i * P:(i + 1) * P], rows[:, e % 3, i, 0:D], sh.ident[:, :])
                last.then_inc(s_turn, 1)

            def up(e):
                pe.wait_ge(s_rowsT, e + 1)
                for f in range(n_up):
                    m = e * n_up + f
                    if m >= 2:
                        pe.wait_ge(s_hidden, m - 1)
                    nc.tensor.matmul(ps_up[m % 2][:, :], w1[:, m * P:(m + 1) * P], rowsT[:, e % 2, :],
                                     start=True, stop=True).then_inc(s_up, 1)

            def down(e):
                pe.wait_ge(s_hidden, (e + 1) * n_up)
                if e >= 2:
                    pe.wait_ge(s_y, e - 1)
                for i in range(n_slot):
                    for f in range(n_up):
                        m = e * n_up + f
                        last = nc.tensor.matmul(ps_y[e % 2][:, i * P:(i + 1) * P], hidden[:, e % 2, f, i * P:(i + 1) * P],
                                                w2[:, m * D:(m + 1) * D], start=(f == 0 and i == 0),
                                                stop=(f == n_up - 1), skip_group_check=True)
                last.then_inc(s_down, 1)

            turn(0)
            pe.wait_ge(s_w1, 16)
            pe.wait_ge(s_w2, 32)
            for e in range(n_exp):
                up(e)
                if e + 1 < n_exp:
                    turn(e + 1)
                if e >= 1:
                    down(e - 1)
            down(n_exp - 1)

        @block.scalar
        def _(act):
            act.wait_ge(sh.wsem[stage], 16)
            ln.scalar(act)
            act.wait_ge(s_less, 1)
            nc.scalar.activation(probs[:, :, :], probs[:, :, :], ACT.Exp).then_inc(s_exp, 1)
            for e in range(n_exp):
                act.wait_ge(s_turn, e + 1)
                if e >= 2:
                    act.wait_ge(s_up, (e - 1) * n_up)
                nc.scalar.copy(rowsT[:, e % 2, :], ps_t[e % 2][:, :]).then_inc(s_rowsT, 1)
                for f in range(n_up):
                    m = e * n_up + f
                    act.wait_ge(s_up, m + 1)
                    if e >= 2 and f == 0:
                        act.wait_ge(s_down, e - 1)
                    nc.scalar.activation(hidden[:, e % 2, f, :], ps_up[m % 2][:, :], ACT.Relu,
                                         bias=w["b1"][:, m:m + 1]).then_inc(s_hidden, 1)

        @block.vector
        def _(dve):
            for e in range(n_exp):
                last = nc.vector.memset(base[:, e:e + 1], float(e * cap))
            last.then_inc(s_base, 1)
            ln.vector(dve)
            dve.wait_ge(s_number, 3)
            nc.vector.tensor_copy(xn[:, :, D], token_i[:, :]).then_inc(s_number, 1)
            nc.vector.tensor_copy(slot[:, :], slot_i[:, :]).then_inc(s_number, 1)
            st = Steps(dve, s_route, 0, ROUTE_DISPATCH_STEPS)
            logits = ps_route[:, 0:NT * n_exp].rearrange("p (t e) -> p t e", t=NT)
            wide = lambda a: a.unsqueeze(2).broadcast_to([P, a.shape[1], n_exp])
            per_e = lambda a: a.unsqueeze(1).broadcast_to([P, U, n_exp])
            twice = lambda a: a.unsqueeze(1).broadcast_to([P, top] + a.shape[1:])
            by_choice = lambda a: a.rearrange("p (k t) e -> p k t e", k=top)
            dve.wait_ge(s_logits, 1)
            st.then(nc.vector.tensor_reduce(stat[:, :], logits, AX.X, ALU.max))
            nc.vector.tensor_tensor(probs[:, :, :], logits, wide(stat[:, :]), ALU.subtract).then_inc(s_less, 1)
            dve.wait_ge(s_exp, 1)
            st.then(nc.vector.tensor_reduce(stat[:, :], probs[:, :, :], AX.X, ALU.add))
            st.then(nc.vector.reciprocal(stat[:, :], stat[:, :]))
            st.then(nc.vector.tensor_tensor(probs[:, :, :], probs[:, :, :], wide(stat[:, :]), ALU.mult))
            dve.wait_ge(s_before, 2)
            dve.wait_ge(s_base, 1)
            ranks(nc, st, rank[:, :, :], probs[:, :, :], before[:, :, :], gt[:, :, :, :], eq[:, :, :, :])
            for k in range(top):
                last = nc.vector.tensor_scalar(chosen[:, k * NT:(k + 1) * NT, :], rank[:, :, :], float(k), None,
                                               ALU.is_equal)
                st.did(last)
            st.wait()
            dve.sem_inc(s_chosen, 1)
            for k in range(top):
                st.did(nc.vector.tensor_tensor(picked[:, k * NT:(k + 1) * NT, :], chosen[:, k * NT:(k + 1) * NT, :],
                                               probs[:, :, :], ALU.mult))
            st.wait()
            st.then(nc.vector.tensor_reduce(gate[:, :], picked[:, :, :], AX.X, ALU.add))
            st.then(nc.vector.tensor_tensor(total[:, :], gate[:, 0:NT], gate[:, NT:], ALU.add))
            st.then(nc.vector.reciprocal(total[:, :], total[:, :]))
            for k in range(top):
                st.did(nc.vector.tensor_tensor(gate[:, k * NT:(k + 1) * NT], gate[:, k * NT:(k + 1) * NT], total[:, :],
                                               ALU.mult))
            dve.wait_ge(s_count, 1)
            dve.wait_ge(s_const, 3)
            counts = ps_count[:, U * n_exp:].rearrange("p (u e) -> p u e", u=U)
            within = ps_count[:, 0:U * n_exp].rearrange("p (u e) -> p u e", u=U)
            st.then(nc.vector.tensor_copy(upto[:, 0, NT:, :], counts))
            shift, k = 1, 0
            while shift < U:
                st.then(nc.vector.tensor_tensor(upto[:, 1 - k, NT:, :], upto[:, k, NT:, :],
                                                upto[:, k, NT - shift:NT + U - shift, :], ALU.add))
                shift, k = 2 * shift, 1 - k
            st.then(nc.vector.tensor_tensor(picked[:, :, :], within, upto[:, k, NT - 1:NT + U - 1, :], ALU.add))
            st.then(nc.vector.tensor_tensor(picked[:, :, :], picked[:, :, :], chosen[:, :, :], ALU.mult))
            st.then(nc.vector.tensor_reduce(loc[:, :], picked[:, :, :], AX.X, ALU.add))
            st.then(nc.vector.tensor_tensor(picked[:, :, :], chosen[:, :, :], per_e(base[:, :]), ALU.mult))
            st.then(nc.vector.tensor_reduce(first[:, :], picked[:, :, :], AX.X, ALU.add))
            st.did(nc.vector.tensor_scalar(valid[:, :], loc[:, :], cap - 0.5, None, ALU.is_lt))
            st.did(nc.vector.tensor_copy(spare[:, :], spare_i[:, :]))
            st.then(nc.vector.scalar_tensor_tensor(out=where[:, :], in0=loc[:, :], scalar=cap - 1.0, in1=first[:, :],
                                                   op0=ALU.min, op1=ALU.add))
            st.did(nc.vector.tensor_tensor(gate[:, :], gate[:, :], valid[:, :], ALU.mult))
            st.then(nc.vector.tensor_tensor(where[:, :], where[:, :], spare[:, :], ALU.subtract))
            st.then(nc.vector.tensor_tensor(where[:, :], where[:, :], valid[:, :], ALU.mult))
            st.then(nc.vector.tensor_tensor(where[:, :], where[:, :], spare[:, :], ALU.add))
            st.end()
            dve.wait_ge(s_number, 5)
            nc.vector.tensor_copy(idx[:, :], where[:, :]).then_inc(s_idx, 1)
            at = Steps(dve, s_place, 0, 2 + n_exp)
            n_first = upto[:, k, NT + NT - 1, :].unsqueeze(2).broadcast_to([P, n_exp, n_slot])
            at.then(nc.vector.tensor_tensor(second[:, :, :], slot[:, :].unsqueeze(1).broadcast_to([P, n_exp, n_slot]),
                                            n_first, ALU.is_ge))
            at.then(nc.vector.tensor_scalar(second[:, :, :], second[:, :, :], float(T), None, ALU.mult))
            dve.wait_ge(s_w2, 32)
            for e in range(n_exp):
                dve.wait_ge(s_rows[e % 3], 16 * (e // 3 + 1))
                if e >= 2:
                    dve.wait_ge(s_out[e % 2], 16 * n_slot * (e // 2))
                at.then(nc.vector.tensor_tensor(place[:, e % 2, :], rows[:, e % 3, :, D], second[:, e, :], ALU.add))
                nc.vector.tensor_copy(place_i[:, e % 2, :], place[:, e % 2, :]).then_inc(s_placed, 1)
                dve.wait_ge(s_down, e + 1)
                nc.vector.tensor_tensor(y[:, e % 2, :, :], ps_y[e % 2][:, :].rearrange("p (t d) -> p t d", t=n_slot),
                                        b2[:, e * D:(e + 1) * D].unsqueeze(1).broadcast_to([P, n_slot, D]),
                                        ALU.add).then_inc(s_y, 1)
            at.end()
            for n, u in enumerate(g * GROUP + i for g in groups for i in range(GROUP)):
                if u % GROUP == 0:
                    dve.wait_ge(s_back[u // GROUP], 16)
                if u >= NT:
                    dve.wait_ge(s_x, n - GROUP + 1)
                nc.vector.scalar_tensor_tensor(out=sh.x[:, u % NT, :], in0=back[:, u, :], scalar=gate[:, u:u + 1],
                                               in1=sh.x[:, u % NT, :], op0=ALU.mult, op1=ALU.add).then_inc(s_x, 1)


ROUTE_DISPATCH_STEPS = 36


def program(nc, x_in, weights, extra, out):
    with ExitStack() as ctx:
        sh = Shared(nc, ctx, weights, extra)
        sem = lambda n: ctx.enter_context(nc.semaphore(n))
        s_x, s_zero, s_id, s_half, s_out = (sem("x_loaded"), sem("ident_cleared"), sem("ident_made"),
                                            sem("mhalf_made"), sem("x_stored"))
        with nc.Block() as block:
            @block.sync
            def _(sp):
                for c in range(B):
                    sp.dma_start(sh.x[:, c * TPC:(c + 1) * TPC, :],
                                 x_in[c].rearrange("(t p) d -> p t d", p=P)).then_inc(s_x, 16)
                sh.load_weights(sp, list(weights)[0])
                sp.wait_ge(s_x, 16 * B)

            @block.gpsimd
            def _(pool):
                nc.gpsimd.memset(sh.mhalf[:, :], -0.5).then_inc(s_half, 1)
                for n, m in enumerate((sh.ident, sh.identb)):
                    nc.gpsimd.memset(m[:, :], 0.0).then_inc(s_zero, 1)
                    pool.wait_ge(s_zero, n + 1)
                    nc.gpsimd.affine_select(out=m[:, :], in_=m[:, :], compare_op=ALU.not_equal, fill=1.0,
                                            base=0, pattern=[[-1, P]], channel_multiplier=1).then_inc(s_id, 1)
        for stage in weights:
            RUN[stage](sh, stage)
            sh.stage_over()
        with nc.Block() as block:
            @block.sync
            def _(sp):
                for c in range(B):
                    sp.dma_start(out[c].rearrange("(t p) d -> p t d", p=P),
                                 sh.x[:, c * TPC:(c + 1) * TPC, :]).then_inc(s_out, 16)
                sp.wait_ge(s_out, 16 * B)
        sh.old_sems.close()


RUN = {
    0: gated_linear_attention,
    1: lambda sh, s: routed_ffn(sh, s, 16, 64, 128, ACT.Sigmoid, route_groups, ROUTE_GROUPS_STEPS),
    3: lambda sh, s: routed_ffn(sh, s, 8, 256, 256, ACT.Copy, route_top1, ROUTE_TOP1_STEPS),
    2: low_rank_attention,
    4: generated_block,
    5: ternary_ffn,
    6: full_attention,
    7: dispatched_ffn,
}


def _t(a):
    import numpy as np
    return np.moveaxis(a, -1, 0).reshape(a.shape[-1], -1)


def _fold(a):
    k = a.shape[0] // P
    return a.reshape(k, P, -1).transpose(1, 0, 2).reshape(P, -1)


def _col(v):
    return v.reshape(-1, P).T


def _rows(v):
    import numpy as np
    return np.broadcast_to(v.reshape(1, -1), (P, v.size))


def _layout(stage, a):
    import numpy as np
    cat = lambda *parts: np.concatenate(parts, axis=1)
    if stage == 0:
        return [("wq", _t(a["Wq"])), ("wk", _t(a["Wk"])), ("wgk1", _t(a["Wgk1"])), ("wgk2", _t(a["Wgk2"])),
                ("wvg", cat(_t(a["Wv"]), _t(a["Wg"]))), ("wout", _fold(_t(a["Wout"]))),
                ("bgk2", _rows(a["bgk2"])), ("rms_w", _rows(a["rms_w"]))]
    if stage == 1:
        down = cat(_fold(_t(a["w2_s"])), _fold(a["w2_e"].transpose(0, 2, 1).reshape(-1, D)))
        return [("router", _t(a["w_gate"])), ("gate", cat(_t(a["w1_s"]), _t(a["w1_e"]))),
                ("up", cat(_t(a["w3_s"]), _t(a["w3_e"]))), ("down", down)]
    if stage == 2:
        factor = np.concatenate([a["q_a"].transpose(2, 0, 1).reshape(64, -1), a["k_a"].transpose(2, 0, 1).reshape(64, -1)])
        other = np.concatenate([a["q_b"].transpose(1, 0, 2).reshape(64, -1), a["k_b"].transpose(1, 0, 2).reshape(64, -1)])
        return [("a", factor), ("b", other), ("v", _t(a["v_w"])), ("o", _t(a["o_w"])), ("v_b", _rows(a["v_b"])),
                ("o_b", _rows(a["o_b"]))]
    if stage == 3:
        down = cat(_fold(_t(a["w_down_s"])), _fold(a["down"].transpose(0, 2, 1).reshape(-1, D)))
        return [("router", _t(a["router"])), ("gate", cat(_t(a["w_gate_s"]), _t(a["gate"]))),
                ("up", cat(_t(a["w_up_s"]), _t(a["up"]))), ("down", down)]
    if stage == 4:
        def column(p):
            ca_b, cf_b = a["ca_" + p + "_b"], a["cf_" + p + "_b"]
            return cat(_t(a["ca_" + p + "_w"]), _t(a["cp_" + p + "_w"]), _t(a["cf_" + p + "_w"]),
                       _fold(_t(a["cm_" + p + "_w"])), _col(ca_b[:2 * D]), _rows(ca_b[2 * D:]),
                       _rows(a["cp_" + p + "_b"]), _col(cf_b), _rows(a["cm_" + p + "_b"]))
        subs = {}
        for k in range(2):
            for m in ("ca", "cp", "cf", "cm"):
                for p in "wb":
                    subs[f"{m}_{k}_{p}"] = a[f"{m}_sub_{p}"][k]
        a = dict(a, **subs)
        mix = cat(*[_rows(a[f"{m}_Wl_{p}"]) for p in "wb" for m in ("ca", "cp", "cf", "cm")])
        return [("sub0", column("0")), ("a", mix)] + \
            [(f"ln{i}_{p}", _col(a[f"ln{i}_{p}"])) for i in (1, 2) for p in "gb"] + \
            [("extra", cat(column("1"), column("W"), column("B")))]
    if stage == 6:
        double = lambda b: np.tile(b.reshape(16, 64).T, (2, 1))
        return [("wq", _t(a["Wq"])), ("wk", _t(a["Wk"])), ("wv", _t(a["Wv"])),
                ("wo", _fold(_t(a["Wo"]))), ("bq", double(a["bq"])), ("bk", double(a["bk"])),
                ("bv", _col(a["bv"])), ("bo", _rows(a["bo"]))]
    if stage == 7:
        down = a["w2"].reshape(8, 4, P, D).transpose(2, 0, 1, 3).reshape(P, -1)
        return [("wg", a["wg"]), ("b1", a["b1"].reshape(-1, P).T),
                ("extra", cat(a["w1"].transpose(1, 0, 2).reshape(D, -1), down, _rows(a["b2"])))]
    if stage == 5:
        return [("w1", _t(a["w1_w"])), ("w2", _t(a["w2_w"])), ("h1", _fold(_t(a["h1_w"]))),
                ("h2", _fold(_t(a["h2_w"]))), ("w3", _fold(_t(a["w3_w"]))), ("w1_s", _col(a["w1_s"])),
                ("w2_s", _col(a["w2_s"])), ("h1_s", _col(a["h1_s"])), ("h2_s", _col(a["h2_s"])),
                ("w3_s", _rows(a["w3_s"]))]


_NAMES = ["L0_attn", "L0_ffn", "L1_attn", "L1_ffn", "L2_attn", "L2_ffn", "L3_attn", "L3_ffn"]


def kernel(**inputs):
    import numpy as np
    import concourse.bacc as bacc
    from concourse.bass_utils import run_bass_kernel_spmd

    nc = bacc.Bacc("TRN2", target_bir_lowering=False, num_devices=1)
    arrays, weights = {"x_in": np.ascontiguousarray(inputs["L0_attn_x"])}, {}
    x_in = nc.dram_tensor("x_in", [B, S, D], F32, kind="ExternalInput").ap()
    extra = {}
    for stage in STAGES:
        mine = {k[len(_NAMES[stage]) + 1:]: np.asarray(v) for k, v in inputs.items()
                if k.startswith(_NAMES[stage] + "_")}
        parts = _layout(stage, mine)
        if parts[-1][0] == "extra":
            late = np.ascontiguousarray(parts.pop()[1])
            arrays[f"extra{stage}"] = late
            extra[stage] = nc.dram_tensor(f"extra{stage}", list(late.shape), F32, kind="ExternalInput").ap()
        packed = np.zeros((P, sum(v.shape[1] for _, v in parts)), np.float32)
        at, table = 0, []
        for name, v in parts:
            packed[:v.shape[0], at:at + v.shape[1]] = v
            at += v.shape[1]
            table.append((name, v.shape[0], v.shape[1]))
        arrays[f"w{stage}"] = packed
        weights[stage] = (nc.dram_tensor(f"w{stage}", list(packed.shape), F32, kind="ExternalInput").ap(), table)
    out = nc.dram_tensor("out", [B, S, D], F32, kind="ExternalOutput").ap()
    program(nc, x_in, weights, extra, out)
    return run_bass_kernel_spmd(nc, [arrays], core_ids=[0]).results[0]["out"]
```
